# Optimizing a Trainium2 kernel written in Bass

```python
import numpy as np
import jax
import jax.numpy as jnp

def _softmax(x, axis=-1):
    return jax.nn.softmax(x, axis=axis)

def _gelu(x):
    return jax.nn.gelu(x, approximate=True)

def _silu(x):
    return jax.nn.silu(x)

def _sigmoid(x):
    return jax.nn.sigmoid(x)

def _layernorm(x, axis=-1, eps=1e-05):
    m = jnp.mean(x, axis=axis, keepdims=True)
    v = jnp.var(x, axis=axis, keepdims=True)
    return (x - m) / jnp.sqrt(v + eps)

def _scatter_add(tgt, idx, src, axis=0):
    return tgt.at[idx].add(src)

def _segment_sum(src, seg, n):
    return jax.ops.segment_sum(src, seg, n)
kernel_name = 'mk_gnn_ffn_d4_gnn_r32_06ce2b'

def setup_inputs(seed: int=0):
    np.random.seed(seed)
    _w = jnp.asarray

    def _rec_inputs():
        import jax
        import jax.numpy as jnp
        _gk = jax.random.key(seed)
        x = -0.0003713 + 1 * jax.random.normal(jax.random.fold_in(_gk, 1), (3125, 256), jnp.float32)
        src = jax.random.randint(jax.random.fold_in(_gk, 2), (50000,), 0, 3125, jnp.int32)
        dst = jax.random.randint(jax.random.fold_in(_gk, 3), (50000,), 0, 3125, jnp.int32)
        _o = jnp.argsort(dst, stable=True)
        src = src[_o]
        dst = dst[_o]
        edge_attr_50 = jax.random.uniform(jax.random.fold_in(_gk, 12), (50000, 50), jnp.float32, 0.0, 1)
        edge_type_8 = jax.random.randint(jax.random.fold_in(_gk, 14), (50000,), 0, 8, jnp.int32)
        edge_weight = jax.random.uniform(jax.random.fold_in(_gk, 15), (50000,), jnp.float32, 0.0, 1)
        node_vec = jax.random.uniform(jax.random.fold_in(_gk, 16), (3125,), jnp.float32, 0.0, 0.999833)
        return (x, src, dst, edge_attr_50, edge_type_8, edge_weight, node_vec)
    x, src, dst, edge_attr_50, edge_type_8, edge_weight, node_vec = _rec_inputs()

    def _L0_gnn_setup():
        import jax, jax.numpy as jnp
        import numpy as np
        N_NODES = 50000
        N_EDGES = 25000
        IN_FEAT = 256
        OUT_FEAT = 256
        NUM_RELS = 8
        NUM_BASES = 8
        SUBMAT_IN = IN_FEAT // NUM_BASES
        SUBMAT_OUT = OUT_FEAT // NUM_BASES
        key = jax.random.key(seed)
        k_h, k_w, k_src, k_dst, k_rel, k_norm = jax.random.split(key, 6)
        h = jax.random.normal(k_h, (N_NODES, IN_FEAT), dtype=jnp.float32)
        weight = jax.random.normal(k_w, (NUM_RELS, NUM_BASES * SUBMAT_IN * SUBMAT_OUT), dtype=jnp.float32) * 0.05
        edge_src = jax.random.randint(k_src, (N_EDGES,), 0, N_NODES, dtype=jnp.int32)
        edge_dst = jax.random.randint(k_dst, (N_EDGES,), 0, N_NODES, dtype=jnp.int32)
        edge_rel = jax.random.randint(k_rel, (N_EDGES,), 0, NUM_RELS, dtype=jnp.int32)
        edge_norm = jax.random.uniform(k_norm, (N_EDGES,), dtype=jnp.float32)
        return {'h': h, 'weight': weight, 'edge_src': edge_src, 'edge_dst': edge_dst, 'edge_rel': edge_rel, 'edge_norm': edge_norm}
    _L0_gnn_all = _L0_gnn_setup()
    _L0_gnn_in = {k: v for k, v in _L0_gnn_all.items() if k in ('weight',)}
    del _L0_gnn_all

    def _L0_ffn_setup():
        import jax, jax.numpy as jnp
        import numpy as np
        B, S, H, F, E, K = (8, 128, 256, 512, 16, 2)
        EPS = 1e-05
        key = jax.random.key(seed)
        ks = jax.random.split(key, 9)
        sc = 0.02
        return {'x': jax.random.normal(ks[0], (B, S, H), dtype=jnp.float32), 'gate_w': jax.random.normal(ks[1], (H, E), dtype=jnp.float32) * sc, 'gate_b': jnp.zeros((E,), dtype=jnp.float32), 'w1': jax.random.normal(ks[2], (E, H, F), dtype=jnp.float32) * sc, 'b1': jnp.zeros((E, F), dtype=jnp.float32), 'w2': jax.random.normal(ks[3], (E, F, H), dtype=jnp.float32) * sc, 'b2': jnp.zeros((E, H), dtype=jnp.float32), 'gamma': jnp.ones((H,), dtype=jnp.float32), 'beta': jnp.zeros((H,), dtype=jnp.float32)}
    _L0_ffn_all = _L0_ffn_setup()
    _L0_ffn_in = {k: v for k, v in _L0_ffn_all.items() if k in ('gate_w', 'gate_b', 'w1', 'b1', 'w2', 'b2', 'gamma', 'beta')}
    del _L0_ffn_all

    def _L1_gnn_setup():
        import jax, jax.numpy as jnp
        import numpy as np
        from jax import lax
        N, E, D = (256, 8192, 256)
        NH, FOUT = (4, 64)
        D_STATE, D_CONV, DT_RANK = (16, 4, 16)

        def _layer_norm(x, g, b, eps=1e-05):
            mu = jnp.mean(x, -1, keepdims=True)
            var = jnp.var(x, -1, keepdims=True)
            return (x - mu) * lax.rsqrt(var + eps) * g + b

        def _mamba(xs, in_proj_w, conv_w, conv_b, x_proj_w, dt_proj_w, dt_proj_b, A_log, D_param, out_proj_w):
            n = xs.shape[0]
            xz = xs @ in_proj_w.T
            xc, z = jnp.split(xz, 2, axis=-1)
            K = conv_w.shape[1]
            xp = jnp.pad(xc, ((K - 1, 0), (0, 0)))
            xc = sum((xp[k:k + n] * conv_w[:, k] for k in range(K))) + conv_b
            xc = jax.nn.silu(xc)
            dbc = xc @ x_proj_w.T
            dt = jax.nn.softplus(dbc[:, :DT_RANK] @ dt_proj_w.T + dt_proj_b)
            Bm = dbc[:, DT_RANK:DT_RANK + D_STATE]
            Cm = dbc[:, DT_RANK + D_STATE:]
            A = -jnp.exp(A_log)
            dA = jnp.exp(dt[:, :, None] * A)
            dBx = (dt * xc)[:, :, None] * Bm[:, None, :]

            def step(h, t):
                dA_t, dBx_t, C_t = t
                h = dA_t * h + dBx_t
                return (h, h @ C_t)
            _, y = lax.scan(step, jnp.zeros((xc.shape[1], D_STATE), xs.dtype), (dA, dBx, Cm))
            y = y + xc * D_param
            y = y * jax.nn.silu(z)
            return y @ out_proj_w.T

        def _forward(x, edge_index, deg_noise, gat_w, gat_a_src, gat_a_tgt, gat_b, ln_local_g, ln_local_b, ln_global_g, ln_global_b, ln2_g, ln2_b, in_proj_w, conv_w, conv_b, x_proj_w, dt_proj_w, dt_proj_b, A_log, D_param, out_proj_w, wl, wg, ff1_w, ff1_b, ff2_w, ff2_b):
            n = x.shape[0]
            src, tgt = (edge_index[0], edge_index[1])
            proj = (x @ gat_w.T).reshape(n, NH, FOUT)
            s_src = jnp.sum(proj * gat_a_src, -1)
            s_tgt = jnp.sum(proj * gat_a_tgt, -1)
            e = jax.nn.leaky_relu(s_src[src] + s_tgt[tgt], 0.2)
            exp_e = jnp.exp(e - jnp.max(e))
            denom = jax.ops.segment_sum(exp_e, tgt, num_segments=n)
            attn = exp_e / (denom[tgt] + 1e-16)
            agg = jax.ops.segment_sum(proj[src] * attn[:, :, None], tgt, num_segments=n)
            h_local = jax.nn.elu((agg + x.reshape(n, NH, FOUT)).reshape(n, NH * FOUT) + gat_b)
            h_local = _layer_norm(h_local, ln_local_g, ln_local_b)
            deg = jax.ops.segment_sum(jnp.ones((src.shape[0],), x.dtype), src, num_segments=n)
            perm = jnp.argsort(deg + deg_noise, stable=True)
            inv = jnp.argsort(perm)
            y = _mamba(x[perm], in_proj_w, conv_w, conv_b, x_proj_w, dt_proj_w, dt_proj_b, A_log, D_param, out_proj_w)
            h_attn = _layer_norm(x + y[inv], ln_global_g, ln_global_b)
            gate = jax.nn.sigmoid(h_local @ wl.T + h_attn @ wg.T)
            h = gate * h_local + (1.0 - gate) * h_attn
            ff = jax.nn.relu(h @ ff1_w.T + ff1_b) @ ff2_w.T + ff2_b
            return _layer_norm(h + ff, ln2_g, ln2_b)
        key = jax.random.key(seed)
        ks = jax.random.split(key, 24)
        w = lambda i, shape, s=0.05: jax.random.normal(ks[i], shape, dtype=jnp.float32) * s
        return {'x': jax.random.normal(ks[0], (N, D), dtype=jnp.float32), 'edge_index': jax.random.randint(ks[1], (2, E), 0, N, dtype=jnp.int32), 'edge_prob': jax.random.uniform(ks[2], (E,), dtype=jnp.float32), 'deg_noise': jax.random.uniform(ks[3], (N,), dtype=jnp.float32), 'gat_w': w(4, (NH * FOUT, D)), 'gat_a_src': w(5, (NH, FOUT)), 'gat_a_tgt': w(6, (NH, FOUT)), 'gat_b': jnp.zeros((NH * FOUT,), jnp.float32), 'ln_local_g': jnp.ones((D,), jnp.float32), 'ln_local_b': jnp.zeros((D,), jnp.float32), 'ln_global_g': jnp.ones((D,), jnp.float32), 'ln_global_b': jnp.zeros((D,), jnp.float32), 'ln2_g': jnp.ones((D,), jnp.float32), 'ln2_b': jnp.zeros((D,), jnp.float32), 'in_proj_w': w(7, (2 * D, D)), 'conv_w': w(8, (D, D_CONV), 0.2), 'conv_b': jnp.zeros((D,), jnp.float32), 'x_proj_w': w(9, (DT_RANK + 2 * D_STATE, D)), 'dt_proj_w': w(10, (D, DT_RANK)), 'dt_proj_b': w(11, (D,), 0.1) - 4.0, 'A_log': jnp.log(jnp.tile(jnp.arange(1, D_STATE + 1, dtype=jnp.float32), (D, 1))), 'D_param': jnp.ones((D,), jnp.float32), 'out_proj_w': w(12, (D, D)), 'wl': w(13, (D, D)), 'wg': w(14, (D, D)), 'ff1_w': w(15, (2 * D, D)), 'ff1_b': jnp.zeros((2 * D,), jnp.float32), 'ff2_w': w(16, (D, 2 * D)), 'ff2_b': jnp.zeros((D,), jnp.float32)}
    _L1_gnn_all = _L1_gnn_setup()
    _L1_gnn_in = {k: v for k, v in _L1_gnn_all.items() if k in ('gat_w', 'gat_a_src', 'gat_a_tgt', 'gat_b', 'ln_local_g', 'ln_local_b', 'ln_global_g', 'ln_global_b', 'ln2_g', 'ln2_b', 'in_proj_w', 'conv_w', 'conv_b', 'x_proj_w', 'dt_proj_w', 'dt_proj_b', 'A_log', 'D_param', 'out_proj_w', 'wl', 'wg', 'ff1_w', 'ff1_b', 'ff2_w', 'ff2_b')}
    del _L1_gnn_all

    def _L1_ffn_setup():
        import jax, jax.numpy as jnp
        import numpy as np
        B, N, D = (16, 128, 256)
        NUM_EXPERTS, TOP_K, HEADS = (4, 2, 4)
        N_EDGES = 32768
        LN_EPS = 1e-05

        def _layernorm(x, g, b):
            mu = x.mean(-1, keepdims=True)
            var = ((x - mu) ** 2).mean(-1, keepdims=True)
            return (x - mu) * jax.lax.rsqrt(var + LN_EPS) * g + b

        def _forward(x, edge_index, W_gat, att_src, att_dst, b_gat, ln_gamma, ln_beta, W1, b1, W2, b2):
            Bc, Nc, Dc = x.shape
            M = Bc * Nc
            x_flat = x.reshape(M, Dc)
            h = (x_flat @ W_gat).reshape(M, HEADS, NUM_EXPERTS)
            loops = jnp.arange(M, dtype=edge_index.dtype)
            src = jnp.concatenate([edge_index[0], loops])
            dst = jnp.concatenate([edge_index[1], loops])
            a_src = (h * att_src).sum(-1)
            a_dst = (h * att_dst).sum(-1)
            e = jax.nn.leaky_relu(a_src[src] + a_dst[dst], negative_slope=0.2)
            e_max = jax.ops.segment_max(e, dst, num_segments=M)
            ee = jnp.exp(e - e_max[dst])
            denom = jax.ops.segment_sum(ee, dst, num_segments=M)
            alpha = ee / (denom[dst] + 1e-16)
            msg = h[src] * alpha[:, :, None]
            agg = jax.ops.segment_sum(msg, dst, num_segments=M).reshape(M, HEADS * NUM_EXPERTS) + b_gat
            scores = _layernorm(agg, ln_gamma, ln_beta).reshape(M, HEADS, NUM_EXPERTS).mean(1)
            scores = scores.reshape(Bc, Nc, NUM_EXPERTS)
            topk_s, topk_i = jax.lax.top_k(scores, TOP_K)
            w = jax.nn.softmax(topk_s, axis=-1)
            out = jnp.zeros_like(x)
            for ei in range(NUM_EXPERTS):
                g = jnp.where(topk_i == ei, w, 0.0).sum(-1)
                hh = jax.nn.gelu(x @ W1[ei] + b1[ei], approximate=False)
                out = out + g[..., None] * (hh @ W2[ei] + b2[ei])
            return out
        key = jax.random.key(seed)
        ks = jax.random.split(key, 8)
        s = 0.05
        return {'x': jax.random.normal(ks[0], (B, N, D), jnp.float32), 'W_gat': jax.random.normal(ks[1], (D, HEADS * NUM_EXPERTS), jnp.float32) * s, 'att_src': jax.random.normal(ks[2], (HEADS, NUM_EXPERTS), jnp.float32) * s, 'att_dst': jax.random.normal(ks[3], (HEADS, NUM_EXPERTS), jnp.float32) * s, 'b_gat': jnp.zeros((HEADS * NUM_EXPERTS,), jnp.float32), 'ln_gamma': jnp.ones((HEADS * NUM_EXPERTS,), jnp.float32), 'ln_beta': jnp.zeros((HEADS * NUM_EXPERTS,), jnp.float32), 'W1': jax.random.normal(ks[4], (NUM_EXPERTS, D, 2 * D), jnp.float32) * s, 'b1': jnp.zeros((NUM_EXPERTS, 2 * D), jnp.float32), 'W2': jax.random.normal(ks[5], (NUM_EXPERTS, 2 * D, D), jnp.float32) * s, 'b2': jnp.zeros((NUM_EXPERTS, D), jnp.float32), 'edge_index': jax.random.randint(ks[6], (2, N_EDGES), 0, B * N, jnp.int32)}
    _L1_ffn_all = _L1_ffn_setup()
    _L1_ffn_in = {k: v for k, v in _L1_ffn_all.items() if k in ('W_gat', 'att_src', 'att_dst', 'b_gat', 'ln_gamma', 'ln_beta', 'W1', 'b1', 'W2', 'b2', 'edge_index')}
    del _L1_ffn_all

    def _L2_gnn_setup():
        import jax, jax.numpy as jnp
        import numpy as np
        ALPHA = 0.2
        N_NODES, N_EDGES, N_FEAT, N_HID, N_HEADS = (50000, 25000, 256, 32, 8)
        key = jax.random.key(seed)
        k_h, k_w, k_a, k_s, k_d = jax.random.split(key, 5)
        h = jax.random.normal(k_h, (N_NODES, N_FEAT), dtype=jnp.float32)
        W = jax.random.normal(k_w, (N_HEADS, N_FEAT, N_HID), dtype=jnp.float32) * 0.05
        a = jax.random.normal(k_a, (N_HEADS, 2 * N_HID), dtype=jnp.float32) * 0.05
        src = jax.random.randint(k_s, (N_EDGES,), 0, N_NODES, dtype=jnp.int32)
        dst = jax.random.randint(k_d, (N_EDGES,), 0, N_NODES, dtype=jnp.int32)
        return {'h': h, 'W': W, 'a': a, 'src': src, 'dst': dst}
    _L2_gnn_all = _L2_gnn_setup()
    _L2_gnn_in = {k: v for k, v in _L2_gnn_all.items() if k in ('W', 'a')}
    del _L2_gnn_all

    def _L2_ffn_setup():
        import math
        import jax, jax.numpy as jnp
        import numpy as np
        CAPACITY_FACTOR = 1.25
        key = jax.random.key(seed)
        ks = jax.random.split(key, 5)
        B, L, D, F, E = (8, 256, 256, 1024, 8)
        h = jax.random.normal(ks[0], (B, L, D), dtype=jnp.float32)
        gate_w = jax.random.normal(ks[1], (D, E), dtype=jnp.float32) * 0.02
        gate_b = jnp.zeros((E,), dtype=jnp.float32)
        w1 = jax.random.normal(ks[2], (E, D, F), dtype=jnp.float32) * (1.0 / math.sqrt(D))
        b1 = jnp.zeros((E, F), dtype=jnp.float32)
        w2 = jax.random.normal(ks[3], (E, F, D), dtype=jnp.float32) * (1.0 / math.sqrt(F))
        b2 = jnp.zeros((E, D), dtype=jnp.float32)
        return {'h': h, 'gate_w': gate_w, 'gate_b': gate_b, 'w1': w1, 'b1': b1, 'w2': w2, 'b2': b2}
    _L2_ffn_all = _L2_ffn_setup()
    _L2_ffn_in = {k: v for k, v in _L2_ffn_all.items() if k in ('gate_w', 'gate_b', 'w1', 'b1', 'w2', 'b2')}
    del _L2_ffn_all

    def _L3_gnn_setup():
        import math
        import jax, jax.numpy as jnp
        import numpy as np
        N_NODES = 625
        N_EDGES = 10000
        HIDDEN = 256
        N_GAUSS = 50
        N_FILTERS = 256
        CUTOFF = 10.0
        LOG2 = math.log(2.0)

        def ssp(x):
            return jax.nn.softplus(x) - LOG2

        def _xavier(key, shape):
            fan_in, fan_out = (shape[0], shape[1])
            limit = math.sqrt(6.0 / (fan_in + fan_out))
            return jax.random.uniform(key, shape, jnp.float32, -limit, limit)
        key = jax.random.key(seed)
        ks = jax.random.split(key, 10)
        x = jax.random.normal(ks[0], (N_NODES, HIDDEN), jnp.float32)
        edge_index = jax.random.randint(ks[1], (2, N_EDGES), 0, N_NODES)
        edge_weight = jax.random.uniform(ks[2], (N_EDGES,), jnp.float32) * CUTOFF
        edge_attr = jax.random.uniform(ks[3], (N_EDGES, N_GAUSS), jnp.float32)
        mlp_w1 = _xavier(ks[4], (N_GAUSS, N_FILTERS))
        mlp_b1 = jnp.zeros((N_FILTERS,), jnp.float32)
        mlp_w2 = _xavier(ks[5], (N_FILTERS, N_FILTERS))
        mlp_b2 = jnp.zeros((N_FILTERS,), jnp.float32)
        lin1_w = _xavier(ks[6], (HIDDEN, N_FILTERS))
        lin2_w = _xavier(ks[7], (N_FILTERS, HIDDEN))
        lin2_b = jnp.zeros((HIDDEN,), jnp.float32)
        lin_w = _xavier(ks[8], (HIDDEN, HIDDEN))
        lin_b = jnp.zeros((HIDDEN,), jnp.float32)
        return {'x': x, 'edge_index': edge_index, 'edge_weight': edge_weight, 'edge_attr': edge_attr, 'mlp_w1': mlp_w1, 'mlp_b1': mlp_b1, 'mlp_w2': mlp_w2, 'mlp_b2': mlp_b2, 'lin1_w': lin1_w, 'lin2_w': lin2_w, 'lin2_b': lin2_b, 'lin_w': lin_w, 'lin_b': lin_b}
    _L3_gnn_all = _L3_gnn_setup()
    _L3_gnn_in = {k: v for k, v in _L3_gnn_all.items() if k in ('mlp_w1', 'mlp_b1', 'mlp_w2', 'mlp_b2', 'lin1_w', 'lin2_w', 'lin2_b', 'lin_w', 'lin_b')}
    del _L3_gnn_all

    def _L3_ffn_setup():
        import jax, jax.numpy as jnp
        import numpy as np
        E, D, H, TOP_K = (6, 256, 256, 2)
        ROUTER_H = D // 2
        key = jax.random.key(seed)
        ks = jax.random.split(key, 12)
        s = 1.0 / np.sqrt(D)
        sh = 1.0 / np.sqrt(H)
        sr = 1.0 / np.sqrt(ROUTER_H)
        return {'features': jax.random.normal(ks[0], (8, 128, D), dtype=jnp.float32), 'router_w1': jax.random.uniform(ks[1], (D, ROUTER_H), jnp.float32, -s, s), 'router_b1': jnp.zeros((ROUTER_H,), jnp.float32), 'router_w2': jax.random.uniform(ks[2], (ROUTER_H, E), jnp.float32, -sr, sr), 'router_b2': jnp.zeros((E,), jnp.float32), 'expert_w1': jax.random.uniform(ks[3], (E, D, H), jnp.float32, -s, s), 'expert_b1': jnp.zeros((E, H), jnp.float32), 'expert_w2': jax.random.uniform(ks[4], (E, H, H), jnp.float32, -sh, sh), 'expert_b2': jnp.zeros((E, H), jnp.float32), 'expert_w3': jax.random.uniform(ks[5], (E, H, D), jnp.float32, -sh, sh), 'expert_b3': jnp.zeros((E, D), jnp.float32)}
    _L3_ffn_all = _L3_ffn_setup()
    _L3_ffn_in = {k: v for k, v in _L3_ffn_all.items() if k in ('router_w1', 'router_b1', 'router_w2', 'router_b2', 'expert_w1', 'expert_b1', 'expert_w2', 'expert_b2', 'expert_w3', 'expert_b3')}
    del _L3_ffn_all
    return {'x': x, 'src': src, 'dst': dst, 'edge_attr_50': edge_attr_50, 'edge_type_8': edge_type_8, 'edge_weight': edge_weight, 'node_vec': node_vec, 'L0_gnn_weight': _L0_gnn_in['weight'], 'L0_ffn_gate_w': _L0_ffn_in['gate_w'], 'L0_ffn_gate_b': _L0_ffn_in['gate_b'], 'L0_ffn_w1': _L0_ffn_in['w1'], 'L0_ffn_b1': _L0_ffn_in['b1'], 'L0_ffn_w2': _L0_ffn_in['w2'], 'L0_ffn_b2': _L0_ffn_in['b2'], 'L0_ffn_gamma': _L0_ffn_in['gamma'], 'L0_ffn_beta': _L0_ffn_in['beta'], 'L1_gnn_gat_w': _L1_gnn_in['gat_w'], 'L1_gnn_gat_a_src': _L1_gnn_in['gat_a_src'], 'L1_gnn_gat_a_tgt': _L1_gnn_in['gat_a_tgt'], 'L1_gnn_gat_b': _L1_gnn_in['gat_b'], 'L1_gnn_ln_local_g': _L1_gnn_in['ln_local_g'], 'L1_gnn_ln_local_b': _L1_gnn_in['ln_local_b'], 'L1_gnn_ln_global_g': _L1_gnn_in['ln_global_g'], 'L1_gnn_ln_global_b': _L1_gnn_in['ln_global_b'], 'L1_gnn_ln2_g': _L1_gnn_in['ln2_g'], 'L1_gnn_ln2_b': _L1_gnn_in['ln2_b'], 'L1_gnn_in_proj_w': _L1_gnn_in['in_proj_w'], 'L1_gnn_conv_w': _L1_gnn_in['conv_w'], 'L1_gnn_conv_b': _L1_gnn_in['conv_b'], 'L1_gnn_x_proj_w': _L1_gnn_in['x_proj_w'], 'L1_gnn_dt_proj_w': _L1_gnn_in['dt_proj_w'], 'L1_gnn_dt_proj_b': _L1_gnn_in['dt_proj_b'], 'L1_gnn_A_log': _L1_gnn_in['A_log'], 'L1_gnn_D_param': _L1_gnn_in['D_param'], 'L1_gnn_out_proj_w': _L1_gnn_in['out_proj_w'], 'L1_gnn_wl': _L1_gnn_in['wl'], 'L1_gnn_wg': _L1_gnn_in['wg'], 'L1_gnn_ff1_w': _L1_gnn_in['ff1_w'], 'L1_gnn_ff1_b': _L1_gnn_in['ff1_b'], 'L1_gnn_ff2_w': _L1_gnn_in['ff2_w'], 'L1_gnn_ff2_b': _L1_gnn_in['ff2_b'], 'L1_ffn_W_gat': _L1_ffn_in['W_gat'], 'L1_ffn_att_src': _L1_ffn_in['att_src'], 'L1_ffn_att_dst': _L1_ffn_in['att_dst'], 'L1_ffn_b_gat': _L1_ffn_in['b_gat'], 'L1_ffn_ln_gamma': _L1_ffn_in['ln_gamma'], 'L1_ffn_ln_beta': _L1_ffn_in['ln_beta'], 'L1_ffn_W1': _L1_ffn_in['W1'], 'L1_ffn_b1': _L1_ffn_in['b1'], 'L1_ffn_W2': _L1_ffn_in['W2'], 'L1_ffn_b2': _L1_ffn_in['b2'], 'L1_ffn_edge_index': _L1_ffn_in['edge_index'], 'L2_gnn_W': _L2_gnn_in['W'], 'L2_gnn_a': _L2_gnn_in['a'], 'L2_ffn_gate_w': _L2_ffn_in['gate_w'], 'L2_ffn_gate_b': _L2_ffn_in['gate_b'], 'L2_ffn_w1': _L2_ffn_in['w1'], 'L2_ffn_b1': _L2_ffn_in['b1'], 'L2_ffn_w2': _L2_ffn_in['w2'], 'L2_ffn_b2': _L2_ffn_in['b2'], 'L3_gnn_mlp_w1': _L3_gnn_in['mlp_w1'], 'L3_gnn_mlp_b1': _L3_gnn_in['mlp_b1'], 'L3_gnn_mlp_w2': _L3_gnn_in['mlp_w2'], 'L3_gnn_mlp_b2': _L3_gnn_in['mlp_b2'], 'L3_gnn_lin1_w': _L3_gnn_in['lin1_w'], 'L3_gnn_lin2_w': _L3_gnn_in['lin2_w'], 'L3_gnn_lin2_b': _L3_gnn_in['lin2_b'], 'L3_gnn_lin_w': _L3_gnn_in['lin_w'], 'L3_gnn_lin_b': _L3_gnn_in['lin_b'], 'L3_ffn_router_w1': _L3_ffn_in['router_w1'], 'L3_ffn_router_b1': _L3_ffn_in['router_b1'], 'L3_ffn_router_w2': _L3_ffn_in['router_w2'], 'L3_ffn_router_b2': _L3_ffn_in['router_b2'], 'L3_ffn_expert_w1': _L3_ffn_in['expert_w1'], 'L3_ffn_expert_b1': _L3_ffn_in['expert_b1'], 'L3_ffn_expert_w2': _L3_ffn_in['expert_w2'], 'L3_ffn_expert_b2': _L3_ffn_in['expert_b2'], 'L3_ffn_expert_w3': _L3_ffn_in['expert_w3'], 'L3_ffn_expert_b3': _L3_ffn_in['expert_b3']}

def reference(x, src, dst, edge_attr_50, edge_type_8, edge_weight, node_vec, L0_gnn_weight, L0_ffn_gate_w, L0_ffn_gate_b, L0_ffn_w1, L0_ffn_b1, L0_ffn_w2, L0_ffn_b2, L0_ffn_gamma, L0_ffn_beta, L1_gnn_gat_w, L1_gnn_gat_a_src, L1_gnn_gat_a_tgt, L1_gnn_gat_b, L1_gnn_ln_local_g, L1_gnn_ln_local_b, L1_gnn_ln_global_g, L1_gnn_ln_global_b, L1_gnn_ln2_g, L1_gnn_ln2_b, L1_gnn_in_proj_w, L1_gnn_conv_w, L1_gnn_conv_b, L1_gnn_x_proj_w, L1_gnn_dt_proj_w, L1_gnn_dt_proj_b, L1_gnn_A_log, L1_gnn_D_param, L1_gnn_out_proj_w, L1_gnn_wl, L1_gnn_wg, L1_gnn_ff1_w, L1_gnn_ff1_b, L1_gnn_ff2_w, L1_gnn_ff2_b, L1_ffn_W_gat, L1_ffn_att_src, L1_ffn_att_dst, L1_ffn_b_gat, L1_ffn_ln_gamma, L1_ffn_ln_beta, L1_ffn_W1, L1_ffn_b1, L1_ffn_W2, L1_ffn_b2, L1_ffn_edge_index, L2_gnn_W, L2_gnn_a, L2_ffn_gate_w, L2_ffn_gate_b, L2_ffn_w1, L2_ffn_b1, L2_ffn_w2, L2_ffn_b2, L3_gnn_mlp_w1, L3_gnn_mlp_b1, L3_gnn_mlp_w2, L3_gnn_mlp_b2, L3_gnn_lin1_w, L3_gnn_lin2_w, L3_gnn_lin2_b, L3_gnn_lin_w, L3_gnn_lin_b, L3_ffn_router_w1, L3_ffn_router_b1, L3_ffn_router_w2, L3_ffn_router_b2, L3_ffn_expert_w1, L3_ffn_expert_b1, L3_ffn_expert_w2, L3_ffn_expert_b2, L3_ffn_expert_w3, L3_ffn_expert_b3):
    import jax
    import jax.numpy as jnp

    def _L0_gnn_ref(h, weight, edge_src, edge_dst, edge_rel, edge_norm):
        import jax, jax.numpy as jnp
        import numpy as np
        N_NODES = 50000
        N_EDGES = 25000
        IN_FEAT = 256
        OUT_FEAT = 256
        NUM_RELS = 8
        NUM_BASES = 8
        SUBMAT_IN = IN_FEAT // NUM_BASES
        SUBMAT_OUT = OUT_FEAT // NUM_BASES
        'RGCNBlockLayer forward (self_loop=False, bias=None, activation=None).\n\n            Per relation r: agg_r[v] = sum_{(u->v) in rel r} norm_e * h[u]\n            then block-diagonal matmul out_r = blockmm(agg_r, W_r); output = sum_r out_r.\n            '
        N, in_feat = h.shape
        R = weight.shape[0]
        msg = h[edge_src] * edge_norm[:, None]
        seg = edge_rel * N + edge_dst
        agg = jax.ops.segment_sum(msg, seg, num_segments=R * N)
        agg = agg.reshape(R, N, NUM_BASES, SUBMAT_IN)
        W = weight.reshape(R, NUM_BASES, SUBMAT_IN, SUBMAT_OUT)
        out = jnp.einsum('rnbi,rbio->nbo', agg, W)
        return out.reshape(N, NUM_BASES * SUBMAT_OUT)

    def _L0_ffn_ref(x, gate_w, gate_b, w1, b1, w2, b2, gamma, beta):
        import jax, jax.numpy as jnp
        import numpy as np
        B, S, H, F, E, K = (8, 128, 256, 512, 16, 2)
        EPS = 1e-05
        gate_logits = x @ gate_w + gate_b
        topk_vals, topk_idx = jax.lax.top_k(gate_logits, K)
        topk_w = jax.nn.softmax(topk_vals, axis=-1)
        h = jax.nn.relu(jnp.einsum('bsh,ehf->bsef', x, w1) + b1)
        expert_out = jnp.einsum('bsef,efh->bseh', h, w2) + b2
        sel = jnp.take_along_axis(expert_out, topk_idx[:, :, :, None], axis=2)
        moe = jnp.sum(topk_w[..., None] * sel, axis=2)
        y = x + moe
        mu = jnp.mean(y, axis=-1, keepdims=True)
        var = jnp.var(y, axis=-1, keepdims=True)
        return (y - mu) / jnp.sqrt(var + EPS) * gamma + beta

    def _L1_gnn_ref(x, edge_index, edge_prob, deg_noise, gat_w, gat_a_src, gat_a_tgt, gat_b, ln_local_g, ln_local_b, ln_global_g, ln_global_b, ln2_g, ln2_b, in_proj_w, conv_w, conv_b, x_proj_w, dt_proj_w, dt_proj_b, A_log, D_param, out_proj_w, wl, wg, ff1_w, ff1_b, ff2_w, ff2_b):
        import jax, jax.numpy as jnp
        import numpy as np
        from jax import lax
        N, E, D = (256, 8192, 256)
        NH, FOUT = (4, 64)
        D_STATE, D_CONV, DT_RANK = (16, 4, 16)

        def _layer_norm(x, g, b, eps=1e-05):
            mu = jnp.mean(x, -1, keepdims=True)
            var = jnp.var(x, -1, keepdims=True)
            return (x - mu) * lax.rsqrt(var + eps) * g + b

        def _mamba(xs, in_proj_w, conv_w, conv_b, x_proj_w, dt_proj_w, dt_proj_b, A_log, D_param, out_proj_w):
            n = xs.shape[0]
            xz = xs @ in_proj_w.T
            xc, z = jnp.split(xz, 2, axis=-1)
            K = conv_w.shape[1]
            xp = jnp.pad(xc, ((K - 1, 0), (0, 0)))
            xc = sum((xp[k:k + n] * conv_w[:, k] for k in range(K))) + conv_b
            xc = jax.nn.silu(xc)
            dbc = xc @ x_proj_w.T
            dt = jax.nn.softplus(dbc[:, :DT_RANK] @ dt_proj_w.T + dt_proj_b)
            Bm = dbc[:, DT_RANK:DT_RANK + D_STATE]
            Cm = dbc[:, DT_RANK + D_STATE:]
            A = -jnp.exp(A_log)
            dA = jnp.exp(dt[:, :, None] * A)
            dBx = (dt * xc)[:, :, None] * Bm[:, None, :]

            def step(h, t):
                dA_t, dBx_t, C_t = t
                h = dA_t * h + dBx_t
                return (h, h @ C_t)
            _, y = lax.scan(step, jnp.zeros((xc.shape[1], D_STATE), xs.dtype), (dA, dBx, Cm))
            y = y + xc * D_param
            y = y * jax.nn.silu(z)
            return y @ out_proj_w.T

        def _forward(x, edge_index, deg_noise, gat_w, gat_a_src, gat_a_tgt, gat_b, ln_local_g, ln_local_b, ln_global_g, ln_global_b, ln2_g, ln2_b, in_proj_w, conv_w, conv_b, x_proj_w, dt_proj_w, dt_proj_b, A_log, D_param, out_proj_w, wl, wg, ff1_w, ff1_b, ff2_w, ff2_b):
            n = x.shape[0]
            src, tgt = (edge_index[0], edge_index[1])
            proj = (x @ gat_w.T).reshape(n, NH, FOUT)
            s_src = jnp.sum(proj * gat_a_src, -1)
            s_tgt = jnp.sum(proj * gat_a_tgt, -1)
            e = jax.nn.leaky_relu(s_src[src] + s_tgt[tgt], 0.2)
            exp_e = jnp.exp(e - jnp.max(e))
            denom = jax.ops.segment_sum(exp_e, tgt, num_segments=n)
            attn = exp_e / (denom[tgt] + 1e-16)
            agg = jax.ops.segment_sum(proj[src] * attn[:, :, None], tgt, num_segments=n)
            h_local = jax.nn.elu((agg + x.reshape(n, NH, FOUT)).reshape(n, NH * FOUT) + gat_b)
            h_local = _layer_norm(h_local, ln_local_g, ln_local_b)
            deg = jax.ops.segment_sum(jnp.ones((src.shape[0],), x.dtype), src, num_segments=n)
            perm = jnp.argsort(deg + deg_noise, stable=True)
            inv = jnp.argsort(perm)
            y = _mamba(x[perm], in_proj_w, conv_w, conv_b, x_proj_w, dt_proj_w, dt_proj_b, A_log, D_param, out_proj_w)
            h_attn = _layer_norm(x + y[inv], ln_global_g, ln_global_b)
            gate = jax.nn.sigmoid(h_local @ wl.T + h_attn @ wg.T)
            h = gate * h_local + (1.0 - gate) * h_attn
            ff = jax.nn.relu(h @ ff1_w.T + ff1_b) @ ff2_w.T + ff2_b
            return _layer_norm(h + ff, ln2_g, ln2_b)
        return _forward(x, edge_index, deg_noise, gat_w, gat_a_src, gat_a_tgt, gat_b, ln_local_g, ln_local_b, ln_global_g, ln_global_b, ln2_g, ln2_b, in_proj_w, conv_w, conv_b, x_proj_w, dt_proj_w, dt_proj_b, A_log, D_param, out_proj_w, wl, wg, ff1_w, ff1_b, ff2_w, ff2_b)

    def _L1_ffn_ref(x, W_gat, att_src, att_dst, b_gat, ln_gamma, ln_beta, W1, b1, W2, b2, edge_index):
        import jax, jax.numpy as jnp
        import numpy as np
        B, N, D = (16, 128, 256)
        NUM_EXPERTS, TOP_K, HEADS = (4, 2, 4)
        N_EDGES = 32768
        LN_EPS = 1e-05

        def _layernorm(x, g, b):
            mu = x.mean(-1, keepdims=True)
            var = ((x - mu) ** 2).mean(-1, keepdims=True)
            return (x - mu) * jax.lax.rsqrt(var + LN_EPS) * g + b

        def _forward(x, edge_index, W_gat, att_src, att_dst, b_gat, ln_gamma, ln_beta, W1, b1, W2, b2):
            Bc, Nc, Dc = x.shape
            M = Bc * Nc
            x_flat = x.reshape(M, Dc)
            h = (x_flat @ W_gat).reshape(M, HEADS, NUM_EXPERTS)
            loops = jnp.arange(M, dtype=edge_index.dtype)
            src = jnp.concatenate([edge_index[0], loops])
            dst = jnp.concatenate([edge_index[1], loops])
            a_src = (h * att_src).sum(-1)
            a_dst = (h * att_dst).sum(-1)
            e = jax.nn.leaky_relu(a_src[src] + a_dst[dst], negative_slope=0.2)
            e_max = jax.ops.segment_max(e, dst, num_segments=M)
            ee = jnp.exp(e - e_max[dst])
            denom = jax.ops.segment_sum(ee, dst, num_segments=M)
            alpha = ee / (denom[dst] + 1e-16)
            msg = h[src] * alpha[:, :, None]
            agg = jax.ops.segment_sum(msg, dst, num_segments=M).reshape(M, HEADS * NUM_EXPERTS) + b_gat
            scores = _layernorm(agg, ln_gamma, ln_beta).reshape(M, HEADS, NUM_EXPERTS).mean(1)
            scores = scores.reshape(Bc, Nc, NUM_EXPERTS)
            topk_s, topk_i = jax.lax.top_k(scores, TOP_K)
            w = jax.nn.softmax(topk_s, axis=-1)
            out = jnp.zeros_like(x)
            for ei in range(NUM_EXPERTS):
                g = jnp.where(topk_i == ei, w, 0.0).sum(-1)
                hh = jax.nn.gelu(x @ W1[ei] + b1[ei], approximate=False)
                out = out + g[..., None] * (hh @ W2[ei] + b2[ei])
            return out
        return _forward(x, edge_index, W_gat, att_src, att_dst, b_gat, ln_gamma, ln_beta, W1, b1, W2, b2)

    def _L2_gnn_ref(h, W, a, src, dst):
        import jax, jax.numpy as jnp
        import numpy as np
        ALPHA = 0.2
        N_NODES, N_EDGES, N_FEAT, N_HID, N_HEADS = (50000, 25000, 256, 32, 8)
        N = h.shape[0]
        H, _, D = W.shape
        Wh = jnp.einsum('nf,hfd->hnd', h, W)
        a1, a2 = (a[:, :D], a[:, D:])
        s1 = jnp.einsum('hnd,hd->hn', Wh, a1)
        s2 = jnp.einsum('hnd,hd->hn', Wh, a2)
        e = jax.nn.leaky_relu(s1[:, src] + s2[:, dst], ALPHA)
        seg_max = jax.vmap(lambda x: jax.ops.segment_max(x, dst, num_segments=N))(e)
        ex = jnp.exp(e - seg_max[:, dst])
        denom = jax.vmap(lambda x: jax.ops.segment_sum(x, dst, num_segments=N))(ex)
        attn = ex / denom[:, dst]
        msg = attn[:, :, None] * Wh[:, src]
        out = jax.vmap(lambda m: jax.ops.segment_sum(m, dst, num_segments=N))(msg)
        return jnp.transpose(out, (1, 0, 2)).reshape(N, H * D)

    def _L2_ffn_ref(h, gate_w, gate_b, w1, b1, w2, b2):
        import math
        import jax, jax.numpy as jnp
        import numpy as np
        CAPACITY_FACTOR = 1.25
        B, L, D = h.shape
        E = gate_w.shape[1]
        T = B * L
        C = max(1, math.ceil(CAPACITY_FACTOR * T / E))
        x = h.reshape(T, D)
        logits = x @ gate_w + gate_b
        probs = jax.nn.softmax(logits, axis=-1)
        idx = jnp.argmax(probs, axis=-1)
        prb = jnp.take_along_axis(probs, idx[:, None], axis=1)[:, 0]
        one_hot = jax.nn.one_hot(idx, E, dtype=jnp.float32)
        pos = (jnp.cumsum(one_hot, axis=0) * one_hot).sum(-1).astype(jnp.int32) - 1
        kept = pos < C
        pos_safe = jnp.where(kept, pos, C)
        buf = jnp.zeros((E, C, D), dtype=h.dtype).at[idx, pos_safe].set(x, mode='drop')
        hmid = jax.nn.relu(jnp.einsum('ecd,edf->ecf', buf, w1) + b1[:, None, :])
        ybuf = jnp.einsum('ecf,efd->ecd', hmid, w2) + b2[:, None, :]
        pos_g = jnp.minimum(pos, C - 1)
        y_tok = ybuf[idx, pos_g] * (prb * kept)[:, None]
        y = y_tok.reshape(B, L, D)
        y = jnp.nan_to_num(y, nan=0.0, posinf=10000.0, neginf=-10000.0)
        return y

    def _L3_gnn_ref(x, edge_index, edge_weight, edge_attr, mlp_w1, mlp_b1, mlp_w2, mlp_b2, lin1_w, lin2_w, lin2_b, lin_w, lin_b):
        import math
        import jax, jax.numpy as jnp
        import numpy as np
        N_NODES = 625
        N_EDGES = 10000
        HIDDEN = 256
        N_GAUSS = 50
        N_FILTERS = 256
        CUTOFF = 10.0
        LOG2 = math.log(2.0)

        def ssp(x):
            return jax.nn.softplus(x) - LOG2

        def _xavier(key, shape):
            fan_in, fan_out = (shape[0], shape[1])
            limit = math.sqrt(6.0 / (fan_in + fan_out))
            return jax.random.uniform(key, shape, jnp.float32, -limit, limit)
        src, dst = (edge_index[0], edge_index[1])
        C = 0.5 * (jnp.cos(edge_weight * (math.pi / CUTOFF)) + 1.0)
        W = ssp(edge_attr @ mlp_w1 + mlp_b1) @ mlp_w2 + mlp_b2
        W = W * C[:, None]
        h = x @ lin1_w
        msg = h[src] * W
        agg = jax.ops.segment_sum(msg, dst, num_segments=x.shape[0])
        out = agg @ lin2_w + lin2_b
        out = ssp(out)
        out = out @ lin_w + lin_b
        return out

    def _L3_ffn_ref(features, router_w1, router_b1, router_w2, router_b2, expert_w1, expert_b1, expert_w2, expert_b2, expert_w3, expert_b3):
        import jax, jax.numpy as jnp
        import numpy as np
        E, D, H, TOP_K = (6, 256, 256, 2)
        ROUTER_H = D // 2
        rh = jax.nn.relu(features @ router_w1 + router_b1)
        expert_logits = jax.nn.softmax(rh @ router_w2 + router_b2, axis=-1)
        top_w, top_i = jax.lax.top_k(expert_logits, TOP_K)
        routing_weights = jax.nn.softmax(top_w, axis=-1)
        h1 = jax.nn.relu(jnp.einsum('bsd,edh->bseh', features, expert_w1) + expert_b1)
        h2 = jax.nn.relu(jnp.einsum('bseh,ehf->bsef', h1, expert_w2) + expert_b2)
        expert_out = jnp.einsum('bsef,efo->bseo', h2, expert_w3) + expert_b3
        sel = jnp.take_along_axis(expert_out, top_i[:, :, :, None], axis=2)
        combined = jnp.sum(sel * routing_weights[..., None], axis=2)
        return combined
    edge_index = jnp.stack([src, dst])
    x = x + _L0_gnn_ref(_layernorm(x, axis=-1), L0_gnn_weight, src, dst, edge_type_8, edge_weight)
    x = x + _L0_ffn_ref(_layernorm(x, axis=-1)[None], L0_ffn_gate_w, L0_ffn_gate_b, L0_ffn_w1, L0_ffn_b1, L0_ffn_w2, L0_ffn_b2, L0_ffn_gamma, L0_ffn_beta)[0]
    x = x + _L1_gnn_ref(_layernorm(x, axis=-1), edge_index, edge_weight, node_vec, L1_gnn_gat_w, L1_gnn_gat_a_src, L1_gnn_gat_a_tgt, L1_gnn_gat_b, L1_gnn_ln_local_g, L1_gnn_ln_local_b, L1_gnn_ln_global_g, L1_gnn_ln_global_b, L1_gnn_ln2_g, L1_gnn_ln2_b, L1_gnn_in_proj_w, L1_gnn_conv_w, L1_gnn_conv_b, L1_gnn_x_proj_w, L1_gnn_dt_proj_w, L1_gnn_dt_proj_b, L1_gnn_A_log, L1_gnn_D_param, L1_gnn_out_proj_w, L1_gnn_wl, L1_gnn_wg, L1_gnn_ff1_w, L1_gnn_ff1_b, L1_gnn_ff2_w, L1_gnn_ff2_b)
    x = x + _L1_ffn_ref(_layernorm(x, axis=-1)[None], L1_ffn_W_gat, L1_ffn_att_src, L1_ffn_att_dst, L1_ffn_b_gat, L1_ffn_ln_gamma, L1_ffn_ln_beta, L1_ffn_W1, L1_ffn_b1, L1_ffn_W2, L1_ffn_b2, L1_ffn_edge_index)[0]
    x = x + _L2_gnn_ref(_layernorm(x, axis=-1), L2_gnn_W, L2_gnn_a, src, dst)
    x = x + _L2_ffn_ref(_layernorm(x, axis=-1)[None], L2_ffn_gate_w, L2_ffn_gate_b, L2_ffn_w1, L2_ffn_b1, L2_ffn_w2, L2_ffn_b2)[0]
    x = x + _L3_gnn_ref(_layernorm(x, axis=-1), edge_index, edge_weight, edge_attr_50, L3_gnn_mlp_w1, L3_gnn_mlp_b1, L3_gnn_mlp_w2, L3_gnn_mlp_b2, L3_gnn_lin1_w, L3_gnn_lin2_w, L3_gnn_lin2_b, L3_gnn_lin_w, L3_gnn_lin_b)
    x = x + _L3_ffn_ref(_layernorm(x, axis=-1)[None], L3_ffn_router_w1, L3_ffn_router_b1, L3_ffn_router_w2, L3_ffn_router_b2, L3_ffn_expert_w1, L3_ffn_expert_b1, L3_ffn_expert_w2, L3_ffn_expert_b2, L3_ffn_expert_w3, L3_ffn_expert_b3)[0]
    return x

_drawn_inputs = setup_inputs


def setup_inputs(seed=0):
    import zlib

    import numpy as np

    out = dict(_drawn_inputs(seed))
    spreads = {'L0_ffn_gate_b': (0.0, 0.1),
     'L0_ffn_b1': (0.0, 0.483),
     'L0_ffn_b2': (0.0, 0.1),
     'L0_ffn_gamma': (1.0, 0.2),
     'L0_ffn_beta': (0.0, 0.1),
     'L1_gnn_gat_b': (0.0, 0.284),
     'L1_gnn_ln_local_g': (1.0, 0.2),
     'L1_gnn_ln_local_b': (0.0, 0.322),
     'L1_gnn_ln_global_g': (1.0, 0.2),
     'L1_gnn_ln_global_b': (0.0, 0.328),
     'L1_gnn_ln2_g': (1.0, 0.2),
     'L1_gnn_ln2_b': (0.0, 0.1),
     'L1_gnn_conv_b': (0.0, 0.8),
     'L1_gnn_D_param': (1.0, 0.6),
     'L1_gnn_ff1_b': (0.0, 0.27),
     'L1_gnn_ff2_b': (0.0, 0.1),
     'L1_ffn_b_gat': (0.0, 0.1),
     'L1_ffn_ln_gamma': (1.0, 0.2),
     'L1_ffn_ln_beta': (0.0, 0.1),
     'L1_ffn_b1': (0.0, 0.399),
     'L1_ffn_b2': (0.0, 0.291),
     'L2_ffn_gate_b': (0.0, 0.1),
     'L2_ffn_b1': (0.0, 0.8),
     'L2_ffn_b2': (0.0, 0.8),
     'L3_gnn_mlp_b1': (0.0, 0.1),
     'L3_gnn_mlp_b2': (0.0, 0.1),
     'L3_gnn_lin2_b': (0.0, 0.452),
     'L3_gnn_lin_b': (0.0, 0.1),
     'L3_ffn_router_b1': (0.0, 0.601),
     'L3_ffn_router_b2': (0.0, 0.499),
     'L3_ffn_expert_b1': (0.0, 0.8),
     'L3_ffn_expert_b2': (0.0, 0.8),
     'L3_ffn_expert_b3': (0.0, 0.37)}
    factors = {'node_vec': 4.192,
     'L1_gnn_gat_a_src': 3.875,
     'L1_gnn_gat_a_tgt': 8.0,
     'L1_gnn_in_proj_w': 3.795,
     'L1_gnn_conv_w': 3.826,
     'L1_gnn_x_proj_w': 8.0,
     'L1_gnn_dt_proj_w': 8.0,
     'L1_gnn_dt_proj_b': 8.0,
     'L1_gnn_A_log': 8.0,
     'L1_gnn_out_proj_w': 3.742,
     'L1_ffn_att_src': 3.515,
     'L1_ffn_att_dst': 5.097,
     'L2_gnn_a': 4.156,
     'L3_ffn_expert_w1': 3.548,
     'L3_ffn_expert_w2': 3.012}
    for name, (base, spread) in spreads.items():
        noise = np.random.default_rng([zlib.crc32(name.encode()), seed]).standard_normal(out[name].shape)
        drawn = base * np.exp(spread * noise) if base else spread * noise
        out[name] = jnp.asarray(drawn.astype(out[name].dtype))
    for name, factor in factors.items():
        out[name] = (out[name] * factor).astype(out[name].dtype)
    return out
```

```python
import math
from contextlib import ExitStack

import numpy as np

import concourse.bass as bass
from concourse import mybir

ALU = mybir.AluOpType
ACT = mybir.ActivationFunctionType
AX_X = mybir.AxisListType.X
F32 = mybir.dt.float32
I32 = mybir.dt.int32
RMAX = bass.bass_isa.ReduceOp.max
ds = bass.ds

N, D, E = 3125, 256, 50000
P = 125
NT, ET = N // P, E // P
G = 4
NG = ET // G
PAD_ROW = N
AT = NT + 1
REL, BASES, SUB = 8, 8, 32
EPS = 1e-5


class Core:
    pass


def stage(k):
    return Stage(k)


class Stage:
    def __init__(self, k):
        self.k, self.nc = k, k.nc
        self.ctx = ExitStack()
        self.sems = []

    def __enter__(self):
        return self

    def __exit__(self, *e):
        if e[0] is not None:
            return False
        self.ctx.close()
        self.nc.clear_and_free_semaphores(self.sems)
        self.nc.all_engine_barrier()

    def sb(self, name, shape, dt=F32):
        self.k.uid += 1
        return self.ctx.enter_context(self.nc.sbuf_tensor(f"{name}_{self.k.uid}", shape, dt))

    def ps(self, name, shape, dt=F32):
        self.k.uid += 1
        return self.ctx.enter_context(self.nc.psum_tensor(f"{name}_{self.k.uid}", shape, dt))

    def sem(self, name):
        self.k.uid += 1
        s = self.nc.alloc_semaphore(f"{name}_{self.k.uid}")
        self.sems.append(s)
        return s

    def block(self):
        return self.nc.Block()


class Chain:

    def __init__(self, eng, sem):
        self.eng, self.sem, self.n = eng, sem, 0

    def step(self, ins):
        self.n += 1
        ins.then_inc(self.sem, 1)

    def wait(self):
        self.eng.wait_ge(self.sem, self.n)

    def link(self, ins):
        self.step(ins)
        self.wait()


def prepare_edges(k):
    nc = k.nc
    with stage(k) as s:
        src, typ, gidx = s.sb("src", [P, ET], I32), s.sb("typ", [P, ET], I32), s.sb("gidx", [P, ET], I32)
        dst = s.sb("dst", [P, ET], I32)
        before = s.sb("before", [P, P])
        first = s.sb("first", [P, ET])
        prior = s.sb("prior", [P, ET])
        pad = s.sb("pad", [P, 1])
        dmask = s.sb("dmask", [P, ET])
        rows = s.sb("rows", [P, 2, G * P], I32)
        hits = s.sb("hits", [P, 2, G * P])
        loaded, ramps, chain = s.sem("loaded"), s.sem("ramps"), s.sem("chain")
        row_in = [s.sem("row_in0"), s.sem("row_in1")]
        row_used = [s.sem("row_used0"), s.sem("row_used1")]
        out = s.sem("out")
        with s.block() as block:
            @block.sync
            def _(sp):
                sp.dma_start(src[:], k.src_c).then_inc(loaded, 16)
                sp.dma_start(dst[:], k.dst_c).then_inc(loaded, 16)
                sp.dma_start(typ[:], k.type_c).then_inc(loaded, 16)
                sp.dma_start(k.edge_w[:], k.weight_c).then_inc(loaded, 16)
                with sp.Fori(0, NG // 2) as i:
                    for b in range(2):
                        sp.wait_ge(row_used[b], i + 1)
                        sp.dma_start(rows[:, b, :], k.dst_r[ds((i * 2 + b) * (G * P), G * P)].partition_broadcast(P)).then_inc(row_in[b], 16)

            @block.gpsimd
            def _(pool):
                nc.gpsimd.memset(before[:], 1.0).then_inc(ramps, 1)
                pool.wait_ge(ramps, 1)
                nc.gpsimd.affine_select(out=before[:], in_=before[:], compare_op=ALU.is_gt, fill=0.0, base=0,
                                        pattern=[[-1, P]], channel_multiplier=1).then_inc(ramps, 1)
                nc.gpsimd.iota(pad[:], [[0, 1]], base=PAD_ROW, channel_multiplier=1,
                               allow_small_or_imprecise_dtypes=True).then_inc(ramps, 1)

            @block.vector
            def _(dve):
                for b in range(2):
                    dve.sem_inc(row_used[b], 1)
                c = Chain(dve, chain)
                dve.wait_ge(loaded, 64)
                for idx in (k.src_i, k.src_rel_i, k.dst_i, k.row_i):
                    nc.vector.memset(idx[:, ET:ET + G], 0)
                c.step(nc.vector.tensor_copy(k.dst_f[:], dst[:]))
                c.step(nc.vector.tensor_copy(k.dst_i[:, 0:ET], dst[:]))
                c.link(nc.vector.tensor_scalar(dmask[:], src[:], float(REL), None, ALU.mult))
                c.link(nc.vector.tensor_tensor(dmask[:], dmask[:], typ[:], ALU.add))
                c.step(nc.vector.tensor_copy(k.src_rel_i[:, 0:ET], dmask[:]))
                c.link(nc.vector.tensor_copy(k.src_i[:, 0:ET], src[:]))
                base = c.n
                dve.wait_ge(ramps, 3)
                with dve.Fori(0, NG // 2) as i:
                    for b in range(2):
                        dve.wait_ge(row_in[b], 16 * i + 16)
                        for j in range(G):
                            t = (i * 2 + b) * G + j
                            ins = nc.vector.scalar_tensor_tensor(hits[:, b, j * P:(j + 1) * P], rows[:, b, j * P:(j + 1) * P],
                                                                 k.dst_f[:, ds(t, 1)], before[:], ALU.is_equal, ALU.mult)
                            ins.then_inc(chain, 1)
                        dve.wait_ge(chain, base + (i * 2 + b) * (G + 1) + G)
                        nc.vector.tensor_reduce(prior[:, ds((i * 2 + b) * G, G)], hits[:, b, :].rearrange("p (g q) -> p g q", g=G),
                                                AX_X, ALU.add).then_inc(chain, 1)
                        dve.sem_inc(row_used[b], 1)
                c.n = base + NG * (G + 1)
                c.wait()
                c.link(nc.vector.tensor_scalar(first[:], prior[:], 0.0, None, ALU.is_equal))
                c.link(nc.vector.tensor_scalar(dmask[:], k.dst_f[:], pad[:], None, ALU.subtract))
                c.link(nc.vector.tensor_tensor(dmask[:], dmask[:], first[:], ALU.mult))
                c.link(nc.vector.tensor_scalar(dmask[:], dmask[:], pad[:], None, ALU.add))
                c.link(nc.vector.tensor_copy(k.row_i[:, 0:ET], dmask[:]))


def normalise_all(k, rows, cols, eps=EPS):
    nc = k.nc
    with stage(k) as s:
        stats = s.sb("stats", [P, NT, 6])
        mv = s.sb("mv", [P, NT, 2])
        veps = s.sb("veps", [P, NT])
        rstd = s.sb("rstd", [P, NT])
        ps = s.ps("turned", [128, 4, 512])
        chain, var, sd, rows_done, turned, copied = (s.sem(n) for n in ("chain", "var", "sd", "rows_done", "turned", "copied"))
        with s.block() as block:
            @block.vector
            def _(dve):
                c = Chain(dve, chain)
                for t in range(NT):
                    c.step(nc.vector.bn_stats(stats[:, t, :], k.x[:, t, :]))
                c.wait()
                for t in range(NT):
                    c.step(nc.vector.bn_aggr(mv[:, t, :], stats[:, t, :]))
                c.wait()
                nc.vector.tensor_scalar(veps[:], mv[:, :, 1], eps, None, ALU.add).then_inc(var, 1)
                dve.wait_ge(sd, 1)
                c.link(nc.vector.reciprocal(rstd[:], veps[:]))
                for t in range(NT):
                    nc.vector.tensor_scalar(rows[:, t, :], k.x[:, t, :], mv[:, t, 0:1], rstd[:, t:t + 1],
                                            ALU.subtract, ALU.mult).then_inc(rows_done, 1)

            @block.scalar
            def _(act):
                act.wait_ge(var, 1)
                nc.scalar.activation(veps[:], veps[:], ACT.Sqrt).then_inc(sd, 1)
                for t in range(NT):
                    act.wait_ge(turned, t + 1)
                    nc.scalar.activation(cols[:, :, t * P:(t + 1) * P],
                                         ps[:, t % 4, 0:2 * P].rearrange("p (c n) -> p c n", c=2), ACT.Copy).then_inc(copied, 1)

            @block.tensor
            def _(pe):
                for t in range(NT):
                    pe.wait_ge(rows_done, t + 1)
                    if t >= 4:
                        pe.wait_ge(copied, t - 3)
                    nc.tensor.transpose(ps[:, t % 4, 0:P], rows[:, t, 0:128], k.ident[0:P, 0:P])
                    nc.tensor.transpose(ps[:, t % 4, P:2 * P], rows[:, t, 128:256], k.ident[0:P, 0:P]).then_inc(turned, 1)


def relation_tables(k, cols):
    nc = k.nc
    with stage(k) as s:
        w = s.sb("w_rel", [128, 2, REL, 128])
        row = s.sb("row", [P, 5, REL, D])
        ps = s.ps("ps", [P, 8, 512])
        zeroed, w_in, mm, evac = (s.sem(n) for n in ("zeroed", "w_in", "mm", "evac"))
        stored = [s.sem(f"stored{j}") for j in range(5)]
        with s.block() as block:
            @block.sync
            def _(sp):
                sp.wait_ge(zeroed, 1)
                for b in range(BASES):
                    lo = SUB * (b % 4)
                    sp.dma_start(w[lo:lo + SUB, b // 4, :, lo:lo + SUB], k.w_rel[b]).then_inc(w_in, 16)
                with sp.Fori(0, NT // 5) as i:
                    for j in range(5):
                        sp.wait_ge(evac, (i * 5 + j) * 4 + 4)
                        sp.dma_start(k.rel_rows[ds((i * 5 + j) * P, P), :], row[:, j, :, :].rearrange("p r f -> p (r f)")).then_inc(stored[j], 16)
                for j in range(5):
                    sp.wait_ge(stored[j], 16 * (NT // 5))

            @block.vector
            def _(dve):
                nc.vector.memset(w[:], 0.0).then_inc(zeroed, 1)

            @block.tensor
            def _(pe):
                pe.wait_ge(w_in, 16 * BASES)
                for t in range(NT):
                    for q in range(4):
                        c, half = q // 2, q % 2
                        n = t * 4 + q
                        if n >= 8:
                            pe.wait_ge(evac, n - 7)
                        nc.tensor.matmul(ps[:, n % 8, :], cols[:, c, t * P:(t + 1) * P],
                                         w[:, c, 4 * half:4 * half + 4, :].rearrange("p r o -> p (r o)"),
                                         start=True, stop=True).then_inc(mm, 1)

            @block.scalar
            def _(act):
                for t in range(NT):
                    if t >= 5:
                        act.wait_ge(stored[t % 5], 16 * (t // 5))
                    for q in range(4):
                        c, half = q // 2, q % 2
                        act.wait_ge(mm, t * 4 + q + 1)
                        nc.scalar.activation(row[:, t % 5, 4 * half:4 * half + 4, c * 128:(c + 1) * 128],
                                             ps[:, (t * 4 + q) % 8, :].rearrange("p (r o) -> p r o", r=4), ACT.Copy).then_inc(evac, 1)


class Mlp:

    def __init__(self, n_in, attr, w1, b1, w2, b2):
        self.n_in, self.attr, self.w1, self.b1, self.w2, self.b2 = n_in, attr, w1, b1, w2, b2


def upto(g, j, back=0):
    return (g - back + 2) * G + j + 1


def edge_sums(k, table, src_idx, width, weight=None, heads=0, att_rows=None, mlp=None):
    nc = k.nc
    att = heads > 0
    HD = D // heads if att else 0
    with stage(k) as s:
        rows = s.sb("rows", [P, 2, G * P], I32)
        gi = s.sb("gi", [P, 2, G], I32)
        di = s.sb("di", [P, 2, G], I32)
        si = s.sb("si", [P, 2, G], I32)
        msg = s.sb("msg", [P, 2, G, width])
        same = s.sb("same", [P, 2, G, P])
        z = s.sb("z", [P, 2, G, width])
        zero = s.sb("zero", [P, width])
        ps = s.ps("ps", [P, G, 512])
        if att:
            arow = s.sb("arow", [P, 2, G, 2 * heads])
            e1 = s.sb("e1", [P, 2, G, heads])
            e2 = s.sb("e2", [P, 2, G, heads])
        if mlp:
            attr = s.sb("attr", [mlp.n_in, 2, G * P])
            hid = s.sb("hid", [128, 2, 2, G * P])
            pos = s.sb("pos", [128, 2, 2, G * P])
            hs = s.sb("hs", [128, 2, 2, G * P])
            w1, b1 = s.sb("w1", [mlp.n_in, D]), s.sb("b1", [128, 2])
            w2, b2 = s.sb("w2", [128, 2, D]), s.sb("b2", [1, D])
            w_in, hid_ln = s.sem("w_in"), s.sem("hid_ln")
            ps_h = s.ps("ps_h", [128, 2, 512])
            ps_f = s.ps("ps_f", [P, G, D])
        turns = s.sem("turns")
        zeroed, idx_done, mm, z_done, same_done, si_done = (s.sem(n) for n in ("zeroed", "idx", "mm", "z_done", "same", "si"))
        e_done, a_done, ready, chain = (s.sem(n) for n in ("e_done", "a_done", "ready", "chain"))
        hid_mm, hid_act, hid_done, fil_mm, fil_used = (s.sem(n) for n in ("hid_mm", "hid_act", "hid_done", "fil_mm", "fil_used"))
        row_in = [s.sem("row_in0"), s.sem("row_in1")]
        msg_in = [s.sem("msg_in0"), s.sem("msg_in1")]
        attr_in = [s.sem("attr_in0"), s.sem("attr_in1")]
        added = [s.sem(f"added{j}") for j in range(G)]
        gathers = 2 * G if att else G
        with s.block() as block:
            @block.sync
            def _(sp):
                if mlp:
                    sp.dma_start(w1[:], mlp.w1).then_inc(w_in, 16)
                    sp.dma_start(b1[:], mlp.b1.rearrange("(c p) -> p c", p=128), allow_slow_non_contiguous=True).then_inc(w_in, 16)
                    sp.dma_start(w2[:], mlp.w2.rearrange("(c p) f -> p c f", p=128)).then_inc(w_in, 16)
                    sp.dma_start(b2[:], mlp.b2.rearrange("(a f) -> a f", a=1)).then_inc(w_in, 16)
                with sp.Fori(0, NG // 2) as i:
                    for b in range(2):
                        g = i * 2 + b
                        sp.wait_ge(same_done, upto(g, G - 1, back=2))
                        sp.dma_start(rows[:, b, :], k.dst_r[ds(g * (G * P), G * P)].partition_broadcast(P)).then_inc(row_in[b], 16)
                        if mlp:
                            sp.wait_ge(hid_mm, 2 * g + 2)
                            sp.dma_start(attr[:, b, :], mlp.attr[:, ds(g * (G * P), G * P)]).then_inc(attr_in[b], 16)

            @block.gpsimd
            def _(pool):
                nc.gpsimd.memset(zero[:], 0.0).then_inc(zeroed, 1)
                pool.wait_ge(zeroed, 1)
                for half in range(2):
                    for j in range(G):
                        if half:
                            pool.wait_ge(added[j], 16)
                        pool.dma_start(k.acc[width][j].rearrange("(h t p) f -> h p t f", p=P, h=2)[half],
                                       zero[:].unsqueeze(1).to_broadcast([P, AT // 2, width])).then_inc(added[j], 16)

                def gather(b, g):
                    pool.wait_ge(idx_done, g + 1)
                    pool.wait_ge(mm, upto(g, G - 1, back=2))
                    pool.sem_inc(turns, 1)
                    for j in range(G):
                        nc.gpsimd.indirect_dma_start(msg[:, b, j, :], None, table, bass.IndirectOffsetOnAxis(gi[:, b, j:j + 1], 0)).then_inc(msg_in[b], 16)
                        if att:
                            nc.gpsimd.indirect_dma_start(arow[:, b, j, :], None, att_rows, bass.IndirectOffsetOnAxis(di[:, b, j:j + 1], 0)).then_inc(msg_in[b], 16)

                def scatter(b, g):
                    pool.wait_ge(si_done, g + 1)
                    for j in range(G):
                        pool.wait_ge(z_done, upto(g, j))
                        pool.wait_ge(added[j], (g + 2) * 16)
                        pool.sem_inc(turns, 1)
                        nc.gpsimd.indirect_dma_start(k.acc[width][j], bass.IndirectOffsetOnAxis(si[:, b, j:j + 1], 0), z[:, b, j, :], None,
                                                     compute_op=ALU.add).then_inc(added[j], 16)

                gather(0, 0)
                last = NG // 2 - 1
                with pool.Fori(0, last) as i:
                    gather(1, i * 2 + 1)
                    scatter(0, i * 2)
                    gather(0, i * 2 + 2)
                    scatter(1, i * 2 + 1)
                gather(1, NG - 1)
                scatter(0, NG - 2)
                scatter(1, NG - 1)
                for j in range(G):
                    pool.wait_ge(added[j], (NG + 2) * 16)

            @block.vector
            def _(dve):
                dve.sem_inc(same_done, 2 * G)
                dve.sem_inc(hid_done, 2)

                def indices(b, g):
                    dve.wait_ge(mm, upto(g, G - 1, back=2))
                    if att:
                        nc.vector.tensor_copy(di[:, b, :], k.dst_i[:, ds(g * G, G)]).then_inc(chain, 1)
                        dve.wait_ge(chain, g + 1)
                    nc.vector.tensor_copy(gi[:, b, :], src_idx[:, ds(g * G, G)]).then_inc(idx_done, 1)

                def compare(b, g, i):
                    dve.wait_ge(row_in[b], 16 * i + 16)
                    for j in range(G):
                        args = (weight[:, ds(g * G + j, 1)], ALU.is_equal, ALU.mult) if weight is not None else (None, ALU.is_equal)
                        nc.vector.tensor_scalar(same[:, b, j, :], rows[:, b, j * P:(j + 1) * P], k.dst_f[:, ds(g * G + j, 1)], *args).then_inc(same_done, 1)

                def messages(b, g, i):
                    dve.wait_ge(msg_in[b], 16 * gathers * (i + 1))
                    if att:
                        c0 = 3 * g
                        nc.vector.tensor_tensor(e1[:, b, :, :], msg[:, b, :, D:D + heads], arow[:, b, :, 0:heads], ALU.add).then_inc(e_done, 1)
                        dve.wait_ge(e_done, c0 + 1)
                        nc.vector.scalar_tensor_tensor(e2[:, b, :, :], e1[:, b, :, :], 0.2, e1[:, b, :, :], ALU.mult, ALU.max).then_inc(e_done, 1)
                        dve.wait_ge(e_done, c0 + 2)
                        nc.vector.tensor_tensor(e1[:, b, :, :], e2[:, b, :, :], arow[:, b, :, heads:2 * heads], ALU.subtract).then_inc(e_done, 1)
                        dve.wait_ge(a_done, g + 1)
                        for j in range(G):
                            m = msg[:, b, j, 0:D].rearrange("p (h d) -> p h d", h=heads)
                            nc.vector.tensor_tensor(m, m, msg[:, b, j, D:D + heads].unsqueeze(2).to_broadcast([P, heads, HD]), ALU.mult).then_inc(ready, 1)
                    if mlp:
                        for j in range(G):
                            dve.wait_ge(fil_mm, g * G + (j | 1) + 1)
                            nc.vector.tensor_tensor(msg[:, b, j, :], msg[:, b, j, :], ps_f[:, j, :], ALU.mult).then_inc(ready, 1)

                indices(0, 0)
                with dve.Fori(0, NG // 2) as i:
                    for b in range(2):
                        g = i * 2 + b
                        indices(1 - b, g + 1)
                        compare(b, g, i)
                        if mlp:
                            dve.wait_ge(hid_ln, 2 * g + 2)
                            nc.vector.scalar_tensor_tensor(hs[:, b, :, :], hid[:, b, :, :], -math.log(2.0), pos[:, b, :, :], ALU.add, ALU.add).then_inc(hid_done, 1)
                        if att or mlp:
                            messages(b, g, i)

            @block.tensor
            def _(pe):
                pe.sem_inc(mm, 2 * G)
                if mlp:
                    pe.sem_inc(hid_mm, 4)
                    pe.wait_ge(w_in, 64)

                def filters(b, g, i):
                    pe.wait_ge(attr_in[b], 16 * i + 16)
                    for c in range(2):
                        pe.wait_ge(hid_act, 2 * g + c + 1)
                        nc.tensor.matmul(ps_h[:, c, 0:G * P], w1[:, c * 128:(c + 1) * 128], attr[:, b, :], start=True, stop=True).then_inc(hid_mm, 1)
                    pe.wait_ge(hid_done, g + 3)
                    for j in range(G):
                        pe.wait_ge(ready, upto(g, j | 1, back=1) - G)
                        nc.tensor.matmul(ps_f[:, j, :], hs[:, b, 0, j * P:(j + 1) * P], w2[:, 0, :], start=True, stop=False)
                        nc.tensor.matmul(ps_f[:, j, :], hs[:, b, 1, j * P:(j + 1) * P], w2[:, 1, :], start=False, stop=False)
                        nc.tensor.matmul(ps_f[:, j, :], k.ones[0:1, 0:P], b2[:], start=False, stop=True).then_inc(fil_mm, 1)

                with pe.Fori(0, NG // 2) as i:
                    for b in range(2):
                        g = i * 2 + b
                        if mlp:
                            filters(b, g, i)
                        pe.wait_ge(msg_in[b], 16 * gathers * (i + 1))
                        for j in range(G):
                            pe.wait_ge(same_done, upto(g, j))
                            if att or mlp:
                                pe.wait_ge(ready, upto(g, j) - G)
                            pe.wait_ge(z_done, upto(g, j, back=1))
                            nc.tensor.matmul(ps[:, j, 0:width], same[:, b, j, :], msg[:, b, j, :], start=True, stop=True).then_inc(mm, 1)

            @block.scalar
            def _(act):
                act.sem_inc(z_done, 2 * G)
                act.sem_inc(ready, G)
                act.sem_inc(hid_act, 2)

                def weights(b, g):
                    act.wait_ge(e_done, 3 * g + 3)
                    nc.scalar.activation(msg[:, b, :, D:D + heads], e1[:, b, :, :], ACT.Exp).then_inc(a_done, 1)

                def hidden(b, g):
                    act.wait_ge(hid_done, g + 1)
                    for c in range(2):
                        act.wait_ge(hid_mm, 2 * g + c + 5)
                        nc.scalar.activation(pos[:, b, c, :], ps_h[:, c, 0:G * P], ACT.Relu, bias=b1[:, c:c + 1])
                        nc.scalar.activation(hid[:, b, c, :], ps_h[:, c, 0:G * P], ACT.Abs, bias=b1[:, c:c + 1]).then_inc(hid_act, 1)
                    act.wait_ge(hid_act, 2 * g + 4)
                    nc.scalar.activation(hid[:, b, :, :], hid[:, b, :, :], ACT.Exp, scale=-1.0).then_inc(hid_ln, 1)
                    act.wait_ge(hid_ln, 2 * g + 1)
                    nc.scalar.activation(hid[:, b, :, :], hid[:, b, :, :], ACT.Ln, bias=1.0).then_inc(hid_ln, 1)

                if mlp:
                    act.wait_ge(w_in, 64)

                with act.Fori(0, NG // 2) as i:
                    for b in range(2):
                        g = i * 2 + b
                        if att:
                            weights(b, g)
                        if mlp:
                            hidden(b, g)
                        for j in range(G):
                            act.wait_ge(added[j], (g + 1) * 16)
                        nc.scalar.activation(si[:, b, :], k.row_i[:, ds(g * G, G)], ACT.Copy).then_inc(si_done, 1)
                        for j in range(G):
                            act.wait_ge(mm, upto(g, j))
                            nc.scalar.activation(z[:, b, j, :], ps[:, j, 0:width], ACT.Copy).then_inc(z_done, 1)


def collect(k, agg, width):
    nc = k.nc
    with stage(k) as s:
        part = s.sb("part", [P, 5, G, width])
        pair = s.sb("pair", [P, 5, 2, width])
        part_in = [s.sem(f"part_in{j}") for j in range(5)]
        paired, summed = s.sem("paired"), s.sem("summed")
        acc = [q.rearrange("(t p) f -> t p f", p=P) for q in k.acc[width]]
        with s.block() as block:
            @block.sync
            def _(sp):
                for t in range(NT):
                    if t >= 5:
                        sp.wait_ge(paired, t - 4)
                    for j in range(G):
                        sp.dma_start(part[:, t % 5, j, :], acc[j][t, :, :]).then_inc(part_in[t % 5], 16)

            @block.vector
            def _(dve):
                for t in range(NT):
                    j = t % 5
                    dve.wait_ge(part_in[j], 16 * G * (t // 5 + 1))
                    nc.vector.tensor_tensor(pair[:, j, :, :], part[:, j, 0:2, :], part[:, j, 2:4, :], ALU.add).then_inc(paired, 1)
                    dve.wait_ge(paired, t + 1)
                    nc.vector.tensor_tensor(agg[:, t, 0:width], pair[:, j, 0, :], pair[:, j, 1, :], ALU.add).then_inc(summed, 1)


def add_to_x(k, agg):
    nc = k.nc
    with stage(k) as s:
        done = s.sem("done")
        with s.block() as block:
            @block.vector
            def _(dve):
                nc.vector.tensor_tensor(k.x[:], k.x[:], agg[:], ALU.add).then_inc(done, 1)


def first_of_max(nc, dve, c, score, best, onehot, ramp, tmp, pick):
    L = score.shape[-1]
    wide = lambda a: a.unsqueeze(2).to_broadcast([P, NT, L])
    c.link(nc.vector.tensor_reduce(best, score, AX_X, ALU.max))
    c.link(nc.vector.tensor_tensor(tmp, score, wide(best), ALU.is_equal))
    c.link(nc.vector.tensor_tensor(tmp, tmp, ramp, ALU.mult))
    c.link(nc.vector.tensor_reduce(pick, tmp, AX_X, ALU.max))
    c.link(nc.vector.tensor_tensor(onehot, ramp, wide(pick), ALU.is_equal))


def gates(k, cols, gate, n_exp, w, bias, mode, router=None, capacity=0, scores=None):
    nc = k.nc
    L = n_exp
    with stage(k) as s:
        sb3 = lambda n: s.sb(n, [P, NT, L])
        lg, tmp, oh1, oh2, rest = (sb3(n) for n in ("lg", "tmp", "oh1", "oh2", "rest"))
        ramp = s.sb("ramp", [P, NT, L])
        m1, m2, pick, w1, w2 = (s.sb(n, [P, NT]) for n in ("m1", "m2", "pick", "w1", "w2"))
        w_sb, b_sb = s.sb("w", [128, 2, L]), s.sb("b", [P, L])
        tri = s.sb("tri", [P, P])
        ps = s.ps("ps", [P, 512])
        ps_pre, ps_tot = s.ps("pre", [P, 512]), s.ps("tot", [P, 512])
        tot = s.sb("tot_sb", [P, NT + 1, L])
        w_in, mm, ramps, chain, to_act, from_act, counted = (s.sem(n) for n in ("w_in", "mm", "ramps", "chain", "to_act", "from_act", "counted"))
        if router:
            rw1, rb1, rw2 = s.sb("rw1", [128, 2, 128]), s.sb("rb1", [128, 1]), s.sb("rw2", [128, L])
            rh = s.sb("rh", [128, N])
            ps_r = s.ps("ps_r", [128, 4, 512])
            r_mm, r_act = s.sem("r_mm"), s.sem("r_act")
        with s.block() as block:
            @block.sync
            def _(sp):
                if scores is None:
                    sp.dma_start(b_sb[:], bias.partition_broadcast(P)).then_inc(w_in, 16)
                if router:
                    sp.dma_start(rw1[:], router.w1.rearrange("(c p) h -> p c h", p=128)).then_inc(w_in, 16)
                    sp.dma_start(rb1[:], router.b1.rearrange("(p a) -> p a", a=1)).then_inc(w_in, 16)
                    sp.dma_start(rw2[:], router.w2).then_inc(w_in, 16)
                elif scores is None:
                    sp.dma_start(w_sb[:], w.rearrange("(c p) e -> p c e", p=128)).then_inc(w_in, 16)

            @block.gpsimd
            def _(pool):
                nc.gpsimd.iota(ramp[:], [[0, NT], [-1, L]], base=L, channel_multiplier=0, allow_small_or_imprecise_dtypes=True).then_inc(ramps, 1)
                nc.gpsimd.memset(tri[:], 1.0).then_inc(ramps, 1)
                pool.wait_ge(ramps, 2)
                nc.gpsimd.affine_select(out=tri[:], in_=tri[:], compare_op=ALU.is_gt, fill=0.0, base=0,
                                        pattern=[[1, P]], channel_multiplier=-1).then_inc(ramps, 1)

            @block.tensor
            def _(pe):
                if scores is None:
                    pe.wait_ge(w_in, 64 if router else 32)
                if router:
                    for q, n0 in enumerate(range(0, N, 500)):
                        m = min(500, N - n0)
                        if q >= 4:
                            pe.wait_ge(r_act, q - 3)
                        nc.tensor.matmul(ps_r[:, q % 4, 0:m], rw1[:, 0, :], cols[:, 0, n0:n0 + m], start=True, stop=False)
                        nc.tensor.matmul(ps_r[:, q % 4, 0:m], rw1[:, 1, :], cols[:, 1, n0:n0 + m], start=False, stop=True).then_inc(r_mm, 1)
                    pe.wait_ge(r_act, (N + 499) // 500)
                    for t in range(NT):
                        ins = nc.tensor.matmul(ps[:, t * L:(t + 1) * L], rh[:, t * P:(t + 1) * P], rw2[:], start=True, stop=True)
                    ins.then_inc(mm, 1)
                elif scores is None:
                    for t in range(NT):
                        nc.tensor.matmul(ps[:, t * L:(t + 1) * L], cols[:, 0, t * P:(t + 1) * P], w_sb[:, 0, :], start=True, stop=False)
                        ins = nc.tensor.matmul(ps[:, t * L:(t + 1) * L], cols[:, 1, t * P:(t + 1) * P], w_sb[:, 1, :], start=False, stop=True)
                    ins.then_inc(mm, 1)
                if mode == "top1":
                    pe.wait_ge(ramps, 3)
                    pe.wait_ge(counted, 1)
                    flat = oh1[:].rearrange("p t e -> p (t e)")
                    nc.tensor.matmul(ps_pre[:, 0:NT * L], tri[:], flat, start=True, stop=True)
                    nc.tensor.matmul(ps_tot[:, 0:NT * L], k.ones[0:P, 0:P], flat, start=True, stop=True).then_inc(mm, 1)

            @block.scalar
            def _(act):
                if router:
                    act.wait_ge(w_in, 64)
                    for q, n0 in enumerate(range(0, N, 500)):
                        m = min(500, N - n0)
                        act.wait_ge(r_mm, q + 1)
                        nc.scalar.activation(rh[:, n0:n0 + m], ps_r[:, q % 4, 0:m], ACT.Relu, bias=rb1[:]).then_inc(r_act, 1)
                n = 0
                if mode != "top2":
                    act.wait_ge(to_act, 1)
                    nc.scalar.activation(lg[:], tmp[:], ACT.Exp).then_inc(from_act, 1)
                    n = 1
                if mode != "top1":
                    act.wait_ge(to_act, n + 1)
                    nc.scalar.activation(w2[:], pick[:], ACT.Exp).then_inc(from_act, 1)

            @block.vector
            def _(dve):
                c = Chain(dve, chain)
                wide = lambda a: a.unsqueeze(2).to_broadcast([P, NT, L])
                dve.wait_ge(ramps, 1)
                acts = 0
                score = lg[:]
                if scores is None:
                    dve.wait_ge(mm, 1)
                    dve.wait_ge(w_in, 64 if router else 32)
                    c.link(nc.vector.tensor_tensor(lg[:], ps[:, 0:NT * L].rearrange("p (t e) -> p t e", e=L),
                                                   b_sb[:].unsqueeze(1).to_broadcast([P, NT, L]), ALU.add))
                else:
                    score = scores
                if mode != "top2":
                    c.link(nc.vector.tensor_reduce(m1[:], lg[:], AX_X, ALU.max))
                    nc.vector.tensor_tensor(tmp[:], lg[:], wide(m1[:]), ALU.subtract).then_inc(to_act, 1)
                    acts += 1
                    dve.wait_ge(from_act, acts)
                    c.link(nc.vector.tensor_reduce(m2[:], lg[:], AX_X, ALU.add))
                    c.link(nc.vector.reciprocal(w1[:], m2[:]))
                    c.link(nc.vector.tensor_tensor(lg[:], lg[:], wide(w1[:]), ALU.mult))
                first_of_max(nc, dve, c, score, m1[:], oh1[:], ramp[:], tmp[:], pick[:])
                if mode == "top1":
                    dve.sem_inc(counted, 1)
                    dve.wait_ge(mm, 2)
                    c.step(nc.vector.memset(tot[:, 0, :], 0.0))
                    c.link(nc.vector.tensor_copy(tot[:, 1:NT + 1, :], ps_tot[:, 0:NT * L].rearrange("p (t e) -> p t e", e=L)))
                    for t in range(1, NT + 1):
                        c.link(nc.vector.tensor_tensor(tot[:, t, :], tot[:, t, :], tot[:, t - 1, :], ALU.add))
                    c.link(nc.vector.tensor_tensor(tmp[:], ps_pre[:, 0:NT * L].rearrange("p (t e) -> p t e", e=L), tot[:, 0:NT, :], ALU.add))
                    c.link(nc.vector.tensor_scalar(tmp[:], tmp[:], float(capacity), None, ALU.is_lt))
                    c.link(nc.vector.tensor_tensor(tmp[:], tmp[:], oh1[:], ALU.mult))
                    c.link(nc.vector.tensor_tensor(gate[:], tmp[:], wide(m1[:]), ALU.mult))
                    return
                c.link(nc.vector.tensor_scalar(tmp[:], oh1[:], -3.0e38, None, ALU.mult))
                c.link(nc.vector.tensor_tensor(rest[:], score, tmp[:], ALU.add))
                first_of_max(nc, dve, c, rest[:], m2[:], oh2[:], ramp[:], tmp[:], pick[:])
                nc.vector.tensor_tensor(pick[:], m2[:], m1[:], ALU.subtract).then_inc(to_act, 1)
                acts += 1
                dve.wait_ge(from_act, acts)
                c.link(nc.vector.tensor_scalar(w1[:], w2[:], 1.0, None, ALU.add))
                c.link(nc.vector.reciprocal(w1[:], w1[:]))
                c.link(nc.vector.tensor_tensor(w2[:], w2[:], w1[:], ALU.mult))
                c.link(nc.vector.tensor_tensor(oh1[:], oh1[:], wide(w1[:]), ALU.mult))
                c.link(nc.vector.tensor_tensor(oh2[:], oh2[:], wide(w2[:]), ALU.mult))
                c.link(nc.vector.tensor_tensor(gate[:], oh1[:], oh2[:], ALU.add))


class Experts:

    def __init__(self, n, f, func, w1, b1, w2, b2, wm=None, bm=None):
        self.n, self.f, self.func, self.w1, self.b1, self.w2, self.b2, self.wm, self.bm = n, f, func, w1, b1, w2, b2, wm, bm


def experts(k, cols, gate, acc, x):
    nc = k.nc
    FC = x.f // 128
    FM = 2 if x.wm is not None else 0
    NB, TB = NT // 5, 5
    PARTS = ((0, 3 * P), (3 * P, 2 * P))
    UP, MID = 2 * FC, 2 * FM
    EV = UP + MID
    BU = 2 if x.n % 2 == 0 else 1
    with stage(k) as s:
        w1 = s.sb("w1", [128, 2, 2, x.f])
        w2 = s.sb("w2", [128, 2, FM or FC, D])
        b1 = s.sb("b1", [128, 2, FC])
        b2 = s.sb("b2", [P, 2, D])
        hid = s.sb("hid", [128, FC, TB * P])
        tmp = s.sb("tmp", [P, TB, D])
        ps_h = s.ps("ps_h", [128, 4, 512])
        ps_o = s.ps("ps_o", [P, 3, 512])
        if FM:
            wm, bm = s.sb("wm", [128, 2, 2, D]), s.sb("bm", [128, 2, FM])
            mid = s.sb("mid", [128, FM, TB * P])
        zeroed, h_mm, h_sb, o_mm, o_used, chain = (s.sem(n) for n in ("zeroed", "h_mm", "h_sb", "o_mm", "o_used", "chain"))
        w_in = [s.sem("w_in0"), s.sem("w_in1")]
        n_w = 6 if FM else 4
        pair_end = lambda j: min(j | 1, TB - 1)
        out_at = lambda j: ps_o[:, j // 2, (j % 2) * D:(j % 2 + 1) * D]
        with s.block() as block:
            @block.sync
            def _(sp):
                with sp.Fori(0, x.n // BU) as i:
                    for b in range(BU):
                        e = i * BU + b
                        sp.wait_ge(o_used, e * NT + TB)
                        sp.dma_start(w1[:, b, :, :], x.w1[ds(e, 1)].rearrange("e (c p) f -> p (e c) f", p=128)).then_inc(w_in[b], 16)
                        if FM:
                            sp.dma_start(wm[:, b, :, :], x.wm[ds(e, 1)].rearrange("e (c p) f -> p (e c) f", p=128)).then_inc(w_in[b], 16)
                        sp.dma_start(b1[:, b, :], x.b1[ds(e * 128, 128), :]).then_inc(w_in[b], 16)
                        if FM:
                            sp.dma_start(bm[:, b, :], x.bm[ds(e * 128, 128), :]).then_inc(w_in[b], 16)
                        sp.dma_start(w2[:, b, :, :], x.w2[ds(e, 1)].rearrange("e (c p) f -> p (e c) f", p=128)).then_inc(w_in[b], 16)
                        sp.dma_start(b2[:, b, :], x.b2[ds(e * D, D)].partition_broadcast(P)).then_inc(w_in[b], 16)

            @block.tensor
            def _(pe):
                def layer(nq, lhs, rhs, count, chunks_in):
                    n = 0
                    for f in range(count):
                        for q, (lo, m) in enumerate(PARTS):
                            pe.wait_ge(h_sb, nq + n + 1)
                            for c in range(chunks_in):
                                ins = nc.tensor.matmul(ps_h[:, n % 4, 0:m], lhs(c, f), rhs(c, lo, m), start=c == 0, stop=c == chunks_in - 1)
                            ins.then_inc(h_mm, 1)
                            n += 1

                with pe.Fori(0, x.n // BU) as i:
                    for b in range(BU):
                        e = i * BU + b
                        with pe.Fori(0, NB) as blk:
                            pe.wait_ge(w_in[b], 16 * n_w * (i + 1))
                            turn = e * NB + blk
                            layer(turn * EV, lambda c, f: w1[:, b, c, f * 128:(f + 1) * 128],
                                  lambda c, lo, m: cols[:, c, ds(blk * (TB * P) + lo, m)], FC, 2)
                            last, n_last = hid, FC
                            if FM:
                                pe.wait_ge(h_sb, turn * EV + UP + 4)
                                layer(turn * EV + UP, lambda c, f: wm[:, b, c, f * 128:(f + 1) * 128],
                                      lambda c, lo, m: hid[:, c, lo:lo + m], FM, FC)
                                last, n_last = mid, FM
                            pe.wait_ge(h_sb, turn * EV + EV + 4)
                            for j in range(TB):
                                pe.wait_ge(o_used, turn * TB + pair_end(j) + 1 + NT)
                                for c in range(n_last):
                                    ins = nc.tensor.matmul(out_at(j), last[:, c, j * P:(j + 1) * P], w2[:, b, c, :], start=c == 0, stop=c == n_last - 1)
                                ins.then_inc(o_mm, 1)

            @block.scalar
            def _(act):
                act.sem_inc(h_sb, 4)
                with act.Fori(0, x.n // BU) as i:
                    for b in range(BU):
                        e = i * BU + b
                        with act.Fori(0, NB) as blk:
                            act.wait_ge(w_in[b], 16 * n_w * (i + 1))
                            turn = e * NB + blk
                            n = 0
                            for f in range(FC):
                                for lo, m in PARTS:
                                    act.wait_ge(h_mm, turn * EV + n + 1)
                                    nc.scalar.activation(hid[:, f, lo:lo + m], ps_h[:, n % 4, 0:m], x.func, bias=b1[:, b, f:f + 1]).then_inc(h_sb, 1)
                                    n += 1
                            for f in range(FM):
                                for lo, m in PARTS:
                                    act.wait_ge(h_mm, turn * EV + n + 1)
                                    nc.scalar.activation(mid[:, f, lo:lo + m], ps_h[:, n % 4, 0:m], x.func, bias=bm[:, b, f:f + 1]).then_inc(h_sb, 1)
                                    n += 1

            @block.vector
            def _(dve):
                nc.vector.memset(acc[:], 0.0).then_inc(chain, 1)
                dve.sem_inc(o_used, NT + TB)
                with dve.Fori(0, x.n // BU) as i:
                    for b in range(BU):
                        e = i * BU + b
                        with dve.Fori(0, NB) as blk:
                            dve.wait_ge(w_in[b], 16 * n_w * (i + 1))
                            for j in range(TB):
                                t = blk * TB + j
                                n = e * NT + t
                                dve.wait_ge(o_mm, e * NT + blk * TB + pair_end(j) + 1)
                                nc.vector.tensor_tensor(tmp[:, j, :], out_at(j), b2[:, b, :], ALU.add).then_inc(o_used, 1)
                                dve.wait_ge(o_used, n + 1 + NT + TB)
                                nc.vector.scalar_tensor_tensor(acc[:, ds(t, 1), :].rearrange("p t f -> p (t f)"), tmp[:, j, :], gate[:, ds(t, 1), ds(e, 1)].rearrange("p t e -> p (t e)"),
                                                               acc[:, ds(t, 1), :].rearrange("p t f -> p (t f)"), ALU.mult, ALU.add).then_inc(chain, 1)


def finish_norm(k, v, add=None, gamma=None, beta=None, to_x=True, width=D):
    nc = k.nc
    with stage(k) as s:
        stats = s.sb("stats", [P, NT, 6])
        mv = s.sb("mv", [P, NT, 2])
        veps, rstd = s.sb("veps", [P, NT]), s.sb("rstd", [P, NT])
        g_sb, b_sb = s.sb("gamma", [P, width]), s.sb("beta", [P, width])
        g_in, chain, var, sd = (s.sem(n) for n in ("g_in", "chain", "var", "sd"))
        wide = lambda a: a.unsqueeze(1).to_broadcast([P, NT, width])
        with s.block() as block:
            @block.sync
            def _(sp):
                sp.dma_start(g_sb[:], gamma.partition_broadcast(P)).then_inc(g_in, 16)
                sp.dma_start(b_sb[:], beta.partition_broadcast(P)).then_inc(g_in, 16)

            @block.scalar
            def _(act):
                act.wait_ge(var, 1)
                nc.scalar.activation(veps[:], veps[:], ACT.Sqrt).then_inc(sd, 1)

            @block.vector
            def _(dve):
                c = Chain(dve, chain)
                if add is not None:
                    c.link(nc.vector.tensor_tensor(v[:], v[:], add[:], ALU.add))
                for t in range(NT):
                    c.step(nc.vector.bn_stats(stats[:, t, :], v[:, t, :]))
                c.wait()
                for t in range(NT):
                    c.step(nc.vector.bn_aggr(mv[:, t, :], stats[:, t, :]))
                c.wait()
                nc.vector.tensor_scalar(veps[:], mv[:, :, 1], EPS, None, ALU.add).then_inc(var, 1)
                dve.wait_ge(sd, 1)
                c.link(nc.vector.reciprocal(rstd[:], veps[:]))
                for t in range(NT):
                    c.step(nc.vector.tensor_scalar(v[:, t, :], v[:, t, :], mv[:, t, 0:1], rstd[:, t:t + 1], ALU.subtract, ALU.mult))
                c.wait()
                dve.wait_ge(g_in, 32)
                c.link(nc.vector.tensor_tensor(v[:], v[:], wide(g_sb[:]), ALU.mult))
                c.link(nc.vector.tensor_tensor(v[:], v[:], wide(b_sb[:]), ALU.add))
                if to_x:
                    c.link(nc.vector.tensor_tensor(k.x[:], k.x[:], v[:], ALU.add))


def transfer(k, out, in_):
    with stage(k) as s:
        moved = s.sem("moved")
        with s.block() as block:
            @block.sync
            def _(sp):
                sp.dma_start(out, in_).then_inc(moved, 16)
                sp.wait_ge(moved, 16)


def turn_all(k, rows, cols):
    nc = k.nc
    with stage(k) as s:
        ps = s.ps("turned", [128, 4, 512])
        turned, copied = s.sem("turned"), s.sem("copied")
        with s.block() as block:
            @block.tensor
            def _(pe):
                for t in range(NT):
                    if t >= 4:
                        pe.wait_ge(copied, t - 3)
                    nc.tensor.transpose(ps[:, t % 4, 0:P], rows[:, t, 0:128], k.ident[0:P, 0:P])
                    nc.tensor.transpose(ps[:, t % 4, P:2 * P], rows[:, t, 128:256], k.ident[0:P, 0:P]).then_inc(turned, 1)

            @block.scalar
            def _(act):
                for t in range(NT):
                    act.wait_ge(turned, t + 1)
                    nc.scalar.activation(cols[:, :, t * P:(t + 1) * P],
                                         ps[:, t % 4, 0:2 * P].rearrange("p (c n) -> p c n", c=2), ACT.Copy).then_inc(copied, 1)


def project(k, cols, w, width, rows=None, table=None):
    nc = k.nc
    with stage(k) as s:
        w_sb = s.sb("w", [128, 2, width])
        row = s.sb("row", [P, 5, width]) if rows is None else rows
        at = (lambda t: row[:, t % 5, :]) if rows is None else (lambda t: row[:, t, :])
        ps = s.ps("ps", [P, 4, 512])
        w_in, mm, evac = s.sem("w_in"), s.sem("mm"), s.sem("evac")
        stored = [s.sem(f"stored{j}") for j in range(5)]
        with s.block() as block:
            @block.sync
            def _(sp):
                sp.dma_start(w_sb[:], w.rearrange("(c p) f -> p c f", p=128)).then_inc(w_in, 16)
                if table is not None:
                    for t in range(NT):
                        sp.wait_ge(evac, t + 1)
                        sp.dma_start(table[t * P:(t + 1) * P, 0:width], at(t)).then_inc(stored[t % 5], 16)
                    for j in range(5):
                        sp.wait_ge(stored[j], 16 * (NT // 5))

            @block.tensor
            def _(pe):
                pe.wait_ge(w_in, 16)
                for t in range(NT):
                    if t >= 4:
                        pe.wait_ge(evac, t - 3)
                    nc.tensor.matmul(ps[:, t % 4, 0:width], cols[:, 0, t * P:(t + 1) * P], w_sb[:, 0, :], start=True, stop=False)
                    nc.tensor.matmul(ps[:, t % 4, 0:width], cols[:, 1, t * P:(t + 1) * P], w_sb[:, 1, :], start=False, stop=True).then_inc(mm, 1)

            @block.scalar
            def _(act):
                for t in range(NT):
                    if rows is None and t >= 5:
                        act.wait_ge(stored[t % 5], 16 * (t // 5))
                    act.wait_ge(mm, t + 1)
                    nc.scalar.activation(at(t), ps[:, t % 4, 0:width], ACT.Copy).then_inc(evac, 1)


def scores(k, rows, width, heads, a_src, a_tgt, src_out, tgt_out):
    nc = k.nc
    with stage(k) as s:
        a_sb = s.sb("a", [P, 2, width])
        prod = s.sb("prod", [P, 2, 2, width])
        s_src, att = s.sb("s_src", [P, NT, heads]), s.sb("att", [P, NT, 2 * heads])
        top, top_all = s.sb("top", [P, heads]), s.sb("top_all", [P, heads])
        e1 = s.sb("e1", [P, NT, heads])
        a_in, chain, topped, reduced, ready, out = (s.sem(n) for n in ("a_in", "chain", "topped", "reduced", "ready", "out"))
        with s.block() as block:
            @block.sync
            def _(sp):
                sp.dma_start(a_sb[:, 0, :], a_src.partition_broadcast(P)).then_inc(a_in, 16)
                sp.dma_start(a_sb[:, 1, :], a_tgt.partition_broadcast(P)).then_inc(a_in, 16)
                sp.wait_ge(ready, 1)
                with nc.allow_non_contiguous_dma(reason="a few numbers a node"):
                    sp.dma_start(src_out, s_src[:]).then_inc(out, 16)
                    sp.dma_start(tgt_out, att[:]).then_inc(out, 16)
                sp.wait_ge(out, 32)

            @block.gpsimd
            def _(pool):
                pool.wait_ge(topped, 1)
                nc.gpsimd.partition_all_reduce(top_all[:], top[:], P, RMAX).then_inc(reduced, 1)

            @block.vector
            def _(dve):
                c = Chain(dve, chain)
                dve.wait_ge(a_in, 32)
                for t in range(NT):
                    r = rows[:, t, :].unsqueeze(1).to_broadcast([P, 2, width])
                    c.link(nc.vector.tensor_tensor(prod[:, t % 2, :, :], r, a_sb[:], ALU.mult))
                    c.step(nc.vector.tensor_reduce(s_src[:, t, :], prod[:, t % 2, 0, :].rearrange("p (h d) -> p h d", h=heads), AX_X, ALU.add))
                    c.step(nc.vector.tensor_reduce(att[:, t, 0:heads], prod[:, t % 2, 1, :].rearrange("p (h d) -> p h d", h=heads), AX_X, ALU.add))
                c.wait()
                nc.vector.tensor_reduce(top[:], s_src[:].rearrange("p t h -> p h t"), AX_X, ALU.max).then_inc(topped, 1)
                dve.wait_ge(reduced, 1)
                c.link(nc.vector.tensor_tensor(e1[:], att[:, :, 0:heads], top_all[:].unsqueeze(1).to_broadcast([P, NT, heads]), ALU.add))
                nc.vector.scalar_tensor_tensor(att[:, :, heads:2 * heads], e1[:], 0.2, e1[:], ALU.mult, ALU.max).then_inc(ready, 1)


def divide(k, agg, out, heads, eps, add=None, bias=None, width=D):
    nc = k.nc
    HD = width // heads
    with stage(k) as s:
        den, none = s.sb("den", [P, NT, heads]), s.sb("none", [P, NT, heads])
        b_sb = s.sb("bias", [P, width])
        low = s.sb("low", [P, NT, width]) if add is not None else None
        b_in, chain, lows, exps = (s.sem(n) for n in ("b_in", "chain", "lows", "exps"))
        with s.block() as block:
            @block.sync
            def _(sp):
                if bias is not None:
                    sp.dma_start(b_sb[:], bias.partition_broadcast(P)).then_inc(b_in, 16)

            @block.vector
            def _(dve):
                c = Chain(dve, chain)
                d = agg[:, :, width:width + heads]
                if eps:
                    c.link(nc.vector.tensor_scalar(den[:], d, eps, None, ALU.add))
                else:
                    c.link(nc.vector.tensor_scalar(none[:], d, 0.0, None, ALU.is_equal))
                    c.link(nc.vector.tensor_tensor(den[:], d, none[:], ALU.add))
                c.link(nc.vector.reciprocal(none[:], den[:]))
                for t in range(NT):
                    c.step(nc.vector.tensor_tensor(out[:, t, :].rearrange("p (h d) -> p h d", h=heads), agg[:, t, 0:width].rearrange("p (h d) -> p h d", h=heads),
                                                   none[:, t, :].unsqueeze(2).to_broadcast([P, heads, HD]), ALU.mult))
                c.wait()
                if add is not None:
                    c.link(nc.vector.tensor_tensor(out[:], out[:], add[:], ALU.add))
                if bias is not None:
                    dve.wait_ge(b_in, 16)
                    c.link(nc.vector.tensor_tensor(out[:], out[:], b_sb[:].unsqueeze(1).to_broadcast([P, NT, width]), ALU.add))
                if add is not None:
                    nc.vector.tensor_scalar(low[:], out[:], 0.0, None, ALU.min).then_inc(lows, 1)
                    c.link(nc.vector.tensor_scalar(out[:], out[:], 0.0, -1.0, ALU.max, ALU.add))
                    dve.wait_ge(exps, 1)
                    c.link(nc.vector.tensor_tensor(out[:], out[:], low[:], ALU.add))

            @block.scalar
            def _(act):
                if add is not None:
                    act.wait_ge(lows, 1)
                    nc.scalar.activation(low[:], low[:], ACT.Exp).then_inc(exps, 1)


def sort_nodes(k, rank_i, noise):
    nc = k.nc
    U = 8
    BF = mybir.dt.bfloat16
    with stage(k) as s:
        tile_of, lo = s.sb("tile_of", [P, ET]), s.sb("lo", [P, ET])
        srcf = s.sb("srcf", [P, ET])
        r125, r25 = s.sb("r125", [P, P]), s.sb("r25", [P, NT])
        oh_lo, oh_hi = s.sb("oh_lo", [P, U, P], BF), s.sb("oh_hi", [P, U, NT], BF)
        zero = s.sb("zero", [P, P], BF)
        before = s.sb("before", [P, P])
        noise_sb, key = s.sb("noise", [P, NT]), s.sb("key", [P, NT])
        keys = s.sb("keys", [P, N])
        junk = s.sb("junk", [P, N])
        parts = s.sb("parts", [P, 3, NT])
        rank = s.sb("rank", [P, NT])
        ps = s.ps("ps", [P, 512])
        in_, made, chain, hot, mm, keyed, out, back = (s.sem(n) for n in ("in", "made", "chain", "hot", "mm", "keyed", "out", "back"))
        with s.block() as block:
            @block.sync
            def _(sp):
                with nc.allow_non_contiguous_dma(reason="one number a node"):
                    sp.dma_start(noise_sb[:], noise.rearrange("(t p) -> p t", p=P)).then_inc(in_, 16)
                    sp.wait_ge(keyed, 1)
                    sp.dma_start(k.keys_d.rearrange("(t p) -> p t", p=P), key[:]).then_inc(out, 16)
                sp.wait_ge(out, 16)
                sp.dma_start(keys[:], k.keys_d.partition_broadcast(P)).then_inc(back, 16)

            @block.gpsimd
            def _(pool):
                nc.gpsimd.iota(r125[:], [[1, P]], base=0, channel_multiplier=0, allow_small_or_imprecise_dtypes=True).then_inc(made, 1)
                nc.gpsimd.iota(r25[:], [[1, NT]], base=0, channel_multiplier=0, allow_small_or_imprecise_dtypes=True).then_inc(made, 1)
                nc.gpsimd.memset(zero[:], 0.0).then_inc(made, 1)
                nc.gpsimd.memset(before[:], 1.0).then_inc(made, 1)
                pool.wait_ge(made, 4)
                nc.gpsimd.affine_select(out=before[:], in_=before[:], compare_op=ALU.is_gt, fill=0.0, base=0,
                                        pattern=[[-1, P]], channel_multiplier=1).then_inc(made, 1)

            @block.tensor
            def _(pe):
                pe.sem_inc(mm, U)
                pe.wait_ge(made, 5)
                nc.tensor.matmul(ps[:, 0:NT], zero[:], zero[:, 0:NT], start=True, stop=False)
                with pe.Fori(0, ET // U) as i:
                    for j in range(U):
                        pe.wait_ge(hot, i * U + j + 1)
                        nc.tensor.matmul(ps[:, 0:NT], oh_lo[:, j, :], oh_hi[:, j, :], start=False, stop=False).then_inc(mm, 1)
                nc.tensor.matmul(ps[:, 0:NT], zero[:], zero[:, 0:NT], start=False, stop=True).then_inc(mm, 1)

            @block.vector
            def _(dve):
                c = Chain(dve, chain)
                c.step(nc.vector.tensor_copy(srcf[:], k.src_i[:, 0:ET]))
                c.link(nc.vector.memset(tile_of[:], 0.0))
                for t in range(1, NT):
                    c.link(nc.vector.scalar_tensor_tensor(tile_of[:], srcf[:], float(P * t), tile_of[:], ALU.is_ge, ALU.add))
                c.link(nc.vector.tensor_scalar(lo[:], tile_of[:], float(-P), None, ALU.mult))
                c.link(nc.vector.tensor_tensor(lo[:], lo[:], srcf[:], ALU.add))
                dve.wait_ge(made, 5)
                with dve.Fori(0, ET // U) as i:
                    for j in range(U):
                        t = i * U + j
                        dve.wait_ge(mm, t + 1)
                        nc.vector.tensor_scalar(oh_lo[:, j, :], r125[:], lo[:, ds(t, 1)], None, ALU.is_equal)
                        nc.vector.tensor_scalar(oh_hi[:, j, :], r25[:], tile_of[:, ds(t, 1)], None, ALU.is_equal).then_inc(hot, 1)
                dve.wait_ge(mm, U + ET + 1)
                dve.wait_ge(in_, 16)
                c.link(nc.vector.tensor_tensor(key[:], ps[:, 0:NT], noise_sb[:], ALU.add))
                dve.sem_inc(keyed, 1)
                dve.wait_ge(back, 16)
                c.link(nc.vector.memset(parts[:], 0.0))
                for t in range(NT):
                    me = key[:, t:t + 1]
                    if t:
                        c.link(nc.vector.tensor_scalar(junk[:, 0:t * P], keys[:, 0:t * P], me, None, ALU.is_le, ALU.add, accum_out=parts[:, 0, t:t + 1]))
                    c.link(nc.vector.tensor_scalar(junk[:, t * P:N], keys[:, t * P:N], me, None, ALU.is_lt, ALU.add, accum_out=parts[:, 1, t:t + 1]))
                    c.link(nc.vector.scalar_tensor_tensor(junk[:, 0:P], keys[:, t * P:(t + 1) * P], me, before[:], ALU.is_equal, ALU.mult,
                                                          accum_out=parts[:, 2, t:t + 1]))
                c.link(nc.vector.tensor_tensor(rank[:], parts[:, 0, :], parts[:, 1, :], ALU.add))
                c.link(nc.vector.tensor_tensor(rank[:], rank[:], parts[:, 2, :], ALU.add))
                c.link(nc.vector.tensor_copy(rank_i[:], rank[:]))


def permute(k, rows, dram, rank_i, scatter):
    nc = k.nc
    with stage(k) as s:
        moved = s.sem("moved")
        with s.block() as block:
            @block.gpsimd
            def _(pool):
                for t in range(NT):
                    at = bass.IndirectOffsetOnAxis(rank_i[:, t:t + 1], 0)
                    if scatter:
                        nc.gpsimd.indirect_dma_start(dram, at, rows[:, t, :], None).then_inc(moved, 16)
                    else:
                        nc.gpsimd.indirect_dma_start(rows[:, t, :], None, dram, at).then_inc(moved, 16)
                pool.wait_ge(moved, 16 * NT)


def mamba_inputs(k, cols, xc, z, dbc, w_in, conv_w, conv_b, x_proj):
    nc = k.nc
    KW = 4
    BLK = [(n0, min(500, N - n0)) for n0 in range(0, N, 500)]
    NBK = len(BLK)
    with stage(k) as s:
        w = s.sb("w", [128, 2, 2 * D])
        cw, cb = s.sb("cw", [128, 2, KW]), s.sb("cb", [128, 2])
        xp = s.sb("xp", [128, 2, N + KW - 1])
        wx = s.sb("wx", [128, 2, 48])
        ps = s.ps("ps", [128, 4, 512])
        ps_d = s.ps("ps_d", [48, 2, 512])
        loaded, mm, evac, chain, convd, acted, dmm, dev = (s.sem(n) for n in ("loaded", "mm", "evac", "chain", "convd", "acted", "dmm", "dev"))
        with s.block() as block:
            @block.sync
            def _(sp):
                sp.dma_start(w[:], w_in.rearrange("(c p) f -> p c f", p=128)).then_inc(loaded, 16)
                sp.dma_start(cw[:], conv_w.rearrange("(c p) f -> p c f", p=128)).then_inc(loaded, 16)
                with nc.allow_non_contiguous_dma(reason="one number a channel"):
                    sp.dma_start(cb[:], conv_b.rearrange("(c p) -> p c", p=128)).then_inc(loaded, 16)
                sp.dma_start(wx[:], x_proj.rearrange("(c p) f -> p c f", p=128)).then_inc(loaded, 16)

            @block.tensor
            def _(pe):
                pe.wait_ge(loaded, 64)
                n = 0
                for o in range(4):
                    for n0, m in BLK:
                        if n >= 4:
                            pe.wait_ge(evac, n - 3)
                        for c in range(2):
                            ins = nc.tensor.matmul(ps[:, n % 4, 0:m], w[:, c, o * 128:(o + 1) * 128], cols[:, c, n0:n0 + m], start=c == 0, stop=c == 1)
                        ins.then_inc(mm, 1)
                        n += 1
                pe.wait_ge(acted, 2)
                for q, (n0, m) in enumerate(BLK):
                    if q >= 2:
                        pe.wait_ge(dev, q - 1)
                    for c in range(2):
                        ins = nc.tensor.matmul(ps_d[:, q % 2, 0:m], wx[:, c, :], xc[:, c, n0:n0 + m], start=c == 0, stop=c == 1)
                    ins.then_inc(dmm, 1)

            @block.scalar
            def _(act):
                n = 0
                for o in range(4):
                    for n0, m in BLK:
                        act.wait_ge(mm, n + 1)
                        if o < 2:
                            ins = nc.scalar.activation(xp[:, o, KW - 1 + n0:KW - 1 + n0 + m], ps[:, n % 4, 0:m], ACT.Copy)
                        else:
                            ins = nc.scalar.activation(z[:, o - 2, n0:n0 + m], ps[:, n % 4, 0:m], ACT.Silu)
                        ins.then_inc(evac, 1)
                        n += 1
                for c in range(2):
                    act.wait_ge(convd, c + 1)
                    nc.scalar.activation(xc[:, c, :], xc[:, c, :], ACT.Silu, bias=cb[:, c:c + 1]).then_inc(acted, 1)
                for q, (n0, m) in enumerate(BLK):
                    act.wait_ge(dmm, q + 1)
                    nc.scalar.activation(dbc[:, n0:n0 + m], ps_d[:, q % 2, 0:m], ACT.Copy).then_inc(dev, 1)

            @block.vector
            def _(dve):
                c = Chain(dve, chain)
                c.link(nc.vector.memset(xp[:, :, 0:KW - 1], 0.0))
                dve.wait_ge(loaded, 64)
                for h in range(2):
                    dve.wait_ge(evac, (h + 1) * NBK)
                    c.link(nc.vector.tensor_scalar(xc[:, h, :], xp[:, h, 0:N], cw[:, h, 0:1], None, ALU.mult))
                    for q in range(1, KW):
                        ins = nc.vector.scalar_tensor_tensor(xc[:, h, :], xp[:, h, q:q + N], cw[:, h, q:q + 1], xc[:, h, :], ALU.mult, ALU.add)
                        if q < KW - 1:
                            c.link(ins)
                    ins.then_inc(convd, 1)


def selective_scan(k, h, xc, z, dbc, dt_w, dt_b, a_log, d_param):
    nc = k.nc
    SN, R, CH, NC = 16, 16, 625, 5
    BLK = [(n0, min(500, N - n0)) for n0 in range(0, N, 500)]
    CUT = [(0, 512), (512, CH - 512)]
    with stage(k) as s:
        dt, u, y, poly = (s.sb(n, [128, N]) for n in ("dt", "u", "y", "poly"))
        w48, dtb, dp = s.sb("w48", [48, D]), s.sb("dtb", [128, 1]), s.sb("dp", [128, 1])
        al, A = s.sb("al", [128, SN]), s.sb("A", [128, SN + 1])
        a_s = s.sb("a_s", [128, 2])
        sel = s.sb("sel", [48, 2, 2, 128])
        dA, dB, hh, hc = (s.sb(n, [128, 2, CH]) for n in ("dA", "dB", "hh", "hc"))
        ps = s.ps("ps", [128, 2, 2, 1024])
        loaded, made, mm, dts, chain, exps, prods, adds, sels, bcs = (
            s.sem(n) for n in ("loaded", "made", "mm", "dts", "chain", "exps", "prods", "adds", "sels", "bcs"))
        dt_done = s.sem("dt_done")
        with s.block() as block:
            @block.sync
            def _(sp):
                sp.wait_ge(made, 1)
                sp.dma_start(w48[0:R, :], dt_w).then_inc(loaded, 16)
                hs = slice(h * 128, (h + 1) * 128)
                sp.dma_start(dtb[:], dt_b[hs].rearrange("(p a) -> p a", a=1)).then_inc(loaded, 16)
                sp.dma_start(dp[:], d_param[hs].rearrange("(p a) -> p a", a=1)).then_inc(loaded, 16)
                sp.dma_start(al[:], a_log[hs, :]).then_inc(loaded, 16)

            @block.gpsimd
            def _(pool):
                nc.gpsimd.memset(w48[:], 0.0).then_inc(made, 1)
                pool.sem_inc(adds, 2)
                with pool.Fori(0, SN // 2) as i:
                    for q in range(2 * NC):
                        n, b, c = i * (2 * NC) + q, q % 2, q % NC
                        pool.wait_ge(prods, n + 3)
                        ycut = y[:, c * CH:(c + 1) * CH]
                        nc.gpsimd.tensor_tensor(ycut, ycut, hc[:, b, :], ALU.add).then_inc(adds, 1)

            @block.tensor
            def _(pe):
                pe.wait_ge(loaded, 64)
                for q, (n0, m) in enumerate(BLK):
                    if q >= 4:
                        pe.wait_ge(dts, q - 3)
                    nc.tensor.matmul(ps[:, q % 4 // 2, q % 2, 0:m], w48[:, h * 128:(h + 1) * 128], dbc[:, n0:n0 + m], start=True, stop=True).then_inc(mm, 1)
                pe.wait_ge(dts, len(BLK))
                with pe.Fori(0, SN // 2) as i:
                    for q in range(2 * NC):
                        n, b, c = i * (2 * NC) + q, q % 2, q % NC
                        pe.wait_ge(sels, i * 2 + q // NC + 1)
                        pe.wait_ge(prods, n + 1)
                        for v in range(2):
                            for lo, m in CUT:
                                ins = nc.tensor.matmul(ps[:, b, v, lo:lo + m], sel[:, q // NC, v, :], dbc[:, c * CH + lo:c * CH + lo + m], start=True, stop=True)
                        ins.then_inc(bcs, 1)

            @block.scalar
            def _(act):
                act.wait_ge(loaded, 64)
                nc.scalar.activation(A[:, 0:SN], al[:], ACT.Exp).then_inc(exps, 1)
                for q, (n0, m) in enumerate(BLK):
                    act.wait_ge(mm, q + 1)
                    nc.scalar.activation(dt[:, n0:n0 + m], ps[:, q % 4 // 2, q % 2, 0:m], ACT.Identity, bias=dtb[:]).then_inc(dts, 1)
                act.wait_ge(dts, len(BLK))
                nc.scalar.activation(u[:], dt[:], ACT.Abs).then_inc(dts, 1)
                act.wait_ge(dts, len(BLK) + 1)
                nc.scalar.activation(u[:], u[:], ACT.Exp, scale=-1.0).then_inc(dts, 1)
                act.wait_ge(dt_done, 1)
                with act.Fori(0, SN // 2) as i:
                    for q in range(2 * NC):
                        n, b, c = i * (2 * NC) + q, q % 2, q % NC
                        act.wait_ge(sels, i * 2 + q // NC + 1)
                        act.wait_ge(prods, n + 1)
                        nc.scalar.activation(dA[:, b, :], dt[:, c * CH:(c + 1) * CH], ACT.Exp, scale=a_s[:, q // NC:q // NC + 1]).then_inc(exps, 1)

            @block.vector
            def _(dve):
                c_ = Chain(dve, chain)
                dve.wait_ge(exps, 1)
                c_.step(nc.vector.memset(A[:, SN:SN + 1], 0.0))
                c_.link(nc.vector.tensor_scalar(A[:, 0:SN], A[:, 0:SN], -1.0, None, ALU.mult))
                dve.wait_ge(dts, len(BLK) + 2)
                c_.link(nc.vector.tensor_scalar(y[:], u[:], 2.0, None, ALU.add))
                c_.link(nc.vector.reciprocal(y[:], y[:]))
                c_.link(nc.vector.tensor_tensor(y[:], y[:], u[:], ALU.mult))
                c_.link(nc.vector.tensor_tensor(u[:], y[:], y[:], ALU.mult))
                c_.link(nc.vector.tensor_scalar(poly[:], u[:], 1.0 / 15, None, ALU.mult))
                for odd in (13, 11, 9, 7, 5, 3):
                    c_.link(nc.vector.scalar_tensor_tensor(poly[:], poly[:], 1.0 / odd, u[:], ALU.add, ALU.mult))
                c_.link(nc.vector.scalar_tensor_tensor(poly[:], poly[:], 1.0, y[:], ALU.add, ALU.mult))
                c_.link(nc.vector.tensor_scalar(dt[:], dt[:], 0.0, None, ALU.max))
                c_.link(nc.vector.scalar_tensor_tensor(dt[:], poly[:], 2.0, dt[:], ALU.mult, ALU.add))
                c_.link(nc.vector.memset(y[:], 0.0))
                dve.sem_inc(dt_done, 1)
                c_.link(nc.vector.tensor_tensor(u[:], dt[:], xc[:, h, :], ALU.mult))
                dve.sem_inc(prods, 2)

                def state(st, v):
                    nc.vector.tensor_copy(a_s[:, v:v + 1], A[:, ds(st, 1)])
                    nc.vector.tensor_copy(sel[:, v, 0, :], k.ident[0:48, ds(R + st, 1)].to_broadcast([48, 128]))
                    nc.vector.tensor_copy(sel[:, v, 1, :], k.ident[0:48, ds(R + SN + st, 1)].to_broadcast([48, 128])).then_inc(sels, 1)

                state(0, 0)
                base = c_.n
                with dve.Fori(0, SN // 2) as i:
                    for q in range(2 * NC):
                        n, b, c = i * (2 * NC) + q, q % 2, q % NC
                        if c == 2:
                            state(i * 2 + q // NC + 1, 1 - q // NC)
                        dve.wait_ge(bcs, n + 1)
                        nc.vector.tensor_tensor(dB[:, b, :], ps[:, b, 0, 0:CH], u[:, c * CH:(c + 1) * CH], ALU.mult).then_inc(chain, 1)
                        dve.wait_ge(chain, base + 2 * n + 1)
                        dve.wait_ge(exps, n + 2)
                        nc.vector.tensor_tensor_scan(hh[:, b, :], dA[:, b, :], dB[:, b, :], 0.0 if c == 0 else hh[:, 1 - b, CH - 1:CH],
                                                     ALU.mult, ALU.add).then_inc(chain, 1)
                        dve.wait_ge(chain, base + 2 * n + 2)
                        dve.wait_ge(adds, n + 1)
                        nc.vector.tensor_tensor(hc[:, b, :], ps[:, b, 1, 0:CH], hh[:, b, :], ALU.mult).then_inc(prods, 1)
                        dve.wait_ge(prods, n + 3)
                c_.n = base + 2 * SN * NC
                dve.wait_ge(adds, SN * NC + 2)
                c_.link(nc.vector.scalar_tensor_tensor(y[:], xc[:, h, :], dp[:], y[:], ALU.mult, ALU.add))
                c_.link(nc.vector.tensor_tensor(z[:, h, :], y[:], z[:, h, :], ALU.mult))


def mix(k, a_rows, b_rows, a_cols, b_cols, wa, wb):
    nc = k.nc
    with stage(k) as s:
        w = s.sb("w", [128, 4, D])
        g = s.sb("g", [P, 2, D])
        ps = s.ps("ps", [P, 2, 512])
        w_in, mm, gated, chain = (s.sem(n) for n in ("w_in", "mm", "gated", "chain"))
        with s.block() as block:
            @block.sync
            def _(sp):
                sp.dma_start(w[:, 0:2, :], wa.rearrange("(c p) f -> p c f", p=128)).then_inc(w_in, 16)
                sp.dma_start(w[:, 2:4, :], wb.rearrange("(c p) f -> p c f", p=128)).then_inc(w_in, 16)

            @block.tensor
            def _(pe):
                pe.wait_ge(w_in, 32)
                for t in range(NT):
                    if t >= 2:
                        pe.wait_ge(gated, t - 1)
                    for c in range(4):
                        src = (a_cols, b_cols)[c // 2]
                        ins = nc.tensor.matmul(ps[:, t % 2, 0:D], src[:, c % 2, t * P:(t + 1) * P], w[:, c, :], start=c == 0, stop=c == 3)
                    ins.then_inc(mm, 1)

            @block.scalar
            def _(act):
                for t in range(NT):
                    if t >= 2:
                        act.wait_ge(chain, 3 * (t - 1))
                    act.wait_ge(mm, t + 1)
                    nc.scalar.activation(g[:, t % 2, :], ps[:, t % 2, 0:D], ACT.Sigmoid).then_inc(gated, 1)

            @block.vector
            def _(dve):
                c = Chain(dve, chain)
                for t in range(NT):
                    c.link(nc.vector.tensor_tensor(a_rows[:, t, :], a_rows[:, t, :], b_rows[:, t, :], ALU.subtract))
                    dve.wait_ge(gated, t + 1)
                    c.link(nc.vector.tensor_tensor(a_rows[:, t, :], a_rows[:, t, :], g[:, t % 2, :], ALU.mult))
                    c.link(nc.vector.tensor_tensor(a_rows[:, t, :], a_rows[:, t, :], b_rows[:, t, :], ALU.add))


def small_edge_sums(k, table, att_rows, s_rows, agg, src_c, dst_c):
    nc = k.nc
    H, F = 4, 16
    W = F + H
    Q, GT = 128, 256
    with stage(k) as s:
        idx, dsti = s.sb("idx", [Q, GT + G], I32), s.sb("dsti", [Q, GT + G], I32)
        dstf, tile_of, lo = s.sb("dstf", [Q, GT]), s.sb("tile_of", [Q, GT]), s.sb("lo", [Q, GT])
        r125, r25 = s.sb("r125", [Q, P]), s.sb("r25", [Q, NT])
        gi, di = s.sb("gi", [Q, 2, G], I32), s.sb("di", [Q, 2, G], I32)
        msg, arow = s.sb("msg", [Q, 2, G, W]), s.sb("arow", [Q, 2, G, 2 * H])
        e1, e2 = s.sb("e1", [Q, 2, G, H]), s.sb("e2", [Q, 2, G, H])
        oh_lo, oh_hi = s.sb("oh_lo", [Q, 2, G, P]), s.sb("oh_hi", [Q, 2, G, NT])
        spread = s.sb("spread", [Q, 2, G, NT * W])
        zero = s.sb("zero", [Q, NT * W])
        own, att = s.sb("own", [P, NT, W]), s.sb("att", [P, NT, 2 * H])
        v1, v2 = s.sb("v1", [P, NT, H]), s.sb("v2", [P, NT, H])
        ps = s.ps("ps", [P, 512])
        loaded, made, chain, idx_done, mm, e_done, a_done, ready = (s.sem(n) for n in ("loaded", "made", "chain", "idx", "mm", "e_done", "a_done", "ready"))
        turns, own_e, own_a, scaled = s.sem("turns"), s.sem("own_e"), s.sem("own_a"), s.sem("scaled")
        msg_in = [s.sem("msg_in0"), s.sem("msg_in1")]
        LG = GT // G
        with s.block() as block:
            @block.sync
            def _(sp):
                sp.dma_start(idx[:, 0:GT], src_c).then_inc(loaded, 16)
                sp.dma_start(dsti[:, 0:GT], dst_c).then_inc(loaded, 16)
                sp.dma_start(own[:], s_rows.rearrange("(t p) f -> p t f", p=P)).then_inc(loaded, 16)
                sp.dma_start(att[:], att_rows.rearrange("(t p) f -> p t f", p=P)).then_inc(loaded, 16)

            @block.gpsimd
            def _(pool):
                nc.gpsimd.iota(r125[:], [[1, P]], base=0, channel_multiplier=0, allow_small_or_imprecise_dtypes=True).then_inc(made, 1)
                nc.gpsimd.iota(r25[:], [[1, NT]], base=0, channel_multiplier=0, allow_small_or_imprecise_dtypes=True).then_inc(made, 1)
                nc.gpsimd.memset(zero[:], 0.0).then_inc(made, 1)

                def gather(b, g):
                    pool.wait_ge(idx_done, g + 1)
                    pool.wait_ge(mm, upto(g, G - 1, back=2))
                    pool.sem_inc(turns, 1)
                    for j in range(G):
                        nc.gpsimd.indirect_dma_start(msg[:, b, j, :], None, table, bass.IndirectOffsetOnAxis(gi[:, b, j:j + 1], 0)).then_inc(msg_in[b], 16)
                        nc.gpsimd.indirect_dma_start(arow[:, b, j, :], None, att_rows, bass.IndirectOffsetOnAxis(di[:, b, j:j + 1], 0)).then_inc(msg_in[b], 16)

                with pool.Fori(0, LG // 2) as i:
                    gather(0, i * 2)
                    gather(1, i * 2 + 1)

            @block.tensor
            def _(pe):
                pe.sem_inc(mm, 2 * G)
                pe.wait_ge(made, 3)
                nc.tensor.matmul(ps[:, 0:NT * W], zero[:, 0:P], zero[:], start=True, stop=False)
                with pe.Fori(0, LG // 2) as i:
                    for b in range(2):
                        g = i * 2 + b
                        for j in range(G):
                            pe.wait_ge(ready, g * G + j + 1)
                            nc.tensor.matmul(ps[:, 0:NT * W], oh_lo[:, b, j, :], spread[:, b, j, :], start=False, stop=False).then_inc(mm, 1)
                nc.tensor.matmul(ps[:, 0:NT * W], zero[:, 0:P], zero[:], start=False, stop=True).then_inc(mm, 1)

            @block.scalar
            def _(act):
                with act.Fori(0, LG // 2) as i:
                    for b in range(2):
                        g = i * 2 + b
                        act.wait_ge(e_done, 3 * g + 3)
                        nc.scalar.activation(msg[:, b, :, F:W], e1[:, b, :, :], ACT.Exp).then_inc(a_done, 1)
                act.wait_ge(own_e, 1)
                nc.scalar.activation(own[:, :, F:W], v1[:], ACT.Exp).then_inc(own_a, 1)

            @block.vector
            def _(dve):
                c = Chain(dve, chain)
                c.step(nc.vector.memset(idx[:, GT:GT + G], 0))
                c.step(nc.vector.memset(dsti[:, GT:GT + G], 0))
                dve.wait_ge(loaded, 64)
                c.step(nc.vector.memset(tile_of[:], 0.0))
                c.link(nc.vector.tensor_copy(dstf[:], dsti[:, 0:GT]))
                for t in range(1, NT):
                    c.link(nc.vector.scalar_tensor_tensor(tile_of[:], dstf[:], float(P * t), tile_of[:], ALU.is_ge, ALU.add))
                c.link(nc.vector.tensor_scalar(lo[:], tile_of[:], float(-P), None, ALU.mult))
                c.link(nc.vector.tensor_tensor(lo[:], lo[:], dstf[:], ALU.add))
                dve.wait_ge(made, 3)
                base = c.n

                def indices(b, g):
                    dve.wait_ge(mm, upto(g, G - 1, back=2))
                    nc.vector.tensor_copy(di[:, b, :], dsti[:, ds(g * G, G)]).then_inc(chain, 1)
                    dve.wait_ge(chain, base + g + 1)
                    nc.vector.tensor_copy(gi[:, b, :], idx[:, ds(g * G, G)]).then_inc(idx_done, 1)

                indices(0, 0)
                with dve.Fori(0, LG // 2) as i:
                    for b in range(2):
                        g = i * 2 + b
                        indices(1 - b, g + 1)
                        dve.wait_ge(msg_in[b], 16 * 2 * G * (i + 1))
                        nc.vector.tensor_tensor(e1[:, b, :, :], msg[:, b, :, F:W], arow[:, b, :, 0:H], ALU.add).then_inc(e_done, 1)
                        dve.wait_ge(e_done, 3 * g + 1)
                        nc.vector.scalar_tensor_tensor(e2[:, b, :, :], e1[:, b, :, :], 0.2, e1[:, b, :, :], ALU.mult, ALU.max).then_inc(e_done, 1)
                        dve.wait_ge(e_done, 3 * g + 2)
                        nc.vector.tensor_tensor(e1[:, b, :, :], e2[:, b, :, :], arow[:, b, :, H:2 * H], ALU.subtract).then_inc(e_done, 1)
                        for j in range(G):
                            t = g * G + j
                            nc.vector.tensor_scalar(oh_lo[:, b, j, :], r125[:], lo[:, ds(t, 1)], None, ALU.is_equal)
                            nc.vector.tensor_scalar(oh_hi[:, b, j, :], r25[:], tile_of[:, ds(t, 1)], None, ALU.is_equal)
                        dve.wait_ge(a_done, g + 1)
                        m = msg[:, b, :, 0:F].rearrange("p g (h d) -> p g h d", h=H)
                        nc.vector.tensor_tensor(m, m, msg[:, b, :, F:W].unsqueeze(3).to_broadcast([Q, G, H, F // H]), ALU.mult).then_inc(scaled, 1)
                        dve.wait_ge(scaled, g + 1)
                        for j in range(G):
                            nc.vector.tensor_tensor(spread[:, b, j, :].rearrange("p (t f) -> p t f", t=NT), oh_hi[:, b, j, :].unsqueeze(2).to_broadcast([Q, NT, W]),
                                                    msg[:, b, j, :].unsqueeze(1).to_broadcast([Q, NT, W]), ALU.mult).then_inc(ready, 1)
                c.n = base + LG + 1
                c.link(nc.vector.tensor_tensor(v1[:], own[:, :, F:W], att[:, :, 0:H], ALU.add))
                c.link(nc.vector.scalar_tensor_tensor(v2[:], v1[:], 0.2, v1[:], ALU.mult, ALU.max))
                nc.vector.tensor_tensor(v1[:], v2[:], att[:, :, H:2 * H], ALU.subtract).then_inc(own_e, 1)
                dve.wait_ge(own_a, 1)
                for h in range(H):
                    c.step(nc.vector.tensor_tensor(own[:, :, 4 * h:4 * h + 4], own[:, :, 4 * h:4 * h + 4], own[:, :, F + h:F + h + 1].to_broadcast([P, NT, 4]), ALU.mult))
                c.wait()
                dve.wait_ge(mm, 2 * G + GT + 1)
                c.link(nc.vector.tensor_tensor(agg[:], ps[:, 0:NT * W].rearrange("p (t f) -> p t f", t=NT), own[:], ALU.add))


def mean_heads(k, v, score):
    nc = k.nc
    with stage(k) as s:
        total = s.sb("total", [P, NT, 4])
        chain = s.sem("chain")
        with s.block() as block:
            @block.vector
            def _(dve):
                c = Chain(dve, chain)
                c.link(nc.vector.tensor_reduce(total[:], v.rearrange("p t (h e) -> p t e h", e=4), AX_X, ALU.add))
                c.link(nc.vector.tensor_scalar(score[:], total[:], 0.25, None, ALU.mult))


def cutoff(k, cut):
    nc = k.nc
    with stage(k) as s:
        turns_i, q = s.sb("turns", [P, ET], I32), s.sb("q", [P, ET])
        chain, red, sines = s.sem("chain"), s.sem("red"), s.sem("sines")
        with s.block() as block:
            @block.vector
            def _(dve):
                c = Chain(dve, chain)
                c.link(nc.vector.tensor_scalar(turns_i[:], k.edge_w[:], 1.0 / 20, None, ALU.mult))
                c.link(nc.vector.tensor_scalar(q[:], turns_i[:], -20.0, None, ALU.mult))
                nc.vector.tensor_tensor(q[:], q[:], k.edge_w[:], ALU.add).then_inc(red, 1)
                dve.wait_ge(sines, 1)
                c.link(nc.vector.tensor_tensor(q[:], cut[:], cut[:], ALU.mult))
                c.link(nc.vector.tensor_scalar(cut[:], q[:], -1.0, 1.0, ALU.mult, ALU.add))

            @block.scalar
            def _(act):
                act.wait_ge(red, 1)
                nc.scalar.activation(cut[:], q[:], ACT.Sin, scale=math.pi / 20).then_inc(sines, 1)


def add_bias(k, rows, bias, softplus=False, to_x=False):
    nc = k.nc
    with stage(k) as s:
        b_sb = s.sb("bias", [P, D])
        soft = s.sb("soft", [P, NT, D]) if softplus else None
        b_in, chain, biased, done = (s.sem(n) for n in ("b_in", "chain", "biased", "done"))
        with s.block() as block:
            @block.sync
            def _(sp):
                sp.dma_start(b_sb[:], bias.partition_broadcast(P)).then_inc(b_in, 16)

            @block.vector
            def _(dve):
                c = Chain(dve, chain)
                dve.wait_ge(b_in, 16)
                nc.vector.tensor_tensor(rows[:], rows[:], b_sb[:].unsqueeze(1).to_broadcast([P, NT, D]), ALU.add).then_inc(biased, 1)
                dve.wait_ge(biased, 1)
                if to_x:
                    c.link(nc.vector.tensor_tensor(k.x[:], k.x[:], rows[:], ALU.add))
                if softplus:
                    dve.wait_ge(done, 3)
                    c.link(nc.vector.tensor_scalar(rows[:], rows[:], 0.0, -math.log(2.0), ALU.max, ALU.add))
                    c.link(nc.vector.tensor_tensor(rows[:], rows[:], soft[:], ALU.add))

            @block.scalar
            def _(act):
                if softplus:
                    act.wait_ge(biased, 1)
                    nc.scalar.activation(soft[:], rows[:], ACT.Abs).then_inc(done, 1)
                    act.wait_ge(done, 1)
                    nc.scalar.activation(soft[:], soft[:], ACT.Exp, scale=-1.0).then_inc(done, 1)
                    act.wait_ge(done, 2)
                    nc.scalar.activation(soft[:], soft[:], ACT.Ln, bias=1.0).then_inc(done, 1)


def ones_gate(k, gate):
    with stage(k) as s:
        done = s.sem("done")
        with s.block() as block:
            @block.vector
            def _(dve):
                k.nc.vector.memset(gate[:], 1.0).then_inc(done, 1)


def nan_to_num_to_x(k, v):
    nc = k.nc
    BIG = 3.4028234e38
    U8 = mybir.dt.uint8
    with stage(k) as s:
        mask = s.sb("mask", [P, NT, D], U8)
        const = s.sb("const", [P, 3])
        chain = s.sem("chain")
        with s.block() as block:
            @block.vector
            def _(dve):
                c = Chain(dve, chain)
                c.step(nc.vector.memset(const[:, 0:1], 0.0))
                c.step(nc.vector.memset(const[:, 1:2], 1.0e4))
                c.link(nc.vector.memset(const[:, 2:3], -1.0e4))
                for q, (other, op) in enumerate(((v[:], ALU.not_equal), (BIG, ALU.is_gt), (-BIG, ALU.is_lt))):
                    if q == 0:
                        c.link(nc.vector.tensor_tensor(mask[:], v[:], v[:], op))
                    else:
                        c.link(nc.vector.tensor_scalar(mask[:], v[:], other, None, op))
                    for t in range(NT):
                        c.step(nc.vector.copy_predicated(v[:, t, :], mask[:, t, :], const[:, q:q + 1].to_broadcast([P, D])))
                    c.wait()
                c.link(nc.vector.tensor_tensor(k.x[:], k.x[:], v[:], ALU.add))


def build(nc, a, out, layers=8):
    k = Core()
    k.nc, k.uid = nc, 0
    ctx = ExitStack()
    with ctx:
        keep = lambda name, shape, dt=F32: ctx.enter_context(nc.sbuf_tensor(name, shape, dt))
        sbt = lambda name, shape=(P, NT, D), dt=F32: nc.sbuf_tensor(name, list(shape), dt)
        k.x = keep("x", [P, NT, D])
        k.edge_w, k.dst_f = keep("edge_w", [P, ET]), keep("dst_f", [P, ET])
        k.src_i, k.src_rel_i, k.dst_i, k.row_i = (keep(n, [P, ET + G], I32) for n in ("src_i", "src_rel_i", "dst_i", "row_i"))
        k.ident, k.ones = keep("ident", [128, 128]), keep("ones", [128, 128])
        k.acc = {w: [nc.dram_tensor(f"acc{w}_{j}", [AT * P, w], F32, kind="Internal").ap() for j in range(G)] for w in (D, D + 4, D + 8)}
        k.rel_rows = nc.dram_tensor("rel_rows", [N, REL * D], F32, kind="Internal").ap()
        dram = lambda n, w: nc.dram_tensor(n, [N, w], F32, kind="Internal").ap()
        d = {n: dram("d_" + n, w) for n, w in (("xn", D), ("local", D), ("sorted", D), ("gat4", D + 4), ("gat8", D + 8), ("att4", 8), ("att8", 16), ("small", 20), ("lin1", D))}
        k.keys_d = nc.dram_tensor("keys_d", [N], F32, kind="Internal").ap()
        k.src_c, k.dst_c, k.type_c, k.weight_c = a["src_c"], a["dst_c"], a["type_c"], a["weight_c"]
        k.dst_r, k.w_rel = a["dst"], a["w_rel"]
        x_rows = a["x"].rearrange("(t p) f -> p t f", p=P)
        out_rows = out.rearrange("(t p) f -> p t f", p=P)

        with stage(k) as s:
            x_in, made = s.sem("x_in"), s.sem("made")
            with s.block() as block:
                @block.sync
                def _(sp):
                    sp.dma_start(k.x[:], x_rows).then_inc(x_in, 16)
                    sp.wait_ge(x_in, 16)

                @block.gpsimd
                def _(pool):
                    nc.gpsimd.memset(k.ones[:], 1.0).then_inc(made, 1)
                    nc.gpsimd.memset(k.ident[:], 0.0).then_inc(made, 1)
                    pool.wait_ge(made, 2)
                    nc.gpsimd.affine_select(out=k.ident[:], in_=k.ident[:], compare_op=ALU.not_equal, fill=1.0, base=0,
                                            pattern=[[-1, 128]], channel_multiplier=1).then_inc(made, 1)

        prepare_edges(k)

        if layers >= 1:
            with nc.sbuf_tensor("rows_a", [P, NT, D], F32) as rows, nc.sbuf_tensor("cols_a", [128, 2, N], F32) as cols:
                normalise_all(k, rows, cols)
                relation_tables(k, cols)
            table = k.rel_rows.rearrange("n (r f) -> (n r) f", r=REL)
            edge_sums(k, table, k.src_rel_i, D, weight=k.edge_w)
            with nc.sbuf_tensor("agg_a", [P, NT, D], F32) as agg:
                collect(k, agg, D)
                add_to_x(k, agg)

        if layers >= 2:
            with sbt("rows_b") as rows, sbt("gate_b", [P, NT, 16]) as gate, sbt("moe_b") as moe, sbt("cols_b", [128, 2, N]) as cols:
                normalise_all(k, rows, cols)
                gates(k, cols, gate, 16, a["L0_ffn_gate_w"], a["L0_ffn_gate_b"], "top2")
                experts(k, cols, gate, moe, Experts(16, 512, ACT.Relu, a["L0_ffn_w1"], a["L0_ffn_b1"], a["L0_ffn_w2"], a["L0_ffn_b2"]))
                finish_norm(k, rows, moe, a["L0_ffn_gamma"], a["L0_ffn_beta"])

        if layers >= 3:
            with sbt("rows_c") as rows:
                with sbt("cols_c", [128, 2, N]) as cols, sbt("proj_c") as proj:
                    normalise_all(k, rows, cols)
                    transfer(k, d["xn"].rearrange("(t p) f -> p t f", p=P), rows[:])
                    project(k, cols, a["gat_w"], D, rows=proj, table=d["gat4"])
                    scores(k, proj, D, 4, a["gat_a_src"], a["gat_a_tgt"], d["gat4"].rearrange("(t p) f -> p t f", p=P)[:, :, D:D + 4],
                           d["att4"].rearrange("(t p) f -> p t f", p=P))
            edge_sums(k, d["gat4"], k.src_i, D + 4, heads=4, att_rows=d["att4"])
            with sbt("agg_c", [P, NT, D + 4]) as agg, sbt("rows_d") as rows, sbt("local_d") as local:
                transfer(k, rows[:], d["xn"].rearrange("(t p) f -> p t f", p=P))
                collect(k, agg, D + 4)
                divide(k, agg, local, 4, 1e-16, add=rows, bias=a["L1_gnn_gat_b"])
                finish_norm(k, local, None, a["L1_gnn_ln_local_g"], a["L1_gnn_ln_local_b"], to_x=False)
                transfer(k, d["local"].rearrange("(t p) f -> p t f", p=P), local[:])
            with sbt("rank_i", [P, NT], I32) as rank_i:
                sort_nodes(k, rank_i, a["node_vec"])
                with sbt("xc", [128, 2, N]) as xc, sbt("z", [128, 2, N]) as z, sbt("dbc", [48, N]) as dbc:
                    with sbt("cols_e", [128, 2, N]) as cols:
                        with sbt("rows_e") as rows:
                            transfer(k, rows[:], d["xn"].rearrange("(t p) f -> p t f", p=P))
                            permute(k, rows, d["sorted"], rank_i, scatter=True)
                            transfer(k, rows[:], d["sorted"].rearrange("(t p) f -> p t f", p=P))
                            turn_all(k, rows, cols)
                        mamba_inputs(k, cols, xc, z, dbc, a["in_proj_w"], a["L1_gnn_conv_w"], a["L1_gnn_conv_b"], a["x_proj_w"])
                    for h in range(2):
                        selective_scan(k, h, xc, z, dbc, a["dt_proj_w"], a["L1_gnn_dt_proj_b"], a["L1_gnn_A_log"], a["L1_gnn_D_param"])
                    project(k, z, a["out_proj_w"], D, table=d["sorted"])
                with sbt("y_f") as y, sbt("rows_f") as rows, sbt("local_f") as local:
                    permute(k, y, d["sorted"], rank_i, scatter=False)
                    transfer(k, rows[:], d["xn"].rearrange("(t p) f -> p t f", p=P))
                    transfer(k, local[:], d["local"].rearrange("(t p) f -> p t f", p=P))
                    finish_norm(k, y, rows, a["L1_gnn_ln_global_g"], a["L1_gnn_ln_global_b"], to_x=False)
                    with sbt("cols_f", [128, 2, N]) as la, sbt("cols_g", [128, 2, N]) as ya:
                        turn_all(k, local, la)
                        turn_all(k, y, ya)
                        mix(k, local, y, la, ya, a["wl"], a["wg"])
                    transfer(k, d["local"].rearrange("(t p) f -> p t f", p=P), local[:])
            with sbt("h_g") as hrow, sbt("ff_g") as ff, sbt("gate_g", [P, NT, 1]) as gate, sbt("cols_h", [128, 2, N]) as cols:
                transfer(k, hrow[:], d["local"].rearrange("(t p) f -> p t f", p=P))
                turn_all(k, hrow, cols)
                ones_gate(k, gate)
                experts(k, cols, gate, ff, Experts(1, 512, ACT.Relu, a["ff1_w"], a["ff1_b"], a["ff2_w"], a["L1_gnn_ff2_b"]))
                finish_norm(k, hrow, ff, a["L1_gnn_ln2_g"], a["L1_gnn_ln2_b"])

        if layers >= 4:
            with sbt("gate_i", [P, NT, 4]) as gate, sbt("cols_i", [128, 2, N]) as cols:
                with sbt("rows_i") as rows:
                    normalise_all(k, rows, cols)
                with sbt("h16", [P, NT, 16]) as h16, sbt("agg_i", [P, NT, 20]) as agg, sbt("score_i", [P, NT, 4]) as score:
                    project(k, cols, a["L1_ffn_W_gat"], 16, rows=h16, table=d["small"])
                    scores(k, h16, 16, 4, a["L1_ffn_att_src"], a["L1_ffn_att_dst"], d["small"].rearrange("(t p) f -> p t f", p=P)[:, :, 16:20],
                           d["att4"].rearrange("(t p) f -> p t f", p=P))
                    small_edge_sums(k, d["small"], d["att4"], d["small"], agg, a["ffn_src_c"], a["ffn_dst_c"])
                    divide(k, agg, h16, 4, 1e-16, bias=a["L1_ffn_b_gat"], width=16)
                    finish_norm(k, h16, None, a["L1_ffn_ln_gamma"], a["L1_ffn_ln_beta"], to_x=False, width=16)
                    mean_heads(k, h16, score)
                    gates(k, cols, gate, 4, None, None, "top2", scores=score[:])
                with sbt("moe_i") as moe:
                    experts(k, cols, gate, moe, Experts(4, 512, ACT.Gelu, a["L1_ffn_W1"], a["L1_ffn_b1"], a["L1_ffn_W2"], a["L1_ffn_b2"]))
                    add_to_x(k, moe)

        if layers >= 5:
            with sbt("rows_j") as rows, sbt("cols_j", [128, 2, N]) as cols:
                normalise_all(k, rows, cols)
                project(k, cols, a["gat2_w"], D, rows=rows, table=d["gat8"])
                scores(k, rows, D, 8, a["gat2_a1"], a["gat2_a2"], d["gat8"].rearrange("(t p) f -> p t f", p=P)[:, :, D:D + 8],
                       d["att8"].rearrange("(t p) f -> p t f", p=P))
            edge_sums(k, d["gat8"], k.src_i, D + 8, heads=8, att_rows=d["att8"])
            with sbt("agg_j", [P, NT, D + 8]) as agg, sbt("out_j") as o:
                collect(k, agg, D + 8)
                divide(k, agg, o, 8, 0.0)
                add_to_x(k, o)

        if layers >= 6:
            with sbt("gate_k", [P, NT, 8]) as gate, sbt("moe_k") as moe, sbt("cols_k", [128, 2, N]) as cols:
                with sbt("rows_k") as rows:
                    normalise_all(k, rows, cols)
                gates(k, cols, gate, 8, a["L2_ffn_gate_w"], a["L2_ffn_gate_b"], "top1", capacity=math.ceil(1.25 * N / 8))
                experts(k, cols, gate, moe, Experts(8, 1024, ACT.Relu, a["L2_ffn_w1"], a["L2_ffn_b1"], a["L2_ffn_w2"], a["L2_ffn_b2"]))
                nan_to_num_to_x(k, moe)

        if layers >= 7:
            with sbt("rows_l") as rows, sbt("cols_l", [128, 2, N]) as cols:
                normalise_all(k, rows, cols)
                project(k, cols, a["L3_gnn_lin1_w"], D, table=d["lin1"])
            with sbt("cut", [P, ET]) as cut:
                cutoff(k, cut)
                edge_sums(k, d["lin1"], k.src_i, D, weight=cut, mlp=Mlp(50, a["attr"], a["L3_gnn_mlp_w1"], a["L3_gnn_mlp_b1"], a["L3_gnn_mlp_w2"], a["L3_gnn_mlp_b2"]))
            with sbt("agg_m") as agg, sbt("cols_m", [128, 2, N]) as cols:
                collect(k, agg, D)
                turn_all(k, agg, cols)
                project(k, cols, a["L3_gnn_lin2_w"], D, rows=agg)
                add_bias(k, agg, a["L3_gnn_lin2_b"], softplus=True)
                turn_all(k, agg, cols)
                project(k, cols, a["L3_gnn_lin_w"], D, rows=agg)
                add_bias(k, agg, a["L3_gnn_lin_b"], to_x=True)

        if layers >= 8:
            with sbt("gate_n", [P, NT, 6]) as gate, sbt("moe_n") as moe, sbt("cols_n", [128, 2, N]) as cols:
                with sbt("rows_n") as rows:
                    normalise_all(k, rows, cols)
                gates(k, cols, gate, 6, None, a["L3_ffn_router_b2"], "top2_probs", router=Experts(1, 128, None, a["L3_ffn_router_w1"], a["L3_ffn_router_b1"], a["L3_ffn_router_w2"], None))
                experts(k, cols, gate, moe, Experts(6, 256, ACT.Relu, a["L3_ffn_expert_w1"], a["L3_ffn_expert_b1"], a["L3_ffn_expert_w3"], a["L3_ffn_expert_b3"],
                                                    wm=a["L3_ffn_expert_w2"], bm=a["L3_ffn_expert_b2"]))
                add_to_x(k, moe)

        with stage(k) as s:
            stored = s.sem("stored")
            with s.block() as block:
                @block.sync
                def _(sp):
                    sp.dma_start(out_rows, k.x[:]).then_inc(stored, 16)
                    sp.wait_ge(stored, 16)


def layouts(v):
    col = lambda e: np.ascontiguousarray(e.reshape(ET, P).T)
    hid = lambda b: np.ascontiguousarray(b.reshape(b.shape[0], -1, 128).transpose(0, 2, 1).reshape(b.shape[0] * 128, -1))
    w_rel = v["L0_gnn_weight"].reshape(REL, BASES, SUB, SUB)
    return {
        "x": v["x"], "dst": v["dst"], "src_c": col(v["src"]), "dst_c": col(v["dst"]), "type_c": col(v["edge_type_8"]),
        "weight_c": col(v["edge_weight"]), "w_rel": np.ascontiguousarray(w_rel.transpose(1, 2, 0, 3)),
        **{n: v[n] for n in ("L0_ffn_gate_w", "L0_ffn_gate_b", "L0_ffn_w1", "L0_ffn_w2", "L0_ffn_gamma", "L0_ffn_beta")},
        **{n: v[n] for n in (
            "node_vec", "L1_gnn_gat_b", "L1_gnn_ln_local_g", "L1_gnn_ln_local_b", "L1_gnn_ln_global_g", "L1_gnn_ln_global_b", "L1_gnn_ln2_g", "L1_gnn_ln2_b",
            "L1_gnn_conv_w", "L1_gnn_conv_b", "L1_gnn_dt_proj_b", "L1_gnn_A_log", "L1_gnn_D_param", "L1_gnn_ff2_b",
            "L1_ffn_W_gat", "L1_ffn_b_gat", "L1_ffn_ln_gamma", "L1_ffn_ln_beta", "L1_ffn_W1", "L1_ffn_W2",
            "L2_ffn_gate_w", "L2_ffn_gate_b", "L2_ffn_w1", "L2_ffn_w2",
            "L3_gnn_mlp_w1", "L3_gnn_mlp_b1", "L3_gnn_mlp_w2", "L3_gnn_mlp_b2", "L3_gnn_lin1_w", "L3_gnn_lin2_w", "L3_gnn_lin2_b", "L3_gnn_lin_w", "L3_gnn_lin_b",
            "L3_ffn_router_w1", "L3_ffn_router_b1", "L3_ffn_router_w2", "L3_ffn_router_b2", "L3_ffn_expert_w1", "L3_ffn_expert_w2", "L3_ffn_expert_w3")},
        "gat_w": v["L1_gnn_gat_w"].T, "gat_a_src": v["L1_gnn_gat_a_src"].reshape(-1), "gat_a_tgt": v["L1_gnn_gat_a_tgt"].reshape(-1),
        "in_proj_w": v["L1_gnn_in_proj_w"].T, "x_proj_w": v["L1_gnn_x_proj_w"].T, "dt_proj_w": v["L1_gnn_dt_proj_w"].T, "out_proj_w": v["L1_gnn_out_proj_w"].T,
        "wl": v["L1_gnn_wl"].T, "wg": v["L1_gnn_wg"].T, "ff1_w": v["L1_gnn_ff1_w"].T[None], "ff1_b": hid(v["L1_gnn_ff1_b"][None]), "ff2_w": v["L1_gnn_ff2_w"].T[None],
        "L1_ffn_att_src": v["L1_ffn_att_src"].reshape(-1), "L1_ffn_att_dst": v["L1_ffn_att_dst"].reshape(-1),
        "ffn_src_c": v["L1_ffn_edge_index"][0].reshape(-1, 128).T, "ffn_dst_c": v["L1_ffn_edge_index"][1].reshape(-1, 128).T,
        "L1_ffn_b1": hid(v["L1_ffn_b1"]), "L1_ffn_b2": v["L1_ffn_b2"].reshape(-1),
        "gat2_w": v["L2_gnn_W"].transpose(1, 0, 2).reshape(D, D), "gat2_a1": v["L2_gnn_a"][:, :32].reshape(-1), "gat2_a2": v["L2_gnn_a"][:, 32:].reshape(-1),
        "L2_ffn_b1": hid(v["L2_ffn_b1"]), "L2_ffn_b2": v["L2_ffn_b2"].reshape(-1),
        "attr": v["edge_attr_50"].T,
        "L3_ffn_expert_b1": hid(v["L3_ffn_expert_b1"]), "L3_ffn_expert_b2": hid(v["L3_ffn_expert_b2"]), "L3_ffn_expert_b3": v["L3_ffn_expert_b3"].reshape(-1),
        "L0_ffn_b1": hid(v["L0_ffn_b1"]), "L0_ffn_b2": v["L0_ffn_b2"].reshape(-1),
    }


def kernel(**inputs):
    import concourse.bacc as bacc
    from concourse.bass_utils import run_bass_kernel_spmd

    nc = bacc.Bacc("TRN2", target_bir_lowering=False, num_devices=1)
    arrays = layouts({n: np.asarray(v) for n, v in inputs.items()})
    arrays = {f"in_{n}": np.ascontiguousarray(v) for n, v in arrays.items()}
    args = {n[3:]: nc.dram_tensor(n, v.shape, mybir.dt.from_np(v.dtype), kind="ExternalInput").ap() for n, v in arrays.items()}
    out = nc.dram_tensor("out_0", (N, D), F32, kind="ExternalOutput").ap()
    build(nc, args, out, 8)
    r = run_bass_kernel_spmd(nc, [arrays], core_ids=[0])
    return r.results[0]["out_0"]
```

```python
import math
from contextlib import ExitStack

import numpy as np

import concourse.bass as bass
from concourse import mybir

ALU = mybir.AluOpType
ACT = mybir.ActivationFunctionType
AX_X = mybir.AxisListType.X
F32 = mybir.dt.float32
I32 = mybir.dt.int32
RMAX = bass.bass_isa.ReduceOp.max
ds = bass.ds

N, D, E = 3125, 256, 50000
P = 125
NT, ET = N // P, E // P
G = 4
NG = ET // G
PAD_ROW = N
AT = NT + 1
REL, BASES, SUB = 8, 8, 32
EPS = 1e-5


class Core:
    pass


def stage(k):
    return Stage(k)


class Stage:
    def __init__(self, k):
        self.k, self.nc = k, k.nc
        self.ctx = ExitStack()
        self.sems = []

    def __enter__(self):
        return self

    def __exit__(self, *e):
        if e[0] is not None:
            return False
        self.ctx.close()
        self.nc.clear_and_free_semaphores(self.sems)
        self.nc.all_engine_barrier()

    def sb(self, name, shape, dt=F32):
        self.k.uid += 1
        return self.ctx.enter_context(self.nc.sbuf_tensor(f"{name}_{self.k.uid}", shape, dt))

    def ps(self, name, shape, dt=F32):
        self.k.uid += 1
        return self.ctx.enter_context(self.nc.psum_tensor(f"{name}_{self.k.uid}", shape, dt))

    def sem(self, name):
        self.k.uid += 1
        s = self.nc.alloc_semaphore(f"{name}_{self.k.uid}")
        self.sems.append(s)
        return s

    def block(self):
        return self.nc.Block()


class Chain:

    def __init__(self, eng, sem):
        self.eng, self.sem, self.n = eng, sem, 0

    def step(self, ins):
        self.n += 1
        ins.then_inc(self.sem, 1)

    def wait(self):
        self.eng.wait_ge(self.sem, self.n)

    def link(self, ins):
        self.step(ins)
        self.wait()


def split_index(nc, c, node, tile_of, lo):
    c.link(nc.vector.memset(tile_of, 0.0))
    for t in range(1, NT):
        c.link(nc.vector.scalar_tensor_tensor(tile_of, node, float(P * t), tile_of, ALU.is_ge, ALU.add))
    c.link(nc.vector.tensor_scalar(lo, tile_of, float(-P), None, ALU.mult))
    c.link(nc.vector.tensor_tensor(lo, lo, node, ALU.add))


def prepare_edges(k):
    nc = k.nc
    with stage(k) as s:
        src, typ, dst, dst_n, small = (s.sb(n, sh, I32) for n, sh in (("src", [P, ET]), ("typ", [P, ET]), ("dst", [P, ET]), ("dst_n", [P, ET]), ("small", [128, 256])))
        mix_ = s.sb("mix", [P, ET])
        f_n, t_n, lo_n = (s.sb(n, [P, ET]) for n in ("f_n", "t_n", "lo_n"))
        f_s, t_s, lo_s = (s.sb(n, [128, 256]) for n in ("f_s", "t_s", "lo_s"))
        lo_c = s.sb("lo_c", [P, ET])
        loaded, chain, ready, stored = (s.sem(n) for n in ("loaded", "chain", "ready", "stored"))
        with s.block() as block:
            @block.sync
            def _(sp):
                sp.dma_start(src[:], k.src_c).then_inc(loaded, 16)
                sp.dma_start(dst[:], k.dst_c).then_inc(loaded, 16)
                sp.dma_start(typ[:], k.type_c).then_inc(loaded, 16)
                sp.dma_start(k.edge_w[:], k.weight_c).then_inc(loaded, 16)
                sp.dma_start(dst_n[:], k.dst_r.rearrange("(p c) -> p c", p=P)).then_inc(loaded, 16)
                sp.dma_start(small[:], k.ffn_dst_r.rearrange("(p c) -> p c", p=128)).then_inc(loaded, 16)
                sp.wait_ge(ready, 1)
                sp.dma_start(k.lo_r.rearrange("(p c) -> p c", p=P), lo_n[:]).then_inc(stored, 16)
                sp.dma_start(k.ffn_lo_r.rearrange("(p c) -> p c", p=128), lo_s[:]).then_inc(stored, 16)
                sp.wait_ge(stored, 32)

            @block.gpsimd
            def _(pool):
                nc.gpsimd.iota(k.ramp_p[:], [[0, 1]], base=0, channel_multiplier=1, allow_small_or_imprecise_dtypes=True)
                nc.gpsimd.iota(k.ramp_t[:], [[1, NT]], base=0, channel_multiplier=0, allow_small_or_imprecise_dtypes=True)

            @block.vector
            def _(dve):
                c = Chain(dve, chain)
                dve.wait_ge(loaded, 96)
                for idx in (k.src_i, k.src_rel_i, k.row_i):
                    c.step(nc.vector.memset(idx[:, ET:ET + G], 0))
                c.step(nc.vector.tensor_copy(k.dst_f[:], dst[:]))
                c.step(nc.vector.tensor_copy(f_n[:], dst_n[:]))
                c.step(nc.vector.tensor_copy(f_s[:], small[:]))
                c.step(nc.vector.tensor_copy(k.src_i[:, 0:ET], src[:]))
                c.link(nc.vector.tensor_scalar(mix_[:], src[:], float(REL), None, ALU.mult))
                c.link(nc.vector.tensor_tensor(mix_[:], mix_[:], typ[:], ALU.add))
                c.link(nc.vector.tensor_copy(k.src_rel_i[:, 0:ET], mix_[:]))
                split_index(nc, c, f_n[:], t_n[:], lo_n[:])
                split_index(nc, c, f_s[:], t_s[:], lo_s[:])
                dve.sem_inc(ready, 1)
                split_index(nc, c, k.dst_f[:], k.dst_hi[:], lo_c[:])


def normalise_all(k, rows, cols, eps=EPS):
    nc = k.nc
    with stage(k) as s:
        stats = s.sb("stats", [P, NT, 6])
        mv = s.sb("mv", [P, NT, 2])
        veps = s.sb("veps", [P, NT])
        rstd = s.sb("rstd", [P, NT])
        ps = s.ps("turned", [128, 4, 512])
        chain, var, sd, rows_done, turned, copied = (s.sem(n) for n in ("chain", "var", "sd", "rows_done", "turned", "copied"))
        with s.block() as block:
            @block.vector
            def _(dve):
                c = Chain(dve, chain)
                for t in range(NT):
                    c.step(nc.vector.bn_stats(stats[:, t, :], k.x[:, t, :]))
                c.wait()
                for t in range(NT):
                    c.step(nc.vector.bn_aggr(mv[:, t, :], stats[:, t, :]))
                c.wait()
                nc.vector.tensor_scalar(veps[:], mv[:, :, 1], eps, None, ALU.add).then_inc(var, 1)
                dve.wait_ge(sd, 1)
                c.link(nc.vector.reciprocal(rstd[:], veps[:]))
                for t in range(NT):
                    nc.vector.tensor_scalar(rows[:, t, :], k.x[:, t, :], mv[:, t, 0:1], rstd[:, t:t + 1],
                                            ALU.subtract, ALU.mult).then_inc(rows_done, 1)

            @block.scalar
            def _(act):
                act.wait_ge(var, 1)
                nc.scalar.activation(veps[:], veps[:], ACT.Sqrt).then_inc(sd, 1)
                for t in range(NT):
                    act.wait_ge(turned, t + 1)
                    nc.scalar.activation(cols[:, :, t * P:(t + 1) * P],
                                         ps[:, t % 4, 0:2 * P].rearrange("p (c n) -> p c n", c=2), ACT.Copy).then_inc(copied, 1)

            @block.tensor
            def _(pe):
                for t in range(NT):
                    pe.wait_ge(rows_done, t + 1)
                    if t >= 4:
                        pe.wait_ge(copied, t - 3)
                    nc.tensor.transpose(ps[:, t % 4, 0:P], rows[:, t, 0:128], k.ident[0:P, 0:P])
                    nc.tensor.transpose(ps[:, t % 4, P:2 * P], rows[:, t, 128:256], k.ident[0:P, 0:P]).then_inc(turned, 1)


def relation_tables(k, cols):
    nc = k.nc
    with stage(k) as s:
        w = s.sb("w_rel", [128, 2, REL, 128])
        row = s.sb("row", [P, 5, REL, D])
        ps = s.ps("ps", [P, 8, 512])
        zeroed, w_in, mm, evac = (s.sem(n) for n in ("zeroed", "w_in", "mm", "evac"))
        stored = [s.sem(f"stored{j}") for j in range(5)]
        with s.block() as block:
            @block.sync
            def _(sp):
                sp.wait_ge(zeroed, 1)
                for b in range(BASES):
                    lo = SUB * (b % 4)
                    sp.dma_start(w[lo:lo + SUB, b // 4, :, lo:lo + SUB], k.w_rel[b]).then_inc(w_in, 16)
                with sp.Fori(0, NT // 5) as i:
                    for j in range(5):
                        sp.wait_ge(evac, (i * 5 + j) * 4 + 4)
                        sp.dma_start(k.rel_rows[ds((i * 5 + j) * P, P), :], row[:, j, :, :].rearrange("p r f -> p (r f)")).then_inc(stored[j], 16)
                for j in range(5):
                    sp.wait_ge(stored[j], 16 * (NT // 5))

            @block.vector
            def _(dve):
                nc.vector.memset(w[:], 0.0).then_inc(zeroed, 1)

            @block.tensor
            def _(pe):
                pe.wait_ge(w_in, 16 * BASES)
                for t in range(NT):
                    for q in range(4):
                        c, half = q // 2, q % 2
                        n = t * 4 + q
                        if n >= 8:
                            pe.wait_ge(evac, n - 7)
                        nc.tensor.matmul(ps[:, n % 8, :], cols[:, c, t * P:(t + 1) * P],
                                         w[:, c, 4 * half:4 * half + 4, :].rearrange("p r o -> p (r o)"),
                                         start=True, stop=True).then_inc(mm, 1)

            @block.scalar
            def _(act):
                for t in range(NT):
                    if t >= 5:
                        act.wait_ge(stored[t % 5], 16 * (t // 5))
                    for q in range(4):
                        c, half = q // 2, q % 2
                        act.wait_ge(mm, t * 4 + q + 1)
                        nc.scalar.activation(row[:, t % 5, 4 * half:4 * half + 4, c * 128:(c + 1) * 128],
                                             ps[:, (t * 4 + q) % 8, :].rearrange("p (r o) -> p r o", r=4), ACT.Copy).then_inc(evac, 1)


class Mlp:

    def __init__(self, n_in, attr, w1, b1, w2, b2):
        self.n_in, self.attr, self.w1, self.b1, self.w2, self.b2 = n_in, attr, w1, b1, w2, b2


def upto(g, j, back=0):
    return (g - back + 2) * G + j + 1


def edge_sums(k, table, src_idx, width, weight=None, heads=0, tgt=None, top=None, mlp=None, make_rows=False):
    nc = k.nc
    att = heads > 0
    HD = D // heads if att else 0
    with stage(k) as s:
        rows = s.sb("rows", [P, 2, G * P], I32)
        gi = s.sb("gi", [P, 2, G], I32)
        si = s.sb("si", [P, 2, G], I32)
        msg = s.sb("msg", [P, 2, G, width])
        same = s.sb("same", [P, 2, G, P])
        z = s.sb("z", [P, 2, G, width])
        zero = s.sb("zero", [P, width])
        ps = s.ps("ps", [P, G, 512])
        if att:
            lo_rows = s.sb("lo_rows", [P, 2, G * P])
            pick = s.sb("pick", [P, 2, G * P])
            in_tile = s.sb("in_tile", [P, 2, G, NT])
            picked = s.sb("picked", [P, G * heads, NT])
            s_dst = s.sb("s_dst", [P, G, heads])
            e1 = s.sb("e1", [P, G, 2, heads])
            e2 = s.sb("e2", [P, G, 2, heads])
            e = s.sb("e", [P, 2, G, heads])
            ps_s = s.ps("ps_s", [P, 2, 2, 512])
            HT = heads * NT
        if make_rows:
            before, hits = s.sb("before", [P, P]), s.sb("hits", [P, G, P])
            prior, row = s.sb("prior", [P, G]), s.sb("row", [P, G])
            pad = s.sb("pad", [P, 1])
            ramps, rows_made = s.sem("ramps"), s.sem("rows_made")
        if mlp:
            attr = s.sb("attr", [mlp.n_in, 2, G * P])
            hid = s.sb("hid", [128, 2, 2, G * P])
            pos = s.sb("pos", [128, 2, 2, G * P])
            hs = s.sb("hs", [128, 2, 2, G * P])
            w1, b1 = s.sb("w1", [mlp.n_in, D]), s.sb("b1", [128, 2])
            w2, b2 = s.sb("w2", [128, 2, D]), s.sb("b2", [P, D])
            fil = s.sb("fil", [P, G, D])
            w_in, hid_ln = s.sem("w_in"), s.sem("hid_ln")
            ps_h = s.ps("ps_h", [128, 2, 512])
            ps_f = s.ps("ps_f", [P, G, D])
        turns = s.sem("turns")
        zeroed, idx_done, mm, z_done, same_done, si_done = (s.sem(n) for n in ("zeroed", "idx", "mm", "z_done", "same", "si"))
        e_done, a_done, ready, chain, pick_done, sc_mm = (s.sem(n) for n in ("e_done", "a_done", "ready", "chain", "pick", "sc_mm"))
        hid_mm, hid_act, hid_done, fil_mm, fil_used = (s.sem(n) for n in ("hid_mm", "hid_act", "hid_done", "fil_mm", "fil_used"))
        row_in = [s.sem("row_in0"), s.sem("row_in1")]
        msg_in = [s.sem("msg_in0"), s.sem("msg_in1")]
        attr_in = [s.sem("attr_in0"), s.sem("attr_in1")]
        added = [s.sem(f"added{j}") for j in range(G)]
        n_rows = 2 if att else 1
        with s.block() as block:
            @block.sync
            def _(sp):
                if mlp:
                    sp.dma_start(w1[:], mlp.w1).then_inc(w_in, 16)
                    sp.dma_start(w2[:], mlp.w2.rearrange("(c p) f -> p c f", p=128)).then_inc(w_in, 16)
                    sp.dma_start(b2[:], mlp.b2.partition_broadcast(P)).then_inc(w_in, 16)
                    sp.dma_start(b1[:], mlp.b1.rearrange("(c p) -> p c", p=128), allow_slow_non_contiguous=True).then_inc(w_in, 16)
                with sp.Fori(0, NG // 2) as i:
                    for b in range(2):
                        g = i * 2 + b
                        sp.wait_ge(same_done, upto(g, G - 1, back=2))
                        sp.dma_start(rows[:, b, :], k.dst_r[ds(g * (G * P), G * P)].partition_broadcast(P)).then_inc(row_in[b], 16)
                        if att:
                            sp.dma_start(lo_rows[:, b, :], k.lo_r[ds(g * (G * P), G * P)].partition_broadcast(P)).then_inc(row_in[b], 16)
                        if mlp:
                            sp.wait_ge(hid_mm, 2 * g + 2)
                            sp.dma_start(attr[:, b, :], mlp.attr[:, ds(g * (G * P), G * P)]).then_inc(attr_in[b], 16)

            @block.gpsimd
            def _(pool):
                nc.gpsimd.memset(zero[:], 0.0).then_inc(zeroed, 1)
                if make_rows:
                    nc.gpsimd.memset(before[:], 1.0).then_inc(ramps, 1)
                    pool.wait_ge(ramps, 1)
                    nc.gpsimd.affine_select(out=before[:], in_=before[:], compare_op=ALU.is_gt, fill=0.0, base=0,
                                            pattern=[[-1, P]], channel_multiplier=1).then_inc(ramps, 1)
                    nc.gpsimd.iota(pad[:], [[0, 1]], base=PAD_ROW, channel_multiplier=1, allow_small_or_imprecise_dtypes=True).then_inc(ramps, 1)
                pool.wait_ge(zeroed, 1)
                for half in range(2):
                    for j in range(G):
                        if half:
                            pool.wait_ge(added[j], 16)
                        pool.dma_start(k.acc[width][j].rearrange("(h t p) f -> h p t f", p=P, h=2)[half],
                                       zero[:].unsqueeze(1).to_broadcast([P, AT // 2, width])).then_inc(added[j], 16)

                def gather(b, g):
                    pool.wait_ge(idx_done, g + 1)
                    pool.wait_ge(mm, upto(g, G - 1, back=2))
                    pool.sem_inc(turns, 1)
                    for j in range(G):
                        nc.gpsimd.indirect_dma_start(msg[:, b, j, :], None, table, bass.IndirectOffsetOnAxis(gi[:, b, j:j + 1], 0)).then_inc(msg_in[b], 16)

                def scatter(b, g):
                    pool.wait_ge(si_done, g + 1)
                    for j in range(G):
                        pool.wait_ge(z_done, upto(g, j))
                        pool.wait_ge(added[j], (g + 2) * 16)
                        pool.sem_inc(turns, 1)
                        nc.gpsimd.indirect_dma_start(k.acc[width][j], bass.IndirectOffsetOnAxis(si[:, b, j:j + 1], 0), z[:, b, j, :], None,
                                                     compute_op=ALU.add).then_inc(added[j], 16)

                gather(0, 0)
                last = NG // 2 - 1
                with pool.Fori(0, last) as i:
                    gather(1, i * 2 + 1)
                    scatter(0, i * 2)
                    gather(0, i * 2 + 2)
                    scatter(1, i * 2 + 1)
                gather(1, NG - 1)
                scatter(0, NG - 2)
                scatter(1, NG - 1)
                for j in range(G):
                    pool.wait_ge(added[j], (NG + 2) * 16)

            @block.vector
            def _(dve):
                dve.sem_inc(same_done, 2 * G)
                dve.sem_inc(hid_done, 2)

                def indices(b, g):
                    dve.wait_ge(mm, upto(g, G - 1, back=2))
                    nc.vector.tensor_copy(gi[:, b, :], src_idx[:, ds(g * G, G)]).then_inc(idx_done, 1)

                def compare(b, g, i):
                    dve.wait_ge(row_in[b], 16 * n_rows * (i + 1))
                    if make_rows:
                        sum_rows(b, g)
                    if att:
                        dve.wait_ge(sc_mm, 2 * g + 2)
                        nc.vector.tensor_scalar(pick[:, b, :], lo_rows[:, b, :], k.ramp_p[:], None, ALU.is_equal).then_inc(pick_done, 1)
                        nc.vector.tensor_tensor(in_tile[:, b, :, :], k.dst_hi[:, ds(g * G, G)].unsqueeze(2).to_broadcast([P, G, NT]),
                                                k.ramp_t[:].unsqueeze(1).to_broadcast([P, G, NT]), ALU.is_equal).then_inc(chain, 1)
                    for j in range(G):
                        args = (weight[:, ds(g * G + j, 1)], ALU.is_equal, ALU.mult) if weight is not None else (None, ALU.is_equal)
                        nc.vector.tensor_scalar(same[:, b, j, :], rows[:, b, j * P:(j + 1) * P], k.dst_f[:, ds(g * G + j, 1)], *args).then_inc(same_done, 1)

                def messages(b, g, i):
                    dve.wait_ge(msg_in[b], 16 * G * (i + 1))
                    if att:
                        c0 = 8 * g
                        dve.wait_ge(sc_mm, 2 * g + 6)
                        dve.wait_ge(chain, g + 1)
                        for q in range(2):
                            nc.vector.tensor_tensor(picked[:, 2 * q * heads:2 * (q + 1) * heads, :].rearrange("p (j h) t -> p j h t", j=2),
                                                    ps_s[:, b, q, 0:2 * HT].rearrange("p (j h t) -> p j h t", j=2, t=NT),
                                                    in_tile[:, b, 2 * q:2 * q + 2, :].unsqueeze(2).to_broadcast([P, 2, heads, NT]), ALU.mult).then_inc(e_done, 1)
                        dve.wait_ge(e_done, c0 + 2)
                        nc.vector.tensor_reduce(s_dst[:].rearrange("p g h -> p (g h)"), picked[:], AX_X, ALU.add).then_inc(e_done, 1)
                        dve.wait_ge(e_done, c0 + 3)
                        nc.vector.tensor_tensor(e1[:, :, 0, :], msg[:, b, :, D:D + heads], s_dst[:], ALU.add).then_inc(e_done, 1)
                        nc.vector.tensor_tensor(e1[:, :, 1, :], top[:].unsqueeze(1).to_broadcast([P, G, heads]), s_dst[:], ALU.add).then_inc(e_done, 1)
                        dve.wait_ge(e_done, c0 + 5)
                        nc.vector.scalar_tensor_tensor(e2[:], e1[:], 0.2, e1[:], ALU.mult, ALU.max).then_inc(e_done, 1)
                        dve.wait_ge(e_done, c0 + 6)
                        nc.vector.tensor_tensor(e[:, b, :, :], e2[:, :, 0, :], e2[:, :, 1, :], ALU.subtract).then_inc(e_done, 1)
                        dve.wait_ge(e_done, c0 + 7)
                        dve.sem_inc(e_done, 1)
                        dve.wait_ge(a_done, g + 1)
                        for j in range(G):
                            m = msg[:, b, j, 0:D].rearrange("p (h d) -> p h d", h=heads)
                            nc.vector.tensor_tensor(m, m, msg[:, b, j, D:D + heads].unsqueeze(2).to_broadcast([P, heads, HD]), ALU.mult).then_inc(ready, 1)
                    if mlp:
                        for j in range(G):
                            dve.wait_ge(fil_mm, g * G + (j | 1) + 1)
                            nc.vector.tensor_tensor(fil[:, j, :], ps_f[:, j, :], b2[:], ALU.add).then_inc(fil_used, 1)
                        for j in range(G):
                            dve.wait_ge(fil_used, g * G + j + 1 + G)
                            nc.vector.tensor_tensor(msg[:, b, j, :], msg[:, b, j, :], fil[:, j, :], ALU.mult).then_inc(ready, 1)

                def shifted(b, g):
                    dve.wait_ge(hid_ln, 2 * g + 2)
                    nc.vector.scalar_tensor_tensor(hs[:, b, :, :], hid[:, b, :, :], -math.log(2.0), pos[:, b, :, :], ALU.add, ALU.add).then_inc(hid_done, 1)

                def sum_rows(b, g):
                    for j in range(G):
                        nc.vector.scalar_tensor_tensor(hits[:, j, :], rows[:, b, j * P:(j + 1) * P], k.dst_f[:, ds(g * G + j, 1)], before[:], ALU.is_equal, ALU.mult).then_inc(chain, 1)
                    dve.wait_ge(chain, 8 * g + 4)
                    nc.vector.tensor_reduce(prior[:], hits[:], AX_X, ALU.add).then_inc(chain, 1)
                    dve.wait_ge(chain, 8 * g + 5)
                    nc.vector.tensor_scalar(prior[:], prior[:], 0.0, None, ALU.is_equal).then_inc(chain, 1)
                    dve.wait_ge(chain, 8 * g + 6)
                    nc.vector.scalar_tensor_tensor(row[:], k.dst_f[:, ds(g * G, G)], pad[:], prior[:], ALU.subtract, ALU.mult).then_inc(chain, 1)
                    dve.wait_ge(chain, 8 * g + 7)
                    nc.vector.tensor_scalar(k.row_i[:, ds(g * G, G)], row[:], pad[:], None, ALU.add).then_inc(rows_made, 1)
                    dve.wait_ge(rows_made, g + 1)
                    dve.sem_inc(chain, 1)

                def turn(b, g, i, ahead):
                    indices(1 - b, g + 1)
                    compare(b, g, i)
                    if att or mlp:
                        messages(b, g, i)
                    if mlp and ahead:
                        shifted(b, g + 2)

                if make_rows:
                    dve.wait_ge(ramps, 3)
                indices(0, 0)
                if mlp:
                    dve.wait_ge(w_in, 64)
                    shifted(0, 0)
                    shifted(1, 1)
                last = NG // 2 - 1
                with dve.Fori(0, last) as i:
                    for b in range(2):
                        turn(b, i * 2 + b, i, True)
                for b in range(2):
                    turn(b, last * 2 + b, last, False)

            @block.tensor
            def _(pe):
                pe.sem_inc(mm, 2 * G)
                if mlp:
                    pe.sem_inc(hid_mm, 4)
                    pe.wait_ge(w_in, 64)

                def hidden(b, g, n):
                    pe.wait_ge(attr_in[b], 16 * n)
                    for c in range(2):
                        pe.wait_ge(hid_act, 2 * g + c + 1)
                        nc.tensor.matmul(ps_h[:, c, 0:G * P], w1[:, c * 128:(c + 1) * 128], attr[:, b, :], start=True, stop=True).then_inc(hid_mm, 1)

                def filters(b, g):
                    pe.wait_ge(hid_done, g + 3)
                    for j in range(G):
                        pe.wait_ge(fil_used, g * G + (j | 1) + 1)
                        nc.tensor.matmul(ps_f[:, j, :], hs[:, b, 0, j * P:(j + 1) * P], w2[:, 0, :], start=True, stop=False)
                        nc.tensor.matmul(ps_f[:, j, :], hs[:, b, 1, j * P:(j + 1) * P], w2[:, 1, :], start=False, stop=True).then_inc(fil_mm, 1)

                def target_scores(b, g, i):
                    pe.wait_ge(pick_done, g + 1)
                    for q in range(2):
                        for j in (2 * q, 2 * q + 1):
                            ins = nc.tensor.matmul(ps_s[:, b, q, (j % 2) * HT:(j % 2 + 1) * HT], pick[:, b, j * P:(j + 1) * P], tgt[:].rearrange("p h t -> p (h t)"),
                                                   start=True, stop=True)
                        ins.then_inc(sc_mm, 1)

                def sums(b, g, i):
                    pe.wait_ge(msg_in[b], 16 * G * (i + 1))
                    for j in range(G):
                        pe.wait_ge(same_done, upto(g, j))
                        if att or mlp:
                            pe.wait_ge(ready, upto(g, j) - G)
                        pe.wait_ge(z_done, upto(g, j, back=1))
                        nc.tensor.matmul(ps[:, j, 0:width], same[:, b, j, :], msg[:, b, j, :], start=True, stop=True).then_inc(mm, 1)

                last = NG // 2 - 1
                if att:
                    pe.sem_inc(sc_mm, 4)
                if mlp:
                    hidden(0, 0, 1)
                    hidden(1, 1, 1)
                    filters(0, 0)
                    with pe.Fori(0, last) as i:
                        for b in range(2):
                            g = i * 2 + b
                            hidden(b, g + 2, i + 2)
                            sums(b, g, i)
                            filters(1 - b, g + 1)
                    sums(0, NG - 2, last)
                    filters(1, NG - 1)
                    sums(1, NG - 1, last)
                else:
                    with pe.Fori(0, NG // 2) as i:
                        for b in range(2):
                            g = i * 2 + b
                            if att:
                                target_scores(b, g, i)
                            sums(b, g, i)

            @block.scalar
            def _(act):
                act.sem_inc(z_done, 2 * G)
                act.sem_inc(ready, G)
                act.sem_inc(hid_act, 2)
                act.sem_inc(fil_used, G)

                def weights(b, g):
                    act.wait_ge(e_done, 8 * g + 8)
                    nc.scalar.activation(msg[:, b, :, D:D + heads], e[:, b, :, :], ACT.Exp).then_inc(a_done, 1)

                def hidden(b, g):
                    act.wait_ge(hid_done, g + 1)
                    for c in range(2):
                        act.wait_ge(hid_mm, 2 * g + c + 5)
                        nc.scalar.activation(pos[:, b, c, :], ps_h[:, c, 0:G * P], ACT.Relu, bias=b1[:, c:c + 1])
                        nc.scalar.activation(hid[:, b, c, :], ps_h[:, c, 0:G * P], ACT.Abs, bias=b1[:, c:c + 1]).then_inc(hid_act, 1)
                    act.wait_ge(hid_act, 2 * g + 4)
                    nc.scalar.activation(hid[:, b, :, :], hid[:, b, :, :], ACT.Exp, scale=-1.0).then_inc(hid_ln, 1)
                    act.wait_ge(hid_ln, 2 * g + 1)
                    nc.scalar.activation(hid[:, b, :, :], hid[:, b, :, :], ACT.Ln, bias=1.0).then_inc(hid_ln, 1)

                if mlp:
                    act.wait_ge(w_in, 64)

                def leave(b, g):
                    for j in range(G):
                        act.wait_ge(added[j], (g + 1) * 16)
                    if make_rows:
                        act.wait_ge(rows_made, g + 1)
                    nc.scalar.activation(si[:, b, :], k.row_i[:, ds(g * G, G)], ACT.Copy).then_inc(si_done, 1)
                    for j in range(G):
                        act.wait_ge(mm, upto(g, j))
                        nc.scalar.activation(z[:, b, j, :], ps[:, j, 0:width], ACT.Copy).then_inc(z_done, 1)

                if mlp:
                    hidden(0, 0)
                    hidden(1, 1)
                last = NG // 2 - 1
                with act.Fori(0, last) as i:
                    for b in range(2):
                        g = i * 2 + b
                        if att:
                            weights(b, g)
                        if mlp:
                            hidden(b, g + 2)
                        leave(b, g)
                for b in range(2):
                    g = last * 2 + b
                    if att:
                        weights(b, g)
                    leave(b, g)


def collect(k, agg, width):
    nc = k.nc
    with stage(k) as s:
        part = s.sb("part", [P, 5, G, width])
        pair = s.sb("pair", [P, 5, 2, width])
        part_in = [s.sem(f"part_in{j}") for j in range(5)]
        paired, summed = s.sem("paired"), s.sem("summed")
        acc = [q.rearrange("(t p) f -> t p f", p=P) for q in k.acc[width]]
        with s.block() as block:
            @block.sync
            def _(sp):
                for t in range(NT):
                    if t >= 5:
                        sp.wait_ge(paired, t - 4)
                    for j in range(G):
                        sp.dma_start(part[:, t % 5, j, :], acc[j][t, :, :]).then_inc(part_in[t % 5], 16)

            @block.vector
            def _(dve):
                for t in range(NT):
                    j = t % 5
                    dve.wait_ge(part_in[j], 16 * G * (t // 5 + 1))
                    nc.vector.tensor_tensor(pair[:, j, :, :], part[:, j, 0:2, :], part[:, j, 2:4, :], ALU.add).then_inc(paired, 1)
                    dve.wait_ge(paired, t + 1)
                    nc.vector.tensor_tensor(agg[:, t, 0:width], pair[:, j, 0, :], pair[:, j, 1, :], ALU.add).then_inc(summed, 1)


def add_to_x(k, agg):
    nc = k.nc
    with stage(k) as s:
        done = s.sem("done")
        with s.block() as block:
            @block.vector
            def _(dve):
                nc.vector.tensor_tensor(k.x[:], k.x[:], agg[:], ALU.add).then_inc(done, 1)


def first_of_max(nc, dve, c, score, best, onehot, ramp, tmp, pick):
    L = score.shape[-1]
    wide = lambda a: a.unsqueeze(2).to_broadcast([P, NT, L])
    c.link(nc.vector.tensor_reduce(best, score, AX_X, ALU.max))
    c.link(nc.vector.tensor_tensor(tmp, score, wide(best), ALU.is_equal))
    c.link(nc.vector.tensor_tensor(tmp, tmp, ramp, ALU.mult))
    c.link(nc.vector.tensor_reduce(pick, tmp, AX_X, ALU.max))
    c.link(nc.vector.tensor_tensor(onehot, ramp, wide(pick), ALU.is_equal))


def gates(k, cols, gate, n_exp, w, bias, mode, router=None, scores=None, choice=None):
    nc = k.nc
    L = n_exp
    with stage(k) as s:
        sb3 = lambda n: s.sb(n, [P, NT, L])
        lg, tmp, oh1, oh2, rest = (sb3(n) for n in ("lg", "tmp", "oh1", "oh2", "rest"))
        ramp = s.sb("ramp", [P, NT, L])
        m1, m2, pick, w1, w2 = (s.sb(n, [P, NT]) for n in ("m1", "m2", "pick", "w1", "w2"))
        w_sb, b_sb = s.sb("w", [128, 2, L]), s.sb("b", [P, L])
        ps = s.ps("ps", [P, 512])
        w_in, mm, ramps, chain, to_act, from_act = (s.sem(n) for n in ("w_in", "mm", "ramps", "chain", "to_act", "from_act"))
        if router:
            rw1, rb1, rw2 = s.sb("rw1", [128, 2, 128]), s.sb("rb1", [128, 1]), s.sb("rw2", [128, L])
            rh = s.sb("rh", [128, N])
            ps_r = s.ps("ps_r", [128, 4, 512])
            r_mm, r_act = s.sem("r_mm"), s.sem("r_act")
        with s.block() as block:
            @block.sync
            def _(sp):
                if scores is None:
                    sp.dma_start(b_sb[:], bias.partition_broadcast(P)).then_inc(w_in, 16)
                if router:
                    sp.dma_start(rw1[:], router.w1.rearrange("(c p) h -> p c h", p=128)).then_inc(w_in, 16)
                    sp.dma_start(rb1[:], router.b1.rearrange("(p a) -> p a", a=1)).then_inc(w_in, 16)
                    sp.dma_start(rw2[:], router.w2).then_inc(w_in, 16)
                elif scores is None:
                    sp.dma_start(w_sb[:], w.rearrange("(c p) e -> p c e", p=128)).then_inc(w_in, 16)

            @block.gpsimd
            def _(pool):
                nc.gpsimd.iota(ramp[:], [[0, NT], [-1, L]], base=L, channel_multiplier=0, allow_small_or_imprecise_dtypes=True).then_inc(ramps, 1)

            @block.tensor
            def _(pe):
                if scores is None:
                    pe.wait_ge(w_in, 64 if router else 32)
                if router:
                    for q, n0 in enumerate(range(0, N, 500)):
                        m = min(500, N - n0)
                        if q >= 4:
                            pe.wait_ge(r_act, q - 3)
                        nc.tensor.matmul(ps_r[:, q % 4, 0:m], rw1[:, 0, :], cols[:, 0, n0:n0 + m], start=True, stop=False)
                        nc.tensor.matmul(ps_r[:, q % 4, 0:m], rw1[:, 1, :], cols[:, 1, n0:n0 + m], start=False, stop=True).then_inc(r_mm, 1)
                    pe.wait_ge(r_act, (N + 499) // 500)
                    for t in range(NT):
                        ins = nc.tensor.matmul(ps[:, t * L:(t + 1) * L], rh[:, t * P:(t + 1) * P], rw2[:], start=True, stop=True)
                    ins.then_inc(mm, 1)
                elif scores is None:
                    for t in range(NT):
                        nc.tensor.matmul(ps[:, t * L:(t + 1) * L], cols[:, 0, t * P:(t + 1) * P], w_sb[:, 0, :], start=True, stop=False)
                        ins = nc.tensor.matmul(ps[:, t * L:(t + 1) * L], cols[:, 1, t * P:(t + 1) * P], w_sb[:, 1, :], start=False, stop=True)
                    ins.then_inc(mm, 1)
            @block.scalar
            def _(act):
                if router:
                    act.wait_ge(w_in, 64)
                    for q, n0 in enumerate(range(0, N, 500)):
                        m = min(500, N - n0)
                        act.wait_ge(r_mm, q + 1)
                        nc.scalar.activation(rh[:, n0:n0 + m], ps_r[:, q % 4, 0:m], ACT.Relu, bias=rb1[:]).then_inc(r_act, 1)
                n = 0
                if mode != "top2":
                    act.wait_ge(to_act, 1)
                    nc.scalar.activation(lg[:], tmp[:], ACT.Exp).then_inc(from_act, 1)
                    n = 1
                if mode != "top1":
                    act.wait_ge(to_act, n + 1)
                    nc.scalar.activation(w2[:], pick[:], ACT.Exp).then_inc(from_act, 1)

            @block.vector
            def _(dve):
                c = Chain(dve, chain)
                wide = lambda a: a.unsqueeze(2).to_broadcast([P, NT, L])
                dve.wait_ge(ramps, 1)
                acts = 0
                score = lg[:]
                if scores is None:
                    dve.wait_ge(mm, 1)
                    dve.wait_ge(w_in, 64 if router else 32)
                    c.link(nc.vector.tensor_tensor(lg[:], ps[:, 0:NT * L].rearrange("p (t e) -> p t e", e=L),
                                                   b_sb[:].unsqueeze(1).to_broadcast([P, NT, L]), ALU.add))
                else:
                    score = scores
                if mode != "top2":
                    c.link(nc.vector.tensor_reduce(m1[:], lg[:], AX_X, ALU.max))
                    nc.vector.tensor_tensor(tmp[:], lg[:], wide(m1[:]), ALU.subtract).then_inc(to_act, 1)
                    acts += 1
                    dve.wait_ge(from_act, acts)
                    c.link(nc.vector.tensor_reduce(m2[:], lg[:], AX_X, ALU.add))
                    c.link(nc.vector.reciprocal(w1[:], m2[:]))
                    c.link(nc.vector.tensor_tensor(lg[:], lg[:], wide(w1[:]), ALU.mult))
                first_of_max(nc, dve, c, score, m1[:], oh1[:], ramp[:], tmp[:], pick[:])
                if mode == "top1":
                    c.step(nc.vector.tensor_copy(choice[0][:, 0, :, :], oh1[:]))
                    c.link(nc.vector.tensor_copy(choice[1][:, 0, :], m1[:]))
                    return
                c.link(nc.vector.tensor_scalar(tmp[:], oh1[:], -3.0e38, None, ALU.mult))
                c.link(nc.vector.tensor_tensor(rest[:], score, tmp[:], ALU.add))
                first_of_max(nc, dve, c, rest[:], m2[:], oh2[:], ramp[:], tmp[:], pick[:])
                nc.vector.tensor_tensor(pick[:], m2[:], m1[:], ALU.subtract).then_inc(to_act, 1)
                acts += 1
                dve.wait_ge(from_act, acts)
                c.link(nc.vector.tensor_scalar(w1[:], w2[:], 1.0, None, ALU.add))
                c.link(nc.vector.reciprocal(w1[:], w1[:]))
                c.link(nc.vector.tensor_tensor(w2[:], w2[:], w1[:], ALU.mult))
                if choice is not None:
                    for q, (oh, wt) in enumerate(((oh1, w1), (oh2, w2))):
                        c.step(nc.vector.tensor_copy(choice[0][:, q, :, :], oh[:]))
                        c.link(nc.vector.tensor_copy(choice[1][:, q, :], wt[:]))
                    return
                c.link(nc.vector.tensor_tensor(oh1[:], oh1[:], wide(w1[:]), ALU.mult))
                c.link(nc.vector.tensor_tensor(oh2[:], oh2[:], wide(w2[:]), ALU.mult))
                c.link(nc.vector.tensor_tensor(gate[:], oh1[:], oh2[:], ALU.add))


BR = 250


def most_blocks(chosen, n_exp, rows=N):
    return (chosen * rows + n_exp * (BR - 1)) // BR


def route(k, choice, slot_i, block_i, n_exp, chosen, blocks, capacity=None):
    nc = k.nc
    L = n_exp
    oh, wt = choice
    with stage(k) as s:
        total = s.sb("total", [P, NT, L])
        tot, pos, part = s.sb("tot", [P, NT + 1, L]), s.sb("pos", [P, NT, L]), s.sb("part", [P, NT, L])
        cnt, nb, end, start, ones = (s.sb(n, [P, L]) for n in ("cnt", "nb", "end", "start", "one"))
        slot = s.sb("slot", [P, NT])
        kept = s.sb("kept", [P, NT])
        pad = s.sb("pad", [P, 1])
        tri = s.sb("tri", [P, P])
        ramp_b = s.sb("ramp_b", [1, blocks, L])
        past = s.sb("past", [1, blocks, L])
        owner = s.sb("owner", [1, blocks])
        ps_pre, ps_tot = s.ps("pre", [P, 512]), s.ps("tot", [P, 512])
        made, chain, summed, mm = s.sem("made"), s.sem("chain"), s.sem("summed"), s.sem("mm")
        with s.block() as block:
            @block.gpsimd
            def _(pool):
                nc.gpsimd.memset(tri[:], 1.0).then_inc(made, 1)
                pool.wait_ge(made, 1)
                nc.gpsimd.affine_select(out=tri[:], in_=tri[:], compare_op=ALU.is_gt, fill=0.0, base=0,
                                        pattern=[[1, P]], channel_multiplier=-1).then_inc(made, 1)
                nc.gpsimd.iota(pad[:], [[0, 1]], base=blocks * BR, channel_multiplier=0, allow_small_or_imprecise_dtypes=True).then_inc(made, 1)
                nc.gpsimd.iota(ramp_b[:], [[1, blocks], [0, L]], base=0, channel_multiplier=0, allow_small_or_imprecise_dtypes=True).then_inc(made, 1)

            @block.tensor
            def _(pe):
                pe.wait_ge(made, 2)
                pe.wait_ge(summed, 1)
                flat = total[:].rearrange("p t e -> p (t e)")
                nc.tensor.matmul(ps_pre[:, 0:NT * L], tri[:], flat, start=True, stop=True)
                nc.tensor.matmul(ps_tot[:, 0:NT * L], k.ones[0:P, 0:P], flat, start=True, stop=True).then_inc(mm, 1)

            @block.vector
            def _(dve):
                c = Chain(dve, chain)
                as_te = lambda q: q[:, 0:NT * L].rearrange("p (t e) -> p t e", e=L)
                if chosen == 2:
                    nc.vector.tensor_tensor(total[:], oh[:, 0, :, :], oh[:, 1, :, :], ALU.add).then_inc(summed, 1)
                else:
                    nc.vector.tensor_copy(total[:], oh[:, 0, :, :]).then_inc(summed, 1)
                c.step(nc.vector.memset(tot[:, 0, :], 0.0))
                c.step(nc.vector.memset(nb[:], 0.0))
                c.step(nc.vector.memset(ones[:], 1.0))
                dve.wait_ge(mm, 1)
                c.link(nc.vector.tensor_copy(tot[:, 1:NT + 1, :], as_te(ps_tot)))
                for t in range(1, NT + 1):
                    c.link(nc.vector.tensor_tensor(tot[:, t, :], tot[:, t, :], tot[:, t - 1, :], ALU.add))
                c.step(nc.vector.tensor_tensor(pos[:], as_te(ps_pre), tot[:, 0:NT, :], ALU.add))
                c.link(nc.vector.tensor_scalar(cnt[:], tot[:, NT, :], float(capacity or N), None, ALU.min))
                for m in range((N + BR - 1) // BR):
                    c.link(nc.vector.scalar_tensor_tensor(nb[:], cnt[:], float(BR * m), nb[:], ALU.is_gt, ALU.add))
                c.link(nc.vector.tensor_tensor_scan(end[:], ones[:], nb[:], 0.0, ALU.mult, ALU.add))
                c.link(nc.vector.tensor_tensor(start[:], end[:], nb[:], ALU.subtract))
                c.link(nc.vector.tensor_scalar(start[:], start[:], float(BR), None, ALU.mult))
                dve.wait_ge(made, 4)
                if capacity:
                    c.link(nc.vector.tensor_scalar(part[:], pos[:], float(capacity), None, ALU.is_lt))
                    c.link(nc.vector.tensor_tensor(part[:], part[:], oh[:, 0, :, :], ALU.mult))
                    c.link(nc.vector.tensor_reduce(kept[:], part[:], AX_X, ALU.add))
                    c.link(nc.vector.tensor_tensor(wt[:, 0, :], wt[:, 0, :], kept[:], ALU.mult))
                c.link(nc.vector.tensor_tensor(pos[:], pos[:], start[:].unsqueeze(1).to_broadcast([P, NT, L]), ALU.add))
                for q in range(chosen):
                    c.link(nc.vector.tensor_tensor(part[:], pos[:], oh[:, q, :, :], ALU.mult))
                    c.link(nc.vector.tensor_reduce(slot[:], part[:], AX_X, ALU.add))
                    if capacity:
                        c.link(nc.vector.tensor_scalar(slot[:], slot[:], pad[:], None, ALU.subtract))
                        c.link(nc.vector.tensor_tensor(slot[:], slot[:], kept[:], ALU.mult))
                        c.link(nc.vector.tensor_scalar(slot[:], slot[:], pad[:], None, ALU.add))
                    c.link(nc.vector.tensor_copy(slot_i[:, q, :], slot[:]))
                c.link(nc.vector.tensor_tensor(past[:], ramp_b[:], end[0:1, :].unsqueeze(1).to_broadcast([1, blocks, L]), ALU.is_ge))
                c.link(nc.vector.tensor_reduce(owner[:], past[:], AX_X, ALU.add))
                c.link(nc.vector.tensor_scalar(block_i[:], owner[:], float(L - 1), None, ALU.min))


def clear_rows(k, table, n_rows):
    nc = k.nc
    with stage(k) as s:
        zero = s.sb("zero", [P, D])
        made, cleared = s.sem("made"), s.sem("cleared")
        with s.block() as block:
            @block.vector
            def _(dve):
                nc.vector.memset(zero[:], 0.0).then_inc(made, 1)

            @block.sync
            def _(sp):
                sp.wait_ge(made, 1)
                sp.dma_start(table[0:n_rows, :].rearrange("(t p) f -> p t f", p=P),
                             zero[:].unsqueeze(1).to_broadcast([P, n_rows // P, D])).then_inc(cleared, 16)
                sp.wait_ge(cleared, 16)


def send_rows(k, rows, table, slot_i, chosen, blocks):
    nc = k.nc
    with stage(k) as s:
        moved = s.sem("moved")
        with s.block() as block:
            @block.gpsimd
            def _(pool):
                for q in range(chosen):
                    for t in range(NT):
                        nc.gpsimd.indirect_dma_start(table, bass.IndirectOffsetOnAxis(slot_i[:, q, t:t + 1], 0), rows[:, t, :], None,
                                                         bounds_check=blocks * BR - 1, oob_is_err=False).then_inc(moved, 16)
                pool.wait_ge(moved, 16 * NT * chosen)


def fetch_rows(k, acc, table, slot_i, wt, chosen):
    nc = k.nc
    RING = 6
    with stage(k) as s:
        got = s.sb("got", [P, RING, D])
        got_in = [s.sem(f"got_in{j}") for j in range(RING)]
        used = s.sem("used")
        with s.block() as block:
            @block.gpsimd
            def _(pool):
                for n in range(NT * chosen):
                    t, q = n // chosen, n % chosen
                    if n >= RING:
                        pool.wait_ge(used, n - RING + 1)
                    nc.gpsimd.indirect_dma_start(got[:, n % RING, :], None, table, bass.IndirectOffsetOnAxis(slot_i[:, q, t:t + 1], 0)).then_inc(got_in[n % RING], 16)

            @block.vector
            def _(dve):
                for n in range(NT * chosen):
                    t, q = n // chosen, n % chosen
                    dve.wait_ge(got_in[n % RING], 16 * (n // RING + 1))
                    if q == 0:
                        ins = nc.vector.tensor_scalar(acc[:, t, :], got[:, n % RING, :], wt[:, q, t:t + 1], None, ALU.mult)
                    else:
                        dve.wait_ge(used, n)
                        ins = nc.vector.scalar_tensor_tensor(acc[:, t, :], got[:, n % RING, :], wt[:, q, t:t + 1], acc[:, t, :], ALU.mult, ALU.add)
                    ins.then_inc(used, 1)


def block_experts(k, table, result, block_i, x, blocks):
    nc = k.nc
    FC = x.f // 128
    FM = 2 if x.wm is not None else 0
    EV = FC + FM
    TB = BR // P
    SEMS = 6 if FM else 4
    with stage(k) as s:
        rows = s.sb("rows", [P, 2, TB, D])
        xT = s.sb("xT", [128, 2, 2, BR])
        w1, w2 = s.sb("w1", [128, 2, 2, x.f]), s.sb("w2", [128, 2, FM or FC, D])
        b1, b2 = s.sb("b1", [128, 2, FC]), s.sb("b2", [P, 2, D])
        hid = s.sb("hid", [128, FC, BR])
        y = s.sb("y", [P, 2, TB, D])
        zero = s.sb("zero", [P, D])
        if FM:
            wm, bm, mid = s.sb("wm", [128, 2, 2, D]), s.sb("bm", [128, 2, FM]), s.sb("mid", [128, FM, BR])
        ps_t, ps_h, ps_o = s.ps("ps_t", [128, 2, 512]), s.ps("ps_h", [128, 4, 512]), s.ps("ps_o", [P, 2, 512])
        w_in, rows_in, stored = ([s.sem(n + "0"), s.sem(n + "1")] for n in ("w_in", "rows_in", "stored"))
        t_mm, t_ev, h_mm, h_sb, o_mm, o_done, made, turns = (s.sem(n) for n in ("t_mm", "t_ev", "h_mm", "h_sb", "o_mm", "o_done", "made", "turns"))
        with s.block() as block:
            @block.sync
            def _(sp):
                def load_rows(buf, c):
                    sp.wait_ge(t_mm, c + 1)
                    sp.dma_start(rows[:, buf, :, :], table[ds(c * BR, BR), :].rearrange("(t p) f -> p t f", p=P)).then_inc(rows_in[buf], 16)

                load_rows(0, 0)
                with sp.Fori(0, blocks // 2) as i:
                    for b in range(2):
                        n = i * 2 + b
                        e = sp.value_load(block_i[0:1, ds(n, 1)], min_val=0, max_val=x.n - 1)
                        load_rows(1 - b, n + 1)
                        sp.wait_ge(o_done, 2 * n + 2)
                        sp.dma_start(w1[:, b, :, :], x.w1[ds(e, 1)].rearrange("e (c p) f -> p (e c) f", p=128)).then_inc(w_in[b], 16)
                        sp.dma_start(b1[:, b, :], x.b1[ds(e * 128, 128), :]).then_inc(w_in[b], 16)
                        if FM:
                            sp.dma_start(wm[:, b, :, :], x.wm[ds(e, 1)].rearrange("e (c p) f -> p (e c) f", p=128)).then_inc(w_in[b], 16)
                            sp.dma_start(bm[:, b, :], x.bm[ds(e * 128, 128), :]).then_inc(w_in[b], 16)
                        sp.dma_start(w2[:, b, :, :], x.w2[ds(e, 1)].rearrange("e (c p) f -> p (e c) f", p=128)).then_inc(w_in[b], 16)
                        sp.dma_start(b2[:, b, :], x.b2[ds(e * D, D)].partition_broadcast(P)).then_inc(w_in[b], 16)

            @block.tensor
            def _(pe):
                pe.sem_inc(t_mm, 2)

                def turn(buf, c, i):
                    pe.wait_ge(rows_in[buf], i)
                    pe.wait_ge(t_ev, c + 1)
                    for t in range(TB):
                        for half in range(2):
                            ins = nc.tensor.transpose(ps_t[:, buf, half * BR + t * P:half * BR + (t + 1) * P], rows[:, buf, t, half * 128:(half + 1) * 128], k.ident[0:P, 0:P])
                    ins.then_inc(t_mm, 1)

                def layer(n0, lhs, rhs, count, chunks):
                    for f in range(count):
                        pe.wait_ge(h_sb, n0 + f + 1)
                        for c in range(chunks):
                            ins = nc.tensor.matmul(ps_h[:, f % 4, 0:BR], lhs(c, f), rhs(c), start=c == 0, stop=c == chunks - 1)
                        ins.then_inc(h_mm, 1)

                turn(0, 0, 16)
                with pe.Fori(0, blocks // 2) as i:
                    for b in range(2):
                        n = i * 2 + b
                        pe.wait_ge(w_in[b], 16 * SEMS * (i + 1))
                        pe.wait_ge(t_ev, n + 3)
                        layer(n * EV, lambda c, f: w1[:, b, c, f * 128:(f + 1) * 128], lambda c: xT[:, b, c, :], FC, 2)
                        turn(1 - b, n + 1, 16 * i + 16 * (b + 1))
                        last, n_last = hid, FC
                        if FM:
                            pe.wait_ge(h_sb, n * EV + FC + 4)
                            layer(n * EV + FC, lambda c, f: wm[:, b, c, f * 128:(f + 1) * 128], lambda c: hid[:, c, :], FM, FC)
                            last, n_last = mid, FM
                        pe.wait_ge(h_sb, n * EV + EV + 4)
                        for t in range(TB):
                            pe.wait_ge(o_done, 2 * n + t + 3)
                            for c in range(n_last):
                                ins = nc.tensor.matmul(ps_o[:, t, 0:D], last[:, c, t * P:(t + 1) * P], w2[:, b, c, :], start=c == 0, stop=c == n_last - 1)
                            ins.then_inc(o_mm, 1)

            @block.scalar
            def _(act):
                act.sem_inc(h_sb, 4)
                with act.Fori(0, blocks // 2) as i:
                    for b in range(2):
                        n = i * 2 + b
                        act.wait_ge(w_in[b], 16 * SEMS * (i + 1))
                        for f in range(EV):
                            act.wait_ge(h_mm, n * EV + f + 1)
                            if f < FC:
                                ins = nc.scalar.activation(hid[:, f, :], ps_h[:, f % 4, 0:BR], x.func, bias=b1[:, b, f:f + 1])
                            else:
                                ins = nc.scalar.activation(mid[:, f - FC, :], ps_h[:, (f - FC) % 4, 0:BR], x.func, bias=bm[:, b, f - FC:f - FC + 1])
                            ins.then_inc(h_sb, 1)

            @block.vector
            def _(dve):
                dve.sem_inc(t_ev, 2)
                dve.sem_inc(o_done, 4)
                nc.vector.memset(zero[:], 0.0).then_inc(made, 1)

                def columns(buf, c):
                    dve.wait_ge(t_mm, c + 3)
                    nc.vector.tensor_copy(xT[:, buf, :, :], ps_t[:, buf, 0:2 * BR].rearrange("p (c n) -> p c n", c=2)).then_inc(t_ev, 1)

                columns(0, 0)
                with dve.Fori(0, blocks // 2) as i:
                    for b in range(2):
                        n = i * 2 + b
                        columns(1 - b, n + 1)
                        dve.wait_ge(w_in[b], 16 * SEMS * (i + 1))
                        dve.wait_ge(stored[b], 16 * (i + 1))
                        for t in range(TB):
                            dve.wait_ge(o_mm, 2 * n + t + 1)
                            nc.vector.tensor_tensor(y[:, b, t, :], ps_o[:, t, 0:D], b2[:, b, :], ALU.add).then_inc(o_done, 1)

            @block.gpsimd
            def _(pool):
                pool.wait_ge(made, 1)
                for b in range(2):
                    pool.dma_start(result[blocks * BR + b * P:blocks * BR + (b + 1) * P, :], zero[:]).then_inc(stored[b], 16)
                with pool.Fori(0, blocks // 2) as i:
                    for b in range(2):
                        n = i * 2 + b
                        pool.wait_ge(o_done, 2 * n + 6)
                        pool.sem_inc(turns, 1)
                        pool.dma_start(result[ds(n * BR, BR), :].rearrange("(t p) f -> p t f", p=P), y[:, b, :, :]).then_inc(stored[b], 16)
                for b in range(2):
                    pool.wait_ge(stored[b], 16 * (blocks // 2 + 1))


class Experts:

    def __init__(self, n, f, func, w1, b1, w2, b2, wm=None, bm=None):
        self.n, self.f, self.func, self.w1, self.b1, self.w2, self.b2, self.wm, self.bm = n, f, func, w1, b1, w2, b2, wm, bm


def experts(k, cols, gate, acc, x):
    nc = k.nc
    FC = x.f // 128
    FM = 2 if x.wm is not None else 0
    NB, TB = NT // 5, 5
    PARTS = ((0, 3 * P), (3 * P, 2 * P))
    UP, MID = 2 * FC, 2 * FM
    EV = UP + MID
    BU = 2 if x.n % 2 == 0 else 1
    with stage(k) as s:
        w1 = s.sb("w1", [128, 2, 2, x.f])
        w2 = s.sb("w2", [128, 2, FM or FC, D])
        b1 = s.sb("b1", [128, 2, FC])
        b2 = s.sb("b2", [P, 2, D])
        hid = s.sb("hid", [128, FC, TB * P])
        tmp = s.sb("tmp", [P, TB, D])
        ps_h = s.ps("ps_h", [128, 4, 512])
        ps_o = s.ps("ps_o", [P, 3, 512])
        if FM:
            wm, bm = s.sb("wm", [128, 2, 2, D]), s.sb("bm", [128, 2, FM])
            mid = s.sb("mid", [128, FM, TB * P])
        zeroed, h_mm, h_sb, o_mm, o_used, chain = (s.sem(n) for n in ("zeroed", "h_mm", "h_sb", "o_mm", "o_used", "chain"))
        w_in = [s.sem("w_in0"), s.sem("w_in1")]
        n_w = 6 if FM else 4
        pair_end = lambda j: min(j | 1, TB - 1)
        out_at = lambda j: ps_o[:, j // 2, (j % 2) * D:(j % 2 + 1) * D]
        with s.block() as block:
            @block.sync
            def _(sp):
                with sp.Fori(0, x.n // BU) as i:
                    for b in range(BU):
                        e = i * BU + b
                        sp.wait_ge(o_used, e * NT + TB)
                        sp.dma_start(w1[:, b, :, :], x.w1[ds(e, 1)].rearrange("e (c p) f -> p (e c) f", p=128)).then_inc(w_in[b], 16)
                        if FM:
                            sp.dma_start(wm[:, b, :, :], x.wm[ds(e, 1)].rearrange("e (c p) f -> p (e c) f", p=128)).then_inc(w_in[b], 16)
                        sp.dma_start(b1[:, b, :], x.b1[ds(e * 128, 128), :]).then_inc(w_in[b], 16)
                        if FM:
                            sp.dma_start(bm[:, b, :], x.bm[ds(e * 128, 128), :]).then_inc(w_in[b], 16)
                        sp.dma_start(w2[:, b, :, :], x.w2[ds(e, 1)].rearrange("e (c p) f -> p (e c) f", p=128)).then_inc(w_in[b], 16)
                        sp.dma_start(b2[:, b, :], x.b2[ds(e * D, D)].partition_broadcast(P)).then_inc(w_in[b], 16)

            @block.tensor
            def _(pe):
                def layer(nq, lhs, rhs, count, chunks_in):
                    n = 0
                    for f in range(count):
                        for q, (lo, m) in enumerate(PARTS):
                            pe.wait_ge(h_sb, nq + n + 1)
                            for c in range(chunks_in):
                                ins = nc.tensor.matmul(ps_h[:, n % 4, 0:m], lhs(c, f), rhs(c, lo, m), start=c == 0, stop=c == chunks_in - 1)
                            ins.then_inc(h_mm, 1)
                            n += 1

                with pe.Fori(0, x.n // BU) as i:
                    for b in range(BU):
                        e = i * BU + b
                        with pe.Fori(0, NB) as blk:
                            pe.wait_ge(w_in[b], 16 * n_w * (i + 1))
                            turn = e * NB + blk
                            layer(turn * EV, lambda c, f: w1[:, b, c, f * 128:(f + 1) * 128],
                                  lambda c, lo, m: cols[:, c, ds(blk * (TB * P) + lo, m)], FC, 2)
                            last, n_last = hid, FC
                            if FM:
                                pe.wait_ge(h_sb, turn * EV + UP + 4)
                                layer(turn * EV + UP, lambda c, f: wm[:, b, c, f * 128:(f + 1) * 128],
                                      lambda c, lo, m: hid[:, c, lo:lo + m], FM, FC)
                                last, n_last = mid, FM
                            pe.wait_ge(h_sb, turn * EV + EV + 4)
                            for j in range(TB):
                                pe.wait_ge(o_used, turn * TB + pair_end(j) + 1 + NT)
                                for c in range(n_last):
                                    ins = nc.tensor.matmul(out_at(j), last[:, c, j * P:(j + 1) * P], w2[:, b, c, :], start=c == 0, stop=c == n_last - 1)
                                ins.then_inc(o_mm, 1)

            @block.scalar
            def _(act):
                act.sem_inc(h_sb, 4)
                with act.Fori(0, x.n // BU) as i:
                    for b in range(BU):
                        e = i * BU + b
                        with act.Fori(0, NB) as blk:
                            act.wait_ge(w_in[b], 16 * n_w * (i + 1))
                            turn = e * NB + blk
                            n = 0
                            for f in range(FC):
                                for lo, m in PARTS:
                                    act.wait_ge(h_mm, turn * EV + n + 1)
                                    nc.scalar.activation(hid[:, f, lo:lo + m], ps_h[:, n % 4, 0:m], x.func, bias=b1[:, b, f:f + 1]).then_inc(h_sb, 1)
                                    n += 1
                            for f in range(FM):
                                for lo, m in PARTS:
                                    act.wait_ge(h_mm, turn * EV + n + 1)
                                    nc.scalar.activation(mid[:, f, lo:lo + m], ps_h[:, n % 4, 0:m], x.func, bias=bm[:, b, f:f + 1]).then_inc(h_sb, 1)
                                    n += 1

            @block.vector
            def _(dve):
                nc.vector.memset(acc[:], 0.0).then_inc(chain, 1)
                dve.sem_inc(o_used, NT + TB)
                with dve.Fori(0, x.n // BU) as i:
                    for b in range(BU):
                        e = i * BU + b
                        with dve.Fori(0, NB) as blk:
                            dve.wait_ge(w_in[b], 16 * n_w * (i + 1))
                            for j in range(TB):
                                t = blk * TB + j
                                n = e * NT + t
                                dve.wait_ge(o_mm, e * NT + blk * TB + pair_end(j) + 1)
                                nc.vector.tensor_tensor(tmp[:, j, :], out_at(j), b2[:, b, :], ALU.add).then_inc(o_used, 1)
                                dve.wait_ge(o_used, n + 1 + NT + TB)
                                nc.vector.scalar_tensor_tensor(acc[:, ds(t, 1), :].rearrange("p t f -> p (t f)"), tmp[:, j, :], gate[:, ds(t, 1), ds(e, 1)].rearrange("p t e -> p (t e)"),
                                                               acc[:, ds(t, 1), :].rearrange("p t f -> p (t f)"), ALU.mult, ALU.add).then_inc(chain, 1)


def finish_norm(k, v, add=None, gamma=None, beta=None, to_x=True, width=D):
    nc = k.nc
    with stage(k) as s:
        stats = s.sb("stats", [P, NT, 6])
        mv = s.sb("mv", [P, NT, 2])
        veps, rstd = s.sb("veps", [P, NT]), s.sb("rstd", [P, NT])
        g_sb, b_sb = s.sb("gamma", [P, width]), s.sb("beta", [P, width])
        g_in, chain, var, sd = (s.sem(n) for n in ("g_in", "chain", "var", "sd"))
        wide = lambda a: a.unsqueeze(1).to_broadcast([P, NT, width])
        with s.block() as block:
            @block.sync
            def _(sp):
                sp.dma_start(g_sb[:], gamma.partition_broadcast(P)).then_inc(g_in, 16)
                sp.dma_start(b_sb[:], beta.partition_broadcast(P)).then_inc(g_in, 16)

            @block.scalar
            def _(act):
                act.wait_ge(var, 1)
                nc.scalar.activation(veps[:], veps[:], ACT.Sqrt).then_inc(sd, 1)

            @block.vector
            def _(dve):
                c = Chain(dve, chain)
                if add is not None:
                    c.link(nc.vector.tensor_tensor(v[:], v[:], add[:], ALU.add))
                for t in range(NT):
                    c.step(nc.vector.bn_stats(stats[:, t, :], v[:, t, :]))
                c.wait()
                for t in range(NT):
                    c.step(nc.vector.bn_aggr(mv[:, t, :], stats[:, t, :]))
                c.wait()
                nc.vector.tensor_scalar(veps[:], mv[:, :, 1], EPS, None, ALU.add).then_inc(var, 1)
                dve.wait_ge(sd, 1)
                c.link(nc.vector.reciprocal(rstd[:], veps[:]))
                for t in range(NT):
                    c.step(nc.vector.tensor_scalar(v[:, t, :], v[:, t, :], mv[:, t, 0:1], rstd[:, t:t + 1], ALU.subtract, ALU.mult))
                c.wait()
                dve.wait_ge(g_in, 32)
                c.link(nc.vector.tensor_tensor(v[:], v[:], wide(g_sb[:]), ALU.mult))
                c.link(nc.vector.tensor_tensor(v[:], v[:], wide(b_sb[:]), ALU.add))
                if to_x:
                    c.link(nc.vector.tensor_tensor(k.x[:], k.x[:], v[:], ALU.add))


def transfer(k, out, in_):
    with stage(k) as s:
        moved = s.sem("moved")
        with s.block() as block:
            @block.sync
            def _(sp):
                sp.dma_start(out, in_).then_inc(moved, 16)
                sp.wait_ge(moved, 16)


def turn_all(k, rows, cols):
    nc = k.nc
    with stage(k) as s:
        ps = s.ps("turned", [128, 4, 512])
        turned, copied = s.sem("turned"), s.sem("copied")
        with s.block() as block:
            @block.tensor
            def _(pe):
                for t in range(NT):
                    if t >= 4:
                        pe.wait_ge(copied, t - 3)
                    nc.tensor.transpose(ps[:, t % 4, 0:P], rows[:, t, 0:128], k.ident[0:P, 0:P])
                    nc.tensor.transpose(ps[:, t % 4, P:2 * P], rows[:, t, 128:256], k.ident[0:P, 0:P]).then_inc(turned, 1)

            @block.scalar
            def _(act):
                for t in range(NT):
                    act.wait_ge(turned, t + 1)
                    nc.scalar.activation(cols[:, :, t * P:(t + 1) * P],
                                         ps[:, t % 4, 0:2 * P].rearrange("p (c n) -> p c n", c=2), ACT.Copy).then_inc(copied, 1)


def project(k, cols, w, width, rows=None, table=None):
    nc = k.nc
    with stage(k) as s:
        w_sb = s.sb("w", [128, 2, width])
        row = s.sb("row", [P, 5, width]) if rows is None else rows
        at = (lambda t: row[:, t % 5, :]) if rows is None else (lambda t: row[:, t, :])
        ps = s.ps("ps", [P, 4, 512])
        w_in, mm, evac = s.sem("w_in"), s.sem("mm"), s.sem("evac")
        stored = [s.sem(f"stored{j}") for j in range(5)]
        with s.block() as block:
            @block.sync
            def _(sp):
                sp.dma_start(w_sb[:], w.rearrange("(c p) f -> p c f", p=128)).then_inc(w_in, 16)
                if table is not None:
                    for t in range(NT):
                        sp.wait_ge(evac, t + 1)
                        sp.dma_start(table[t * P:(t + 1) * P, 0:width], at(t)).then_inc(stored[t % 5], 16)
                    for j in range(5):
                        sp.wait_ge(stored[j], 16 * (NT // 5))

            @block.tensor
            def _(pe):
                pe.wait_ge(w_in, 16)
                for t in range(NT):
                    if t >= 4:
                        pe.wait_ge(evac, t - 3)
                    nc.tensor.matmul(ps[:, t % 4, 0:width], cols[:, 0, t * P:(t + 1) * P], w_sb[:, 0, :], start=True, stop=False)
                    nc.tensor.matmul(ps[:, t % 4, 0:width], cols[:, 1, t * P:(t + 1) * P], w_sb[:, 1, :], start=False, stop=True).then_inc(mm, 1)

            @block.scalar
            def _(act):
                for t in range(NT):
                    if rows is None and t >= 5:
                        act.wait_ge(stored[t % 5], 16 * (t // 5))
                    act.wait_ge(mm, t + 1)
                    nc.scalar.activation(at(t), ps[:, t % 4, 0:width], ACT.Copy).then_inc(evac, 1)


def scores(k, rows, width, heads, a_src, a_tgt, src_out, tgt, top_all):
    nc = k.nc
    with stage(k) as s:
        a_sb = s.sb("a", [P, 2, width])
        prod = s.sb("prod", [P, 2, 2, width])
        s_src = s.sb("s_src", [P, NT, heads])
        top = s.sb("top", [P, heads])
        a_in, chain, topped, out = (s.sem(n) for n in ("a_in", "chain", "topped", "out"))
        with s.block() as block:
            @block.sync
            def _(sp):
                sp.dma_start(a_sb[:, 0, :], a_src.partition_broadcast(P)).then_inc(a_in, 16)
                sp.dma_start(a_sb[:, 1, :], a_tgt.partition_broadcast(P)).then_inc(a_in, 16)
                sp.wait_ge(topped, 1)
                with nc.allow_non_contiguous_dma(reason="a few numbers a node"):
                    sp.dma_start(src_out, s_src[:]).then_inc(out, 16)
                sp.wait_ge(out, 16)

            @block.gpsimd
            def _(pool):
                pool.wait_ge(topped, 1)
                nc.gpsimd.partition_all_reduce(top_all[:], top[:], P, RMAX)

            @block.vector
            def _(dve):
                c = Chain(dve, chain)
                dve.wait_ge(a_in, 32)
                for t in range(NT):
                    r = rows[:, t, :].unsqueeze(1).to_broadcast([P, 2, width])
                    c.link(nc.vector.tensor_tensor(prod[:, t % 2, :, :], r, a_sb[:], ALU.mult))
                    c.step(nc.vector.tensor_reduce(s_src[:, t, :], prod[:, t % 2, 0, :].rearrange("p (h d) -> p h d", h=heads), AX_X, ALU.add))
                    c.step(nc.vector.tensor_reduce(tgt[:, :, t], prod[:, t % 2, 1, :].rearrange("p (h d) -> p h d", h=heads), AX_X, ALU.add))
                c.wait()
                nc.vector.tensor_reduce(top[:], s_src[:].rearrange("p t h -> p h t"), AX_X, ALU.max).then_inc(topped, 1)


def divide(k, agg, out, heads, eps, add=None, bias=None, width=D):
    nc = k.nc
    HD = width // heads
    with stage(k) as s:
        den, none = s.sb("den", [P, NT, heads]), s.sb("none", [P, NT, heads])
        b_sb = s.sb("bias", [P, width])
        low = s.sb("low", [P, NT, width]) if add is not None else None
        b_in, chain, lows, exps = (s.sem(n) for n in ("b_in", "chain", "lows", "exps"))
        with s.block() as block:
            @block.sync
            def _(sp):
                if bias is not None:
                    sp.dma_start(b_sb[:], bias.partition_broadcast(P)).then_inc(b_in, 16)

            @block.vector
            def _(dve):
                c = Chain(dve, chain)
                d = agg[:, :, width:width + heads]
                if eps:
                    c.link(nc.vector.tensor_scalar(den[:], d, eps, None, ALU.add))
                else:
                    c.link(nc.vector.tensor_scalar(none[:], d, 0.0, None, ALU.is_equal))
                    c.link(nc.vector.tensor_tensor(den[:], d, none[:], ALU.add))
                c.link(nc.vector.reciprocal(none[:], den[:]))
                for t in range(NT):
                    c.step(nc.vector.tensor_tensor(out[:, t, :].rearrange("p (h d) -> p h d", h=heads), agg[:, t, 0:width].rearrange("p (h d) -> p h d", h=heads),
                                                   none[:, t, :].unsqueeze(2).to_broadcast([P, heads, HD]), ALU.mult))
                c.wait()
                if add is not None:
                    c.link(nc.vector.tensor_tensor(out[:], out[:], add[:], ALU.add))
                if bias is not None:
                    dve.wait_ge(b_in, 16)
                    c.link(nc.vector.tensor_tensor(out[:], out[:], b_sb[:].unsqueeze(1).to_broadcast([P, NT, width]), ALU.add))
                if add is not None:
                    nc.vector.tensor_scalar(low[:], out[:], 0.0, None, ALU.min).then_inc(lows, 1)
                    c.link(nc.vector.tensor_scalar(out[:], out[:], 0.0, -1.0, ALU.max, ALU.add))
                    dve.wait_ge(exps, 1)
                    c.link(nc.vector.tensor_tensor(out[:], out[:], low[:], ALU.add))

            @block.scalar
            def _(act):
                if add is not None:
                    act.wait_ge(lows, 1)
                    nc.scalar.activation(low[:], low[:], ACT.Exp).then_inc(exps, 1)


def sort_nodes(k, rank_i, noise):
    nc = k.nc
    U = 8
    BF = mybir.dt.bfloat16
    with stage(k) as s:
        tile_of, lo = s.sb("tile_of", [P, ET]), s.sb("lo", [P, ET])
        srcf = s.sb("srcf", [P, ET])
        r125, r25 = s.sb("r125", [P, P]), s.sb("r25", [P, NT])
        oh_lo, oh_hi = s.sb("oh_lo", [P, U, P], BF), s.sb("oh_hi", [P, U, NT], BF)
        zero = s.sb("zero", [P, P], BF)
        before = s.sb("before", [P, P])
        noise_sb, key = s.sb("noise", [P, NT]), s.sb("key", [P, NT])
        keys = s.sb("keys", [P, N])
        junk = s.sb("junk", [P, N])
        parts = s.sb("parts", [P, 3, NT])
        rank = s.sb("rank", [P, NT])
        ps = s.ps("ps", [P, 512])
        in_, made, chain, hot, mm, keyed, out, back = (s.sem(n) for n in ("in", "made", "chain", "hot", "mm", "keyed", "out", "back"))
        with s.block() as block:
            @block.sync
            def _(sp):
                with nc.allow_non_contiguous_dma(reason="one number a node"):
                    sp.dma_start(noise_sb[:], noise.rearrange("(t p) -> p t", p=P)).then_inc(in_, 16)
                    sp.wait_ge(keyed, 1)
                    sp.dma_start(k.keys_d.rearrange("(t p) -> p t", p=P), key[:]).then_inc(out, 16)
                sp.wait_ge(out, 16)
                sp.dma_start(keys[:], k.keys_d.partition_broadcast(P)).then_inc(back, 16)

            @block.gpsimd
            def _(pool):
                nc.gpsimd.iota(r125[:], [[1, P]], base=0, channel_multiplier=0, allow_small_or_imprecise_dtypes=True).then_inc(made, 1)
                nc.gpsimd.iota(r25[:], [[1, NT]], base=0, channel_multiplier=0, allow_small_or_imprecise_dtypes=True).then_inc(made, 1)
                nc.gpsimd.memset(zero[:], 0.0).then_inc(made, 1)
                nc.gpsimd.memset(before[:], 1.0).then_inc(made, 1)
                pool.wait_ge(made, 4)
                nc.gpsimd.affine_select(out=before[:], in_=before[:], compare_op=ALU.is_gt, fill=0.0, base=0,
                                        pattern=[[-1, P]], channel_multiplier=1).then_inc(made, 1)

            @block.tensor
            def _(pe):
                pe.sem_inc(mm, U)
                pe.wait_ge(made, 5)
                nc.tensor.matmul(ps[:, 0:NT], zero[:], zero[:, 0:NT], start=True, stop=False)
                with pe.Fori(0, ET // U) as i:
                    for j in range(U):
                        pe.wait_ge(hot, i * U + j + 1)
                        nc.tensor.matmul(ps[:, 0:NT], oh_lo[:, j, :], oh_hi[:, j, :], start=False, stop=False).then_inc(mm, 1)
                nc.tensor.matmul(ps[:, 0:NT], zero[:], zero[:, 0:NT], start=False, stop=True).then_inc(mm, 1)

            @block.vector
            def _(dve):
                c = Chain(dve, chain)
                c.step(nc.vector.tensor_copy(srcf[:], k.src_i[:, 0:ET]))
                c.link(nc.vector.memset(tile_of[:], 0.0))
                for t in range(1, NT):
                    c.link(nc.vector.scalar_tensor_tensor(tile_of[:], srcf[:], float(P * t), tile_of[:], ALU.is_ge, ALU.add))
                c.link(nc.vector.tensor_scalar(lo[:], tile_of[:], float(-P), None, ALU.mult))
                c.link(nc.vector.tensor_tensor(lo[:], lo[:], srcf[:], ALU.add))
                dve.wait_ge(made, 5)
                with dve.Fori(0, ET // U) as i:
                    for j in range(U):
                        t = i * U + j
                        dve.wait_ge(mm, t + 1)
                        nc.vector.tensor_scalar(oh_lo[:, j, :], r125[:], lo[:, ds(t, 1)], None, ALU.is_equal)
                        nc.vector.tensor_scalar(oh_hi[:, j, :], r25[:], tile_of[:, ds(t, 1)], None, ALU.is_equal).then_inc(hot, 1)
                dve.wait_ge(mm, U + ET + 1)
                dve.wait_ge(in_, 16)
                c.link(nc.vector.tensor_tensor(key[:], ps[:, 0:NT], noise_sb[:], ALU.add))
                dve.sem_inc(keyed, 1)
                dve.wait_ge(back, 16)
                c.link(nc.vector.memset(parts[:], 0.0))
                for t in range(NT):
                    me = key[:, t:t + 1]
                    if t:
                        c.link(nc.vector.tensor_scalar(junk[:, 0:t * P], keys[:, 0:t * P], me, None, ALU.is_le, ALU.add, accum_out=parts[:, 0, t:t + 1]))
                    c.link(nc.vector.tensor_scalar(junk[:, t * P:N], keys[:, t * P:N], me, None, ALU.is_lt, ALU.add, accum_out=parts[:, 1, t:t + 1]))
                    c.link(nc.vector.scalar_tensor_tensor(junk[:, 0:P], keys[:, t * P:(t + 1) * P], me, before[:], ALU.is_equal, ALU.mult,
                                                          accum_out=parts[:, 2, t:t + 1]))
                c.link(nc.vector.tensor_tensor(rank[:], parts[:, 0, :], parts[:, 1, :], ALU.add))
                c.link(nc.vector.tensor_tensor(rank[:], rank[:], parts[:, 2, :], ALU.add))
                c.link(nc.vector.tensor_copy(rank_i[:], rank[:]))


def permute(k, rows, dram, rank_i, scatter):
    nc = k.nc
    with stage(k) as s:
        moved = s.sem("moved")
        with s.block() as block:
            @block.gpsimd
            def _(pool):
                for t in range(NT):
                    at = bass.IndirectOffsetOnAxis(rank_i[:, t:t + 1], 0)
                    if scatter:
                        nc.gpsimd.indirect_dma_start(dram, at, rows[:, t, :], None).then_inc(moved, 16)
                    else:
                        nc.gpsimd.indirect_dma_start(rows[:, t, :], None, dram, at).then_inc(moved, 16)
                pool.wait_ge(moved, 16 * NT)


def mamba_inputs(k, cols, xc, z, dbc, w_in, conv_w, conv_b, x_proj):
    nc = k.nc
    KW = 4
    BLK = [(n0, min(500, N - n0)) for n0 in range(0, N, 500)]
    NBK = len(BLK)
    with stage(k) as s:
        w = s.sb("w", [128, 2, 2 * D])
        cw, cb = s.sb("cw", [128, 2, KW]), s.sb("cb", [128, 2])
        xp = s.sb("xp", [128, 2, N + KW - 1])
        wx = s.sb("wx", [128, 2, 48])
        ps = s.ps("ps", [128, 4, 512])
        ps_d = s.ps("ps_d", [48, 2, 512])
        loaded, mm, evac, chain, convd, acted, dmm, dev = (s.sem(n) for n in ("loaded", "mm", "evac", "chain", "convd", "acted", "dmm", "dev"))
        with s.block() as block:
            @block.sync
            def _(sp):
                sp.dma_start(w[:], w_in.rearrange("(c p) f -> p c f", p=128)).then_inc(loaded, 16)
                sp.dma_start(cw[:], conv_w.rearrange("(c p) f -> p c f", p=128)).then_inc(loaded, 16)
                with nc.allow_non_contiguous_dma(reason="one number a channel"):
                    sp.dma_start(cb[:], conv_b.rearrange("(c p) -> p c", p=128)).then_inc(loaded, 16)
                sp.dma_start(wx[:], x_proj.rearrange("(c p) f -> p c f", p=128)).then_inc(loaded, 16)

            @block.tensor
            def _(pe):
                pe.wait_ge(loaded, 64)
                n = 0
                for o in range(4):
                    for n0, m in BLK:
                        if n >= 4:
                            pe.wait_ge(evac, n - 3)
                        for c in range(2):
                            ins = nc.tensor.matmul(ps[:, n % 4, 0:m], w[:, c, o * 128:(o + 1) * 128], cols[:, c, n0:n0 + m], start=c == 0, stop=c == 1)
                        ins.then_inc(mm, 1)
                        n += 1
                pe.wait_ge(acted, 2)
                for q, (n0, m) in enumerate(BLK):
                    if q >= 2:
                        pe.wait_ge(dev, q - 1)
                    for c in range(2):
                        ins = nc.tensor.matmul(ps_d[:, q % 2, 0:m], wx[:, c, :], xc[:, c, n0:n0 + m], start=c == 0, stop=c == 1)
                    ins.then_inc(dmm, 1)

            @block.scalar
            def _(act):
                n = 0
                for o in range(4):
                    for n0, m in BLK:
                        act.wait_ge(mm, n + 1)
                        if o < 2:
                            ins = nc.scalar.activation(xp[:, o, KW - 1 + n0:KW - 1 + n0 + m], ps[:, n % 4, 0:m], ACT.Copy)
                        else:
                            ins = nc.scalar.activation(z[:, o - 2, n0:n0 + m], ps[:, n % 4, 0:m], ACT.Silu)
                        ins.then_inc(evac, 1)
                        n += 1
                for c in range(2):
                    act.wait_ge(convd, c + 1)
                    nc.scalar.activation(xc[:, c, :], xc[:, c, :], ACT.Silu, bias=cb[:, c:c + 1]).then_inc(acted, 1)
                for q, (n0, m) in enumerate(BLK):
                    act.wait_ge(dmm, q + 1)
                    nc.scalar.activation(dbc[:, n0:n0 + m], ps_d[:, q % 2, 0:m], ACT.Copy).then_inc(dev, 1)

            @block.vector
            def _(dve):
                c = Chain(dve, chain)
                c.link(nc.vector.memset(xp[:, :, 0:KW - 1], 0.0))
                dve.wait_ge(loaded, 64)
                for h in range(2):
                    dve.wait_ge(evac, (h + 1) * NBK)
                    c.link(nc.vector.tensor_scalar(xc[:, h, :], xp[:, h, 0:N], cw[:, h, 0:1], None, ALU.mult))
                    for q in range(1, KW):
                        ins = nc.vector.scalar_tensor_tensor(xc[:, h, :], xp[:, h, q:q + N], cw[:, h, q:q + 1], xc[:, h, :], ALU.mult, ALU.add)
                        if q < KW - 1:
                            c.link(ins)
                    ins.then_inc(convd, 1)


def selective_scan(k, h, xc, z, dbc, dt_w, dt_b, a_log, d_param):
    nc = k.nc
    SN, R, CH, NC = 16, 16, 625, 5
    BLK = [(n0, min(500, N - n0)) for n0 in range(0, N, 500)]
    CUT = [(0, 512), (512, CH - 512)]
    with stage(k) as s:
        dt, u, y, poly = (s.sb(n, [128, N]) for n in ("dt", "u", "y", "poly"))
        w48, dtb, dp = s.sb("w48", [48, D]), s.sb("dtb", [128, 1]), s.sb("dp", [128, 1])
        al, A = s.sb("al", [128, SN]), s.sb("A", [128, SN + 1])
        a_s = s.sb("a_s", [128, 2])
        sel = s.sb("sel", [48, 2, 2, 128])
        dA, dB, hh, hc = (s.sb(n, [128, 2, CH]) for n in ("dA", "dB", "hh", "hc"))
        ps = s.ps("ps", [128, 2, 2, 1024])
        loaded, made, mm, dts, chain, exps, prods, adds, sels, bcs = (
            s.sem(n) for n in ("loaded", "made", "mm", "dts", "chain", "exps", "prods", "adds", "sels", "bcs"))
        dt_done = s.sem("dt_done")
        with s.block() as block:
            @block.sync
            def _(sp):
                sp.wait_ge(made, 1)
                sp.dma_start(w48[0:R, :], dt_w).then_inc(loaded, 16)
                hs = slice(h * 128, (h + 1) * 128)
                sp.dma_start(dtb[:], dt_b[hs].rearrange("(p a) -> p a", a=1)).then_inc(loaded, 16)
                sp.dma_start(dp[:], d_param[hs].rearrange("(p a) -> p a", a=1)).then_inc(loaded, 16)
                sp.dma_start(al[:], a_log[hs, :]).then_inc(loaded, 16)

            @block.gpsimd
            def _(pool):
                nc.gpsimd.memset(w48[:], 0.0).then_inc(made, 1)
                pool.sem_inc(adds, 2)
                with pool.Fori(0, SN // 2) as i:
                    for q in range(2 * NC):
                        n, b, c = i * (2 * NC) + q, q % 2, q % NC
                        pool.wait_ge(prods, n + 3)
                        ycut = y[:, c * CH:(c + 1) * CH]
                        nc.gpsimd.tensor_tensor(ycut, ycut, hc[:, b, :], ALU.add).then_inc(adds, 1)

            @block.tensor
            def _(pe):
                pe.wait_ge(loaded, 64)
                for q, (n0, m) in enumerate(BLK):
                    if q >= 4:
                        pe.wait_ge(dts, q - 3)
                    nc.tensor.matmul(ps[:, q % 4 // 2, q % 2, 0:m], w48[:, h * 128:(h + 1) * 128], dbc[:, n0:n0 + m], start=True, stop=True).then_inc(mm, 1)
                pe.wait_ge(dts, len(BLK))
                with pe.Fori(0, SN // 2) as i:
                    for q in range(2 * NC):
                        n, b, c = i * (2 * NC) + q, q % 2, q % NC
                        pe.wait_ge(sels, i * 2 + q // NC + 1)
                        pe.wait_ge(prods, n + 1)
                        for v in range(2):
                            for lo, m in CUT:
                                ins = nc.tensor.matmul(ps[:, b, v, lo:lo + m], sel[:, q // NC, v, :], dbc[:, c * CH + lo:c * CH + lo + m], start=True, stop=True)
                        ins.then_inc(bcs, 1)

            @block.scalar
            def _(act):
                act.wait_ge(loaded, 64)
                nc.scalar.activation(A[:, 0:SN], al[:], ACT.Exp).then_inc(exps, 1)
                for q, (n0, m) in enumerate(BLK):
                    act.wait_ge(mm, q + 1)
                    nc.scalar.activation(dt[:, n0:n0 + m], ps[:, q % 4 // 2, q % 2, 0:m], ACT.Identity, bias=dtb[:]).then_inc(dts, 1)
                act.wait_ge(dts, len(BLK))
                nc.scalar.activation(u[:], dt[:], ACT.Abs).then_inc(dts, 1)
                act.wait_ge(dts, len(BLK) + 1)
                nc.scalar.activation(u[:], u[:], ACT.Exp, scale=-1.0).then_inc(dts, 1)
                act.wait_ge(dt_done, 1)
                with act.Fori(0, SN // 2) as i:
                    for q in range(2 * NC):
                        n, b, c = i * (2 * NC) + q, q % 2, q % NC
                        act.wait_ge(sels, i * 2 + q // NC + 1)
                        act.wait_ge(prods, n + 1)
                        nc.scalar.activation(dA[:, b, :], dt[:, c * CH:(c + 1) * CH], ACT.Exp, scale=a_s[:, q // NC:q // NC + 1]).then_inc(exps, 1)

            @block.vector
            def _(dve):
                c_ = Chain(dve, chain)
                dve.wait_ge(exps, 1)
                c_.step(nc.vector.memset(A[:, SN:SN + 1], 0.0))
                c_.link(nc.vector.tensor_scalar(A[:, 0:SN], A[:, 0:SN], -1.0, None, ALU.mult))
                dve.wait_ge(dts, len(BLK) + 2)
                c_.link(nc.vector.tensor_scalar(y[:], u[:], 2.0, None, ALU.add))
                c_.link(nc.vector.reciprocal(y[:], y[:]))
                c_.link(nc.vector.tensor_tensor(y[:], y[:], u[:], ALU.mult))
                c_.link(nc.vector.tensor_tensor(u[:], y[:], y[:], ALU.mult))
                c_.link(nc.vector.tensor_scalar(poly[:], u[:], 1.0 / 15, None, ALU.mult))
                for odd in (13, 11, 9, 7, 5, 3):
                    c_.link(nc.vector.scalar_tensor_tensor(poly[:], poly[:], 1.0 / odd, u[:], ALU.add, ALU.mult))
                c_.link(nc.vector.scalar_tensor_tensor(poly[:], poly[:], 1.0, y[:], ALU.add, ALU.mult))
                c_.link(nc.vector.tensor_scalar(dt[:], dt[:], 0.0, None, ALU.max))
                c_.link(nc.vector.scalar_tensor_tensor(dt[:], poly[:], 2.0, dt[:], ALU.mult, ALU.add))
                c_.link(nc.vector.memset(y[:], 0.0))
                dve.sem_inc(dt_done, 1)
                c_.link(nc.vector.tensor_tensor(u[:], dt[:], xc[:, h, :], ALU.mult))
                dve.sem_inc(prods, 2)

                def state(st, v):
                    nc.vector.tensor_copy(a_s[:, v:v + 1], A[:, ds(st, 1)])
                    nc.vector.tensor_copy(sel[:, v, 0, :], k.ident[0:48, ds(R + st, 1)].to_broadcast([48, 128]))
                    nc.vector.tensor_copy(sel[:, v, 1, :], k.ident[0:48, ds(R + SN + st, 1)].to_broadcast([48, 128])).then_inc(sels, 1)

                state(0, 0)
                base = c_.n
                with dve.Fori(0, SN // 2) as i:
                    for q in range(2 * NC):
                        n, b, c = i * (2 * NC) + q, q % 2, q % NC
                        if c == 2:
                            state(i * 2 + q // NC + 1, 1 - q // NC)
                        dve.wait_ge(bcs, n + 1)
                        nc.vector.tensor_tensor(dB[:, b, :], ps[:, b, 0, 0:CH], u[:, c * CH:(c + 1) * CH], ALU.mult).then_inc(chain, 1)
                        dve.wait_ge(chain, base + 2 * n + 1)
                        dve.wait_ge(exps, n + 2)
                        nc.vector.tensor_tensor_scan(hh[:, b, :], dA[:, b, :], dB[:, b, :], 0.0 if c == 0 else hh[:, 1 - b, CH - 1:CH],
                                                     ALU.mult, ALU.add).then_inc(chain, 1)
                        dve.wait_ge(chain, base + 2 * n + 2)
                        dve.wait_ge(adds, n + 1)
                        nc.vector.tensor_tensor(hc[:, b, :], ps[:, b, 1, 0:CH], hh[:, b, :], ALU.mult).then_inc(prods, 1)
                        dve.wait_ge(prods, n + 3)
                c_.n = base + 2 * SN * NC
                dve.wait_ge(adds, SN * NC + 2)
                c_.link(nc.vector.scalar_tensor_tensor(y[:], xc[:, h, :], dp[:], y[:], ALU.mult, ALU.add))
                c_.link(nc.vector.tensor_tensor(z[:, h, :], y[:], z[:, h, :], ALU.mult))


def mix(k, a_rows, b_rows, a_cols, b_cols, wa, wb):
    nc = k.nc
    with stage(k) as s:
        w = s.sb("w", [128, 4, D])
        g = s.sb("g", [P, 2, D])
        ps = s.ps("ps", [P, 2, 512])
        w_in, mm, gated, chain = (s.sem(n) for n in ("w_in", "mm", "gated", "chain"))
        with s.block() as block:
            @block.sync
            def _(sp):
                sp.dma_start(w[:, 0:2, :], wa.rearrange("(c p) f -> p c f", p=128)).then_inc(w_in, 16)
                sp.dma_start(w[:, 2:4, :], wb.rearrange("(c p) f -> p c f", p=128)).then_inc(w_in, 16)

            @block.tensor
            def _(pe):
                pe.wait_ge(w_in, 32)
                for t in range(NT):
                    if t >= 2:
                        pe.wait_ge(gated, t - 1)
                    for c in range(4):
                        src = (a_cols, b_cols)[c // 2]
                        ins = nc.tensor.matmul(ps[:, t % 2, 0:D], src[:, c % 2, t * P:(t + 1) * P], w[:, c, :], start=c == 0, stop=c == 3)
                    ins.then_inc(mm, 1)

            @block.scalar
            def _(act):
                for t in range(NT):
                    if t >= 2:
                        act.wait_ge(chain, 3 * (t - 1))
                    act.wait_ge(mm, t + 1)
                    nc.scalar.activation(g[:, t % 2, :], ps[:, t % 2, 0:D], ACT.Sigmoid).then_inc(gated, 1)

            @block.vector
            def _(dve):
                c = Chain(dve, chain)
                for t in range(NT):
                    c.link(nc.vector.tensor_tensor(a_rows[:, t, :], a_rows[:, t, :], b_rows[:, t, :], ALU.subtract))
                    dve.wait_ge(gated, t + 1)
                    c.link(nc.vector.tensor_tensor(a_rows[:, t, :], a_rows[:, t, :], g[:, t % 2, :], ALU.mult))
                    c.link(nc.vector.tensor_tensor(a_rows[:, t, :], a_rows[:, t, :], b_rows[:, t, :], ALU.add))


def small_edge_sums(k, table, tgt, top, agg, src_c, dst_c):
    nc = k.nc
    H, F = 4, 16
    W = F + H
    Q, GT = 128, 256
    with stage(k) as s:
        idx, dsti = s.sb("idx", [Q, GT + G], I32), s.sb("dsti", [Q, GT + G], I32)
        dstf, tile_of, lo = s.sb("dstf", [Q, GT]), s.sb("tile_of", [Q, GT]), s.sb("lo", [Q, GT])
        r125, r25 = s.sb("r125", [Q, P]), s.sb("r25", [Q, NT])
        gi = s.sb("gi", [Q, 2, G], I32)
        msg = s.sb("msg", [Q, 2, G, W])
        HT = H * NT
        lo_rows, pick = s.sb("lo_rows", [P, 2, G * Q]), s.sb("pick", [P, 2, G * Q])
        picked, s_dst = s.sb("picked", [Q, G * H, NT]), s.sb("s_dst", [Q, G, H])
        e1, e2, e = s.sb("e1", [Q, G, 2, H]), s.sb("e2", [Q, G, 2, H]), s.sb("e", [Q, 2, G, H])
        topq, topi = s.sb("topq", [Q, H]), s.sb("topi", [1, H])
        ps_s, ps_q = s.ps("ps_s", [Q, 2, 512]), s.ps("ps_q", [Q, 512])
        row_in = [s.sem("row_in0"), s.sem("row_in1")]
        pick_done, sc_mm, topped = s.sem("pick"), s.sem("sc_mm"), s.sem("topped")
        oh_lo, oh_hi = s.sb("oh_lo", [Q, 2, G, P]), s.sb("oh_hi", [Q, 2, G, NT])
        spread = s.sb("spread", [Q, 2, G, NT * W])
        zero = s.sb("zero", [Q, NT * W])
        own = s.sb("own", [P, NT, W])
        v1, v2 = s.sb("v1", [P, NT, H]), s.sb("v2", [P, NT, H])
        ps = s.ps("ps", [P, 512])
        loaded, made, chain, idx_done, mm, e_done, a_done, ready = (s.sem(n) for n in ("loaded", "made", "chain", "idx", "mm", "e_done", "a_done", "ready"))
        turns, own_e, own_a, scaled = s.sem("turns"), s.sem("own_e"), s.sem("own_a"), s.sem("scaled")
        msg_in = [s.sem("msg_in0"), s.sem("msg_in1")]
        LG = GT // G
        with s.block() as block:
            @block.sync
            def _(sp):
                sp.dma_start(idx[:, 0:GT], src_c).then_inc(loaded, 16)
                sp.dma_start(dsti[:, 0:GT], dst_c).then_inc(loaded, 16)
                sp.dma_start(own[:], table.rearrange("(t p) f -> p t f", p=P)).then_inc(loaded, 16)
                with sp.Fori(0, LG // 2) as i:
                    for b in range(2):
                        sp.wait_ge(pick_done, i * 2 + b + 1)
                        sp.dma_start(lo_rows[:, b, :], k.ffn_lo_r[ds((i * 2 + b) * (G * Q), G * Q)].partition_broadcast(P)).then_inc(row_in[b], 16)

            @block.gpsimd
            def _(pool):
                nc.gpsimd.iota(r125[:], [[1, P]], base=0, channel_multiplier=0, allow_small_or_imprecise_dtypes=True).then_inc(made, 1)
                nc.gpsimd.iota(r25[:], [[1, NT]], base=0, channel_multiplier=0, allow_small_or_imprecise_dtypes=True).then_inc(made, 1)
                nc.gpsimd.memset(zero[:], 0.0).then_inc(made, 1)

                def gather(b, g):
                    pool.wait_ge(idx_done, g + 1)
                    pool.wait_ge(mm, upto(g, G - 1, back=2))
                    pool.sem_inc(turns, 1)
                    for j in range(G):
                        nc.gpsimd.indirect_dma_start(msg[:, b, j, :], None, table, bass.IndirectOffsetOnAxis(gi[:, b, j:j + 1], 0)).then_inc(msg_in[b], 16)

                with pool.Fori(0, LG // 2) as i:
                    gather(0, i * 2)
                    gather(1, i * 2 + 1)

            @block.tensor
            def _(pe):
                pe.sem_inc(mm, 2 * G)
                pe.wait_ge(made, 3)
                nc.tensor.matmul(ps[:, 0:NT * W], zero[:, 0:P], zero[:], start=True, stop=False)
                nc.tensor.matmul(ps_q[:, 0:H], k.ones[0:1, 0:Q], top[0:1, :], start=True, stop=True).then_inc(topped, 1)
                pe.sem_inc(sc_mm, 2)
                with pe.Fori(0, LG // 2) as i:
                    for b in range(2):
                        g = i * 2 + b
                        pe.wait_ge(pick_done, g + 3)
                        pe.wait_ge(e_done, 8 * g + 1)
                        for j in range(G):
                            ins = nc.tensor.matmul(ps_s[:, b, j * HT:(j + 1) * HT], pick[:, b, j * Q:(j + 1) * Q], tgt[:].rearrange("p h t -> p (h t)"), start=True, stop=True)
                        ins.then_inc(sc_mm, 1)
                        for j in range(G):
                            pe.wait_ge(ready, g * G + j + 1)
                            nc.tensor.matmul(ps[:, 0:NT * W], oh_lo[:, b, j, :], spread[:, b, j, :], start=False, stop=False).then_inc(mm, 1)
                nc.tensor.matmul(ps[:, 0:NT * W], zero[:, 0:P], zero[:], start=False, stop=True).then_inc(mm, 1)

            @block.scalar
            def _(act):
                with act.Fori(0, LG // 2) as i:
                    for b in range(2):
                        g = i * 2 + b
                        act.wait_ge(e_done, 8 * g + 8 + 16)
                        nc.scalar.activation(msg[:, b, :, F:W], e[:, b, :, :], ACT.Exp).then_inc(a_done, 1)
                act.wait_ge(own_e, 1)
                nc.scalar.activation(own[:, :, F:W], v1[:], ACT.Exp).then_inc(own_a, 1)

            @block.vector
            def _(dve):
                c = Chain(dve, chain)
                c.step(nc.vector.memset(idx[:, GT:GT + G], 0))
                c.step(nc.vector.memset(dsti[:, GT:GT + G], 0))
                dve.sem_inc(pick_done, 2)
                dve.sem_inc(e_done, 16)
                dve.wait_ge(loaded, 48)
                c.link(nc.vector.tensor_copy(dstf[:], dsti[:, 0:GT]))
                split_index(nc, c, dstf[:], tile_of[:], lo[:])
                dve.wait_ge(topped, 1)
                c.link(nc.vector.tensor_copy(topq[:], ps_q[:, 0:H]))
                dve.wait_ge(made, 3)
                base = c.n

                def indices(b, g):
                    dve.wait_ge(mm, upto(g, G - 1, back=2))
                    nc.vector.tensor_copy(gi[:, b, :], idx[:, ds(g * G, G)]).then_inc(idx_done, 1)

                indices(0, 0)
                with dve.Fori(0, LG // 2) as i:
                    for b in range(2):
                        g = i * 2 + b
                        indices(1 - b, g + 1)
                        dve.wait_ge(row_in[b], 16 * i + 16)
                        dve.wait_ge(sc_mm, g + 1)
                        nc.vector.tensor_scalar(pick[:, b, :], lo_rows[:, b, :], k.ramp_p[:], None, ALU.is_equal).then_inc(pick_done, 1)
                        nc.vector.tensor_tensor(oh_hi[:, b, :, :], tile_of[:, ds(g * G, G)].unsqueeze(2).to_broadcast([Q, G, NT]),
                                                r25[:].unsqueeze(1).to_broadcast([Q, G, NT]), ALU.is_equal).then_inc(chain, 1)
                        for j in range(G):
                            t = g * G + j
                            nc.vector.tensor_scalar(oh_lo[:, b, j, :], r125[:], lo[:, ds(t, 1)], None, ALU.is_equal)
                        c0 = 8 * g + 16
                        dve.wait_ge(msg_in[b], 16 * G * (i + 1))
                        dve.wait_ge(sc_mm, g + 3)
                        dve.wait_ge(chain, base + g + 1)
                        nc.vector.tensor_tensor(picked[:].rearrange("p (j h) t -> p j h t", j=G), ps_s[:, b, 0:G * HT].rearrange("p (j h t) -> p j h t", j=G, t=NT),
                                                oh_hi[:, b, :, :].unsqueeze(2).to_broadcast([Q, G, H, NT]), ALU.mult).then_inc(e_done, 2)
                        dve.wait_ge(e_done, c0 + 2)
                        nc.vector.tensor_reduce(s_dst[:].rearrange("p g h -> p (g h)"), picked[:], AX_X, ALU.add).then_inc(e_done, 1)
                        dve.wait_ge(e_done, c0 + 3)
                        nc.vector.tensor_tensor(e1[:, :, 0, :], msg[:, b, :, F:W], s_dst[:], ALU.add).then_inc(e_done, 1)
                        nc.vector.tensor_tensor(e1[:, :, 1, :], topq[:].unsqueeze(1).to_broadcast([Q, G, H]), s_dst[:], ALU.add).then_inc(e_done, 1)
                        dve.wait_ge(e_done, c0 + 5)
                        nc.vector.scalar_tensor_tensor(e2[:], e1[:], 0.2, e1[:], ALU.mult, ALU.max).then_inc(e_done, 1)
                        dve.wait_ge(e_done, c0 + 6)
                        nc.vector.tensor_tensor(e[:, b, :, :], e2[:, :, 0, :], e2[:, :, 1, :], ALU.subtract).then_inc(e_done, 2)
                        dve.wait_ge(a_done, g + 1)
                        m = msg[:, b, :, 0:F].rearrange("p g (h d) -> p g h d", h=H)
                        nc.vector.tensor_tensor(m, m, msg[:, b, :, F:W].unsqueeze(3).to_broadcast([Q, G, H, F // H]), ALU.mult).then_inc(scaled, 1)
                        dve.wait_ge(scaled, g + 1)
                        for j in range(G):
                            nc.vector.tensor_tensor(spread[:, b, j, :].rearrange("p (t f) -> p t f", t=NT), oh_hi[:, b, j, :].unsqueeze(2).to_broadcast([Q, NT, W]),
                                                    msg[:, b, j, :].unsqueeze(1).to_broadcast([Q, NT, W]), ALU.mult).then_inc(ready, 1)
                c.n = base + LG
                mine = tgt[:].rearrange("p h t -> p t h")
                c.link(nc.vector.tensor_tensor(v1[:], own[:, :, F:W], mine, ALU.add))
                c.link(nc.vector.scalar_tensor_tensor(v2[:], v1[:], 0.2, v1[:], ALU.mult, ALU.max))
                c.link(nc.vector.tensor_tensor(v1[:], mine, top[:].unsqueeze(1).to_broadcast([P, NT, H]), ALU.add))
                c.link(nc.vector.scalar_tensor_tensor(v1[:], v1[:], 0.2, v1[:], ALU.mult, ALU.max))
                nc.vector.tensor_tensor(v1[:], v2[:], v1[:], ALU.subtract).then_inc(own_e, 1)
                dve.wait_ge(own_a, 1)
                for h in range(H):
                    c.step(nc.vector.tensor_tensor(own[:, :, 4 * h:4 * h + 4], own[:, :, 4 * h:4 * h + 4], own[:, :, F + h:F + h + 1].to_broadcast([P, NT, 4]), ALU.mult))
                c.wait()
                dve.wait_ge(mm, 2 * G + GT + 1)
                c.link(nc.vector.tensor_tensor(agg[:], ps[:, 0:NT * W].rearrange("p (t f) -> p t f", t=NT), own[:], ALU.add))


def mean_heads(k, v, score):
    nc = k.nc
    with stage(k) as s:
        total = s.sb("total", [P, NT, 4])
        chain = s.sem("chain")
        with s.block() as block:
            @block.vector
            def _(dve):
                c = Chain(dve, chain)
                c.link(nc.vector.tensor_reduce(total[:], v.rearrange("p t (h e) -> p t e h", e=4), AX_X, ALU.add))
                c.link(nc.vector.tensor_scalar(score[:], total[:], 0.25, None, ALU.mult))


def cutoff(k, cut):
    nc = k.nc
    with stage(k) as s:
        turns_i, q = s.sb("turns", [P, ET], I32), s.sb("q", [P, ET])
        chain, red, sines = s.sem("chain"), s.sem("red"), s.sem("sines")
        with s.block() as block:
            @block.vector
            def _(dve):
                c = Chain(dve, chain)
                c.link(nc.vector.tensor_scalar(turns_i[:], k.edge_w[:], 1.0 / 20, None, ALU.mult))
                c.link(nc.vector.tensor_scalar(q[:], turns_i[:], -20.0, None, ALU.mult))
                nc.vector.tensor_tensor(q[:], q[:], k.edge_w[:], ALU.add).then_inc(red, 1)
                dve.wait_ge(sines, 1)
                c.link(nc.vector.tensor_tensor(q[:], cut[:], cut[:], ALU.mult))
                c.link(nc.vector.tensor_scalar(cut[:], q[:], -1.0, 1.0, ALU.mult, ALU.add))

            @block.scalar
            def _(act):
                act.wait_ge(red, 1)
                nc.scalar.activation(cut[:], q[:], ACT.Sin, scale=math.pi / 20).then_inc(sines, 1)


def add_bias(k, rows, bias, softplus=False, to_x=False):
    nc = k.nc
    with stage(k) as s:
        b_sb = s.sb("bias", [P, D])
        soft = s.sb("soft", [P, NT, D]) if softplus else None
        b_in, chain, biased, done = (s.sem(n) for n in ("b_in", "chain", "biased", "done"))
        with s.block() as block:
            @block.sync
            def _(sp):
                sp.dma_start(b_sb[:], bias.partition_broadcast(P)).then_inc(b_in, 16)

            @block.vector
            def _(dve):
                c = Chain(dve, chain)
                dve.wait_ge(b_in, 16)
                nc.vector.tensor_tensor(rows[:], rows[:], b_sb[:].unsqueeze(1).to_broadcast([P, NT, D]), ALU.add).then_inc(biased, 1)
                dve.wait_ge(biased, 1)
                if to_x:
                    c.link(nc.vector.tensor_tensor(k.x[:], k.x[:], rows[:], ALU.add))
                if softplus:
                    dve.wait_ge(done, 3)
                    c.link(nc.vector.tensor_scalar(rows[:], rows[:], 0.0, -math.log(2.0), ALU.max, ALU.add))
                    c.link(nc.vector.tensor_tensor(rows[:], rows[:], soft[:], ALU.add))

            @block.scalar
            def _(act):
                if softplus:
                    act.wait_ge(biased, 1)
                    nc.scalar.activation(soft[:], rows[:], ACT.Abs).then_inc(done, 1)
                    act.wait_ge(done, 1)
                    nc.scalar.activation(soft[:], soft[:], ACT.Exp, scale=-1.0).then_inc(done, 1)
                    act.wait_ge(done, 2)
                    nc.scalar.activation(soft[:], soft[:], ACT.Ln, bias=1.0).then_inc(done, 1)


def ones_gate(k, gate):
    with stage(k) as s:
        done = s.sem("done")
        with s.block() as block:
            @block.vector
            def _(dve):
                k.nc.vector.memset(gate[:], 1.0).then_inc(done, 1)


def nan_to_num_to_x(k, v):
    nc = k.nc
    BIG = 3.4028234e38
    U8 = mybir.dt.uint8
    with stage(k) as s:
        mask = s.sb("mask", [P, NT, D], U8)
        const = s.sb("const", [P, 3])
        chain = s.sem("chain")
        with s.block() as block:
            @block.vector
            def _(dve):
                c = Chain(dve, chain)
                c.step(nc.vector.memset(const[:, 0:1], 0.0))
                c.step(nc.vector.memset(const[:, 1:2], 1.0e4))
                c.link(nc.vector.memset(const[:, 2:3], -1.0e4))
                for q, (other, op) in enumerate(((v[:], ALU.not_equal), (BIG, ALU.is_gt), (-BIG, ALU.is_lt))):
                    if q == 0:
                        c.link(nc.vector.tensor_tensor(mask[:], v[:], v[:], op))
                    else:
                        c.link(nc.vector.tensor_scalar(mask[:], v[:], other, None, op))
                    for t in range(NT):
                        c.step(nc.vector.copy_predicated(v[:, t, :], mask[:, t, :], const[:, q:q + 1].to_broadcast([P, D])))
                    c.wait()
                c.link(nc.vector.tensor_tensor(k.x[:], k.x[:], v[:], ALU.add))


def routed(k, rows, moe, n_exp, chosen, x, gate_w, gate_b, mode, capacity=None, **more):
    nc = k.nc
    blocks = most_blocks(chosen, n_exp)
    blocks += blocks % 2
    tensor = lambda n, shape, dt=F32: nc.sbuf_tensor(f"{n}_{x.f}_{n_exp}", shape, dt)
    with tensor("oh", [P, chosen, NT, n_exp]) as oh, tensor("wt", [P, chosen, NT]) as wt, \
            tensor("slot_i", [P, chosen, NT], I32) as slot_i, tensor("block_i", [1, blocks], I32) as block_i:
        with nc.sbuf_tensor(f"cols_{x.f}_{n_exp}", [128, 2, N], F32) as cols:
            normalise_all(k, rows, cols)
            gates(k, cols, None, n_exp, gate_w, gate_b, mode, choice=(oh, wt), **more)
        route(k, (oh, wt), slot_i, block_i, n_exp, chosen, blocks, capacity)
        sent, answered = (q[0:(blocks + 1) * BR, :] for q in (k.sent, k.answered))
        clear_rows(k, sent, (blocks + 1) * BR)
        send_rows(k, rows, sent, slot_i, chosen, blocks)
        block_experts(k, sent, answered, block_i, x, blocks)
        fetch_rows(k, moe, answered, slot_i, wt, chosen)


def build(nc, a, out, layers=8):
    k = Core()
    k.nc, k.uid = nc, 0
    ctx = ExitStack()
    with ctx:
        keep = lambda name, shape, dt=F32: ctx.enter_context(nc.sbuf_tensor(name, shape, dt))
        sbt = lambda name, shape=(P, NT, D), dt=F32: nc.sbuf_tensor(name, list(shape), dt)
        k.x = keep("x", [P, NT, D])
        k.edge_w, k.dst_f = keep("edge_w", [P, ET]), keep("dst_f", [P, ET])
        k.src_i, k.src_rel_i, k.row_i = (keep(n, [P, ET + G], I32) for n in ("src_i", "src_rel_i", "row_i"))
        k.dst_hi = keep("dst_hi", [P, ET])
        k.ramp_p, k.ramp_t = keep("ramp_p", [P, 1]), keep("ramp_t", [P, NT])
        tgt4, top4, tgt8, top8 = keep("tgt4", [P, 4, NT]), keep("top4", [P, 4]), keep("tgt8", [P, 8, NT]), keep("top8", [P, 8])
        k.ident, k.ones = keep("ident", [128, 128]), keep("ones", [128, 128])
        k.acc = {w: [nc.dram_tensor(f"acc{w}_{j}", [AT * P, w], F32, kind="Internal").ap() for j in range(G)] for w in (D, D + 4, D + 8)}
        k.rel_rows = nc.dram_tensor("rel_rows", [N, REL * D], F32, kind="Internal").ap()
        dram = lambda n, w: nc.dram_tensor(n, [N, w], F32, kind="Internal").ap()
        d = {n: dram("d_" + n, w) for n, w in (("xn", D), ("local", D), ("sorted", D), ("gat4", D + 4), ("gat8", D + 8), ("small", 20), ("lin1", D))}
        most = (most_blocks(2, 16) + 2) * BR
        k.sent, k.answered = (nc.dram_tensor(n, [most, D], F32, kind="Internal").ap() for n in ("sent", "answered"))
        k.keys_d = nc.dram_tensor("keys_d", [N], F32, kind="Internal").ap()
        k.src_c, k.dst_c, k.type_c, k.weight_c = a["src_c"], a["dst_c"], a["type_c"], a["weight_c"]
        k.dst_r, k.w_rel, k.ffn_dst_r = a["dst"], a["w_rel"], a["ffn_dst"]
        k.lo_r = nc.dram_tensor("lo_r", [E], F32, kind="Internal").ap()
        k.ffn_lo_r = nc.dram_tensor("ffn_lo_r", [32768], F32, kind="Internal").ap()
        x_rows = a["x"].rearrange("(t p) f -> p t f", p=P)
        out_rows = out.rearrange("(t p) f -> p t f", p=P)

        with stage(k) as s:
            x_in, made = s.sem("x_in"), s.sem("made")
            with s.block() as block:
                @block.sync
                def _(sp):
                    sp.dma_start(k.x[:], x_rows).then_inc(x_in, 16)
                    sp.wait_ge(x_in, 16)

                @block.gpsimd
                def _(pool):
                    nc.gpsimd.memset(k.ones[:], 1.0).then_inc(made, 1)
                    nc.gpsimd.memset(k.ident[:], 0.0).then_inc(made, 1)
                    pool.wait_ge(made, 2)
                    nc.gpsimd.affine_select(out=k.ident[:], in_=k.ident[:], compare_op=ALU.not_equal, fill=1.0, base=0,
                                            pattern=[[-1, 128]], channel_multiplier=1).then_inc(made, 1)

        prepare_edges(k)

        if layers >= 1:
            with nc.sbuf_tensor("rows_a", [P, NT, D], F32) as rows, nc.sbuf_tensor("cols_a", [128, 2, N], F32) as cols:
                normalise_all(k, rows, cols)
                relation_tables(k, cols)
            table = k.rel_rows.rearrange("n (r f) -> (n r) f", r=REL)
            edge_sums(k, table, k.src_rel_i, D, weight=k.edge_w, make_rows=True)
            with nc.sbuf_tensor("agg_a", [P, NT, D], F32) as agg:
                collect(k, agg, D)
                add_to_x(k, agg)

        if layers >= 2:
            with sbt("rows_b") as rows, sbt("moe_b") as moe:
                routed(k, rows, moe, 16, 2, Experts(16, 512, ACT.Relu, a["L0_ffn_w1"], a["L0_ffn_b1"], a["L0_ffn_w2"], a["L0_ffn_b2"]),
                       a["L0_ffn_gate_w"], a["L0_ffn_gate_b"], "top2")
                finish_norm(k, rows, moe, a["L0_ffn_gamma"], a["L0_ffn_beta"])

        if layers >= 3:
            with sbt("rows_c") as rows:
                with sbt("cols_c", [128, 2, N]) as cols, sbt("proj_c") as proj:
                    normalise_all(k, rows, cols)
                    transfer(k, d["xn"].rearrange("(t p) f -> p t f", p=P), rows[:])
                    project(k, cols, a["gat_w"], D, rows=proj, table=d["gat4"])
                    scores(k, proj, D, 4, a["gat_a_src"], a["gat_a_tgt"], d["gat4"].rearrange("(t p) f -> p t f", p=P)[:, :, D:D + 4], tgt4, top4)
            edge_sums(k, d["gat4"], k.src_i, D + 4, heads=4, tgt=tgt4, top=top4)
            with sbt("agg_c", [P, NT, D + 4]) as agg, sbt("rows_d") as rows, sbt("local_d") as local:
                transfer(k, rows[:], d["xn"].rearrange("(t p) f -> p t f", p=P))
                collect(k, agg, D + 4)
                divide(k, agg, local, 4, 1e-16, add=rows, bias=a["L1_gnn_gat_b"])
                finish_norm(k, local, None, a["L1_gnn_ln_local_g"], a["L1_gnn_ln_local_b"], to_x=False)
                transfer(k, d["local"].rearrange("(t p) f -> p t f", p=P), local[:])
            with sbt("rank_i", [P, NT], I32) as rank_i:
                sort_nodes(k, rank_i, a["node_vec"])
                with sbt("xc", [128, 2, N]) as xc, sbt("z", [128, 2, N]) as z, sbt("dbc", [48, N]) as dbc:
                    with sbt("cols_e", [128, 2, N]) as cols:
                        with sbt("rows_e") as rows:
                            transfer(k, rows[:], d["xn"].rearrange("(t p) f -> p t f", p=P))
                            permute(k, rows, d["sorted"], rank_i, scatter=True)
                            transfer(k, rows[:], d["sorted"].rearrange("(t p) f -> p t f", p=P))
                            turn_all(k, rows, cols)
                        mamba_inputs(k, cols, xc, z, dbc, a["in_proj_w"], a["L1_gnn_conv_w"], a["L1_gnn_conv_b"], a["x_proj_w"])
                    for h in range(2):
                        selective_scan(k, h, xc, z, dbc, a["dt_proj_w"], a["L1_gnn_dt_proj_b"], a["L1_gnn_A_log"], a["L1_gnn_D_param"])
                    project(k, z, a["out_proj_w"], D, table=d["sorted"])
                with sbt("y_f") as y, sbt("rows_f") as rows, sbt("local_f") as local:
                    permute(k, y, d["sorted"], rank_i, scatter=False)
                    transfer(k, rows[:], d["xn"].rearrange("(t p) f -> p t f", p=P))
                    transfer(k, local[:], d["local"].rearrange("(t p) f -> p t f", p=P))
                    finish_norm(k, y, rows, a["L1_gnn_ln_global_g"], a["L1_gnn_ln_global_b"], to_x=False)
                    with sbt("cols_f", [128, 2, N]) as la, sbt("cols_g", [128, 2, N]) as ya:
                        turn_all(k, local, la)
                        turn_all(k, y, ya)
                        mix(k, local, y, la, ya, a["wl"], a["wg"])
                    transfer(k, d["local"].rearrange("(t p) f -> p t f", p=P), local[:])
            with sbt("h_g") as hrow, sbt("ff_g") as ff, sbt("gate_g", [P, NT, 1]) as gate, sbt("cols_h", [128, 2, N]) as cols:
                transfer(k, hrow[:], d["local"].rearrange("(t p) f -> p t f", p=P))
                turn_all(k, hrow, cols)
                ones_gate(k, gate)
                experts(k, cols, gate, ff, Experts(1, 512, ACT.Relu, a["ff1_w"], a["ff1_b"], a["ff2_w"], a["L1_gnn_ff2_b"]))
                finish_norm(k, hrow, ff, a["L1_gnn_ln2_g"], a["L1_gnn_ln2_b"])

        if layers >= 4:
            with sbt("gate_i", [P, NT, 4]) as gate, sbt("cols_i", [128, 2, N]) as cols:
                with sbt("rows_i") as rows:
                    normalise_all(k, rows, cols)
                with sbt("h16", [P, NT, 16]) as h16, sbt("agg_i", [P, NT, 20]) as agg, sbt("score_i", [P, NT, 4]) as score:
                    project(k, cols, a["L1_ffn_W_gat"], 16, rows=h16, table=d["small"])
                    scores(k, h16, 16, 4, a["L1_ffn_att_src"], a["L1_ffn_att_dst"], d["small"].rearrange("(t p) f -> p t f", p=P)[:, :, 16:20], tgt4, top4)
                    small_edge_sums(k, d["small"], tgt4, top4, agg, a["ffn_src_c"], a["ffn_dst_c"])
                    divide(k, agg, h16, 4, 1e-16, bias=a["L1_ffn_b_gat"], width=16)
                    finish_norm(k, h16, None, a["L1_ffn_ln_gamma"], a["L1_ffn_ln_beta"], to_x=False, width=16)
                    mean_heads(k, h16, score)
                    gates(k, cols, gate, 4, None, None, "top2", scores=score[:])
                with sbt("moe_i") as moe:
                    experts(k, cols, gate, moe, Experts(4, 512, ACT.Gelu, a["L1_ffn_W1"], a["L1_ffn_b1"], a["L1_ffn_W2"], a["L1_ffn_b2"]))
                    add_to_x(k, moe)

        if layers >= 5:
            with sbt("rows_j") as rows, sbt("cols_j", [128, 2, N]) as cols:
                normalise_all(k, rows, cols)
                project(k, cols, a["gat2_w"], D, rows=rows, table=d["gat8"])
                scores(k, rows, D, 8, a["gat2_a1"], a["gat2_a2"], d["gat8"].rearrange("(t p) f -> p t f", p=P)[:, :, D:D + 8], tgt8, top8)
            edge_sums(k, d["gat8"], k.src_i, D + 8, heads=8, tgt=tgt8, top=top8)
            with sbt("agg_j", [P, NT, D + 8]) as agg, sbt("out_j") as o:
                collect(k, agg, D + 8)
                divide(k, agg, o, 8, 0.0)
                add_to_x(k, o)

        if layers >= 6:
            with sbt("rows_k") as rows, sbt("moe_k") as moe:
                routed(k, rows, moe, 8, 1, Experts(8, 1024, ACT.Relu, a["L2_ffn_w1"], a["L2_ffn_b1"], a["L2_ffn_w2"], a["L2_ffn_b2"]),
                       a["L2_ffn_gate_w"], a["L2_ffn_gate_b"], "top1", capacity=math.ceil(1.25 * N / 8))
                nan_to_num_to_x(k, moe)

        if layers >= 7:
            with sbt("rows_l") as rows, sbt("cols_l", [128, 2, N]) as cols:
                normalise_all(k, rows, cols)
                project(k, cols, a["L3_gnn_lin1_w"], D, table=d["lin1"])
            with sbt("cut", [P, ET]) as cut:
                cutoff(k, cut)
                edge_sums(k, d["lin1"], k.src_i, D, weight=cut, mlp=Mlp(50, a["attr"], a["L3_gnn_mlp_w1"], a["L3_gnn_mlp_b1"], a["L3_gnn_mlp_w2"], a["L3_gnn_mlp_b2"]))
            with sbt("agg_m") as agg, sbt("cols_m", [128, 2, N]) as cols:
                collect(k, agg, D)
                turn_all(k, agg, cols)
                project(k, cols, a["L3_gnn_lin2_w"], D, rows=agg)
                add_bias(k, agg, a["L3_gnn_lin2_b"], softplus=True)
                turn_all(k, agg, cols)
                project(k, cols, a["L3_gnn_lin_w"], D, rows=agg)
                add_bias(k, agg, a["L3_gnn_lin_b"], to_x=True)

        if layers >= 8:
            with sbt("rows_n") as rows, sbt("moe_n") as moe:
                routed(k, rows, moe, 6, 2, Experts(6, 256, ACT.Relu, a["L3_ffn_expert_w1"], a["L3_ffn_expert_b1"], a["L3_ffn_expert_w3"], a["L3_ffn_expert_b3"],
                                                   wm=a["L3_ffn_expert_w2"], bm=a["L3_ffn_expert_b2"]),
                       None, a["L3_ffn_router_b2"], "top2_probs", router=Experts(1, 128, None, a["L3_ffn_router_w1"], a["L3_ffn_router_b1"], a["L3_ffn_router_w2"], None))
                add_to_x(k, moe)

        with stage(k) as s:
            stored = s.sem("stored")
            with s.block() as block:
                @block.sync
                def _(sp):
                    sp.dma_start(out_rows, k.x[:]).then_inc(stored, 16)
                    sp.wait_ge(stored, 16)


def layouts(v):
    col = lambda e: np.ascontiguousarray(e.reshape(ET, P).T)
    hid = lambda b: np.ascontiguousarray(b.reshape(b.shape[0], -1, 128).transpose(0, 2, 1).reshape(b.shape[0] * 128, -1))
    w_rel = v["L0_gnn_weight"].reshape(REL, BASES, SUB, SUB)
    return {
        "x": v["x"], "dst": v["dst"], "src_c": col(v["src"]), "dst_c": col(v["dst"]), "type_c": col(v["edge_type_8"]),
        "weight_c": col(v["edge_weight"]), "w_rel": np.ascontiguousarray(w_rel.transpose(1, 2, 0, 3)),
        **{n: v[n] for n in ("L0_ffn_gate_w", "L0_ffn_gate_b", "L0_ffn_w1", "L0_ffn_w2", "L0_ffn_gamma", "L0_ffn_beta")},
        **{n: v[n] for n in (
            "node_vec", "L1_gnn_gat_b", "L1_gnn_ln_local_g", "L1_gnn_ln_local_b", "L1_gnn_ln_global_g", "L1_gnn_ln_global_b", "L1_gnn_ln2_g", "L1_gnn_ln2_b",
            "L1_gnn_conv_w", "L1_gnn_conv_b", "L1_gnn_dt_proj_b", "L1_gnn_A_log", "L1_gnn_D_param", "L1_gnn_ff2_b",
            "L1_ffn_W_gat", "L1_ffn_b_gat", "L1_ffn_ln_gamma", "L1_ffn_ln_beta", "L1_ffn_W1", "L1_ffn_W2",
            "L2_ffn_gate_w", "L2_ffn_gate_b", "L2_ffn_w1", "L2_ffn_w2",
            "L3_gnn_mlp_w1", "L3_gnn_mlp_b1", "L3_gnn_mlp_w2", "L3_gnn_mlp_b2", "L3_gnn_lin1_w", "L3_gnn_lin2_w", "L3_gnn_lin2_b", "L3_gnn_lin_w", "L3_gnn_lin_b",
            "L3_ffn_router_w1", "L3_ffn_router_b1", "L3_ffn_router_w2", "L3_ffn_router_b2", "L3_ffn_expert_w1", "L3_ffn_expert_w2", "L3_ffn_expert_w3")},
        "gat_w": v["L1_gnn_gat_w"].T, "gat_a_src": v["L1_gnn_gat_a_src"].reshape(-1), "gat_a_tgt": v["L1_gnn_gat_a_tgt"].reshape(-1),
        "in_proj_w": v["L1_gnn_in_proj_w"].T, "x_proj_w": v["L1_gnn_x_proj_w"].T, "dt_proj_w": v["L1_gnn_dt_proj_w"].T, "out_proj_w": v["L1_gnn_out_proj_w"].T,
        "wl": v["L1_gnn_wl"].T, "wg": v["L1_gnn_wg"].T, "ff1_w": v["L1_gnn_ff1_w"].T[None], "ff1_b": hid(v["L1_gnn_ff1_b"][None]), "ff2_w": v["L1_gnn_ff2_w"].T[None],
        "L1_ffn_att_src": v["L1_ffn_att_src"].reshape(-1), "L1_ffn_att_dst": v["L1_ffn_att_dst"].reshape(-1),
        "ffn_dst": v["L1_ffn_edge_index"][1],
        "ffn_src_c": v["L1_ffn_edge_index"][0].reshape(-1, 128).T, "ffn_dst_c": v["L1_ffn_edge_index"][1].reshape(-1, 128).T,
        "L1_ffn_b1": hid(v["L1_ffn_b1"]), "L1_ffn_b2": v["L1_ffn_b2"].reshape(-1),
        "gat2_w": v["L2_gnn_W"].transpose(1, 0, 2).reshape(D, D), "gat2_a1": v["L2_gnn_a"][:, :32].reshape(-1), "gat2_a2": v["L2_gnn_a"][:, 32:].reshape(-1),
        "L2_ffn_b1": hid(v["L2_ffn_b1"]), "L2_ffn_b2": v["L2_ffn_b2"].reshape(-1),
        "attr": v["edge_attr_50"].T,
        "L3_ffn_expert_b1": hid(v["L3_ffn_expert_b1"]), "L3_ffn_expert_b2": hid(v["L3_ffn_expert_b2"]), "L3_ffn_expert_b3": v["L3_ffn_expert_b3"].reshape(-1),
        "L0_ffn_b1": hid(v["L0_ffn_b1"]), "L0_ffn_b2": v["L0_ffn_b2"].reshape(-1),
    }


def kernel(**inputs):
    import concourse.bacc as bacc
    from concourse.bass_utils import run_bass_kernel_spmd

    nc = bacc.Bacc("TRN2", target_bir_lowering=False, num_devices=1)
    arrays = layouts({n: np.asarray(v) for n, v in inputs.items()})
    arrays = {f"in_{n}": np.ascontiguousarray(v) for n, v in arrays.items()}
    args = {n[3:]: nc.dram_tensor(n, v.shape, mybir.dt.from_np(v.dtype), kind="ExternalInput").ap() for n, v in arrays.items()}
    out = nc.dram_tensor("out_0", (N, D), F32, kind="ExternalOutput").ap()
    build(nc, args, out, 8)
    r = run_bass_kernel_spmd(nc, [arrays], core_ids=[0])
    return r.results[0]["out_0"]
```

```python
import math
from contextlib import ExitStack

import numpy as np

import concourse.bass as bass
from concourse import mybir

ALU = mybir.AluOpType
ACT = mybir.ActivationFunctionType
AX_X = mybir.AxisListType.X
F32 = mybir.dt.float32
I32 = mybir.dt.int32
BF16 = mybir.dt.bfloat16
RMAX = bass.bass_isa.ReduceOp.max
ds = bass.ds

N, D, E = 3125, 256, 50000
P = 125
NT, ET = N // P, E // P
G = 4
NG = ET // G
PAD_ROW = N
AT = NT + 1
REL, BASES, SUB = 8, 8, 32
EPS = 1e-5


class Core:
    pass


def stage(k):
    return Stage(k)


class Stage:
    def __init__(self, k):
        self.k, self.nc = k, k.nc
        self.ctx = ExitStack()
        self.sems = []

    def __enter__(self):
        return self

    def __exit__(self, *e):
        if e[0] is not None:
            return False
        self.ctx.close()
        self.nc.clear_and_free_semaphores(self.sems)
        self.nc.all_engine_barrier()

    def sb(self, name, shape, dt=F32):
        self.k.uid += 1
        return self.ctx.enter_context(self.nc.sbuf_tensor(f"{name}_{self.k.uid}", shape, dt))

    def ps(self, name, shape, dt=F32):
        self.k.uid += 1
        return self.ctx.enter_context(self.nc.psum_tensor(f"{name}_{self.k.uid}", shape, dt))

    def sem(self, name):
        self.k.uid += 1
        s = self.nc.alloc_semaphore(f"{name}_{self.k.uid}")
        self.sems.append(s)
        return s

    def block(self):
        return self.nc.Block()


class Chain:

    def __init__(self, eng, sem):
        self.eng, self.sem, self.n = eng, sem, 0

    def step(self, ins):
        self.n += 1
        ins.then_inc(self.sem, 1)

    def wait(self):
        self.eng.wait_ge(self.sem, self.n)

    def link(self, ins):
        self.step(ins)
        self.wait()


def split_index(nc, c, node, tile_of, lo, whole):
    c.link(nc.vector.tensor_scalar(whole, node, 1.0 / P, None, ALU.mult))
    c.link(nc.vector.tensor_copy(tile_of, whole))
    c.link(nc.vector.scalar_tensor_tensor(lo, tile_of, float(-P), node, ALU.mult, ALU.add))
    c.link(nc.vector.scalar_tensor_tensor(tile_of, lo, float(P), tile_of, ALU.is_ge, ALU.add))
    c.link(nc.vector.tensor_scalar(lo, lo, 0.0, -1.0, ALU.is_ge, ALU.add))
    c.link(nc.vector.tensor_tensor(tile_of, tile_of, lo, ALU.add))
    c.link(nc.vector.scalar_tensor_tensor(lo, tile_of, float(-P), node, ALU.mult, ALU.add))


def prepare_edges(k, src_tile, src_row, x_rows):
    nc = k.nc
    with stage(k) as s:
        src, typ, dst, dst_n, small = (s.sb(n, sh, I32) for n, sh in (("src", [P, ET]), ("typ", [P, ET]), ("dst", [P, ET]), ("dst_n", [P, ET]), ("small", [128, 256])))
        mix_ = s.sb("mix", [P, ET])
        f_n, t_n, lo_n = (s.sb(n, [P, ET]) for n in ("f_n", "t_n", "lo_n"))
        f_s, t_s, lo_s = (s.sb(n, [128, 256]) for n in ("f_s", "t_s", "lo_s"))
        lo_c = s.sb("lo_c", [P, ET])
        loaded, chain, ready, stored, x_in = (s.sem(n) for n in ("loaded", "chain", "ready", "stored", "x_in"))
        with s.block() as block:
            @block.sync
            def _(sp):
                sp.dma_start(src[:], k.src_c).then_inc(loaded, 16)
                sp.dma_start(dst[:], k.dst_c).then_inc(loaded, 16)
                sp.dma_start(typ[:], k.type_c).then_inc(loaded, 16)
                sp.dma_start(k.edge_w[:], k.weight_c).then_inc(loaded, 16)
                sp.dma_start(dst_n[:], k.dst_r.rearrange("(p c) -> p c", p=P)).then_inc(loaded, 16)
                sp.dma_start(small[:], k.ffn_dst_r.rearrange("(p c) -> p c", p=128)).then_inc(loaded, 16)
                sp.dma_start(k.x[:], x_rows).then_inc(x_in, 16)
                sp.wait_ge(ready, 1)
                sp.dma_start(k.lo_r.rearrange("(p c) -> p c", p=P), lo_n[:]).then_inc(stored, 16)
                sp.dma_start(k.ffn_lo_r.rearrange("(p c) -> p c", p=128), lo_s[:]).then_inc(stored, 16)
                sp.wait_ge(stored, 32)
                sp.wait_ge(x_in, 16)

            @block.gpsimd
            def _(pool):
                nc.gpsimd.iota(k.ramp_p[:], [[0, 1]], base=0, channel_multiplier=1, allow_small_or_imprecise_dtypes=True)
                nc.gpsimd.iota(k.ramp_t[:], [[1, NT]], base=0, channel_multiplier=0, allow_small_or_imprecise_dtypes=True)

            @block.vector
            def _(dve):
                c = Chain(dve, chain)
                dve.wait_ge(loaded, 96)
                for idx in (k.src_i, k.src_rel_i, k.row_i):
                    c.step(nc.vector.memset(idx[:, ET:ET + G], 0))
                c.step(nc.vector.tensor_copy(k.dst_f[:], dst[:]))
                c.step(nc.vector.tensor_copy(f_n[:], dst_n[:]))
                c.step(nc.vector.tensor_copy(f_s[:], small[:]))
                c.step(nc.vector.tensor_copy(k.src_i[:, 0:ET], src[:]))
                c.link(nc.vector.tensor_scalar(mix_[:], src[:], float(REL), None, ALU.mult))
                c.link(nc.vector.tensor_tensor(mix_[:], mix_[:], typ[:], ALU.add))
                c.link(nc.vector.tensor_copy(k.src_rel_i[:, 0:ET], mix_[:]))
                split_index(nc, c, f_n[:], t_n[:], lo_n[:], dst_n[:])
                split_index(nc, c, f_s[:], t_s[:], lo_s[:], small[:])
                dve.sem_inc(ready, 1)
                split_index(nc, c, k.dst_f[:], k.dst_hi[:], lo_c[:], dst[:])
                c.link(nc.vector.tensor_copy(lo_c[:], src[:]))
                split_index(nc, c, lo_c[:], src_tile[:], src_row[:], src[:])


def normalise_all(k, rows, cols, eps=EPS, clear=None):
    nc = k.nc
    with stage(k) as s:
        stats = s.sb("stats", [P, NT, 6])
        mv = s.sb("mv", [P, NT, 2])
        veps = s.sb("veps", [P, NT])
        rstd = s.sb("rstd", [P, NT])
        ps = s.ps("turned", [128, 4, 512])
        chain, var, sd, rows_done, turned, copied = (s.sem(n) for n in ("chain", "var", "sd", "rows_done", "turned", "copied"))
        zero, zeroed, cleared = s.sb("zero", [P, D]), s.sem("zeroed"), s.sem("cleared")
        with s.block() as block:
            @block.gpsimd
            def _(pool):
                if clear is not None:
                    nc.gpsimd.memset(zero[:], 0.0).then_inc(zeroed, 1)

            @block.sync
            def _(sp):
                if clear is not None:
                    sp.wait_ge(zeroed, 1)
                    tiles = clear.shape[0] // P
                    sp.dma_start(clear.rearrange("(t p) f -> p t f", p=P), zero[:].unsqueeze(1).to_broadcast([P, tiles, D])).then_inc(cleared, 16)
                    sp.wait_ge(cleared, 16)

            @block.vector
            def _(dve):
                c = Chain(dve, chain)
                for t in range(NT):
                    c.step(nc.vector.bn_stats(stats[:, t, :], k.x[:, t, :]))
                c.wait()
                for t in range(NT):
                    c.step(nc.vector.bn_aggr(mv[:, t, :], stats[:, t, :]))
                c.wait()
                nc.vector.tensor_scalar(veps[:], mv[:, :, 1], eps, None, ALU.add).then_inc(var, 1)
                dve.wait_ge(sd, 1)
                c.link(nc.vector.reciprocal(rstd[:], veps[:]))
                for t in range(NT):
                    nc.vector.tensor_scalar(rows[:, t, :], k.x[:, t, :], mv[:, t, 0:1], rstd[:, t:t + 1],
                                            ALU.subtract, ALU.mult).then_inc(rows_done, 1)

            @block.scalar
            def _(act):
                act.wait_ge(var, 1)
                nc.scalar.activation(veps[:], veps[:], ACT.Sqrt).then_inc(sd, 1)
                for t in range(NT):
                    act.wait_ge(turned, t + 1)
                    nc.scalar.activation(cols[:, :, t * P:(t + 1) * P],
                                         ps[:, t % 4, 0:2 * P].rearrange("p (c n) -> p c n", c=2), ACT.Copy).then_inc(copied, 1)

            @block.tensor
            def _(pe):
                for t in range(NT):
                    pe.wait_ge(rows_done, t + 1)
                    if t >= 4:
                        pe.wait_ge(copied, t - 3)
                    nc.tensor.transpose(ps[:, t % 4, 0:P], rows[:, t, 0:128], k.ident[0:P, 0:P])
                    nc.tensor.transpose(ps[:, t % 4, P:2 * P], rows[:, t, 128:256], k.ident[0:P, 0:P]).then_inc(turned, 1)


def relation_tables(k, cols):
    nc = k.nc
    with stage(k) as s:
        w = s.sb("w_rel", [128, 2, REL, 128])
        row = s.sb("row", [P, 5, REL, D])
        ps = s.ps("ps", [P, 8, 512])
        zeroed, w_in, mm, evac = (s.sem(n) for n in ("zeroed", "w_in", "mm", "evac"))
        stored = [s.sem(f"stored{j}") for j in range(5)]
        with s.block() as block:
            @block.sync
            def _(sp):
                sp.wait_ge(zeroed, 1)
                for b in range(BASES):
                    lo = SUB * (b % 4)
                    sp.dma_start(w[lo:lo + SUB, b // 4, :, lo:lo + SUB], k.w_rel[b]).then_inc(w_in, 16)
                with sp.Fori(0, NT // 5) as i:
                    for j in range(5):
                        sp.wait_ge(evac, (i * 5 + j) * 4 + 4)
                        sp.dma_start(k.rel_rows[ds((i * 5 + j) * P, P), :], row[:, j, :, :].rearrange("p r f -> p (r f)")).then_inc(stored[j], 16)
                for j in range(5):
                    sp.wait_ge(stored[j], 16 * (NT // 5))

            @block.vector
            def _(dve):
                nc.vector.memset(w[:], 0.0).then_inc(zeroed, 1)

            @block.tensor
            def _(pe):
                pe.wait_ge(w_in, 16 * BASES)
                for t in range(NT):
                    for q in range(4):
                        c, half = q // 2, q % 2
                        n = t * 4 + q
                        if n >= 8:
                            pe.wait_ge(evac, n - 7)
                        nc.tensor.matmul(ps[:, n % 8, :], cols[:, c, t * P:(t + 1) * P],
                                         w[:, c, 4 * half:4 * half + 4, :].rearrange("p r o -> p (r o)"),
                                         start=True, stop=True).then_inc(mm, 1)

            @block.scalar
            def _(act):
                for t in range(NT):
                    if t >= 5:
                        act.wait_ge(stored[t % 5], 16 * (t // 5))
                    for q in range(4):
                        c, half = q // 2, q % 2
                        act.wait_ge(mm, t * 4 + q + 1)
                        nc.scalar.activation(row[:, t % 5, 4 * half:4 * half + 4, c * 128:(c + 1) * 128],
                                             ps[:, (t * 4 + q) % 8, :].rearrange("p (r o) -> p r o", r=4), ACT.Copy).then_inc(evac, 1)


class Mlp:

    def __init__(self, n_in, attr, w1, b1, w2, b2):
        self.n_in, self.attr, self.w1, self.b1, self.w2, self.b2 = n_in, attr, w1, b1, w2, b2


def upto(g, j, back=0):
    return (g - back + 2) * G + j + 1


def edge_sums(k, table, src_idx, width, weight=None, heads=0, tgt=None, top=None, mlp=None, make_rows=False, sources=None):
    nc = k.nc
    att = heads > 0
    HD = D // heads if att else 0
    with stage(k) as s:
        rows = s.sb("rows", [P, 2, G * P], I32)
        gi = s.sb("gi", [P, 2, G], I32)
        si = s.sb("si", [P, 2, G], I32)
        msg = s.sb("msg", [P, 2, G, width])
        same = s.sb("same", [P, 2, G, P])
        z = s.sb("z", [P, 2, G, width])
        zero = s.sb("zero", [P, width])
        ps = s.ps("ps", [P, G, 512])
        if att:
            lo_rows = s.sb("lo_rows", [P, 2, G * P])
            pick = s.sb("pick", [P, 2, G * P])
            in_tile = s.sb("in_tile", [P, 2, G, NT])
            picked = s.sb("picked", [P, G * heads, NT])
            s_dst = s.sb("s_dst", [P, G, heads])
            e1 = s.sb("e1", [P, G, 2, heads])
            e2 = s.sb("e2", [P, G, 2, heads])
            e = s.sb("e", [P, 2, G, heads])
            ps_s = s.ps("ps_s", [P, 2, 2, 512])
            HT = heads * NT
        if make_rows:
            before, hits = s.sb("before", [P, P]), s.sb("hits", [P, G, P])
            prior, row = s.sb("prior", [P, G]), s.sb("row", [P, G])
            pad = s.sb("pad", [P, 1])
            ramps, rows_made = s.sem("ramps"), s.sem("rows_made")
        if sources:
            hot_row, hot_tile = s.sb("hot_row", [P, 2, G, P], BF16), s.sb("hot_tile", [P, 2, G, NT], BF16)
            none, ramp_row = s.sb("none", [P, P], BF16), s.sb("ramp_row", [P, P])
            ps_n = s.ps("ps_n", [P, 512])
            hot, counted, ramped = s.sem("hot"), s.sem("counted"), s.sem("ramped")
        if mlp:
            attr = s.sb("attr", [mlp.n_in, 2, G * P])
            hid = s.sb("hid", [128, 2, 2, G * P])
            pos = s.sb("pos", [128, 2, 2, G * P])
            hs = s.sb("hs", [128, 2, 2, G * P])
            w1, b1 = s.sb("w1", [mlp.n_in, D]), s.sb("b1", [128, 2])
            w2, b2 = s.sb("w2", [128, 2, D]), s.sb("b2", [P, D])
            fil = s.sb("fil", [P, G, D])
            w_in, hid_ln = s.sem("w_in"), s.sem("hid_ln")
            ps_h = s.ps("ps_h", [128, 2, 512])
            ps_f = s.ps("ps_f", [P, G, D])
        turns = s.sem("turns")
        zeroed, idx_done, mm, z_done, same_done, si_done = (s.sem(n) for n in ("zeroed", "idx", "mm", "z_done", "same", "si"))
        e_done, a_done, ready, chain, pick_done, sc_mm = (s.sem(n) for n in ("e_done", "a_done", "ready", "chain", "pick", "sc_mm"))
        hid_mm, hid_act, hid_done, fil_mm, fil_used = (s.sem(n) for n in ("hid_mm", "hid_act", "hid_done", "fil_mm", "fil_used"))
        row_in = [s.sem("row_in0"), s.sem("row_in1")]
        msg_in = [s.sem("msg_in0"), s.sem("msg_in1")]
        attr_in = [s.sem("attr_in0"), s.sem("attr_in1")]
        added = [s.sem(f"added{j}") for j in range(G)]
        lo_in = [s.sem("lo_in0"), s.sem("lo_in1")]
        with s.block() as block:
            @block.sync
            def _(sp):
                if mlp:
                    sp.dma_start(w1[:], mlp.w1).then_inc(w_in, 16)
                    sp.dma_start(w2[:], mlp.w2.rearrange("(c p) f -> p c f", p=128)).then_inc(w_in, 16)
                    sp.dma_start(b2[:], mlp.b2.partition_broadcast(P)).then_inc(w_in, 16)
                    sp.dma_start(b1[:], mlp.b1.rearrange("(c p) -> p c", p=128), allow_slow_non_contiguous=True).then_inc(w_in, 16)

                def edge_features(b, g):
                    sp.wait_ge(hid_mm, 2 * g + 2)
                    sp.dma_start(attr[:, b, :], mlp.attr[:, ds(g * (G * P), G * P)]).then_inc(attr_in[b], 16)

                def destinations(b, g):
                    sp.wait_ge(same_done, upto(g, G - 1, back=2))
                    sp.dma_start(rows[:, b, :], k.dst_r[ds(g * (G * P), G * P)].partition_broadcast(P)).then_inc(row_in[b], 16)
                    if att:
                        sp.wait_ge(pick_done, g + 1)
                        sp.dma_start(lo_rows[:, b, :], k.lo_r[ds(g * (G * P), G * P)].partition_broadcast(P)).then_inc(lo_in[b], 16)

                if mlp:
                    edge_features(0, 0)
                    edge_features(1, 1)
                last = NG // 2 - 1
                with sp.Fori(0, last) as i:
                    for b in range(2):
                        g = i * 2 + b
                        if mlp:
                            edge_features(b, g + 2)
                        destinations(b, g)
                for b in range(2):
                    destinations(b, last * 2 + b)

            @block.gpsimd
            def _(pool):
                nc.gpsimd.memset(zero[:], 0.0).then_inc(zeroed, 1)
                if make_rows:
                    nc.gpsimd.memset(before[:], 1.0).then_inc(ramps, 1)
                    pool.wait_ge(ramps, 1)
                    nc.gpsimd.affine_select(out=before[:], in_=before[:], compare_op=ALU.is_gt, fill=0.0, base=0,
                                            pattern=[[-1, P]], channel_multiplier=1).then_inc(ramps, 1)
                    nc.gpsimd.iota(pad[:], [[0, 1]], base=PAD_ROW, channel_multiplier=1, allow_small_or_imprecise_dtypes=True).then_inc(ramps, 1)
                if sources:
                    nc.gpsimd.memset(none[:], 0.0).then_inc(ramped, 1)
                    nc.gpsimd.iota(ramp_row[:], [[1, P]], base=0, channel_multiplier=0, allow_small_or_imprecise_dtypes=True).then_inc(ramped, 1)
                pool.wait_ge(zeroed, 1)
                for half in range(2):
                    for j in range(G):
                        if half:
                            pool.wait_ge(added[j], 16)
                        pool.dma_start(k.acc[width][j].rearrange("(h t p) f -> h p t f", p=P, h=2)[half],
                                       zero[:].unsqueeze(1).to_broadcast([P, AT // 2, width])).then_inc(added[j], 16)

                def gather(b, g):
                    pool.wait_ge(idx_done, g + 1)
                    pool.wait_ge(mm, upto(g, G - 1, back=2))
                    pool.sem_inc(turns, 1)
                    for j in range(G):
                        nc.gpsimd.indirect_dma_start(msg[:, b, j, :], None, table, bass.IndirectOffsetOnAxis(gi[:, b, j:j + 1], 0)).then_inc(msg_in[b], 16)

                def scatter(b, g):
                    pool.wait_ge(si_done, g + 1)
                    for j in range(G):
                        pool.wait_ge(z_done, upto(g, j))
                        pool.wait_ge(added[j], (g + 2) * 16)
                        pool.sem_inc(turns, 1)
                        nc.gpsimd.indirect_dma_start(k.acc[width][j], bass.IndirectOffsetOnAxis(si[:, b, j:j + 1], 0), z[:, b, j, :], None,
                                                     compute_op=ALU.add).then_inc(added[j], 16)

                gather(0, 0)
                last = NG // 2 - 1
                with pool.Fori(0, last) as i:
                    gather(1, i * 2 + 1)
                    scatter(0, i * 2)
                    gather(0, i * 2 + 2)
                    scatter(1, i * 2 + 1)
                gather(1, NG - 1)
                scatter(0, NG - 2)
                scatter(1, NG - 1)
                for j in range(G):
                    pool.wait_ge(added[j], (NG + 2) * 16)

            @block.vector
            def _(dve):
                dve.sem_inc(same_done, 2 * G)
                dve.sem_inc(hid_done, 2)

                def indices(b, g):
                    nc.vector.tensor_copy(gi[:, b, :], src_idx[:, ds(g * G, G)]).then_inc(idx_done, 1)

                def compare(b, g, i):
                    dve.wait_ge(row_in[b], 16 * (i + 1))
                    if make_rows:
                        sum_rows(b, g)
                    dve.wait_ge(mm, upto(g, G - 1, back=2))
                    for j in range(G):
                        args = (weight[:, ds(g * G + j, 1)], ALU.is_equal, ALU.mult) if weight is not None else (None, ALU.is_equal)
                        nc.vector.tensor_scalar(same[:, b, j, :], rows[:, b, j * P:(j + 1) * P], k.dst_f[:, ds(g * G + j, 1)], *args).then_inc(same_done, 1)

                def pick_rows(b, g, n):
                    dve.wait_ge(lo_in[b], 16 * n)
                    dve.wait_ge(sc_mm, 2 * g + 2)
                    nc.vector.tensor_scalar(pick[:, b, :], lo_rows[:, b, :], k.ramp_p[:], None, ALU.is_equal).then_inc(pick_done, 1)
                    nc.vector.tensor_tensor(in_tile[:, b, :, :], k.dst_hi[:, ds(g * G, G)].unsqueeze(2).to_broadcast([P, G, NT]),
                                            k.ramp_t[:].unsqueeze(1).to_broadcast([P, G, NT]), ALU.is_equal).then_inc(chain, 1)

                def messages(b, g, i):
                    dve.wait_ge(msg_in[b], 16 * G * (i + 1))
                    if att:
                        c0 = 8 * g
                        dve.wait_ge(sc_mm, 2 * g + 6)
                        dve.wait_ge(chain, g + 1)
                        for q in range(2):
                            nc.vector.tensor_tensor(picked[:, 2 * q * heads:2 * (q + 1) * heads, :].rearrange("p (j h) t -> p j h t", j=2),
                                                    ps_s[:, b, q, 0:2 * HT].rearrange("p (j h t) -> p j h t", j=2, t=NT),
                                                    in_tile[:, b, 2 * q:2 * q + 2, :].unsqueeze(2).to_broadcast([P, 2, heads, NT]), ALU.mult).then_inc(e_done, 1)
                        dve.wait_ge(e_done, c0 + 2)
                        nc.vector.tensor_reduce(s_dst[:].rearrange("p g h -> p (g h)"), picked[:], AX_X, ALU.add).then_inc(e_done, 1)
                        dve.wait_ge(e_done, c0 + 3)
                        nc.vector.tensor_tensor(e1[:, :, 0, :], msg[:, b, :, D:D + heads], s_dst[:], ALU.add).then_inc(e_done, 1)
                        nc.vector.tensor_tensor(e1[:, :, 1, :], top[:].unsqueeze(1).to_broadcast([P, G, heads]), s_dst[:], ALU.add).then_inc(e_done, 1)
                        dve.wait_ge(e_done, c0 + 5)
                        nc.vector.scalar_tensor_tensor(e2[:], e1[:], 0.2, e1[:], ALU.mult, ALU.max).then_inc(e_done, 1)
                        dve.wait_ge(e_done, c0 + 6)
                        nc.vector.tensor_tensor(e[:, b, :, :], e2[:, :, 0, :], e2[:, :, 1, :], ALU.subtract).then_inc(e_done, 1)
                        dve.wait_ge(e_done, c0 + 7)
                        dve.sem_inc(e_done, 1)
                        dve.wait_ge(a_done, g + 1)
                        for j in range(G):
                            m = msg[:, b, j, 0:D].rearrange("p (h d) -> p h d", h=heads)
                            nc.vector.tensor_tensor(m, m, msg[:, b, j, D:D + heads].unsqueeze(2).to_broadcast([P, heads, HD]), ALU.mult).then_inc(ready, 1)
                    if mlp:
                        for j in range(G):
                            dve.wait_ge(fil_mm, g * G + (j | 1) + 1)
                            nc.vector.tensor_tensor(fil[:, j, :], ps_f[:, j, :], b2[:], ALU.add).then_inc(fil_used, 1)
                        for j in range(G):
                            dve.wait_ge(fil_used, g * G + j + 1 + G)
                            nc.vector.tensor_tensor(msg[:, b, j, :], msg[:, b, j, :], fil[:, j, :], ALU.mult).then_inc(ready, 1)

                def shifted(b, g):
                    dve.wait_ge(hid_ln, 2 * g + 2)
                    nc.vector.scalar_tensor_tensor(hs[:, b, :, :], hid[:, b, :, :], -math.log(2.0), pos[:, b, :, :], ALU.add, ALU.add).then_inc(hid_done, 1)

                def sum_rows(b, g):
                    for j in range(G):
                        nc.vector.scalar_tensor_tensor(hits[:, j, :], rows[:, b, j * P:(j + 1) * P], k.dst_f[:, ds(g * G + j, 1)], before[:], ALU.is_equal, ALU.mult).then_inc(chain, 1)
                    dve.wait_ge(chain, 8 * g + 4)
                    nc.vector.tensor_reduce(prior[:], hits[:], AX_X, ALU.add).then_inc(chain, 1)
                    dve.wait_ge(chain, 8 * g + 5)
                    nc.vector.tensor_scalar(prior[:], prior[:], 0.0, None, ALU.is_equal).then_inc(chain, 1)
                    dve.wait_ge(chain, 8 * g + 6)
                    nc.vector.scalar_tensor_tensor(row[:], k.dst_f[:, ds(g * G, G)], pad[:], prior[:], ALU.subtract, ALU.mult).then_inc(chain, 1)
                    dve.wait_ge(chain, 8 * g + 7)
                    nc.vector.tensor_scalar(k.row_i[:, ds(g * G, G)], row[:], pad[:], None, ALU.add).then_inc(rows_made, 1)
                    dve.wait_ge(rows_made, g + 1)
                    dve.sem_inc(chain, 1)

                def one_hots(b, g):
                    dve.wait_ge(counted, g + 1)
                    for hots, ramp, which, n in ((hot_row, ramp_row, sources[1], P), (hot_tile, k.ramp_t, sources[0], NT)):
                        ins = nc.vector.tensor_tensor(hots[:, b, :, :], which[:, ds(g * G, G)].unsqueeze(2).to_broadcast([P, G, n]),
                                                      ramp[:].unsqueeze(1).to_broadcast([P, G, n]), ALU.is_equal)
                    ins.then_inc(hot, 1)

                def turn(b, g, i, ahead, first=False):
                    if not (att or mlp or first):
                        dve.wait_ge(msg_in[1 - b], 16 * G * (i + b))
                    indices(1 - b, g + 1)
                    if mlp and ahead:
                        shifted(1 - b, g + 1)
                    if att and ahead:
                        pick_rows(1 - b, g + 1, i + 1 + b)
                    compare(b, g, i)
                    if sources:
                        one_hots(b, g)
                    if att or mlp:
                        messages(b, g, i)

                if make_rows:
                    dve.wait_ge(ramps, 3)
                if sources:
                    dve.wait_ge(ramped, 2)
                indices(0, 0)
                if mlp:
                    dve.wait_ge(w_in, 64)
                    shifted(0, 0)
                if att:
                    dve.sem_inc(pick_done, 2)
                    pick_rows(0, 0, 1)
                last = NG // 2 - 1
                for b in range(2):
                    turn(b, b, 0, True, first=b == 0)
                with dve.Fori(1, last) as i:
                    for b in range(2):
                        turn(b, i * 2 + b, i, True)
                for b in range(2):
                    turn(b, last * 2 + b, last, b == 0)
                if sources:
                    dve.wait_ge(counted, NG + 3)
                    nc.vector.tensor_copy(k.degree[:], ps_n[:, 0:NT])

            @block.tensor
            def _(pe):
                pe.sem_inc(mm, 2 * G)
                if mlp:
                    pe.sem_inc(hid_mm, 4)
                    pe.wait_ge(w_in, 64)

                def hidden(b, g, n):
                    pe.wait_ge(attr_in[b], 16 * n)
                    for c in range(2):
                        pe.wait_ge(hid_act, 2 * g + c + 1)
                        nc.tensor.matmul(ps_h[:, c, 0:G * P], w1[:, c * 128:(c + 1) * 128], attr[:, b, :], start=True, stop=True).then_inc(hid_mm, 1)

                def filters(b, g):
                    pe.wait_ge(hid_done, g + 3)
                    for j in range(G):
                        pe.wait_ge(fil_used, g * G + (j | 1) + 1)
                        nc.tensor.matmul(ps_f[:, j, :], hs[:, b, 0, j * P:(j + 1) * P], w2[:, 0, :], start=True, stop=False)
                        nc.tensor.matmul(ps_f[:, j, :], hs[:, b, 1, j * P:(j + 1) * P], w2[:, 1, :], start=False, stop=True).then_inc(fil_mm, 1)

                def target_scores(b, g):
                    pe.wait_ge(pick_done, g + 3)
                    for q in range(2):
                        for j in (2 * q, 2 * q + 1):
                            ins = nc.tensor.matmul(ps_s[:, b, q, (j % 2) * HT:(j % 2 + 1) * HT], pick[:, b, j * P:(j + 1) * P], tgt[:].rearrange("p h t -> p (h t)"),
                                                   start=True, stop=True)
                        ins.then_inc(sc_mm, 1)

                def sums(b, g, i):
                    pe.wait_ge(msg_in[b], 16 * G * (i + 1))
                    for j in range(G):
                        pe.wait_ge(same_done, upto(g, j))
                        if att or mlp:
                            pe.wait_ge(ready, upto(g, j) - G)
                        pe.wait_ge(z_done, upto(g, j, back=1))
                        nc.tensor.matmul(ps[:, j, 0:width], same[:, b, j, :], msg[:, b, j, :], start=True, stop=True).then_inc(mm, 1)

                last = NG // 2 - 1
                if att:
                    pe.sem_inc(sc_mm, 4)
                if mlp:
                    hidden(0, 0, 1)
                    hidden(1, 1, 1)
                    filters(0, 0)
                    with pe.Fori(0, last) as i:
                        for b in range(2):
                            g = i * 2 + b
                            hidden(b, g + 2, i + 2)
                            sums(b, g, i)
                            filters(1 - b, g + 1)
                    sums(0, NG - 2, last)
                    filters(1, NG - 1)
                    sums(1, NG - 1, last)
                elif att:
                    target_scores(0, 0)
                    with pe.Fori(0, last) as i:
                        for b in range(2):
                            target_scores(1 - b, i * 2 + b + 1)
                            sums(b, i * 2 + b, i)
                    target_scores(1, NG - 1)
                    sums(0, NG - 2, last)
                    sums(1, NG - 1, last)
                else:
                    if sources:
                        pe.sem_inc(counted, 2)
                        pe.wait_ge(ramped, 2)
                        nc.tensor.matmul(ps_n[:, 0:NT], none[:], none[:, 0:NT], start=True, stop=False)
                    with pe.Fori(0, NG // 2) as i:
                        for b in range(2):
                            sums(b, i * 2 + b, i)
                            if sources:
                                pe.wait_ge(hot, i * 2 + b + 1)
                                for j in range(G):
                                    ins = nc.tensor.matmul(ps_n[:, 0:NT], hot_row[:, b, j, :], hot_tile[:, b, j, :], start=False, stop=False)
                                ins.then_inc(counted, 1)
                    if sources:
                        nc.tensor.matmul(ps_n[:, 0:NT], none[:], none[:, 0:NT], start=False, stop=True).then_inc(counted, 1)

            @block.scalar
            def _(act):
                act.sem_inc(z_done, 2 * G)
                act.sem_inc(ready, G)
                act.sem_inc(hid_act, 2)
                act.sem_inc(fil_used, G)

                def weights(b, g):
                    act.wait_ge(e_done, 8 * g + 8)
                    nc.scalar.activation(msg[:, b, :, D:D + heads], e[:, b, :, :], ACT.Exp).then_inc(a_done, 1)

                def hidden(b, g):
                    act.wait_ge(hid_done, g + 1)
                    for c in range(2):
                        act.wait_ge(hid_mm, 2 * g + c + 5)
                        nc.scalar.activation(pos[:, b, c, :], ps_h[:, c, 0:G * P], ACT.Relu, bias=b1[:, c:c + 1])
                        nc.scalar.activation(hid[:, b, c, :], ps_h[:, c, 0:G * P], ACT.Abs, bias=b1[:, c:c + 1]).then_inc(hid_act, 1)
                    act.wait_ge(hid_act, 2 * g + 4)
                    nc.scalar.activation(hid[:, b, :, :], hid[:, b, :, :], ACT.Exp, scale=-1.0).then_inc(hid_ln, 1)
                    act.wait_ge(hid_ln, 2 * g + 1)
                    nc.scalar.activation(hid[:, b, :, :], hid[:, b, :, :], ACT.Ln, bias=1.0).then_inc(hid_ln, 1)

                if mlp:
                    act.wait_ge(w_in, 64)

                def leave(b, g):
                    for j in range(G):
                        act.wait_ge(added[j], (g + 1) * 16)
                    if make_rows:
                        act.wait_ge(rows_made, g + 1)
                    nc.scalar.activation(si[:, b, :], k.row_i[:, ds(g * G, G)], ACT.Copy).then_inc(si_done, 1)
                    for j in range(G):
                        act.wait_ge(mm, upto(g, j))
                        nc.scalar.activation(z[:, b, j, :], ps[:, j, 0:width], ACT.Copy).then_inc(z_done, 1)

                if mlp:
                    hidden(0, 0)
                    hidden(1, 1)
                last = NG // 2 - 1
                with act.Fori(0, last) as i:
                    for b in range(2):
                        g = i * 2 + b
                        if att:
                            weights(b, g)
                        if mlp:
                            hidden(b, g + 2)
                        leave(b, g)
                for b in range(2):
                    g = last * 2 + b
                    if att:
                        weights(b, g)
                    leave(b, g)


def collect(k, agg, width):
    nc = k.nc
    with stage(k) as s:
        part = s.sb("part", [P, 5, G, width])
        pair = s.sb("pair", [P, 5, 2, width])
        part_in = [s.sem(f"part_in{j}") for j in range(5)]
        paired, summed = s.sem("paired"), s.sem("summed")
        acc = [q.rearrange("(t p) f -> t p f", p=P) for q in k.acc[width]]
        with s.block() as block:
            def load(eng, which):
                for t in range(NT):
                    if t >= 5:
                        eng.wait_ge(paired, t - 4)
                    for j in which:
                        eng.dma_start(part[:, t % 5, j, :], acc[j][t, :, :]).then_inc(part_in[t % 5], 16)

            @block.sync
            def _(sp):
                load(sp, (0, 1))

            @block.scalar
            def _(act):
                load(act, (2, 3))

            @block.vector
            def _(dve):
                for t in range(NT):
                    j = t % 5
                    dve.wait_ge(part_in[j], 16 * G * (t // 5 + 1))
                    nc.vector.tensor_tensor(pair[:, j, :, :], part[:, j, 0:2, :], part[:, j, 2:4, :], ALU.add).then_inc(paired, 1)
                    dve.wait_ge(paired, t + 1)
                    if agg is not None:
                        nc.vector.tensor_tensor(agg[:, t, 0:width], pair[:, j, 0, :], pair[:, j, 1, :], ALU.add).then_inc(summed, 1)
                    else:
                        nc.vector.tensor_tensor(pair[:, j, 0, :], pair[:, j, 0, :], pair[:, j, 1, :], ALU.add).then_inc(summed, 1)
                        dve.wait_ge(summed, t + 1)
                        nc.vector.tensor_tensor(k.x[:, t, :], k.x[:, t, :], pair[:, j, 0, :], ALU.add)


def add_to_x(k, agg):
    nc = k.nc
    with stage(k) as s:
        done = s.sem("done")
        with s.block() as block:
            @block.vector
            def _(dve):
                nc.vector.tensor_tensor(k.x[:], k.x[:], agg[:], ALU.add).then_inc(done, 1)


def first_of_max(nc, dve, c, score, best, onehot, ramp, tmp, pick):
    L = score.shape[-1]
    wide = lambda a: a.unsqueeze(2).to_broadcast([P, NT, L])
    c.link(nc.vector.tensor_reduce(best, score, AX_X, ALU.max))
    c.link(nc.vector.tensor_tensor(tmp, score, wide(best), ALU.is_equal))
    c.link(nc.vector.tensor_tensor(tmp, tmp, ramp, ALU.mult))
    c.link(nc.vector.tensor_reduce(pick, tmp, AX_X, ALU.max))
    c.link(nc.vector.tensor_tensor(onehot, ramp, wide(pick), ALU.is_equal))


def gates(k, cols, gate, n_exp, w, bias, mode, router=None, scores=None, choice=None):
    nc = k.nc
    L = n_exp
    with stage(k) as s:
        sb3 = lambda n: s.sb(n, [P, NT, L])
        lg, tmp, oh1, oh2, rest = (sb3(n) for n in ("lg", "tmp", "oh1", "oh2", "rest"))
        ramp = s.sb("ramp", [P, NT, L])
        m1, m2, pick, w1, w2 = (s.sb(n, [P, NT]) for n in ("m1", "m2", "pick", "w1", "w2"))
        w_sb, b_sb = s.sb("w", [128, 2, L]), s.sb("b", [P, L])
        ps = s.ps("ps", [P, 512])
        w_in, mm, ramps, chain, to_act, from_act = (s.sem(n) for n in ("w_in", "mm", "ramps", "chain", "to_act", "from_act"))
        if router:
            rw1, rb1, rw2 = s.sb("rw1", [128, 2, 128]), s.sb("rb1", [128, 1]), s.sb("rw2", [128, L])
            rh = s.sb("rh", [128, N])
            ps_r = s.ps("ps_r", [128, 4, 512])
            r_mm, r_act = s.sem("r_mm"), s.sem("r_act")
        with s.block() as block:
            @block.sync
            def _(sp):
                if scores is None:
                    sp.dma_start(b_sb[:], bias.partition_broadcast(P)).then_inc(w_in, 16)
                if router:
                    sp.dma_start(rw1[:], router.w1.rearrange("(c p) h -> p c h", p=128)).then_inc(w_in, 16)
                    sp.dma_start(rb1[:], router.b1.rearrange("(p a) -> p a", a=1)).then_inc(w_in, 16)
                    sp.dma_start(rw2[:], router.w2).then_inc(w_in, 16)
                elif scores is None:
                    sp.dma_start(w_sb[:], w.rearrange("(c p) e -> p c e", p=128)).then_inc(w_in, 16)

            @block.gpsimd
            def _(pool):
                nc.gpsimd.iota(ramp[:], [[0, NT], [-1, L]], base=L, channel_multiplier=0, allow_small_or_imprecise_dtypes=True).then_inc(ramps, 1)

            @block.tensor
            def _(pe):
                if scores is None:
                    pe.wait_ge(w_in, 64 if router else 32)
                if router:
                    for q, n0 in enumerate(range(0, N, 500)):
                        m = min(500, N - n0)
                        if q >= 4:
                            pe.wait_ge(r_act, q - 3)
                        nc.tensor.matmul(ps_r[:, q % 4, 0:m], rw1[:, 0, :], cols[:, 0, n0:n0 + m], start=True, stop=False)
                        nc.tensor.matmul(ps_r[:, q % 4, 0:m], rw1[:, 1, :], cols[:, 1, n0:n0 + m], start=False, stop=True).then_inc(r_mm, 1)
                    pe.wait_ge(r_act, (N + 499) // 500)
                    for t in range(NT):
                        ins = nc.tensor.matmul(ps[:, t * L:(t + 1) * L], rh[:, t * P:(t + 1) * P], rw2[:], start=True, stop=True)
                    ins.then_inc(mm, 1)
                elif scores is None:
                    for t in range(NT):
                        nc.tensor.matmul(ps[:, t * L:(t + 1) * L], cols[:, 0, t * P:(t + 1) * P], w_sb[:, 0, :], start=True, stop=False)
                        ins = nc.tensor.matmul(ps[:, t * L:(t + 1) * L], cols[:, 1, t * P:(t + 1) * P], w_sb[:, 1, :], start=False, stop=True)
                    ins.then_inc(mm, 1)
            @block.scalar
            def _(act):
                if router:
                    act.wait_ge(w_in, 64)
                    for q, n0 in enumerate(range(0, N, 500)):
                        m = min(500, N - n0)
                        act.wait_ge(r_mm, q + 1)
                        nc.scalar.activation(rh[:, n0:n0 + m], ps_r[:, q % 4, 0:m], ACT.Relu, bias=rb1[:]).then_inc(r_act, 1)
                n = 0
                if mode != "top2":
                    act.wait_ge(to_act, 1)
                    nc.scalar.activation(lg[:], tmp[:], ACT.Exp).then_inc(from_act, 1)
                    n = 1
                if mode != "top1":
                    act.wait_ge(to_act, n + 1)
                    nc.scalar.activation(w2[:], pick[:], ACT.Exp).then_inc(from_act, 1)

            @block.vector
            def _(dve):
                c = Chain(dve, chain)
                wide = lambda a: a.unsqueeze(2).to_broadcast([P, NT, L])
                dve.wait_ge(ramps, 1)
                acts = 0
                score = lg[:]
                if scores is None:
                    dve.wait_ge(mm, 1)
                    dve.wait_ge(w_in, 64 if router else 32)
                    c.link(nc.vector.tensor_tensor(lg[:], ps[:, 0:NT * L].rearrange("p (t e) -> p t e", e=L),
                                                   b_sb[:].unsqueeze(1).to_broadcast([P, NT, L]), ALU.add))
                else:
                    score = scores
                if mode != "top2":
                    c.link(nc.vector.tensor_reduce(m1[:], lg[:], AX_X, ALU.max))
                    nc.vector.tensor_tensor(tmp[:], lg[:], wide(m1[:]), ALU.subtract).then_inc(to_act, 1)
                    acts += 1
                    dve.wait_ge(from_act, acts)
                    c.link(nc.vector.tensor_reduce(m2[:], lg[:], AX_X, ALU.add))
                    c.link(nc.vector.reciprocal(w1[:], m2[:]))
                    c.link(nc.vector.tensor_tensor(lg[:], lg[:], wide(w1[:]), ALU.mult))
                first_of_max(nc, dve, c, score, m1[:], oh1[:], ramp[:], tmp[:], pick[:])
                if mode == "top1":
                    c.step(nc.vector.tensor_copy(choice[0][:, 0, :, :], oh1[:]))
                    c.link(nc.vector.tensor_copy(choice[1][:, 0, :], m1[:]))
                    return
                c.link(nc.vector.tensor_scalar(tmp[:], oh1[:], -3.0e38, None, ALU.mult))
                c.link(nc.vector.tensor_tensor(rest[:], score, tmp[:], ALU.add))
                first_of_max(nc, dve, c, rest[:], m2[:], oh2[:], ramp[:], tmp[:], pick[:])
                nc.vector.tensor_tensor(pick[:], m2[:], m1[:], ALU.subtract).then_inc(to_act, 1)
                acts += 1
                dve.wait_ge(from_act, acts)
                c.link(nc.vector.tensor_scalar(w1[:], w2[:], 1.0, None, ALU.add))
                c.link(nc.vector.reciprocal(w1[:], w1[:]))
                c.link(nc.vector.tensor_tensor(w2[:], w2[:], w1[:], ALU.mult))
                if choice is not None:
                    for q, (oh, wt) in enumerate(((oh1, w1), (oh2, w2))):
                        c.step(nc.vector.tensor_copy(choice[0][:, q, :, :], oh[:]))
                        c.link(nc.vector.tensor_copy(choice[1][:, q, :], wt[:]))
                    return
                c.link(nc.vector.tensor_tensor(oh1[:], oh1[:], wide(w1[:]), ALU.mult))
                c.link(nc.vector.tensor_tensor(oh2[:], oh2[:], wide(w2[:]), ALU.mult))
                c.link(nc.vector.tensor_tensor(gate[:], oh1[:], oh2[:], ALU.add))


BR = 250


def most_blocks(chosen, n_exp, rows=N):
    return (chosen * rows + n_exp * (BR - 1)) // BR


def route(k, choice, slot_i, block_i, n_exp, chosen, blocks, capacity=None):
    nc = k.nc
    L = n_exp
    oh, wt = choice
    with stage(k) as s:
        total = s.sb("total", [P, NT, L])
        tot, pos, part = s.sb("tot", [P, NT + 1, L]), s.sb("pos", [P, NT, L]), s.sb("part", [P, NT, L])
        cnt, nb, end, start, ones = (s.sb(n, [P, L]) for n in ("cnt", "nb", "end", "start", "one"))
        slot = s.sb("slot", [P, NT])
        kept = s.sb("kept", [P, NT])
        pad = s.sb("pad", [P, 1])
        tri = s.sb("tri", [P, P])
        ramp_b = s.sb("ramp_b", [1, blocks, L])
        past = s.sb("past", [1, blocks, L])
        owner = s.sb("owner", [1, blocks])
        ps_pre, ps_tot = s.ps("pre", [P, 512]), s.ps("tot", [P, 512])
        made, chain, summed, mm = s.sem("made"), s.sem("chain"), s.sem("summed"), s.sem("mm")
        with s.block() as block:
            @block.gpsimd
            def _(pool):
                nc.gpsimd.memset(tri[:], 1.0).then_inc(made, 1)
                pool.wait_ge(made, 1)
                nc.gpsimd.affine_select(out=tri[:], in_=tri[:], compare_op=ALU.is_gt, fill=0.0, base=0,
                                        pattern=[[1, P]], channel_multiplier=-1).then_inc(made, 1)
                nc.gpsimd.iota(pad[:], [[0, 1]], base=blocks * BR, channel_multiplier=0, allow_small_or_imprecise_dtypes=True).then_inc(made, 1)
                nc.gpsimd.iota(ramp_b[:], [[1, blocks], [0, L]], base=0, channel_multiplier=0, allow_small_or_imprecise_dtypes=True).then_inc(made, 1)

            @block.tensor
            def _(pe):
                pe.wait_ge(made, 2)
                pe.wait_ge(summed, 1)
                flat = total[:].rearrange("p t e -> p (t e)")
                nc.tensor.matmul(ps_pre[:, 0:NT * L], tri[:], flat, start=True, stop=True)
                nc.tensor.matmul(ps_tot[:, 0:NT * L], k.ones[0:P, 0:P], flat, start=True, stop=True).then_inc(mm, 1)

            @block.vector
            def _(dve):
                c = Chain(dve, chain)
                as_te = lambda q: q[:, 0:NT * L].rearrange("p (t e) -> p t e", e=L)
                if chosen == 2:
                    nc.vector.tensor_tensor(total[:], oh[:, 0, :, :], oh[:, 1, :, :], ALU.add).then_inc(summed, 1)
                else:
                    nc.vector.tensor_copy(total[:], oh[:, 0, :, :]).then_inc(summed, 1)
                c.step(nc.vector.memset(tot[:, 0, :], 0.0))
                c.step(nc.vector.memset(nb[:], 0.0))
                c.step(nc.vector.memset(ones[:], 1.0))
                dve.wait_ge(mm, 1)
                c.link(nc.vector.tensor_copy(tot[:, 1:NT + 1, :], as_te(ps_tot)))
                for t in range(1, NT + 1):
                    c.link(nc.vector.tensor_tensor(tot[:, t, :], tot[:, t, :], tot[:, t - 1, :], ALU.add))
                c.step(nc.vector.tensor_tensor(pos[:], as_te(ps_pre), tot[:, 0:NT, :], ALU.add))
                c.link(nc.vector.tensor_scalar(cnt[:], tot[:, NT, :], float(capacity or N), None, ALU.min))
                for m in range((N + BR - 1) // BR):
                    c.link(nc.vector.scalar_tensor_tensor(nb[:], cnt[:], float(BR * m), nb[:], ALU.is_gt, ALU.add))
                c.link(nc.vector.tensor_tensor_scan(end[:], ones[:], nb[:], 0.0, ALU.mult, ALU.add))
                c.link(nc.vector.tensor_tensor(start[:], end[:], nb[:], ALU.subtract))
                c.link(nc.vector.tensor_scalar(start[:], start[:], float(BR), None, ALU.mult))
                dve.wait_ge(made, 4)
                if capacity:
                    c.link(nc.vector.tensor_scalar(part[:], pos[:], float(capacity), None, ALU.is_lt))
                    c.link(nc.vector.tensor_tensor(part[:], part[:], oh[:, 0, :, :], ALU.mult))
                    c.link(nc.vector.tensor_reduce(kept[:], part[:], AX_X, ALU.add))
                    c.link(nc.vector.tensor_tensor(wt[:, 0, :], wt[:, 0, :], kept[:], ALU.mult))
                c.link(nc.vector.tensor_tensor(pos[:], pos[:], start[:].unsqueeze(1).to_broadcast([P, NT, L]), ALU.add))
                for q in range(chosen):
                    c.link(nc.vector.tensor_tensor(part[:], pos[:], oh[:, q, :, :], ALU.mult))
                    c.link(nc.vector.tensor_reduce(slot[:], part[:], AX_X, ALU.add))
                    if capacity:
                        c.link(nc.vector.tensor_scalar(slot[:], slot[:], pad[:], None, ALU.subtract))
                        c.link(nc.vector.tensor_tensor(slot[:], slot[:], kept[:], ALU.mult))
                        c.link(nc.vector.tensor_scalar(slot[:], slot[:], pad[:], None, ALU.add))
                    c.link(nc.vector.tensor_copy(slot_i[:, q, :], slot[:]))
                c.link(nc.vector.tensor_tensor(past[:], ramp_b[:], end[0:1, :].unsqueeze(1).to_broadcast([1, blocks, L]), ALU.is_ge))
                c.link(nc.vector.tensor_reduce(owner[:], past[:], AX_X, ALU.add))
                c.link(nc.vector.tensor_scalar(block_i[:], owner[:], float(L - 1), None, ALU.min))


def send_rows(k, rows, table, slot_i, chosen, blocks):
    nc = k.nc
    with stage(k) as s:
        moved = s.sem("moved")
        with s.block() as block:
            @block.gpsimd
            def _(pool):
                for q in range(chosen):
                    for t in range(NT):
                        nc.gpsimd.indirect_dma_start(table, bass.IndirectOffsetOnAxis(slot_i[:, q, t:t + 1], 0), rows[:, t, :], None,
                                                         bounds_check=blocks * BR - 1, oob_is_err=False).then_inc(moved, 16)
                pool.wait_ge(moved, 16 * NT * chosen)


def fetch_rows(k, acc, table, slot_i, wt, chosen):
    nc = k.nc
    RING = 6
    with stage(k) as s:
        got = s.sb("got", [P, RING, D])
        got_in = [s.sem(f"got_in{j}") for j in range(RING)]
        used = s.sem("used")
        with s.block() as block:
            @block.gpsimd
            def _(pool):
                for n in range(NT * chosen):
                    t, q = n // chosen, n % chosen
                    if n >= RING:
                        pool.wait_ge(used, n - RING + 1)
                    nc.gpsimd.indirect_dma_start(got[:, n % RING, :], None, table, bass.IndirectOffsetOnAxis(slot_i[:, q, t:t + 1], 0)).then_inc(got_in[n % RING], 16)

            @block.vector
            def _(dve):
                for n in range(NT * chosen):
                    t, q = n // chosen, n % chosen
                    dve.wait_ge(got_in[n % RING], 16 * (n // RING + 1))
                    if q == 0 and acc is not k.x:
                        ins = nc.vector.tensor_scalar(acc[:, t, :], got[:, n % RING, :], wt[:, q, t:t + 1], None, ALU.mult)
                    else:
                        if n:
                            dve.wait_ge(used, n)
                        ins = nc.vector.scalar_tensor_tensor(acc[:, t, :], got[:, n % RING, :], wt[:, q, t:t + 1], acc[:, t, :], ALU.mult, ALU.add)
                    ins.then_inc(used, 1)


def block_experts(k, table, result, block_i, x, blocks):
    nc = k.nc
    FC = x.f // 128
    FM = 2 if x.wm is not None else 0
    EV = FC + FM
    TB = BR // P
    SEMS = 6 if FM else 4
    with stage(k) as s:
        rows = s.sb("rows", [P, 2, TB, D])
        xT = s.sb("xT", [128, 2, 2, BR])
        w1, w2 = s.sb("w1", [128, 2, 2, x.f]), s.sb("w2", [128, 2, FM or FC, D])
        b1, b2 = s.sb("b1", [128, 2, FC]), s.sb("b2", [P, 2, D])
        hid = s.sb("hid", [128, FC, BR])
        y = s.sb("y", [P, 2, TB, D])
        zero = s.sb("zero", [P, D])
        if FM:
            wm, bm, mid = s.sb("wm", [128, 2, 2, D]), s.sb("bm", [128, 2, FM]), s.sb("mid", [128, FM, BR])
        ps_t, ps_h, ps_o = s.ps("ps_t", [128, 2, 512]), s.ps("ps_h", [128, 4, 512]), s.ps("ps_o", [P, 2, 512])
        w_in, rows_in, stored = ([s.sem(n + "0"), s.sem(n + "1")] for n in ("w_in", "rows_in", "stored"))
        t_mm, t_ev, h_mm, h_sb, o_mm, o_done, made, turns = (s.sem(n) for n in ("t_mm", "t_ev", "h_mm", "h_sb", "o_mm", "o_done", "made", "turns"))
        with s.block() as block:
            @block.sync
            def _(sp):
                def load_rows(buf, c):
                    sp.wait_ge(t_mm, c + 1)
                    sp.dma_start(rows[:, buf, :, :], table[ds(c * BR, BR), :].rearrange("(t p) f -> p t f", p=P)).then_inc(rows_in[buf], 16)

                load_rows(0, 0)
                with sp.Fori(0, blocks // 2) as i:
                    for b in range(2):
                        n = i * 2 + b
                        e = sp.value_load(block_i[0:1, ds(n, 1)], min_val=0, max_val=x.n - 1)
                        load_rows(1 - b, n + 1)
                        sp.wait_ge(o_done, 2 * n + 2)
                        sp.dma_start(w1[:, b, :, :], x.w1[ds(e, 1)].rearrange("e (c p) f -> p (e c) f", p=128)).then_inc(w_in[b], 16)
                        sp.dma_start(b1[:, b, :], x.b1[ds(e * 128, 128), :]).then_inc(w_in[b], 16)
                        if FM:
                            sp.dma_start(wm[:, b, :, :], x.wm[ds(e, 1)].rearrange("e (c p) f -> p (e c) f", p=128)).then_inc(w_in[b], 16)
                            sp.dma_start(bm[:, b, :], x.bm[ds(e * 128, 128), :]).then_inc(w_in[b], 16)
                        sp.dma_start(w2[:, b, :, :], x.w2[ds(e, 1)].rearrange("e (c p) f -> p (e c) f", p=128)).then_inc(w_in[b], 16)
                        sp.dma_start(b2[:, b, :], x.b2[ds(e * D, D)].partition_broadcast(P)).then_inc(w_in[b], 16)

            @block.tensor
            def _(pe):
                pe.sem_inc(t_mm, 2)

                def turn(buf, c, i):
                    pe.wait_ge(rows_in[buf], i)
                    pe.wait_ge(t_ev, c + 1)
                    for t in range(TB):
                        for half in range(2):
                            ins = nc.tensor.transpose(ps_t[:, buf, half * BR + t * P:half * BR + (t + 1) * P], rows[:, buf, t, half * 128:(half + 1) * 128], k.ident[0:P, 0:P])
                    ins.then_inc(t_mm, 1)

                def layer(n0, lhs, rhs, count, chunks):
                    for f in range(count):
                        pe.wait_ge(h_sb, n0 + f + 1)
                        for c in range(chunks):
                            ins = nc.tensor.matmul(ps_h[:, f % 4, 0:BR], lhs(c, f), rhs(c), start=c == 0, stop=c == chunks - 1)
                        ins.then_inc(h_mm, 1)

                turn(0, 0, 16)
                with pe.Fori(0, blocks // 2) as i:
                    for b in range(2):
                        n = i * 2 + b
                        pe.wait_ge(w_in[b], 16 * SEMS * (i + 1))
                        pe.wait_ge(t_ev, n + 3)
                        layer(n * EV, lambda c, f: w1[:, b, c, f * 128:(f + 1) * 128], lambda c: xT[:, b, c, :], FC, 2)
                        turn(1 - b, n + 1, 16 * i + 16 * (b + 1))
                        last, n_last = hid, FC
                        if FM:
                            pe.wait_ge(h_sb, n * EV + FC + 4)
                            layer(n * EV + FC, lambda c, f: wm[:, b, c, f * 128:(f + 1) * 128], lambda c: hid[:, c, :], FM, FC)
                            last, n_last = mid, FM
                        pe.wait_ge(h_sb, n * EV + EV + 4)
                        for t in range(TB):
                            pe.wait_ge(o_done, 2 * n + t + 3)
                            for c in range(n_last):
                                ins = nc.tensor.matmul(ps_o[:, t, 0:D], last[:, c, t * P:(t + 1) * P], w2[:, b, c, :], start=c == 0, stop=c == n_last - 1)
                            ins.then_inc(o_mm, 1)

            @block.scalar
            def _(act):
                act.sem_inc(h_sb, 4)
                with act.Fori(0, blocks // 2) as i:
                    for b in range(2):
                        n = i * 2 + b
                        act.wait_ge(w_in[b], 16 * SEMS * (i + 1))
                        for f in range(EV):
                            act.wait_ge(h_mm, n * EV + f + 1)
                            if f < FC:
                                ins = nc.scalar.activation(hid[:, f, :], ps_h[:, f % 4, 0:BR], x.func, bias=b1[:, b, f:f + 1])
                            else:
                                ins = nc.scalar.activation(mid[:, f - FC, :], ps_h[:, (f - FC) % 4, 0:BR], x.func, bias=bm[:, b, f - FC:f - FC + 1])
                            ins.then_inc(h_sb, 1)

            @block.vector
            def _(dve):
                dve.sem_inc(t_ev, 2)
                dve.sem_inc(o_done, 4)
                nc.vector.memset(zero[:], 0.0).then_inc(made, 1)

                def columns(buf, c):
                    dve.wait_ge(t_mm, c + 3)
                    nc.vector.tensor_copy(xT[:, buf, :, :], ps_t[:, buf, 0:2 * BR].rearrange("p (c n) -> p c n", c=2)).then_inc(t_ev, 1)

                columns(0, 0)
                with dve.Fori(0, blocks // 2) as i:
                    for b in range(2):
                        n = i * 2 + b
                        columns(1 - b, n + 1)
                        dve.wait_ge(w_in[b], 16 * SEMS * (i + 1))
                        dve.wait_ge(stored[b], 16 * (i + 1))
                        for t in range(TB):
                            dve.wait_ge(o_mm, 2 * n + t + 1)
                            nc.vector.tensor_tensor(y[:, b, t, :], ps_o[:, t, 0:D], b2[:, b, :], ALU.add).then_inc(o_done, 1)

            @block.gpsimd
            def _(pool):
                pool.wait_ge(made, 1)
                for b in range(2):
                    pool.dma_start(result[blocks * BR + b * P:blocks * BR + (b + 1) * P, :], zero[:]).then_inc(stored[b], 16)
                with pool.Fori(0, blocks // 2) as i:
                    for b in range(2):
                        n = i * 2 + b
                        pool.wait_ge(o_done, 2 * n + 6)
                        pool.sem_inc(turns, 1)
                        pool.dma_start(result[ds(n * BR, BR), :].rearrange("(t p) f -> p t f", p=P), y[:, b, :, :]).then_inc(stored[b], 16)
                for b in range(2):
                    pool.wait_ge(stored[b], 16 * (blocks // 2 + 1))


class Experts:

    def __init__(self, n, f, func, w1, b1, w2, b2, wm=None, bm=None):
        self.n, self.f, self.func, self.w1, self.b1, self.w2, self.b2, self.wm, self.bm = n, f, func, w1, b1, w2, b2, wm, bm


def experts(k, cols, gate, acc, x):
    nc = k.nc
    FC = x.f // 128
    FM = 2 if x.wm is not None else 0
    NB, TB = NT // 5, 5
    PARTS = ((0, 3 * P), (3 * P, 2 * P))
    UP, MID = 2 * FC, 2 * FM
    EV = UP + MID
    BU = 2 if x.n % 2 == 0 else 1
    with stage(k) as s:
        w1 = s.sb("w1", [128, 2, 2, x.f])
        w2 = s.sb("w2", [128, 2, FM or FC, D])
        b1 = s.sb("b1", [128, 2, FC])
        b2 = s.sb("b2", [P, 2, D])
        hid = s.sb("hid", [128, FC, TB * P])
        tmp = s.sb("tmp", [P, TB, D])
        ps_h = s.ps("ps_h", [128, 4, 512])
        ps_o = s.ps("ps_o", [P, 3, 512])
        if FM:
            wm, bm = s.sb("wm", [128, 2, 2, D]), s.sb("bm", [128, 2, FM])
            mid = s.sb("mid", [128, FM, TB * P])
        zeroed, h_mm, h_sb, o_mm, o_used, chain = (s.sem(n) for n in ("zeroed", "h_mm", "h_sb", "o_mm", "o_used", "chain"))
        w_in = [s.sem("w_in0"), s.sem("w_in1")]
        n_w = 6 if FM else 4
        pair_end = lambda j: min(j | 1, TB - 1)
        out_at = lambda j: ps_o[:, j // 2, (j % 2) * D:(j % 2 + 1) * D]
        with s.block() as block:
            @block.sync
            def _(sp):
                with sp.Fori(0, x.n // BU) as i:
                    for b in range(BU):
                        e = i * BU + b
                        sp.wait_ge(o_used, e * NT + TB)
                        sp.dma_start(w1[:, b, :, :], x.w1[ds(e, 1)].rearrange("e (c p) f -> p (e c) f", p=128)).then_inc(w_in[b], 16)
                        if FM:
                            sp.dma_start(wm[:, b, :, :], x.wm[ds(e, 1)].rearrange("e (c p) f -> p (e c) f", p=128)).then_inc(w_in[b], 16)
                        sp.dma_start(b1[:, b, :], x.b1[ds(e * 128, 128), :]).then_inc(w_in[b], 16)
                        if FM:
                            sp.dma_start(bm[:, b, :], x.bm[ds(e * 128, 128), :]).then_inc(w_in[b], 16)
                        sp.dma_start(w2[:, b, :, :], x.w2[ds(e, 1)].rearrange("e (c p) f -> p (e c) f", p=128)).then_inc(w_in[b], 16)
                        sp.dma_start(b2[:, b, :], x.b2[ds(e * D, D)].partition_broadcast(P)).then_inc(w_in[b], 16)

            @block.tensor
            def _(pe):
                def layer(nq, lhs, rhs, count, chunks_in):
                    n = 0
                    for f in range(count):
                        for q, (lo, m) in enumerate(PARTS):
                            pe.wait_ge(h_sb, nq + n + 1)
                            for c in range(chunks_in):
                                ins = nc.tensor.matmul(ps_h[:, n % 4, 0:m], lhs(c, f), rhs(c, lo, m), start=c == 0, stop=c == chunks_in - 1)
                            ins.then_inc(h_mm, 1)
                            n += 1

                with pe.Fori(0, x.n // BU) as i:
                    for b in range(BU):
                        e = i * BU + b
                        with pe.Fori(0, NB) as blk:
                            pe.wait_ge(w_in[b], 16 * n_w * (i + 1))
                            turn = e * NB + blk
                            layer(turn * EV, lambda c, f: w1[:, b, c, f * 128:(f + 1) * 128],
                                  lambda c, lo, m: cols[:, c, ds(blk * (TB * P) + lo, m)], FC, 2)
                            last, n_last = hid, FC
                            if FM:
                                pe.wait_ge(h_sb, turn * EV + UP + 4)
                                layer(turn * EV + UP, lambda c, f: wm[:, b, c, f * 128:(f + 1) * 128],
                                      lambda c, lo, m: hid[:, c, lo:lo + m], FM, FC)
                                last, n_last = mid, FM
                            pe.wait_ge(h_sb, turn * EV + EV + 4)
                            for j in range(TB):
                                pe.wait_ge(o_used, turn * TB + pair_end(j) + 1 + NT)
                                for c in range(n_last):
                                    ins = nc.tensor.matmul(out_at(j), last[:, c, j * P:(j + 1) * P], w2[:, b, c, :], start=c == 0, stop=c == n_last - 1)
                                ins.then_inc(o_mm, 1)

            @block.scalar
            def _(act):
                act.sem_inc(h_sb, 4)
                with act.Fori(0, x.n // BU) as i:
                    for b in range(BU):
                        e = i * BU + b
                        with act.Fori(0, NB) as blk:
                            act.wait_ge(w_in[b], 16 * n_w * (i + 1))
                            turn = e * NB + blk
                            n = 0
                            for f in range(FC):
                                for lo, m in PARTS:
                                    act.wait_ge(h_mm, turn * EV + n + 1)
                                    nc.scalar.activation(hid[:, f, lo:lo + m], ps_h[:, n % 4, 0:m], x.func, bias=b1[:, b, f:f + 1]).then_inc(h_sb, 1)
                                    n += 1
                            for f in range(FM):
                                for lo, m in PARTS:
                                    act.wait_ge(h_mm, turn * EV + n + 1)
                                    nc.scalar.activation(mid[:, f, lo:lo + m], ps_h[:, n % 4, 0:m], x.func, bias=bm[:, b, f:f + 1]).then_inc(h_sb, 1)
                                    n += 1

            @block.vector
            def _(dve):
                if acc is not k.x:
                    nc.vector.memset(acc[:], 0.0).then_inc(chain, 1)
                dve.sem_inc(o_used, NT + TB)
                with dve.Fori(0, x.n // BU) as i:
                    for b in range(BU):
                        e = i * BU + b
                        with dve.Fori(0, NB) as blk:
                            dve.wait_ge(w_in[b], 16 * n_w * (i + 1))
                            for j in range(TB):
                                t = blk * TB + j
                                n = e * NT + t
                                dve.wait_ge(o_mm, e * NT + blk * TB + pair_end(j) + 1)
                                nc.vector.tensor_tensor(tmp[:, j, :], out_at(j), b2[:, b, :], ALU.add).then_inc(o_used, 1)
                                dve.wait_ge(o_used, n + 1 + NT + TB)
                                nc.vector.scalar_tensor_tensor(acc[:, ds(t, 1), :].rearrange("p t f -> p (t f)"), tmp[:, j, :], gate[:, ds(t, 1), ds(e, 1)].rearrange("p t e -> p (t e)"),
                                                               acc[:, ds(t, 1), :].rearrange("p t f -> p (t f)"), ALU.mult, ALU.add).then_inc(chain, 1)


def finish_norm(k, v, add=None, gamma=None, beta=None, to_x=True, width=D, also=()):
    nc = k.nc
    with stage(k) as s:
        stats = s.sb("stats", [P, NT, 6])
        mv = s.sb("mv", [P, NT, 2])
        veps, rstd, shift = s.sb("veps", [P, NT]), s.sb("rstd", [P, NT]), s.sb("shift", [P, NT])
        g_sb, b_sb = s.sb("gamma", [P, width]), s.sb("beta", [P, width])
        g_in, chain, var, sd, shifted, normed, scaled, moved = (s.sem(n) for n in ("g_in", "chain", "var", "sd", "shifted", "normed", "scaled", "moved"))
        into = k.x if to_x else v
        with s.block() as block:
            @block.sync
            def _(sp):
                sp.dma_start(g_sb[:], gamma.partition_broadcast(P)).then_inc(g_in, 16)
                sp.dma_start(b_sb[:], beta.partition_broadcast(P)).then_inc(g_in, 16)
                for dst, src in also:
                    sp.dma_start(dst, src).then_inc(moved, 16)
                if also:
                    sp.wait_ge(moved, 16 * len(also))

            @block.scalar
            def _(act):
                act.wait_ge(var, 1)
                nc.scalar.activation(veps[:], veps[:], ACT.Sqrt).then_inc(sd, 1)
                act.wait_ge(shifted, 1)
                for t in range(NT):
                    nc.scalar.activation(v[:, t, :], v[:, t, :], ACT.Identity, bias=shift[:, t:t + 1], scale=rstd[:, t:t + 1]).then_inc(normed, 1)

            @block.vector
            def _(dve):
                c = Chain(dve, chain)
                if add is not None:
                    c.link(nc.vector.tensor_tensor(v[:], v[:], add[:], ALU.add))
                for t in range(NT):
                    c.step(nc.vector.bn_stats(stats[:, t, :], v[:, t, :]))
                c.wait()
                for t in range(NT):
                    c.step(nc.vector.bn_aggr(mv[:, t, :], stats[:, t, :]))
                c.wait()
                nc.vector.tensor_scalar(veps[:], mv[:, :, 1], EPS, None, ALU.add).then_inc(var, 1)
                dve.wait_ge(sd, 1)
                c.link(nc.vector.reciprocal(rstd[:], veps[:]))
                nc.vector.scalar_tensor_tensor(shift[:], mv[:, :, 0], -1.0, rstd[:], ALU.mult, ALU.mult).then_inc(shifted, 1)
                dve.wait_ge(g_in, 32)
                if to_x:
                    c.link(nc.vector.tensor_tensor(k.x[:], k.x[:], b_sb[:].unsqueeze(1).to_broadcast([P, NT, width]), ALU.add))
                STEP = 5
                for t in range(0, NT, STEP):
                    wide = lambda a: a[:].unsqueeze(1).to_broadcast([P, STEP, width])
                    dve.wait_ge(normed, t + STEP)
                    nc.vector.tensor_tensor(v[:, t:t + STEP, :], v[:, t:t + STEP, :], wide(g_sb), ALU.mult).then_inc(scaled, 1)
                    dve.wait_ge(scaled, t // STEP + 1)
                    c.step(nc.vector.tensor_tensor(into[:, t:t + STEP, :], v[:, t:t + STEP, :], into[:, t:t + STEP, :] if to_x else wide(b_sb), ALU.add))


def transfer(k, out, in_):
    with stage(k) as s:
        moved = s.sem("moved")
        with s.block() as block:
            @block.sync
            def _(sp):
                sp.dma_start(out, in_).then_inc(moved, 16)
                sp.wait_ge(moved, 16)


def turn_all(k, rows, cols):
    nc = k.nc
    with stage(k) as s:
        ps = s.ps("turned", [128, 4, 512])
        turned, copied = s.sem("turned"), s.sem("copied")
        with s.block() as block:
            @block.tensor
            def _(pe):
                for t in range(NT):
                    if t >= 4:
                        pe.wait_ge(copied, t - 3)
                    nc.tensor.transpose(ps[:, t % 4, 0:P], rows[:, t, 0:128], k.ident[0:P, 0:P])
                    nc.tensor.transpose(ps[:, t % 4, P:2 * P], rows[:, t, 128:256], k.ident[0:P, 0:P]).then_inc(turned, 1)

            @block.scalar
            def _(act):
                for t in range(NT):
                    act.wait_ge(turned, t + 1)
                    nc.scalar.activation(cols[:, :, t * P:(t + 1) * P],
                                         ps[:, t % 4, 0:2 * P].rearrange("p (c n) -> p c n", c=2), ACT.Copy).then_inc(copied, 1)


def project(k, cols, w, width, rows=None, table=None, also=()):
    nc = k.nc
    with stage(k) as s:
        w_sb = s.sb("w", [128, 2, width])
        row = s.sb("row", [P, 5, width]) if rows is None else rows
        at = (lambda t: row[:, t % 5, :]) if rows is None else (lambda t: row[:, t, :])
        ps = s.ps("ps", [P, 4, 512])
        w_in, mm, evac, moved = s.sem("w_in"), s.sem("mm"), s.sem("evac"), s.sem("moved")
        stored = [s.sem(f"stored{j}") for j in range(5)]
        with s.block() as block:
            @block.sync
            def _(sp):
                sp.dma_start(w_sb[:], w.rearrange("(c p) f -> p c f", p=128)).then_inc(w_in, 16)
                for dst, src in also:
                    sp.dma_start(dst, src).then_inc(moved, 16)
                if table is not None:
                    for t in range(NT):
                        sp.wait_ge(evac, t + 1)
                        sp.dma_start(table[t * P:(t + 1) * P, 0:width], at(t)).then_inc(stored[t % 5], 16)
                    for j in range(5):
                        sp.wait_ge(stored[j], 16 * (NT // 5))
                if also:
                    sp.wait_ge(moved, 16 * len(also))

            @block.tensor
            def _(pe):
                pe.wait_ge(w_in, 16)
                for t in range(NT):
                    if t >= 4:
                        pe.wait_ge(evac, t - 3)
                    nc.tensor.matmul(ps[:, t % 4, 0:width], cols[:, 0, t * P:(t + 1) * P], w_sb[:, 0, :], start=True, stop=False)
                    nc.tensor.matmul(ps[:, t % 4, 0:width], cols[:, 1, t * P:(t + 1) * P], w_sb[:, 1, :], start=False, stop=True).then_inc(mm, 1)

            @block.scalar
            def _(act):
                for t in range(NT):
                    if rows is None and t >= 5:
                        act.wait_ge(stored[t % 5], 16 * (t // 5))
                    act.wait_ge(mm, t + 1)
                    nc.scalar.activation(at(t), ps[:, t % 4, 0:width], ACT.Copy).then_inc(evac, 1)


def scores(k, rows, width, heads, a_src, a_tgt, src_out, tgt, top_all):
    nc = k.nc
    with stage(k) as s:
        a_sb = s.sb("a", [P, 2, width])
        prod = s.sb("prod", [P, 2, 2, width])
        s_src = s.sb("s_src", [P, NT, heads])
        top = s.sb("top", [P, heads])
        a_in, chain, topped, out = (s.sem(n) for n in ("a_in", "chain", "topped", "out"))
        with s.block() as block:
            @block.sync
            def _(sp):
                sp.dma_start(a_sb[:, 0, :], a_src.partition_broadcast(P)).then_inc(a_in, 16)
                sp.dma_start(a_sb[:, 1, :], a_tgt.partition_broadcast(P)).then_inc(a_in, 16)
                sp.wait_ge(topped, 1)
                with nc.allow_non_contiguous_dma(reason="a few numbers a node"):
                    sp.dma_start(src_out, s_src[:]).then_inc(out, 16)
                sp.wait_ge(out, 16)

            @block.gpsimd
            def _(pool):
                pool.wait_ge(topped, 1)
                nc.gpsimd.partition_all_reduce(top_all[:], top[:], P, RMAX)

            @block.vector
            def _(dve):
                c = Chain(dve, chain)
                dve.wait_ge(a_in, 32)
                for t in range(NT):
                    r = rows[:, t, :].unsqueeze(1).to_broadcast([P, 2, width])
                    c.link(nc.vector.tensor_tensor(prod[:, t % 2, :, :], r, a_sb[:], ALU.mult))
                    c.step(nc.vector.tensor_reduce(s_src[:, t, :], prod[:, t % 2, 0, :].rearrange("p (h d) -> p h d", h=heads), AX_X, ALU.add))
                    c.step(nc.vector.tensor_reduce(tgt[:, :, t], prod[:, t % 2, 1, :].rearrange("p (h d) -> p h d", h=heads), AX_X, ALU.add))
                c.wait()
                nc.vector.tensor_reduce(top[:], s_src[:].rearrange("p t h -> p h t"), AX_X, ALU.max).then_inc(topped, 1)


def divide(k, agg, out, heads, eps, add=None, bias=None, width=D):
    nc = k.nc
    HD = width // heads
    with stage(k) as s:
        den, none = s.sb("den", [P, NT, heads]), s.sb("none", [P, NT, heads])
        b_sb = s.sb("bias", [P, width])
        low = s.sb("low", [P, NT, width]) if add is not None else None
        b_in, chain, lows, exps = (s.sem(n) for n in ("b_in", "chain", "lows", "exps"))
        with s.block() as block:
            @block.sync
            def _(sp):
                if bias is not None:
                    sp.dma_start(b_sb[:], bias.partition_broadcast(P)).then_inc(b_in, 16)

            @block.vector
            def _(dve):
                c = Chain(dve, chain)
                d = agg[:, :, width:width + heads]
                if eps:
                    c.link(nc.vector.tensor_scalar(den[:], d, eps, None, ALU.add))
                else:
                    c.link(nc.vector.tensor_scalar(none[:], d, 0.0, None, ALU.is_equal))
                    c.link(nc.vector.tensor_tensor(den[:], d, none[:], ALU.add))
                c.link(nc.vector.reciprocal(none[:], den[:]))
                for t in range(NT):
                    c.step(nc.vector.tensor_tensor(out[:, t, :].rearrange("p (h d) -> p h d", h=heads), agg[:, t, 0:width].rearrange("p (h d) -> p h d", h=heads),
                                                   none[:, t, :].unsqueeze(2).to_broadcast([P, heads, HD]), ALU.mult))
                c.wait()
                if add is not None:
                    c.link(nc.vector.tensor_tensor(out[:], out[:], add[:], ALU.add))
                if bias is not None:
                    dve.wait_ge(b_in, 16)
                    c.link(nc.vector.tensor_tensor(out[:], out[:], b_sb[:].unsqueeze(1).to_broadcast([P, NT, width]), ALU.add))
                if add is not None:
                    nc.vector.tensor_scalar(low[:], out[:], 0.0, None, ALU.min).then_inc(lows, 1)
                    c.link(nc.vector.tensor_scalar(out[:], out[:], 0.0, -1.0, ALU.max, ALU.add))
                    dve.wait_ge(exps, 1)
                    c.link(nc.vector.tensor_tensor(out[:], out[:], low[:], ALU.add))

            @block.scalar
            def _(act):
                if add is not None:
                    act.wait_ge(lows, 1)
                    nc.scalar.activation(low[:], low[:], ACT.Exp).then_inc(exps, 1)


def sort_nodes(k, rank_i, noise, also=()):
    nc = k.nc
    with stage(k) as s:
        before = s.sb("before", [P, P])
        noise_sb, key = s.sb("noise", [P, NT]), s.sb("key", [P, NT])
        keys = s.sb("keys", [P, N])
        junk = s.sb("junk", [P, N])
        parts = s.sb("parts", [P, 3, NT])
        rank = s.sb("rank", [P, NT])
        in_, made, chain, keyed, out, back, moved = (s.sem(n) for n in ("in", "made", "chain", "keyed", "out", "back", "moved"))
        with s.block() as block:
            @block.sync
            def _(sp):
                with nc.allow_non_contiguous_dma(reason="one number a node"):
                    sp.dma_start(noise_sb[:], noise.rearrange("(t p) -> p t", p=P)).then_inc(in_, 16)
                    for dst, src in also:
                        sp.dma_start(dst, src).then_inc(moved, 16)
                    sp.wait_ge(keyed, 1)
                    sp.dma_start(k.keys_d.rearrange("(t p) -> p t", p=P), key[:]).then_inc(out, 16)
                sp.wait_ge(out, 16)
                sp.dma_start(keys[:], k.keys_d.partition_broadcast(P)).then_inc(back, 16)
                if also:
                    sp.wait_ge(moved, 16 * len(also))

            @block.gpsimd
            def _(pool):
                nc.gpsimd.memset(before[:], 1.0).then_inc(made, 1)
                pool.wait_ge(made, 1)
                nc.gpsimd.affine_select(out=before[:], in_=before[:], compare_op=ALU.is_gt, fill=0.0, base=0,
                                        pattern=[[-1, P]], channel_multiplier=1).then_inc(made, 1)

            @block.vector
            def _(dve):
                c = Chain(dve, chain)
                dve.wait_ge(in_, 16)
                c.link(nc.vector.tensor_tensor(key[:], k.degree[:], noise_sb[:], ALU.add))
                dve.sem_inc(keyed, 1)
                dve.wait_ge(back, 16)
                dve.wait_ge(made, 2)
                c.link(nc.vector.memset(parts[:], 0.0))
                for t in range(NT):
                    me = key[:, t:t + 1]
                    if t:
                        c.link(nc.vector.tensor_scalar(junk[:, 0:t * P], keys[:, 0:t * P], me, None, ALU.is_le, ALU.add, accum_out=parts[:, 0, t:t + 1]))
                    c.link(nc.vector.tensor_scalar(junk[:, t * P:N], keys[:, t * P:N], me, None, ALU.is_lt, ALU.add, accum_out=parts[:, 1, t:t + 1]))
                    c.link(nc.vector.scalar_tensor_tensor(junk[:, 0:P], keys[:, t * P:(t + 1) * P], me, before[:], ALU.is_equal, ALU.mult,
                                                          accum_out=parts[:, 2, t:t + 1]))
                c.link(nc.vector.tensor_tensor(rank[:], parts[:, 0, :], parts[:, 1, :], ALU.add))
                c.link(nc.vector.tensor_tensor(rank[:], rank[:], parts[:, 2, :], ALU.add))
                c.link(nc.vector.tensor_copy(rank_i[:], rank[:]))


def permute(k, rows, dram, rank_i, scatter, also=()):
    nc = k.nc
    with stage(k) as s:
        moved, other = s.sem("moved"), s.sem("other")
        with s.block() as block:
            @block.sync
            def _(sp):
                for dst, src in also:
                    sp.dma_start(dst, src).then_inc(other, 16)
                if also:
                    sp.wait_ge(other, 16 * len(also))

            @block.gpsimd
            def _(pool):
                for t in range(NT):
                    at = bass.IndirectOffsetOnAxis(rank_i[:, t:t + 1], 0)
                    if scatter:
                        nc.gpsimd.indirect_dma_start(dram, at, rows[:, t, :], None).then_inc(moved, 16)
                    else:
                        nc.gpsimd.indirect_dma_start(rows[:, t, :], None, dram, at).then_inc(moved, 16)
                pool.wait_ge(moved, 16 * NT)


STATES, DT_RANK = 16, 16
BC = 2 * STATES
DT_ROW = 3 * BC


def mamba_inputs(k, cols, xc, z, dbc, w_in, conv_w, conv_b, x_proj):
    nc = k.nc
    KW = 4
    BLK = [(n0, min(500, N - n0)) for n0 in range(0, N, 500)]
    NBK = len(BLK)
    with stage(k) as s:
        w = s.sb("w", [128, 2, 2 * D])
        cw, cb = s.sb("cw", [128, 2, KW]), s.sb("cb", [128, 2])
        xp = s.sb("xp", [128, 2, N + KW - 1])
        wx = s.sb("wx", [128, 2, DT_ROW + DT_RANK])
        ps = s.ps("ps", [128, 4, 512])
        ps_d = s.ps("ps_d", [DT_ROW + DT_RANK, 2, 512])
        loaded, mm, evac, chain, convd, acted, dmm, dev = (s.sem(n) for n in ("loaded", "mm", "evac", "chain", "convd", "acted", "dmm", "dev"))
        with s.block() as block:
            @block.sync
            def _(sp):
                sp.dma_start(w[:], w_in.rearrange("(c p) f -> p c f", p=128)).then_inc(loaded, 16)
                sp.dma_start(cw[:], conv_w.rearrange("(c p) f -> p c f", p=128)).then_inc(loaded, 16)
                with nc.allow_non_contiguous_dma(reason="one number a channel"):
                    sp.dma_start(cb[:], conv_b.rearrange("(c p) -> p c", p=128)).then_inc(loaded, 16)
                xw = x_proj.rearrange("(c p) f -> p c f", p=128)
                for part in range(3):
                    sp.dma_start(wx[:, :, part * BC:(part + 1) * BC], xw[:, :, DT_RANK:DT_RANK + BC]).then_inc(loaded, 16)
                sp.dma_start(wx[:, :, DT_ROW:DT_ROW + DT_RANK], xw[:, :, 0:DT_RANK]).then_inc(loaded, 16)

            @block.tensor
            def _(pe):
                pe.wait_ge(loaded, 112)
                n = 0
                for o in range(4):
                    for n0, m in BLK:
                        if n >= 4:
                            pe.wait_ge(evac, n - 3)
                        for c in range(2):
                            ins = nc.tensor.matmul(ps[:, n % 4, 0:m], w[:, c, o * 128:(o + 1) * 128], cols[:, c, n0:n0 + m], start=c == 0, stop=c == 1)
                        ins.then_inc(mm, 1)
                        n += 1
                pe.wait_ge(acted, 2)
                for q, (n0, m) in enumerate(BLK):
                    if q >= 2:
                        pe.wait_ge(dev, q - 1)
                    for c in range(2):
                        ins = nc.tensor.matmul(ps_d[:, q % 2, 0:m], wx[:, c, :], xc[:, c, n0:n0 + m], start=c == 0, stop=c == 1)
                    ins.then_inc(dmm, 1)

            @block.scalar
            def _(act):
                n = 0
                for o in range(4):
                    for n0, m in BLK:
                        act.wait_ge(mm, n + 1)
                        if o < 2:
                            ins = nc.scalar.activation(xp[:, o, KW - 1 + n0:KW - 1 + n0 + m], ps[:, n % 4, 0:m], ACT.Copy)
                        else:
                            ins = nc.scalar.activation(z[:, o - 2, n0:n0 + m], ps[:, n % 4, 0:m], ACT.Silu)
                        ins.then_inc(evac, 1)
                        n += 1
                for c in range(2):
                    act.wait_ge(convd, c + 1)
                    nc.scalar.activation(xc[:, c, :], xc[:, c, :], ACT.Silu, bias=cb[:, c:c + 1]).then_inc(acted, 1)
                for q, (n0, m) in enumerate(BLK):
                    act.wait_ge(dmm, q + 1)
                    nc.scalar.activation(dbc[:, n0:n0 + m], ps_d[:, q % 2, 0:m], ACT.Copy).then_inc(dev, 1)

            @block.vector
            def _(dve):
                c = Chain(dve, chain)
                c.link(nc.vector.memset(xp[:, :, 0:KW - 1], 0.0))
                dve.wait_ge(loaded, 112)
                for h in range(2):
                    dve.wait_ge(evac, (h + 1) * NBK)
                    c.link(nc.vector.tensor_scalar(xc[:, h, :], xp[:, h, 0:N], cw[:, h, 0:1], None, ALU.mult))
                    for q in range(1, KW):
                        ins = nc.vector.scalar_tensor_tensor(xc[:, h, :], xp[:, h, q:q + N], cw[:, h, q:q + 1], xc[:, h, :], ALU.mult, ALU.add)
                        if q < KW - 1:
                            c.link(ins)
                    ins.then_inc(convd, 1)


def scan_steps(k, xc, dbc, dt, u, parts, dt_w, dt_b, d_param):
    nc = k.nc
    BLK = [(n0, min(500, N - n0)) for n0 in range(0, N, 500)]
    NBK = len(BLK)
    with stage(k) as s:
        r, poly = s.sb("r", [128, N]), s.sb("poly", [128, N])
        w_dt, dtb, dp = s.sb("w_dt", [DT_ROW + DT_RANK, D]), s.sb("dtb", [128, 2]), s.sb("dp", [128, 2])
        part, rest = s.sb("part", [DT_ROW, N], mybir.dt.bfloat16), s.sb("rest", [DT_ROW, N])
        ps = s.ps("ps", [128, 4, 512])
        two = s.sb("two", [128, 1])
        loaded, made, mm, dts, chain, exps, parted, rests, r_free, u_done = (
            s.sem(n) for n in ("loaded", "made", "mm", "dts", "chain", "exps", "parted", "rests", "r_free", "u_done"))
        with s.block() as block:
            @block.sync
            def _(sp):
                sp.wait_ge(made, 1)
                sp.dma_start(w_dt[DT_ROW:DT_ROW + DT_RANK, :], dt_w).then_inc(loaded, 16)
                with nc.allow_non_contiguous_dma(reason="one number a channel"):
                    sp.dma_start(dtb[:], dt_b.rearrange("(c p) -> p c", p=128)).then_inc(loaded, 16)
                    sp.dma_start(dp[:], d_param.rearrange("(c p) -> p c", p=128)).then_inc(loaded, 16)

            @block.gpsimd
            def _(pool):
                nc.gpsimd.memset(w_dt[:], 0.0).then_inc(made, 1)
                nc.gpsimd.memset(two[:], 2.0).then_inc(made, 1)
                pool.wait_ge(parted, 1)
                nc.gpsimd.tensor_tensor(rest[:], dbc[0:DT_ROW, :], part[:], ALU.subtract).then_inc(rests, 1)
                pool.wait_ge(parted, 3)
                nc.gpsimd.tensor_tensor(rest[:], rest[:], part[:], ALU.subtract).then_inc(rests, 1)

            @block.tensor
            def _(pe):
                pe.wait_ge(loaded, 48)
                for h in range(2):
                    for q, (n0, m) in enumerate(BLK):
                        n = h * NBK + q
                        if n >= 4:
                            pe.wait_ge(dts, n - 3)
                        nc.tensor.matmul(ps[:, n % 4, 0:m], w_dt[:, h * 128:(h + 1) * 128], dbc[:, n0:n0 + m], start=True, stop=True).then_inc(mm, 1)

            @block.scalar
            def _(act):
                act.wait_ge(loaded, 48)
                for h in range(2):
                    for q, (n0, m) in enumerate(BLK):
                        n = h * NBK + q
                        act.wait_ge(mm, n + 1)
                        nc.scalar.activation(dt[:, h, n0:n0 + m], ps[:, n % 4, 0:m], ACT.Identity, bias=dtb[:, h:h + 1]).then_inc(dts, 1)
                    act.wait_ge(dts, (h + 1) * NBK)
                    nc.scalar.activation(u[:, h, :], dt[:, h, :], ACT.Abs).then_inc(exps, 1)
                    act.wait_ge(exps, 4 * h + 1)
                    nc.scalar.activation(dt[:, h, :], dt[:, h, :], ACT.Relu).then_inc(exps, 1)
                    nc.scalar.activation(u[:, h, :], u[:, h, :], ACT.Exp, scale=-1.0).then_inc(exps, 1)
                    act.wait_ge(exps, 4 * h + 3)
                    if h == 0:
                        act.wait_ge(made, 2)
                    else:
                        act.wait_ge(r_free, 1)
                    nc.scalar.activation(r[:], u[:, h, :], ACT.Identity, bias=two[:]).then_inc(exps, 1)
                nc.scalar.activation(part[:], dbc[0:DT_ROW, :], ACT.Copy).then_inc(parted, 1)
                act.wait_ge(parted, 1)
                nc.scalar.activation(parts[0:BC, :], part[0:BC, :], ACT.Copy).then_inc(parted, 1)
                act.wait_ge(rests, 1)
                act.wait_ge(parted, 2)
                nc.scalar.activation(part[:], rest[:], ACT.Copy).then_inc(parted, 1)
                act.wait_ge(parted, 3)
                nc.scalar.activation(parts[BC:2 * BC, :], part[BC:2 * BC, :], ACT.Copy)
                act.wait_ge(rests, 2)
                nc.scalar.activation(parts[2 * BC:3 * BC, :], rest[2 * BC:3 * BC, :], ACT.Copy)
                for h in range(2):
                    act.wait_ge(u_done, h + 1)
                    nc.scalar.activation(xc[:, h, :], xc[:, h, :], ACT.Identity, scale=dp[:, h:h + 1])

            @block.vector
            def _(dve):
                c = Chain(dve, chain)
                for h in range(2):
                    dth, uh = dt[:, h, :], u[:, h, :]
                    dve.wait_ge(exps, 4 * h + 4)
                    c.link(nc.vector.reciprocal(r[:], r[:]))
                    c.link(nc.vector.tensor_tensor(r[:], r[:], uh, ALU.mult))
                    c.link(nc.vector.tensor_tensor(uh, r[:], r[:], ALU.mult))
                    c.link(nc.vector.tensor_scalar(poly[:], uh, 1.0 / 15, None, ALU.mult))
                    for odd in (13, 11, 9, 7, 5, 3):
                        c.link(nc.vector.scalar_tensor_tensor(poly[:], poly[:], 1.0 / odd, uh, ALU.add, ALU.mult))
                    c.link(nc.vector.scalar_tensor_tensor(poly[:], poly[:], 1.0, r[:], ALU.add, ALU.mult))
                    dve.sem_inc(r_free, 1)
                    c.link(nc.vector.scalar_tensor_tensor(dth, poly[:], 2.0, dth, ALU.mult, ALU.add))
                    nc.vector.tensor_tensor(uh, dth, xc[:, h, :], ALU.mult).then_inc(u_done, 1)


def selective_scan(k, y, z, parts, dt, u, a_log):
    nc = k.nc
    SN, CH, NC = STATES, 625, 5
    CUT = [(0, 512), (512, CH - 512)]
    with stage(k) as s:
        al, A = s.sb("al", [128, 2, SN]), s.sb("A", [128, 2, SN + 1])
        a_s = s.sb("a_s", [128, 2, 2])
        sel, mask = s.sb("sel", [DT_ROW, 2, 2, 128], mybir.dt.bfloat16), s.sb("mask", [DT_ROW, BC + 1])
        dA, dB, hh = (s.sb(n, [128, 2, 2, CH]) for n in ("dA", "dB", "hh"))
        ps = s.ps("ps", [128, 2, 2, 1024])
        loaded, chain, exps, prods, adds, sels, bcs = (s.sem(n) for n in ("loaded", "chain", "exps", "prods", "adds", "sels", "bcs"))
        with s.block() as block:
            @block.sync
            def _(sp):
                sp.dma_start(al[:], a_log.rearrange("(c p) n -> p c n", p=128)).then_inc(loaded, 16)

            @block.gpsimd
            def _(pool):
                pool.sem_inc(adds, 2)
                with pool.Fori(0, SN // 2) as i:
                    for q in range(2 * NC):
                        n, b, c = i * (2 * NC) + q, q % 2, q % NC
                        pool.wait_ge(prods, n + 3)
                        ycut = y[:, :, c * CH:(c + 1) * CH]
                        nc.gpsimd.tensor_tensor(ycut, ycut, dA[:, b, :, :], ALU.add).then_inc(adds, 1)

            @block.tensor
            def _(pe):
                pe.sem_inc(bcs, 2)
                with pe.Fori(0, SN // 2) as i:
                    for q in range(2 * NC):
                        n, b, c = i * (2 * NC) + q, q % 2, q % NC
                        pe.wait_ge(sels, i * 2 + q // NC + 1)
                        pe.wait_ge(prods, n + 1)
                        for v in range(2):
                            for lo, m in CUT:
                                ins = nc.tensor.matmul(ps[:, b, v, lo:lo + m], sel[:, q // NC, v, :], parts[:, c * CH + lo:c * CH + lo + m], start=True, stop=True)
                        ins.then_inc(bcs, 1)

            @block.scalar
            def _(act):
                act.wait_ge(loaded, 16)
                nc.scalar.activation(A[:, :, 0:SN], al[:], ACT.Exp).then_inc(exps, 1)
                with act.Fori(0, SN // 2) as i:
                    for q in range(2 * NC):
                        n, b, c = i * (2 * NC) + q, q % 2, q % NC
                        act.wait_ge(sels, i * 2 + q // NC + 1)
                        act.wait_ge(adds, n + 1)
                        for h in range(2):
                            nc.scalar.activation(dA[:, b, h, :], dt[:, h, c * CH:(c + 1) * CH], ACT.Exp, scale=a_s[:, q // NC, h:h + 1]).then_inc(exps, 1)

            @block.vector
            def _(dve):
                c_ = Chain(dve, chain)
                dve.wait_ge(exps, 1)
                c_.step(nc.vector.memset(A[:, :, SN:SN + 1], 0.0))
                c_.link(nc.vector.tensor_scalar(A[:, :, 0:SN], A[:, :, 0:SN], -1.0, None, ALU.mult))
                c_.link(nc.vector.tensor_tensor(mask[:], k.ident[0:DT_ROW, 0:BC + 1], k.ident[0:DT_ROW, BC:2 * BC + 1], ALU.add))
                c_.link(nc.vector.tensor_tensor(mask[:], mask[:], k.ident[0:DT_ROW, 2 * BC:3 * BC + 1], ALU.add))
                dve.sem_inc(prods, 2)

                def state(st, v):
                    nc.vector.tensor_copy(a_s[:, v, :], A[:, :, ds(st, 1)].rearrange("p c a -> p (c a)"))
                    nc.vector.tensor_copy(sel[:, v, 0, :], mask[:, ds(st, 1)].to_broadcast([DT_ROW, 128]))
                    nc.vector.tensor_copy(sel[:, v, 1, :], mask[:, ds(SN + st, 1)].to_broadcast([DT_ROW, 128])).then_inc(sels, 1)

                def both(row):
                    return row.unsqueeze(1).to_broadcast([128, 2, CH])

                state(0, 0)
                def inputs(b, n, c):
                    dve.wait_ge(bcs, n + 3)
                    nc.vector.tensor_tensor(dB[:, b, :, :], both(ps[:, b, 0, 0:CH]), u[:, :, c * CH:(c + 1) * CH], ALU.mult).then_inc(chain, 1)

                def two_states(i, last):
                    for q in range(2 * NC):
                        n, b, c = i * (2 * NC) + q, q % 2, q % NC
                        if c == 2:
                            state(i * 2 + q // NC + 1, 1 - q // NC)
                        dve.wait_ge(chain, base + 3 * n + 1)
                        dve.wait_ge(exps, 2 * n + 3)
                        for h in range(2):
                            nc.vector.tensor_tensor_scan(hh[:, b, h, :], dA[:, b, h, :], dB[:, b, h, :], 0.0 if c == 0 else hh[:, 1 - b, h, CH - 1:CH],
                                                         ALU.mult, ALU.add).then_inc(chain, 1)
                        if not last or q < 2 * NC - 1:
                            inputs(1 - b, n + 1, (q + 1) % NC)
                        dve.wait_ge(chain, base + 3 * n + 3)
                        nc.vector.tensor_tensor(dA[:, b, :, :], both(ps[:, b, 1, 0:CH]), hh[:, b, :, :], ALU.mult).then_inc(prods, 1)

                base = c_.n
                inputs(0, 0, 0)
                with dve.Fori(0, SN // 2 - 1) as i:
                    two_states(i, False)
                two_states(SN // 2 - 1, True)
                c_.n = base + 3 * SN * NC
                dve.wait_ge(adds, SN * NC + 2)
                c_.link(nc.vector.tensor_tensor(z[:], y[:], z[:], ALU.mult))


def mix(k, a_rows, b_rows, a_cols, b_cols, wa, wb):
    nc = k.nc
    with stage(k) as s:
        w = s.sb("w", [128, 4, D])
        g = s.sb("g", [P, 2, D])
        ps = s.ps("ps", [P, 2, 512])
        w_in, mm, gated, chain = (s.sem(n) for n in ("w_in", "mm", "gated", "chain"))
        with s.block() as block:
            @block.sync
            def _(sp):
                sp.dma_start(w[:, 0:2, :], wa.rearrange("(c p) f -> p c f", p=128)).then_inc(w_in, 16)
                sp.dma_start(w[:, 2:4, :], wb.rearrange("(c p) f -> p c f", p=128)).then_inc(w_in, 16)

            @block.tensor
            def _(pe):
                pe.wait_ge(w_in, 32)
                for t in range(NT):
                    if t >= 2:
                        pe.wait_ge(gated, t - 1)
                    for c in range(4):
                        src = (a_cols, b_cols)[c // 2]
                        ins = nc.tensor.matmul(ps[:, t % 2, 0:D], src[:, c % 2, t * P:(t + 1) * P], w[:, c, :], start=c == 0, stop=c == 3)
                    ins.then_inc(mm, 1)

            @block.scalar
            def _(act):
                for t in range(NT):
                    if t >= 2:
                        act.wait_ge(chain, 3 * (t - 1))
                    act.wait_ge(mm, t + 1)
                    nc.scalar.activation(g[:, t % 2, :], ps[:, t % 2, 0:D], ACT.Sigmoid).then_inc(gated, 1)

            @block.vector
            def _(dve):
                c = Chain(dve, chain)
                for t in range(NT):
                    c.link(nc.vector.tensor_tensor(a_rows[:, t, :], a_rows[:, t, :], b_rows[:, t, :], ALU.subtract))
                    dve.wait_ge(gated, t + 1)
                    c.link(nc.vector.tensor_tensor(a_rows[:, t, :], a_rows[:, t, :], g[:, t % 2, :], ALU.mult))
                    c.link(nc.vector.tensor_tensor(a_rows[:, t, :], a_rows[:, t, :], b_rows[:, t, :], ALU.add))


def small_edge_sums(k, table, tgt, top, agg, src_c, dst_c):
    nc = k.nc
    H, F = 4, 16
    W = F + H
    Q, GT = 128, 256
    with stage(k) as s:
        idx, dsti = s.sb("idx", [Q, GT + G], I32), s.sb("dsti", [Q, GT + G], I32)
        dstf, tile_of, lo = s.sb("dstf", [Q, GT]), s.sb("tile_of", [Q, GT]), s.sb("lo", [Q, GT])
        r125, r25 = s.sb("r125", [Q, P]), s.sb("r25", [Q, NT])
        gi = s.sb("gi", [Q, 2, G], I32)
        msg = s.sb("msg", [Q, 2, G, W])
        HT = H * NT
        lo_rows, pick = s.sb("lo_rows", [P, 2, G * Q]), s.sb("pick", [P, 2, G * Q])
        picked, s_dst = s.sb("picked", [Q, G * H, NT]), s.sb("s_dst", [Q, G, H])
        e1, e2, e = s.sb("e1", [Q, G, 2, H]), s.sb("e2", [Q, G, 2, H]), s.sb("e", [Q, 2, G, H])
        topq, topi = s.sb("topq", [Q, H]), s.sb("topi", [1, H])
        ps_s, ps_q = s.ps("ps_s", [Q, 2, 512]), s.ps("ps_q", [Q, 512])
        row_in = [s.sem("row_in0"), s.sem("row_in1")]
        pick_done, sc_mm, topped = s.sem("pick"), s.sem("sc_mm"), s.sem("topped")
        oh_lo, oh_hi = s.sb("oh_lo", [Q, 2, G, P]), s.sb("oh_hi", [Q, 2, G, NT])
        spread = s.sb("spread", [Q, 2, G, NT * W])
        zero = s.sb("zero", [Q, NT * W])
        own = s.sb("own", [P, NT, W])
        v1, v2 = s.sb("v1", [P, NT, H]), s.sb("v2", [P, NT, H])
        ps = s.ps("ps", [P, 512])
        loaded, made, chain, idx_done, mm, e_done, a_done, ready = (s.sem(n) for n in ("loaded", "made", "chain", "idx", "mm", "e_done", "a_done", "ready"))
        turns, own_e, own_a, scaled = s.sem("turns"), s.sem("own_e"), s.sem("own_a"), s.sem("scaled")
        msg_in = [s.sem("msg_in0"), s.sem("msg_in1")]
        LG = GT // G
        with s.block() as block:
            @block.sync
            def _(sp):
                sp.dma_start(idx[:, 0:GT], src_c).then_inc(loaded, 16)
                sp.dma_start(dsti[:, 0:GT], dst_c).then_inc(loaded, 16)
                sp.dma_start(own[:], table.rearrange("(t p) f -> p t f", p=P)).then_inc(loaded, 16)
                with sp.Fori(0, LG // 2) as i:
                    for b in range(2):
                        sp.wait_ge(pick_done, i * 2 + b + 1)
                        sp.dma_start(lo_rows[:, b, :], k.ffn_lo_r[ds((i * 2 + b) * (G * Q), G * Q)].partition_broadcast(P)).then_inc(row_in[b], 16)

            @block.gpsimd
            def _(pool):
                nc.gpsimd.iota(r125[:], [[1, P]], base=0, channel_multiplier=0, allow_small_or_imprecise_dtypes=True).then_inc(made, 1)
                nc.gpsimd.iota(r25[:], [[1, NT]], base=0, channel_multiplier=0, allow_small_or_imprecise_dtypes=True).then_inc(made, 1)
                nc.gpsimd.memset(zero[:], 0.0).then_inc(made, 1)

                def gather(b, g):
                    pool.wait_ge(idx_done, g + 1)
                    pool.wait_ge(ready, g * G + G)
                    pool.sem_inc(turns, 1)
                    for j in range(G):
                        nc.gpsimd.indirect_dma_start(msg[:, b, j, :], None, table, bass.IndirectOffsetOnAxis(gi[:, b, j:j + 1], 0)).then_inc(msg_in[b], 16)

                with pool.Fori(0, LG // 2) as i:
                    gather(0, i * 2)
                    gather(1, i * 2 + 1)

            @block.tensor
            def _(pe):
                pe.sem_inc(mm, 2 * G)
                pe.wait_ge(made, 3)
                nc.tensor.matmul(ps[:, 0:NT * W], zero[:, 0:P], zero[:], start=True, stop=False)
                nc.tensor.matmul(ps_q[:, 0:H], k.ones[0:1, 0:Q], top[0:1, :], start=True, stop=True).then_inc(topped, 1)
                pe.sem_inc(sc_mm, 2)

                def target_scores(b, g):
                    pe.wait_ge(pick_done, g + 3)
                    for j in range(G):
                        ins = nc.tensor.matmul(ps_s[:, b, j * HT:(j + 1) * HT], pick[:, b, j * Q:(j + 1) * Q], tgt[:].rearrange("p h t -> p (h t)"), start=True, stop=True)
                    ins.then_inc(sc_mm, 1)

                def sums(b, g):
                    for j in range(G):
                        pe.wait_ge(ready, (g + 2) * G + j + 1)
                        nc.tensor.matmul(ps[:, 0:NT * W], oh_lo[:, b, j, :], spread[:, b, j, :], start=False, stop=False).then_inc(mm, 1)

                target_scores(0, 0)
                with pe.Fori(0, LG // 2 - 1) as i:
                    for b in range(2):
                        target_scores(1 - b, i * 2 + b + 1)
                        sums(b, i * 2 + b)
                target_scores(1, LG - 1)
                sums(0, LG - 2)
                sums(1, LG - 1)
                nc.tensor.matmul(ps[:, 0:NT * W], zero[:, 0:P], zero[:], start=False, stop=True).then_inc(mm, 1)

            @block.scalar
            def _(act):
                with act.Fori(0, LG // 2) as i:
                    for b in range(2):
                        g = i * 2 + b
                        act.wait_ge(e_done, 8 * g + 8 + 16)
                        nc.scalar.activation(msg[:, b, :, F:W], e[:, b, :, :], ACT.Exp).then_inc(a_done, 1)
                act.wait_ge(own_e, 1)
                nc.scalar.activation(own[:, :, F:W], v1[:], ACT.Exp).then_inc(own_a, 1)

            @block.vector
            def _(dve):
                c = Chain(dve, chain)
                c.step(nc.vector.memset(idx[:, GT:GT + G], 0))
                c.step(nc.vector.memset(dsti[:, GT:GT + G], 0))
                dve.sem_inc(pick_done, 2)
                dve.sem_inc(e_done, 16)
                dve.sem_inc(ready, 2 * G)
                dve.wait_ge(loaded, 48)
                c.link(nc.vector.tensor_copy(dstf[:], dsti[:, 0:GT]))
                split_index(nc, c, dstf[:], tile_of[:], lo[:], dsti[:, 0:GT])
                dve.wait_ge(topped, 1)
                c.link(nc.vector.tensor_copy(topq[:], ps_q[:, 0:H]))
                dve.wait_ge(made, 3)
                base = c.n

                def indices(b, g):
                    nc.vector.tensor_copy(gi[:, b, :], idx[:, ds(g * G, G)]).then_inc(idx_done, 1)

                def pick_rows(b, g, n):
                    dve.wait_ge(row_in[b], 16 * n)
                    dve.wait_ge(sc_mm, g + 1)
                    nc.vector.tensor_scalar(pick[:, b, :], lo_rows[:, b, :], k.ramp_p[:], None, ALU.is_equal).then_inc(pick_done, 1)

                def turn(b, g, i, ahead):
                    indices(1 - b, g + 1)
                    if ahead:
                        pick_rows(1 - b, g + 1, i + 1 + b)
                    dve.wait_ge(mm, upto(g, G - 1, back=2))
                    nc.vector.tensor_tensor(oh_hi[:, b, :, :], tile_of[:, ds(g * G, G)].unsqueeze(2).to_broadcast([Q, G, NT]),
                                            r25[:].unsqueeze(1).to_broadcast([Q, G, NT]), ALU.is_equal).then_inc(chain, 1)
                    for j in range(G):
                        nc.vector.tensor_scalar(oh_lo[:, b, j, :], r125[:], lo[:, ds(g * G + j, 1)], None, ALU.is_equal)
                    c0 = 8 * g + 16
                    dve.wait_ge(msg_in[b], 16 * G * (i + 1))
                    dve.wait_ge(sc_mm, g + 3)
                    dve.wait_ge(chain, base + g + 1)
                    nc.vector.tensor_tensor(picked[:].rearrange("p (j h) t -> p j h t", j=G), ps_s[:, b, 0:G * HT].rearrange("p (j h t) -> p j h t", j=G, t=NT),
                                            oh_hi[:, b, :, :].unsqueeze(2).to_broadcast([Q, G, H, NT]), ALU.mult).then_inc(e_done, 2)
                    dve.wait_ge(e_done, c0 + 2)
                    nc.vector.tensor_reduce(s_dst[:].rearrange("p g h -> p (g h)"), picked[:], AX_X, ALU.add).then_inc(e_done, 1)
                    dve.wait_ge(e_done, c0 + 3)
                    nc.vector.tensor_tensor(e1[:, :, 0, :], msg[:, b, :, F:W], s_dst[:], ALU.add).then_inc(e_done, 1)
                    nc.vector.tensor_tensor(e1[:, :, 1, :], topq[:].unsqueeze(1).to_broadcast([Q, G, H]), s_dst[:], ALU.add).then_inc(e_done, 1)
                    dve.wait_ge(e_done, c0 + 5)
                    nc.vector.scalar_tensor_tensor(e2[:], e1[:], 0.2, e1[:], ALU.mult, ALU.max).then_inc(e_done, 1)
                    dve.wait_ge(e_done, c0 + 6)
                    nc.vector.tensor_tensor(e[:, b, :, :], e2[:, :, 0, :], e2[:, :, 1, :], ALU.subtract).then_inc(e_done, 2)
                    dve.wait_ge(a_done, g + 1)
                    m = msg[:, b, :, 0:F].rearrange("p g (h d) -> p g h d", h=H)
                    nc.vector.tensor_tensor(m, m, msg[:, b, :, F:W].unsqueeze(3).to_broadcast([Q, G, H, F // H]), ALU.mult).then_inc(scaled, 1)
                    dve.wait_ge(scaled, g + 1)
                    for j in range(G):
                        nc.vector.tensor_tensor(spread[:, b, j, :].rearrange("p (t f) -> p t f", t=NT), oh_hi[:, b, j, :].unsqueeze(2).to_broadcast([Q, NT, W]),
                                                msg[:, b, j, :].unsqueeze(1).to_broadcast([Q, NT, W]), ALU.mult).then_inc(ready, 1)

                indices(0, 0)
                pick_rows(0, 0, 1)
                with dve.Fori(0, LG // 2 - 1) as i:
                    for b in range(2):
                        turn(b, i * 2 + b, i, True)
                for b in range(2):
                    turn(b, LG - 2 + b, LG // 2 - 1, b == 0)
                c.n = base + LG
                mine = tgt[:].rearrange("p h t -> p t h")
                c.link(nc.vector.tensor_tensor(v1[:], own[:, :, F:W], mine, ALU.add))
                c.link(nc.vector.scalar_tensor_tensor(v2[:], v1[:], 0.2, v1[:], ALU.mult, ALU.max))
                c.link(nc.vector.tensor_tensor(v1[:], mine, top[:].unsqueeze(1).to_broadcast([P, NT, H]), ALU.add))
                c.link(nc.vector.scalar_tensor_tensor(v1[:], v1[:], 0.2, v1[:], ALU.mult, ALU.max))
                nc.vector.tensor_tensor(v1[:], v2[:], v1[:], ALU.subtract).then_inc(own_e, 1)
                dve.wait_ge(own_a, 1)
                for h in range(H):
                    c.step(nc.vector.tensor_tensor(own[:, :, 4 * h:4 * h + 4], own[:, :, 4 * h:4 * h + 4], own[:, :, F + h:F + h + 1].to_broadcast([P, NT, 4]), ALU.mult))
                c.wait()
                dve.wait_ge(mm, 2 * G + GT + 1)
                c.link(nc.vector.tensor_tensor(agg[:], ps[:, 0:NT * W].rearrange("p (t f) -> p t f", t=NT), own[:], ALU.add))


def mean_heads(k, v, score):
    nc = k.nc
    with stage(k) as s:
        total = s.sb("total", [P, NT, 4])
        chain = s.sem("chain")
        with s.block() as block:
            @block.vector
            def _(dve):
                c = Chain(dve, chain)
                c.link(nc.vector.tensor_reduce(total[:], v.rearrange("p t (h e) -> p t e h", e=4), AX_X, ALU.add))
                c.link(nc.vector.tensor_scalar(score[:], total[:], 0.25, None, ALU.mult))


def cutoff(k, cut):
    nc = k.nc
    with stage(k) as s:
        turns_i, q = s.sb("turns", [P, ET], I32), s.sb("q", [P, ET])
        chain, red, sines = s.sem("chain"), s.sem("red"), s.sem("sines")
        with s.block() as block:
            @block.vector
            def _(dve):
                c = Chain(dve, chain)
                c.link(nc.vector.tensor_scalar(turns_i[:], k.edge_w[:], 1.0 / 20, None, ALU.mult))
                c.link(nc.vector.tensor_scalar(q[:], turns_i[:], -20.0, None, ALU.mult))
                nc.vector.tensor_tensor(q[:], q[:], k.edge_w[:], ALU.add).then_inc(red, 1)
                dve.wait_ge(sines, 1)
                c.link(nc.vector.tensor_tensor(q[:], cut[:], cut[:], ALU.mult))
                c.link(nc.vector.tensor_scalar(cut[:], q[:], -1.0, 1.0, ALU.mult, ALU.add))

            @block.scalar
            def _(act):
                act.wait_ge(red, 1)
                nc.scalar.activation(cut[:], q[:], ACT.Sin, scale=math.pi / 20).then_inc(sines, 1)


def add_bias(k, rows, bias, softplus=False, to_x=False):
    nc = k.nc
    with stage(k) as s:
        b_sb = s.sb("bias", [P, D])
        soft = s.sb("soft", [P, NT, D]) if softplus else None
        b_in, chain, biased, done = (s.sem(n) for n in ("b_in", "chain", "biased", "done"))
        with s.block() as block:
            @block.sync
            def _(sp):
                sp.dma_start(b_sb[:], bias.partition_broadcast(P)).then_inc(b_in, 16)

            @block.vector
            def _(dve):
                c = Chain(dve, chain)
                dve.wait_ge(b_in, 16)
                nc.vector.tensor_tensor(rows[:], rows[:], b_sb[:].unsqueeze(1).to_broadcast([P, NT, D]), ALU.add).then_inc(biased, 1)
                dve.wait_ge(biased, 1)
                if to_x:
                    c.link(nc.vector.tensor_tensor(k.x[:], k.x[:], rows[:], ALU.add))
                if softplus:
                    dve.wait_ge(done, 3)
                    c.link(nc.vector.tensor_scalar(rows[:], rows[:], 0.0, -math.log(2.0), ALU.max, ALU.add))
                    c.link(nc.vector.tensor_tensor(rows[:], rows[:], soft[:], ALU.add))

            @block.scalar
            def _(act):
                if softplus:
                    act.wait_ge(biased, 1)
                    nc.scalar.activation(soft[:], rows[:], ACT.Abs).then_inc(done, 1)
                    act.wait_ge(done, 1)
                    nc.scalar.activation(soft[:], soft[:], ACT.Exp, scale=-1.0).then_inc(done, 1)
                    act.wait_ge(done, 2)
                    nc.scalar.activation(soft[:], soft[:], ACT.Ln, bias=1.0).then_inc(done, 1)


def ones_gate(k, gate):
    with stage(k) as s:
        done = s.sem("done")
        with s.block() as block:
            @block.vector
            def _(dve):
                k.nc.vector.memset(gate[:], 1.0).then_inc(done, 1)


def nan_to_num_to_x(k, v):
    nc = k.nc
    BIG = 3.4028234e38
    U8 = mybir.dt.uint8
    with stage(k) as s:
        mask = s.sb("mask", [P, NT, D], U8)
        const = s.sb("const", [P, 3])
        chain = s.sem("chain")
        with s.block() as block:
            @block.vector
            def _(dve):
                c = Chain(dve, chain)
                c.step(nc.vector.memset(const[:, 0:1], 0.0))
                c.step(nc.vector.memset(const[:, 1:2], 1.0e4))
                c.link(nc.vector.memset(const[:, 2:3], -1.0e4))
                for q, (other, op) in enumerate(((v[:], ALU.not_equal), (BIG, ALU.is_gt), (-BIG, ALU.is_lt))):
                    if q == 0:
                        c.link(nc.vector.tensor_tensor(mask[:], v[:], v[:], op))
                    else:
                        c.link(nc.vector.tensor_scalar(mask[:], v[:], other, None, op))
                    for t in range(NT):
                        c.step(nc.vector.copy_predicated(v[:, t, :], mask[:, t, :], const[:, q:q + 1].to_broadcast([P, D])))
                    c.wait()
                c.link(nc.vector.tensor_tensor(k.x[:], k.x[:], v[:], ALU.add))


def routed(k, rows, moe, n_exp, chosen, x, gate_w, gate_b, mode, capacity=None, **more):
    nc = k.nc
    blocks = most_blocks(chosen, n_exp)
    blocks += blocks % 2
    sent, answered = (q[0:(blocks + 1) * BR, :] for q in (k.sent, k.answered))
    tensor = lambda n, shape, dt=F32: nc.sbuf_tensor(f"{n}_{x.f}_{n_exp}", shape, dt)
    with tensor("oh", [P, chosen, NT, n_exp]) as oh, tensor("wt", [P, chosen, NT]) as wt, \
            tensor("slot_i", [P, chosen, NT], I32) as slot_i, tensor("block_i", [1, blocks], I32) as block_i:
        with nc.sbuf_tensor(f"cols_{x.f}_{n_exp}", [128, 2, N], F32) as cols:
            normalise_all(k, rows, cols, clear=sent)
            gates(k, cols, None, n_exp, gate_w, gate_b, mode, choice=(oh, wt), **more)
        route(k, (oh, wt), slot_i, block_i, n_exp, chosen, blocks, capacity)
        send_rows(k, rows, sent, slot_i, chosen, blocks)
        block_experts(k, sent, answered, block_i, x, blocks)
        fetch_rows(k, moe, answered, slot_i, wt, chosen)


def build(nc, a, out, layers=8):
    k = Core()
    k.nc, k.uid = nc, 0
    ctx = ExitStack()
    with ctx:
        keep = lambda name, shape, dt=F32: ctx.enter_context(nc.sbuf_tensor(name, shape, dt))
        sbt = lambda name, shape=(P, NT, D), dt=F32: nc.sbuf_tensor(name, list(shape), dt)
        k.x = keep("x", [P, NT, D])
        k.edge_w, k.dst_f = keep("edge_w", [P, ET]), keep("dst_f", [P, ET])
        k.src_i, k.src_rel_i, k.row_i = (keep(n, [P, ET + G], I32) for n in ("src_i", "src_rel_i", "row_i"))
        k.dst_hi = keep("dst_hi", [P, ET])
        k.ramp_p, k.ramp_t = keep("ramp_p", [P, 1]), keep("ramp_t", [P, NT])
        tgt4, top4, tgt8, top8 = keep("tgt4", [P, 4, NT]), keep("top4", [P, 4]), keep("tgt8", [P, 8, NT]), keep("top8", [P, 8])
        k.ident, k.ones = keep("ident", [128, 128]), keep("ones", [128, 128])
        k.acc = {w: [nc.dram_tensor(f"acc{w}_{j}", [AT * P, w], F32, kind="Internal").ap() for j in range(G)] for w in (D, D + 4, D + 8)}
        k.rel_rows = nc.dram_tensor("rel_rows", [N, REL * D], F32, kind="Internal").ap()
        dram = lambda n, w: nc.dram_tensor(n, [N, w], F32, kind="Internal").ap()
        d = {n: dram("d_" + n, w) for n, w in (("xn", D), ("local", D), ("sorted", D), ("gat4", D + 4), ("gat8", D + 8), ("small", 20), ("lin1", D))}
        tiles = lambda n: d[n].rearrange("(t p) f -> p t f", p=P)
        most = (most_blocks(2, 16) + 2) * BR
        k.sent, k.answered = (nc.dram_tensor(n, [most, D], F32, kind="Internal").ap() for n in ("sent", "answered"))
        k.keys_d = nc.dram_tensor("keys_d", [N], F32, kind="Internal").ap()
        k.src_c, k.dst_c, k.type_c, k.weight_c = a["src_c"], a["dst_c"], a["type_c"], a["weight_c"]
        k.dst_r, k.w_rel, k.ffn_dst_r = a["dst"], a["w_rel"], a["ffn_dst"]
        k.lo_r = nc.dram_tensor("lo_r", [E], F32, kind="Internal").ap()
        k.ffn_lo_r = nc.dram_tensor("ffn_lo_r", [32768], F32, kind="Internal").ap()
        x_rows = a["x"].rearrange("(t p) f -> p t f", p=P)
        out_rows = out.rearrange("(t p) f -> p t f", p=P)

        with stage(k) as s:
            made = s.sem("made")
            with s.block() as block:
                @block.gpsimd
                def _(pool):
                    nc.gpsimd.memset(k.ones[:], 1.0).then_inc(made, 1)
                    nc.gpsimd.memset(k.ident[:], 0.0).then_inc(made, 1)
                    pool.wait_ge(made, 2)
                    nc.gpsimd.affine_select(out=k.ident[:], in_=k.ident[:], compare_op=ALU.not_equal, fill=1.0, base=0,
                                            pattern=[[-1, 128]], channel_multiplier=1).then_inc(made, 1)

        k.degree = keep("degree", [P, NT])
        with sbt("src_tile", [P, ET]) as src_tile, sbt("src_row", [P, ET]) as src_row:
            prepare_edges(k, src_tile, src_row, x_rows)
            with nc.sbuf_tensor("rows_a", [P, NT, D], F32) as rows, nc.sbuf_tensor("cols_a", [128, 2, N], F32) as cols:
                normalise_all(k, rows, cols)
                relation_tables(k, cols)
            table = k.rel_rows.rearrange("n (r f) -> (n r) f", r=REL)
            edge_sums(k, table, k.src_rel_i, D, weight=k.edge_w, make_rows=True, sources=(src_tile, src_row))
            collect(k, None, D)

        if layers >= 2:
            with sbt("rows_b") as rows, sbt("moe_b") as moe:
                routed(k, rows, moe, 16, 2, Experts(16, 512, ACT.Relu, a["L0_ffn_w1"], a["L0_ffn_b1"], a["L0_ffn_w2"], a["L0_ffn_b2"]),
                       a["L0_ffn_gate_w"], a["L0_ffn_gate_b"], "top2")
                finish_norm(k, rows, moe, a["L0_ffn_gamma"], a["L0_ffn_beta"])

        if layers >= 3:
            with sbt("rows_c") as rows:
                with sbt("cols_c", [128, 2, N]) as cols, sbt("proj_c") as proj:
                    normalise_all(k, rows, cols)
                    project(k, cols, a["gat_w"], D, rows=proj, table=d["gat4"], also=[(tiles("xn"), rows[:])])
                    scores(k, proj, D, 4, a["gat_a_src"], a["gat_a_tgt"], d["gat4"].rearrange("(t p) f -> p t f", p=P)[:, :, D:D + 4], tgt4, top4)
            edge_sums(k, d["gat4"], k.src_i, D + 4, heads=4, tgt=tgt4, top=top4)
            with sbt("rank_i", [P, NT], I32) as rank_i:
                with sbt("agg_c", [P, NT, D + 4]) as agg, sbt("rows_d") as rows, sbt("local_d") as local:
                    transfer(k, rows[:], tiles("xn"))
                    collect(k, agg, D + 4)
                    divide(k, agg, local, 4, 1e-16, add=rows, bias=a["L1_gnn_gat_b"])
                    finish_norm(k, local, None, a["L1_gnn_ln_local_g"], a["L1_gnn_ln_local_b"], to_x=False)
                    sort_nodes(k, rank_i, a["node_vec"], also=[(tiles("local"), local[:])])
                    permute(k, rows, d["sorted"], rank_i, scatter=True)
                with sbt("xc", [128, 2, N]) as xc, sbt("z", [128, 2, N]) as z, sbt("dbc", [DT_ROW + DT_RANK, N]) as dbc:
                    with sbt("cols_e", [128, 2, N]) as cols:
                        with sbt("rows_e") as rows:
                            transfer(k, rows[:], tiles("sorted"))
                            turn_all(k, rows, cols)
                        mamba_inputs(k, cols, xc, z, dbc, a["in_proj_w"], a["L1_gnn_conv_w"], a["L1_gnn_conv_b"], a["x_proj_w"])
                    with sbt("dt", [128, 2, N]) as dt, sbt("u", [128, 2, N]) as u, sbt("parts", [DT_ROW, N], mybir.dt.bfloat16) as parts:
                        scan_steps(k, xc, dbc, dt, u, parts, a["dt_proj_w"], a["L1_gnn_dt_proj_b"], a["L1_gnn_D_param"])
                        selective_scan(k, xc, z, parts, dt, u, a["L1_gnn_A_log"])
                    project(k, z, a["out_proj_w"], D, table=d["sorted"])
                with sbt("local_f") as local:
                    with sbt("y_f") as y, sbt("rows_f") as rows:
                        permute(k, y, d["sorted"], rank_i, scatter=False, also=[(rows[:], tiles("xn")), (local[:], tiles("local"))])
                        finish_norm(k, y, rows, a["L1_gnn_ln_global_g"], a["L1_gnn_ln_global_b"], to_x=False)
                        with sbt("cols_f", [128, 2, N]) as la, sbt("cols_g", [128, 2, N]) as ya:
                            turn_all(k, local, la)
                            turn_all(k, y, ya)
                            mix(k, local, y, la, ya, a["wl"], a["wg"])
                    with sbt("ff_g") as ff, sbt("gate_g", [P, NT, 1]) as gate, sbt("cols_h", [128, 2, N]) as cols:
                        turn_all(k, local, cols)
                        ones_gate(k, gate)
                        experts(k, cols, gate, ff, Experts(1, 512, ACT.Relu, a["ff1_w"], a["ff1_b"], a["ff2_w"], a["L1_gnn_ff2_b"]))
                        finish_norm(k, local, ff, a["L1_gnn_ln2_g"], a["L1_gnn_ln2_b"])

        if layers >= 4:
            with sbt("gate_i", [P, NT, 4]) as gate, sbt("cols_i", [128, 2, N]) as cols:
                with sbt("rows_i") as rows:
                    normalise_all(k, rows, cols)
                with sbt("h16", [P, NT, 16]) as h16, sbt("agg_i", [P, NT, 20]) as agg, sbt("score_i", [P, NT, 4]) as score:
                    project(k, cols, a["L1_ffn_W_gat"], 16, rows=h16, table=d["small"])
                    scores(k, h16, 16, 4, a["L1_ffn_att_src"], a["L1_ffn_att_dst"], d["small"].rearrange("(t p) f -> p t f", p=P)[:, :, 16:20], tgt4, top4)
                    small_edge_sums(k, d["small"], tgt4, top4, agg, a["ffn_src_c"], a["ffn_dst_c"])
                    divide(k, agg, h16, 4, 1e-16, bias=a["L1_ffn_b_gat"], width=16)
                    finish_norm(k, h16, None, a["L1_ffn_ln_gamma"], a["L1_ffn_ln_beta"], to_x=False, width=16)
                    mean_heads(k, h16, score)
                    gates(k, cols, gate, 4, None, None, "top2", scores=score[:])
                experts(k, cols, gate, k.x, Experts(4, 512, ACT.Gelu, a["L1_ffn_W1"], a["L1_ffn_b1"], a["L1_ffn_W2"], a["L1_ffn_b2"]))

        if layers >= 5:
            with sbt("rows_j") as rows, sbt("cols_j", [128, 2, N]) as cols:
                normalise_all(k, rows, cols)
                project(k, cols, a["gat2_w"], D, rows=rows, table=d["gat8"])
                scores(k, rows, D, 8, a["gat2_a1"], a["gat2_a2"], d["gat8"].rearrange("(t p) f -> p t f", p=P)[:, :, D:D + 8], tgt8, top8)
            edge_sums(k, d["gat8"], k.src_i, D + 8, heads=8, tgt=tgt8, top=top8)
            with sbt("agg_j", [P, NT, D + 8]) as agg, sbt("out_j") as o:
                collect(k, agg, D + 8)
                divide(k, agg, o, 8, 0.0)
                add_to_x(k, o)

        if layers >= 6:
            with sbt("rows_k") as rows, sbt("moe_k") as moe:
                routed(k, rows, moe, 8, 1, Experts(8, 1024, ACT.Relu, a["L2_ffn_w1"], a["L2_ffn_b1"], a["L2_ffn_w2"], a["L2_ffn_b2"]),
                       a["L2_ffn_gate_w"], a["L2_ffn_gate_b"], "top1", capacity=math.ceil(1.25 * N / 8))
                nan_to_num_to_x(k, moe)

        if layers >= 7:
            with sbt("rows_l") as rows, sbt("cols_l", [128, 2, N]) as cols:
                normalise_all(k, rows, cols)
                project(k, cols, a["L3_gnn_lin1_w"], D, table=d["lin1"])
            with sbt("cut", [P, ET]) as cut:
                cutoff(k, cut)
                edge_sums(k, d["lin1"], k.src_i, D, weight=cut, mlp=Mlp(50, a["attr"], a["L3_gnn_mlp_w1"], a["L3_gnn_mlp_b1"], a["L3_gnn_mlp_w2"], a["L3_gnn_mlp_b2"]))
            with sbt("agg_m") as agg, sbt("cols_m", [128, 2, N]) as cols:
                collect(k, agg, D)
                turn_all(k, agg, cols)
                project(k, cols, a["L3_gnn_lin2_w"], D, rows=agg)
                add_bias(k, agg, a["L3_gnn_lin2_b"], softplus=True)
                turn_all(k, agg, cols)
                project(k, cols, a["L3_gnn_lin_w"], D, rows=agg)
                add_bias(k, agg, a["L3_gnn_lin_b"], to_x=True)

        if layers >= 8:
            with sbt("rows_n") as rows:
                routed(k, rows, k.x, 6, 2, Experts(6, 256, ACT.Relu, a["L3_ffn_expert_w1"], a["L3_ffn_expert_b1"], a["L3_ffn_expert_w3"], a["L3_ffn_expert_b3"],
                                                   wm=a["L3_ffn_expert_w2"], bm=a["L3_ffn_expert_b2"]),
                       None, a["L3_ffn_router_b2"], "top2_probs", router=Experts(1, 128, None, a["L3_ffn_router_w1"], a["L3_ffn_router_b1"], a["L3_ffn_router_w2"], None))

        with stage(k) as s:
            stored = s.sem("stored")
            with s.block() as block:
                @block.sync
                def _(sp):
                    sp.dma_start(out_rows, k.x[:]).then_inc(stored, 16)
                    sp.wait_ge(stored, 16)


def layouts(v):
    col = lambda e: np.ascontiguousarray(e.reshape(ET, P).T)
    hid = lambda b: np.ascontiguousarray(b.reshape(b.shape[0], -1, 128).transpose(0, 2, 1).reshape(b.shape[0] * 128, -1))
    w_rel = v["L0_gnn_weight"].reshape(REL, BASES, SUB, SUB)
    return {
        "x": v["x"], "dst": v["dst"], "src_c": col(v["src"]), "dst_c": col(v["dst"]), "type_c": col(v["edge_type_8"]),
        "weight_c": col(v["edge_weight"]), "w_rel": np.ascontiguousarray(w_rel.transpose(1, 2, 0, 3)),
        **{n: v[n] for n in ("L0_ffn_gate_w", "L0_ffn_gate_b", "L0_ffn_w1", "L0_ffn_w2", "L0_ffn_gamma", "L0_ffn_beta")},
        **{n: v[n] for n in (
            "node_vec", "L1_gnn_gat_b", "L1_gnn_ln_local_g", "L1_gnn_ln_local_b", "L1_gnn_ln_global_g", "L1_gnn_ln_global_b", "L1_gnn_ln2_g", "L1_gnn_ln2_b",
            "L1_gnn_conv_w", "L1_gnn_conv_b", "L1_gnn_dt_proj_b", "L1_gnn_A_log", "L1_gnn_D_param", "L1_gnn_ff2_b",
            "L1_ffn_W_gat", "L1_ffn_b_gat", "L1_ffn_ln_gamma", "L1_ffn_ln_beta", "L1_ffn_W1", "L1_ffn_W2",
            "L2_ffn_gate_w", "L2_ffn_gate_b", "L2_ffn_w1", "L2_ffn_w2",
            "L3_gnn_mlp_w1", "L3_gnn_mlp_b1", "L3_gnn_mlp_w2", "L3_gnn_mlp_b2", "L3_gnn_lin1_w", "L3_gnn_lin2_w", "L3_gnn_lin2_b", "L3_gnn_lin_w", "L3_gnn_lin_b",
            "L3_ffn_router_w1", "L3_ffn_router_b1", "L3_ffn_router_w2", "L3_ffn_router_b2", "L3_ffn_expert_w1", "L3_ffn_expert_w2", "L3_ffn_expert_w3")},
        "gat_w": v["L1_gnn_gat_w"].T, "gat_a_src": v["L1_gnn_gat_a_src"].reshape(-1), "gat_a_tgt": v["L1_gnn_gat_a_tgt"].reshape(-1),
        "in_proj_w": v["L1_gnn_in_proj_w"].T, "x_proj_w": v["L1_gnn_x_proj_w"].T, "dt_proj_w": v["L1_gnn_dt_proj_w"].T, "out_proj_w": v["L1_gnn_out_proj_w"].T,
        "wl": v["L1_gnn_wl"].T, "wg": v["L1_gnn_wg"].T, "ff1_w": v["L1_gnn_ff1_w"].T[None], "ff1_b": hid(v["L1_gnn_ff1_b"][None]), "ff2_w": v["L1_gnn_ff2_w"].T[None],
        "L1_ffn_att_src": v["L1_ffn_att_src"].reshape(-1), "L1_ffn_att_dst": v["L1_ffn_att_dst"].reshape(-1),
        "ffn_dst": v["L1_ffn_edge_index"][1],
        "ffn_src_c": v["L1_ffn_edge_index"][0].reshape(-1, 128).T, "ffn_dst_c": v["L1_ffn_edge_index"][1].reshape(-1, 128).T,
        "L1_ffn_b1": hid(v["L1_ffn_b1"]), "L1_ffn_b2": v["L1_ffn_b2"].reshape(-1),
        "gat2_w": v["L2_gnn_W"].transpose(1, 0, 2).reshape(D, D), "gat2_a1": v["L2_gnn_a"][:, :32].reshape(-1), "gat2_a2": v["L2_gnn_a"][:, 32:].reshape(-1),
        "L2_ffn_b1": hid(v["L2_ffn_b1"]), "L2_ffn_b2": v["L2_ffn_b2"].reshape(-1),
        "attr": v["edge_attr_50"].T,
        "L3_ffn_expert_b1": hid(v["L3_ffn_expert_b1"]), "L3_ffn_expert_b2": hid(v["L3_ffn_expert_b2"]), "L3_ffn_expert_b3": v["L3_ffn_expert_b3"].reshape(-1),
        "L0_ffn_b1": hid(v["L0_ffn_b1"]), "L0_ffn_b2": v["L0_ffn_b2"].reshape(-1),
    }


def kernel(**inputs):
    import concourse.bacc as bacc
    from concourse.bass_utils import run_bass_kernel_spmd

    nc = bacc.Bacc("TRN2", target_bir_lowering=False, num_devices=1)
    arrays = layouts({n: np.asarray(v) for n, v in inputs.items()})
    arrays = {f"in_{n}": np.ascontiguousarray(v) for n, v in arrays.items()}
    args = {n[3:]: nc.dram_tensor(n, v.shape, mybir.dt.from_np(v.dtype), kind="ExternalInput").ap() for n, v in arrays.items()}
    out = nc.dram_tensor("out_0", (N, D), F32, kind="ExternalOutput").ap()
    build(nc, args, out, 8)
    r = run_bass_kernel_spmd(nc, [arrays], core_ids=[0])
    return r.results[0]["out_0"]
```
